# Optimizing a Trainium2 kernel written in Bass

```python
import numpy as np
import jax
import jax.numpy as jnp

def _softmax(x, axis=-1):
    return jax.nn.softmax(x, axis=axis)

def _gelu(x):
    return jax.nn.gelu(x, approximate=True)

def _silu(x):
    return jax.nn.silu(x)

def _sigmoid(x):
    return jax.nn.sigmoid(x)

def _layernorm(x, axis=-1, eps=1e-05):
    m = jnp.mean(x, axis=axis, keepdims=True)
    v = jnp.var(x, axis=axis, keepdims=True)
    return (x - m) / jnp.sqrt(v + eps)

def _scatter_add(tgt, idx, src, axis=0):
    return tgt.at[idx].add(src)

def _segment_sum(src, seg, n):
    return jax.ops.segment_sum(src, seg, n)
kernel_name = 'mk_vit_tower_cls_d2_tok_img768_r4_8ee56c'

def setup_inputs(seed: int=0):
    np.random.seed(seed)
    _w = jnp.asarray

    def _rec_inputs():
        import jax
        import jax.numpy as jnp
        _rk = jax.random.key(seed)
        x = 1.64766e-05 + 1.00005 * jax.random.normal(jax.random.fold_in(_rk, 1), (4, 3, 512, 192), jnp.float32)
        cls_tok = 0.02 * jax.random.normal(jax.random.fold_in(_rk, 5), (1, 1, 192), jnp.float32)
        return (x, cls_tok)
    x, cls_tok = _rec_inputs()

    def _L0_tok_setup():
        import jax, jax.numpy as jnp
        import numpy as np
        NUM_BANDS = 6
        D_MODEL = 192
        B, N = (2, 512)
        IN_FEATURES = 3 * NUM_BANDS * 2 * D_MODEL
        key = jax.random.key(seed)
        k_xyz, k_w = jax.random.split(key)
        xyz = jax.random.normal(k_xyz, (B, 3, N, D_MODEL), dtype=jnp.float32)
        freq_bands = 2.0 ** jnp.linspace(0.0, NUM_BANDS - 1, NUM_BANDS).astype(jnp.float32)
        bound = 1.0 / np.sqrt(IN_FEATURES)
        W = jax.random.uniform(k_w, (D_MODEL, IN_FEATURES), dtype=jnp.float32, minval=-bound, maxval=bound)
        return {'xyz': xyz, 'freq_bands': freq_bands, 'W': W}
    _L0_tok_all = _L0_tok_setup()
    _L0_tok_in = {k: v for k, v in _L0_tok_all.items() if k in ('freq_bands', 'W')}
    del _L0_tok_all

    def _L0_attn_setup():
        import jax, jax.numpy as jnp
        import numpy as np
        NUM_HEADS = 12
        OT_REG = 0.1
        SINKHORN_ITERS = 10
        DIAG_VAL = 1000.0

        def _sot(q):
            N = q.shape[-2]
            qn = q / (jnp.linalg.norm(q, axis=-1, keepdims=True) + 1e-08)
            C = 1.0 - jnp.einsum('bhnd,bhmd->bhnm', qn, qn)
            eye = jnp.eye(N, dtype=bool)
            C = jnp.where(eye, DIAG_VAL, C)
            log_K = -C / OT_REG
            log_marg = -jnp.log(jnp.float32(N))
            log_v = jnp.zeros(q.shape[:2] + (N,), dtype=q.dtype)
            for _ in range(SINKHORN_ITERS):
                log_u = log_marg - jax.nn.logsumexp(log_K + log_v[..., None, :], axis=-1)
                log_v = log_marg - jax.nn.logsumexp(log_K + log_u[..., :, None], axis=-2)
            log_T = log_u[..., :, None] + log_K + log_v[..., None, :]
            z = jnp.exp(log_T)
            z = z / jnp.max(z, axis=(-2, -1), keepdims=True)
            z = jnp.where(eye, 1.0, z)
            return z
        key = jax.random.key(seed)
        k1, k2, k3 = jax.random.split(key, 3)
        B, N, C = (64, 64, 192)
        x = jax.random.normal(k1, (B, N, C), dtype=jnp.float32)
        w_qkv = jax.random.normal(k2, (3 * C, C), dtype=jnp.float32) * C ** (-0.5)
        w_proj = jax.random.normal(k3, (C, C), dtype=jnp.float32) * C ** (-0.5)
        b_proj = jnp.zeros((C,), dtype=jnp.float32)
        return {'x': x, 'w_qkv': w_qkv, 'w_proj': w_proj, 'b_proj': b_proj}
    _L0_attn_all = _L0_attn_setup()
    _L0_attn_in = {k: v for k, v in _L0_attn_all.items() if k in ('w_qkv', 'w_proj', 'b_proj')}
    del _L0_attn_all

    def _L0_ffn_setup():
        import jax, jax.numpy as jnp
        import numpy as np
        B, L, D, H, F = (4, 512, 192, 12, 768)
        ROUTE_FRAC = 0.15
        LN_EPS = 1e-05

        def _ln(x, g, b):
            m = jnp.mean(x, axis=-1, keepdims=True)
            v = jnp.mean((x - m) ** 2, axis=-1, keepdims=True)
            return (x - m) * jax.lax.rsqrt(v + LN_EPS) * g + b
        key = jax.random.key(seed)
        ks = jax.random.split(key, 20)
        s = 0.02
        return {'hidden_states': jax.random.normal(ks[0], (B, L, D), dtype=jnp.float32), 'g1': jnp.ones((D,), jnp.float32), 'b1': jnp.zeros((D,), jnp.float32), 'g2': jnp.ones((D,), jnp.float32), 'b2': jnp.zeros((D,), jnp.float32), 'Wr': jax.random.normal(ks[1], (D,), jnp.float32) * s, 'br': jnp.zeros((), jnp.float32), 'Wq': jax.random.normal(ks[2], (D, D), jnp.float32) * s, 'bq': jnp.zeros((D,), jnp.float32), 'Wk': jax.random.normal(ks[3], (D, D), jnp.float32) * s, 'bk': jnp.zeros((D,), jnp.float32), 'Wv': jax.random.normal(ks[4], (D, D), jnp.float32) * s, 'bv': jnp.zeros((D,), jnp.float32), 'Wo': jax.random.normal(ks[5], (D, D), jnp.float32) * s, 'bo': jnp.zeros((D,), jnp.float32), 'Wm': jax.random.normal(ks[6], (D, D), jnp.float32) * s, 'bm': jnp.zeros((D,), jnp.float32), 'W1': jax.random.normal(ks[7], (D, F), jnp.float32) * s, 'bf1': jnp.zeros((F,), jnp.float32), 'W2': jax.random.normal(ks[8], (F, D), jnp.float32) * s, 'bf2': jnp.zeros((D,), jnp.float32)}
    _L0_ffn_all = _L0_ffn_setup()
    _L0_ffn_in = {k: v for k, v in _L0_ffn_all.items() if k in ('g1', 'b1', 'g2', 'b2', 'Wr', 'br', 'Wq', 'bq', 'Wk', 'bk', 'Wv', 'bv', 'Wo', 'bo', 'Wm', 'bm', 'W1', 'bf1', 'W2', 'bf2')}
    del _L0_ffn_all

    def _L1_attn_setup():
        import jax, jax.numpy as jnp
        import numpy as np
        D_MODEL = 192
        H = 6
        DQK = 128
        DV = 64
        SCALE_BASE = 512.0

        def _xpos(x, sign):
            B, T, Hn, d = x.shape
            half = d // 2
            pos = jnp.arange(T, dtype=jnp.float32)
            inv_freq = 1.0 / 10000.0 ** (jnp.arange(half, dtype=jnp.float32) / half)
            angles = pos[:, None] * inv_freq[None, :]
            zeta = (jnp.arange(half, dtype=jnp.float32) + half) / d
            decay = zeta[None, :] ** (sign * pos[:, None] / SCALE_BASE)
            cos_a = (jnp.cos(angles) * decay)[None, :, None, :]
            sin_a = (jnp.sin(angles) * decay)[None, :, None, :]
            x1, x2 = (x[..., :half], x[..., half:])
            return jnp.concatenate([x1 * cos_a - x2 * sin_a, x1 * sin_a + x2 * cos_a], axis=-1)

        def _decay_mask(T):
            gammas = jnp.array([1.0 - 2.0 ** (-(5 + h)) for h in range(H)], dtype=jnp.float32)
            i = jnp.arange(T, dtype=jnp.float32)
            diff = i[:, None] - i[None, :]
            causal = (diff >= 0).astype(jnp.float32)
            D = gammas[:, None, None] ** jnp.clip(diff, 0.0)[None] * causal[None]
            row = jnp.clip(jnp.sum(D, axis=-1, keepdims=True), 1e-06)
            return D / jnp.sqrt(row)
        key = jax.random.key(seed)
        ks = jax.random.split(key, 6)
        B, T = (2, 512)

        def xavier(k, shape):
            lim = float(np.sqrt(6.0 / (shape[0] + shape[1])))
            return jax.random.uniform(k, shape, jnp.float32, -lim, lim)
        return {'x': jax.random.normal(ks[0], (B, T, D_MODEL), jnp.float32), 'Wq': xavier(ks[1], (D_MODEL, H * DQK)), 'Wk': xavier(ks[2], (D_MODEL, H * DQK)), 'Wv': xavier(ks[3], (D_MODEL, H * DV)), 'Wg': xavier(ks[4], (D_MODEL, H * DV)), 'Wo': xavier(ks[5], (H * DV, D_MODEL)), 'gn_weight': jnp.ones((H * DV,), jnp.float32), 'gn_bias': jnp.zeros((H * DV,), jnp.float32)}
    _L1_attn_all = _L1_attn_setup()
    _L1_attn_in = {k: v for k, v in _L1_attn_all.items() if k in ('Wq', 'Wk', 'Wv', 'Wg', 'Wo', 'gn_weight', 'gn_bias')}
    del _L1_attn_all

    def _L1_ffn_setup():
        import jax, jax.numpy as jnp
        import numpy as np
        D_MODEL = 192
        D_FF = 768
        NUM_EXPERTS = 8
        EXPERT_CAPACITY = 256
        key = jax.random.key(seed)
        k0, k1, k2, k3 = jax.random.split(key, 4)
        hidden_states = jax.random.normal(k0, (2, 256, D_MODEL), dtype=jnp.float32)
        router_w = jax.random.normal(k1, (D_MODEL, NUM_EXPERTS), dtype=jnp.float32) * D_MODEL ** (-0.5)
        wi = jax.random.normal(k2, (NUM_EXPERTS, D_MODEL, D_FF), dtype=jnp.float32) * D_MODEL ** (-0.5)
        wo = jax.random.normal(k3, (NUM_EXPERTS, D_FF, D_MODEL), dtype=jnp.float32) * D_FF ** (-0.5)
        return {'hidden_states': hidden_states, 'router_w': router_w, 'wi': wi, 'wo': wo}
    _L1_ffn_all = _L1_ffn_setup()
    _L1_ffn_in = {k: v for k, v in _L1_ffn_all.items() if k in ('router_w', 'wi', 'wo')}
    del _L1_ffn_all
    return {'x': x, 'cls_tok': cls_tok, 'L0_tok_freq_bands': _L0_tok_in['freq_bands'], 'L0_tok_W': _L0_tok_in['W'], 'L0_attn_w_qkv': _L0_attn_in['w_qkv'], 'L0_attn_w_proj': _L0_attn_in['w_proj'], 'L0_attn_b_proj': _L0_attn_in['b_proj'], 'L0_ffn_g1': _L0_ffn_in['g1'], 'L0_ffn_b1': _L0_ffn_in['b1'], 'L0_ffn_g2': _L0_ffn_in['g2'], 'L0_ffn_b2': _L0_ffn_in['b2'], 'L0_ffn_Wr': _L0_ffn_in['Wr'], 'L0_ffn_br': _L0_ffn_in['br'], 'L0_ffn_Wq': _L0_ffn_in['Wq'], 'L0_ffn_bq': _L0_ffn_in['bq'], 'L0_ffn_Wk': _L0_ffn_in['Wk'], 'L0_ffn_bk': _L0_ffn_in['bk'], 'L0_ffn_Wv': _L0_ffn_in['Wv'], 'L0_ffn_bv': _L0_ffn_in['bv'], 'L0_ffn_Wo': _L0_ffn_in['Wo'], 'L0_ffn_bo': _L0_ffn_in['bo'], 'L0_ffn_Wm': _L0_ffn_in['Wm'], 'L0_ffn_bm': _L0_ffn_in['bm'], 'L0_ffn_W1': _L0_ffn_in['W1'], 'L0_ffn_bf1': _L0_ffn_in['bf1'], 'L0_ffn_W2': _L0_ffn_in['W2'], 'L0_ffn_bf2': _L0_ffn_in['bf2'], 'L1_attn_Wq': _L1_attn_in['Wq'], 'L1_attn_Wk': _L1_attn_in['Wk'], 'L1_attn_Wv': _L1_attn_in['Wv'], 'L1_attn_Wg': _L1_attn_in['Wg'], 'L1_attn_Wo': _L1_attn_in['Wo'], 'L1_attn_gn_weight': _L1_attn_in['gn_weight'], 'L1_attn_gn_bias': _L1_attn_in['gn_bias'], 'L1_ffn_router_w': _L1_ffn_in['router_w'], 'L1_ffn_wi': _L1_ffn_in['wi'], 'L1_ffn_wo': _L1_ffn_in['wo']}

def reference(x, cls_tok, L0_tok_freq_bands, L0_tok_W, L0_attn_w_qkv, L0_attn_w_proj, L0_attn_b_proj, L0_ffn_g1, L0_ffn_b1, L0_ffn_g2, L0_ffn_b2, L0_ffn_Wr, L0_ffn_br, L0_ffn_Wq, L0_ffn_bq, L0_ffn_Wk, L0_ffn_bk, L0_ffn_Wv, L0_ffn_bv, L0_ffn_Wo, L0_ffn_bo, L0_ffn_Wm, L0_ffn_bm, L0_ffn_W1, L0_ffn_bf1, L0_ffn_W2, L0_ffn_bf2, L1_attn_Wq, L1_attn_Wk, L1_attn_Wv, L1_attn_Wg, L1_attn_Wo, L1_attn_gn_weight, L1_attn_gn_bias, L1_ffn_router_w, L1_ffn_wi, L1_ffn_wo):
    import jax
    import jax.numpy as jnp

    def _L0_tok_ref(xyz, freq_bands, W):
        import jax, jax.numpy as jnp
        import numpy as np
        NUM_BANDS = 6
        D_MODEL = 192
        B, N = (2, 512)
        IN_FEATURES = 3 * NUM_BANDS * 2 * D_MODEL
        b, c, n, d = xyz.shape
        xb = 2.0 * jnp.pi * xyz[..., None] * freq_bands
        feat = jnp.concatenate([jnp.sin(xb), jnp.cos(xb)], axis=-1)
        feat = feat.reshape(b, n, -1)
        return jnp.einsum('bnf,of->bno', feat, W)

    def _L0_attn_ref(x, w_qkv, w_proj, b_proj):
        import jax, jax.numpy as jnp
        import numpy as np
        NUM_HEADS = 12
        OT_REG = 0.1
        SINKHORN_ITERS = 10
        DIAG_VAL = 1000.0

        def _sot(q):
            N = q.shape[-2]
            qn = q / (jnp.linalg.norm(q, axis=-1, keepdims=True) + 1e-08)
            C = 1.0 - jnp.einsum('bhnd,bhmd->bhnm', qn, qn)
            eye = jnp.eye(N, dtype=bool)
            C = jnp.where(eye, DIAG_VAL, C)
            log_K = -C / OT_REG
            log_marg = -jnp.log(jnp.float32(N))
            log_v = jnp.zeros(q.shape[:2] + (N,), dtype=q.dtype)
            for _ in range(SINKHORN_ITERS):
                log_u = log_marg - jax.nn.logsumexp(log_K + log_v[..., None, :], axis=-1)
                log_v = log_marg - jax.nn.logsumexp(log_K + log_u[..., :, None], axis=-2)
            log_T = log_u[..., :, None] + log_K + log_v[..., None, :]
            z = jnp.exp(log_T)
            z = z / jnp.max(z, axis=(-2, -1), keepdims=True)
            z = jnp.where(eye, 1.0, z)
            return z
        B, N, C = x.shape
        H = NUM_HEADS
        hd = C // H
        scale = hd ** (-0.5)
        qkv = jnp.einsum('bnc,oc->bno', x, w_qkv)
        qkv = qkv.reshape(B, N, 3, H, hd).transpose(2, 0, 3, 1, 4)
        q, k, v = (qkv[0], qkv[1], qkv[2])
        attn = _sot(q)
        attn = jax.nn.softmax(attn * scale, axis=-1)
        out = jnp.einsum('bhnm,bhmd->bhnd', attn, v)
        out = out.transpose(0, 2, 1, 3).reshape(B, N, C)
        out = jnp.einsum('bnc,oc->bno', out, w_proj) + b_proj
        return out

    def _L0_ffn_ref(hidden_states, g1, b1, g2, b2, Wr, br, Wq, bq, Wk, bk, Wv, bv, Wo, bo, Wm, bm, W1, bf1, W2, bf2):
        import jax, jax.numpy as jnp
        import numpy as np
        B, L, D, H, F = (4, 512, 192, 12, 768)
        ROUTE_FRAC = 0.15
        LN_EPS = 1e-05

        def _ln(x, g, b):
            m = jnp.mean(x, axis=-1, keepdims=True)
            v = jnp.mean((x - m) ** 2, axis=-1, keepdims=True)
            return (x - m) * jax.lax.rsqrt(v + LN_EPS) * g + b
        b, l, d = hidden_states.shape
        dh = d // H
        normed = _ln(hidden_states, g1, b1)
        scores = jax.nn.sigmoid(jnp.einsum('bld,d->bl', normed, Wr) + br)
        k = max(1, int(round(ROUTE_FRAC * l)))
        _, idx = jax.lax.top_k(-scores, k)
        attn_mask = jnp.zeros((b, l), bool).at[jnp.arange(b)[:, None], idx].set(True)
        q = (normed @ Wq + bq).reshape(b, l, H, dh)
        kk = (normed @ Wk + bk).reshape(b, l, H, dh)
        v = (normed @ Wv + bv).reshape(b, l, H, dh)
        logits = jnp.einsum('blhd,bmhd->bhlm', q, kk) / jnp.sqrt(jnp.float32(dh))
        probs = jax.nn.softmax(logits, axis=-1)
        ctx = jnp.einsum('bhlm,bmhd->blhd', probs, v).reshape(b, l, d)
        attn_out = ctx @ Wo + bo
        w = scores / (jnp.sum(scores, axis=1, keepdims=True) + 1e-06)
        pooled = jnp.einsum('bl,bld->bd', w, normed)
        mix_out = (normed + scores[..., None] * pooled[:, None, :]) @ Wm + bm
        merged = jnp.where(attn_mask[..., None], attn_out, mix_out)
        h = hidden_states + merged
        n2 = _ln(h, g2, b2)
        ffn = jax.nn.gelu(n2 @ W1 + bf1, approximate=False) @ W2 + bf2
        return h + ffn

    def _L1_attn_ref(x, Wq, Wk, Wv, Wg, Wo, gn_weight, gn_bias):
        import jax, jax.numpy as jnp
        import numpy as np
        D_MODEL = 192
        H = 6
        DQK = 128
        DV = 64
        SCALE_BASE = 512.0

        def _xpos(x, sign):
            B, T, Hn, d = x.shape
            half = d // 2
            pos = jnp.arange(T, dtype=jnp.float32)
            inv_freq = 1.0 / 10000.0 ** (jnp.arange(half, dtype=jnp.float32) / half)
            angles = pos[:, None] * inv_freq[None, :]
            zeta = (jnp.arange(half, dtype=jnp.float32) + half) / d
            decay = zeta[None, :] ** (sign * pos[:, None] / SCALE_BASE)
            cos_a = (jnp.cos(angles) * decay)[None, :, None, :]
            sin_a = (jnp.sin(angles) * decay)[None, :, None, :]
            x1, x2 = (x[..., :half], x[..., half:])
            return jnp.concatenate([x1 * cos_a - x2 * sin_a, x1 * sin_a + x2 * cos_a], axis=-1)

        def _decay_mask(T):
            gammas = jnp.array([1.0 - 2.0 ** (-(5 + h)) for h in range(H)], dtype=jnp.float32)
            i = jnp.arange(T, dtype=jnp.float32)
            diff = i[:, None] - i[None, :]
            causal = (diff >= 0).astype(jnp.float32)
            D = gammas[:, None, None] ** jnp.clip(diff, 0.0)[None] * causal[None]
            row = jnp.clip(jnp.sum(D, axis=-1, keepdims=True), 1e-06)
            return D / jnp.sqrt(row)
        B, T, _ = x.shape
        Q = (x @ Wq).reshape(B, T, H, DQK)
        K = (x @ Wk).reshape(B, T, H, DQK)
        V = (x @ Wv).reshape(B, T, H, DV)
        Q = _xpos(Q, 1.0)
        K = _xpos(K, -1.0)
        scores = jnp.einsum('bihd,bjhd->bhij', Q, K) * DQK ** (-0.5)
        scores = scores * _decay_mask(T)[None]
        out = jnp.einsum('bhij,bjhv->bihv', scores, V)
        concat = out.reshape(B, T, H * DV)
        g = concat.transpose(0, 2, 1).reshape(B, H, DV, T)
        mean = jnp.mean(g, axis=(2, 3), keepdims=True)
        var = jnp.var(g, axis=(2, 3), keepdims=True)
        g = (g - mean) / jnp.sqrt(var + 1e-05)
        g = g.reshape(B, H * DV, T) * gn_weight[None, :, None] + gn_bias[None, :, None]
        normed = g.transpose(0, 2, 1)
        gate = jax.nn.silu(x @ Wg)
        return normed * gate @ Wo

    def _L1_ffn_ref(hidden_states, router_w, wi, wo):
        import jax, jax.numpy as jnp
        import numpy as np
        D_MODEL = 192
        D_FF = 768
        NUM_EXPERTS = 8
        EXPERT_CAPACITY = 256
        B, S, d = hidden_states.shape
        E = router_w.shape[1]
        x = hidden_states.reshape(-1, d)
        logits = x.astype(jnp.float32) @ router_w.astype(jnp.float32)
        probs = jax.nn.softmax(logits, axis=-1).astype(x.dtype)
        p = jnp.max(probs, axis=-1)
        e_idx = jnp.argmax(probs, axis=-1)
        mask = jax.nn.one_hot(e_idx, E, dtype=x.dtype)
        token_priority = jnp.cumsum(mask[:, None, :], axis=-2)[:, 0, :]
        mask = mask * (token_priority <= EXPERT_CAPACITY).astype(x.dtype)
        combine = mask * p[:, None]

        def body(acc, ew):
            Wi_e, Wo_e, w_e = ew
            h = jax.nn.relu(x @ Wi_e) @ Wo_e
            return (acc + w_e[:, None] * h, None)
        out, _ = jax.lax.scan(body, jnp.zeros_like(x), (wi, wo, combine.T))
        return out.reshape(B, S, d)
    h = _L0_tok_ref(x, L0_tok_freq_bands, L0_tok_W)
    h = jnp.concatenate([jnp.broadcast_to(cls_tok, (h.shape[0], 1, h.shape[2])), h], axis=1)
    h = h + _L0_attn_ref(_layernorm(h, axis=-1), L0_attn_w_qkv, L0_attn_w_proj, L0_attn_b_proj)
    h = h + _L0_ffn_ref(_layernorm(h, axis=-1), L0_ffn_g1, L0_ffn_b1, L0_ffn_g2, L0_ffn_b2, L0_ffn_Wr, L0_ffn_br, L0_ffn_Wq, L0_ffn_bq, L0_ffn_Wk, L0_ffn_bk, L0_ffn_Wv, L0_ffn_bv, L0_ffn_Wo, L0_ffn_bo, L0_ffn_Wm, L0_ffn_bm, L0_ffn_W1, L0_ffn_bf1, L0_ffn_W2, L0_ffn_bf2)
    h = h + _L1_attn_ref(_layernorm(h, axis=-1), L1_attn_Wq, L1_attn_Wk, L1_attn_Wv, L1_attn_Wg, L1_attn_Wo, L1_attn_gn_weight, L1_attn_gn_bias)
    h = h + _L1_ffn_ref(_layernorm(h, axis=-1), L1_ffn_router_w, L1_ffn_wi, L1_ffn_wo)
    return h

_drawn_inputs = setup_inputs


def setup_inputs(seed=0):
    import zlib

    import numpy as np

    out = dict(_drawn_inputs(seed))
    spreads = {'L0_attn_b_proj': (0.0, 0.1),
     'L0_ffn_g1': (1.0, 0.2),
     'L0_ffn_b1': (0.0, 0.1),
     'L0_ffn_g2': (1.0, 0.6),
     'L0_ffn_b2': (0.0, 0.569),
     'L0_ffn_bq': (0.0, 0.8),
     'L0_ffn_bk': (0.0, 0.8),
     'L0_ffn_bv': (0.0, 0.6),
     'L0_ffn_bo': (0.0, 0.1),
     'L0_ffn_bm': (0.0, 0.1),
     'L0_ffn_bf1': (0.0, 0.1),
     'L0_ffn_bf2': (0.0, 0.1),
     'L1_attn_gn_weight': (1.0, 0.2),
     'L1_attn_gn_bias': (0.0, 0.1)}
    factors = {'cls_tok': 3.264,
     'L0_ffn_Wq': 8.0,
     'L0_ffn_Wk': 8.0,
     'L0_ffn_Wv': 5.905,
     'L0_ffn_Wo': 4.065}
    for name, (base, spread) in spreads.items():
        noise = np.random.default_rng([zlib.crc32(name.encode()), seed]).standard_normal(out[name].shape)
        drawn = base * np.exp(spread * noise) if base else spread * noise
        out[name] = jnp.asarray(drawn.astype(out[name].dtype))
    for name, factor in factors.items():
        out[name] = (out[name] * factor).astype(out[name].dtype)
    return out
```

```python
from contextlib import ExitStack

import numpy as np

import concourse.bass as bass
from concourse import mybir

F32 = mybir.dt.float32
ALU = mybir.AluOpType
ACT = mybir.ActivationFunctionType
AX_X = mybir.AxisListType.X

B, C, T, D = 4, 3, 512, 192
N = T + 1
P = 128
TPB = T // P
NT = B * TPB + 1
CLS = B * TPB
NTOK = B * N
HALF = 96
NP = 514
BANDS = 6
JT = C * D
LN_EPS = 1e-5

HEADS, HD = 12, 16
HG = 4
GROUPS = HEADS // HG
R = P // HG
CH = T // R + 1
ITERS = 10
INV_REG = 10.0

TWO_PI_BELOW = 6.283185
ROUND = 1.5 * 2.0 ** 23


class Tally:

    def __init__(self, sem):
        self.sem, self.n = sem, 0

    def mark(self, ins):
        ins.then_inc(self.sem, 1)
        self.n += 1
        return self.n


def build_program(nc, A, out, dbg):
    root = ExitStack()
    with root:
        taken = []

        def sem(name):
            s = nc.alloc_semaphore(name)
            taken.append(s)
            return s

        def recycle():
            with nc.Block() as block:
                @block.sync
                def _(sp):
                    for s in taken:
                        sp.sem_clear(s)
            for s in taken:
                nc.release_semaphore(s)
            taken.clear()

        def make_sb(ctx):
            return lambda name, shape, dt=F32: ctx.enter_context(nc.sbuf_tensor(name, shape, dt))

        def make_ps(ctx):
            return lambda name, shape: ctx.enter_context(nc.psum_tensor(name, shape, F32))

        rsb = make_sb(root)
        H = rsb("H", [P, NT, D])
        ident = rsb("ident", [P, P])
        ones = rsb("ones", [P, P])

        constants_stage(nc, sem, H, ident, ones)
        tokenizer_stage(nc, sem, make_sb, make_ps, A, H, ident)
        dump(nc, sem, dbg, "h1", H)
        with ExitStack() as attn:
            asb = make_sb(attn)
            WprojT = asb("WprojT", [64, GROUPS, D])
            bproj = asb("bproj", [1, D])
            QT = asb("QT", [64, GROUPS, B, NP])
            V = asb("V", [P, B, TPB, D])
            VC = asb("VC", [1, B, D])
            with ExitStack() as x_ctx:
                xsb = make_sb(x_ctx)
                WqkvT = xsb("WqkvT", [HALF, 2, 3 * D])
                XT = xsb("XT", [HALF, 2, NTOK])
                X = xsb("X", [P, NT, D])
                norm_stage(nc, sem, make_sb, make_ps, "ln1", H, X, XT, ident)
                sinkhorn_weights_stage(nc, sem, make_sb, make_ps, A, WqkvT, WprojT, bproj, ident)
                sinkhorn_query_stage(nc, sem, make_sb, make_ps, XT, WqkvT, QT, V, VC, ident)
            sinkhorn_stage(nc, sem, make_sb, make_ps, QT, V, VC, ones)
            sinkhorn_out_stage(nc, sem, make_ps, QT, WprojT, bproj, ones, H)
        dump(nc, sem, dbg, "h2", H)
        recycle()
        routed_stage(nc, sem, make_sb, make_ps, A, H, ident, ones)
        dump(nc, sem, dbg, "h3", H)
        recycle()
        retention_stage(nc, sem, make_sb, make_ps, A, H, ident, ones)
        dump(nc, sem, dbg, "h4", H)
        recycle()
        moe_stage(nc, sem, make_sb, make_ps, A, H, ident, ones)
        final_stage(nc, sem, H, out)


def dump(nc, sem, dbg, name, H):
    if name not in dbg:
        return
    s = sem("dump_" + name)
    with nc.Block() as block:
        @block.sync
        def _(sp):
            sp.dma_start(dbg[name], H[:]).then_inc(s, 16)
            sp.wait_ge(s, 16)


def final_stage(nc, sem, H, out):
    stored = sem("out_stored")
    with nc.Block() as block:
        @block.sync
        def _(sp):
            for b in range(B):
                sp.dma_start(out[b, 1:N, :].rearrange("(t p) d -> p t d", p=P),
                             H[:, TPB * b:TPB * b + TPB, :]).then_inc(stored, 16)
            sp.dma_start(out[:, 0, :], H[0:B, CLS, :]).then_inc(stored, 16)
            sp.wait_ge(stored, 16 * (B + 1))


def constants_stage(nc, sem, H, ident, ones):
    filled = sem("const_filled")
    done = sem("const_done")
    with nc.Block() as block:
        @block.gpsimd
        def _(pool):
            nc.gpsimd.memset(ident[:], 0.0).then_inc(filled, 1)
            pool.wait_ge(filled, 1)
            nc.gpsimd.affine_select(out=ident[:], in_=ident[:], compare_op=ALU.not_equal, fill=1.0, base=0,
                                    pattern=[[-1, P]], channel_multiplier=1).then_inc(done, 1)

        @block.vector
        def _(dve):
            nc.vector.memset(ones[:], 1.0)
            nc.vector.memset(H[:, CLS, :], 0.0)


def tokenizer_stage(nc, sem, make_sb, make_ps, A, H, ident):
    ARGS = [(c, k) for c in range(4) for k in range(BANDS)] + [(4, m) for m in range(BANDS // 2)]
    NA, NU = len(ARGS), 2 * len(ARGS)
    FR, MR, XR = 6, 3, 4
    with ExitStack() as ctx:
        sb, ps = make_sb(ctx), make_ps(ctx)
        WT = sb("tok_WT", [P, NU, D])
        XN = sb("tok_x", [P, TPB, JT + 64])
        XJ = sb("tok_xj", [P, 5, T])
        band = sb("tok_band", [P, BANDS])
        pair = sb("tok_pair", [P, BANDS // 2])
        half_pi = sb("tok_half_pi", [P, 1])
        turns = sb("tok_turns", [P, XR, T])
        whole = sb("tok_whole", [P, 2, T])
        back = sb("tok_back", [P, MR, T])
        size = sb("tok_size", [P, 2, T])
        feat = sb("tok_feat", [P, FR, T])
        acc = ps("tok_acc", [P, TPB, 512])
        stage = ps("tok_stage", [P, 4, 512])
        w_loaded = [sem(f"tok_w_loaded{c}") for c in range(5)]
        x_loaded, small_loaded = sem("tok_x_loaded"), sem("tok_small_loaded")
        cls_loaded = sem("tok_cls_loaded")
        wt_turned, wt_kept_dve, wt_kept_act = sem("tok_wt_turned"), sem("tok_wt_kept_dve"), sem("tok_wt_kept_act")
        x_turned, x_kept = sem("tok_x_turned"), sem("tok_x_kept")
        turns_ready, whole_ready, back_ready = sem("tok_turns_ready"), sem("tok_whole_ready"), sem("tok_back_ready")
        size_ready = sem("tok_size_ready")
        feat_ready, feat_used = sem("tok_feat_ready"), sem("tok_feat_used")
        acc_kept = sem("tok_acc_kept")
        const_ready, paired = sem("tok_const_ready"), sem("tok_paired")

        x_dram = A["x"].rearrange("b c n d -> (b c n d)").rearrange("(b t p j) -> b p t j", b=B, t=TPB, p=P)
        f_dram = A["L0_tok_freq_bands"].rearrange("(a s) -> a s", a=1)

        with ExitStack() as w_ctx:
            WN = make_sb(w_ctx)("tok_WN", [HALF, 2, JT * 2 * BANDS])
            WP = make_sb(w_ctx)("tok_WP", [HALF, 2, 2 * BANDS, 64])
            W_s = WN[:].rearrange("p h (j s) -> p h j s", s=2 * BANDS)
            w_paired = sem("tok_w_paired")
            w_dram = A["L0_tok_W"].rearrange("(h p) f -> p h f", p=HALF)
            with nc.Block() as block:
                @block.sync
                def _(sp):
                    for c in range(5):
                        a, z = c * P * 2 * BANDS, min(JT, (c + 1) * P) * 2 * BANDS
                        sp.dma_start(WN[:, :, a:z], w_dram[:, :, a:z]).then_inc(w_loaded[c], 16)

                @block.tensor
                def _(pe):
                    for a, (c, k) in enumerate(ARGS):
                        if c == 4:
                            pe.wait_ge(w_paired, 2)
                        elif a % BANDS == 0:
                            pe.wait_ge(w_loaded[c], 16)
                        if a >= 4:
                            pe.wait_ge(*((wt_kept_dve, (a - 4) // 2 + 1) if a % 2 == 0 else (wt_kept_act, (a - 5) // 2 + 1)))
                        for trig in range(2):
                            for h in range(2):
                                if c < 4:
                                    src = W_s[:, h, c * P:(c + 1) * P, trig * BANDS + k]
                                else:
                                    s = trig * BANDS + 2 * k
                                    src = WP[:, h, s:s + 2, :].rearrange("p s j -> p (s j)")
                                o = trig * D + h * HALF
                                last = nc.tensor.transpose(stage[:, a % 4, o:o + HALF], src, ident[0:HALF, 0:HALF])
                        last.then_inc(wt_turned, 1)

                @block.gpsimd
                def _(pool):
                    pool.wait_ge(w_loaded[4], 16)
                    for h in range(2):
                        nc.gpsimd.tensor_copy(WP[:, h, :, :],
                                              W_s[:, h, 4 * P:JT, :].rearrange("p j s -> p s j")).then_inc(w_paired, 1)

                @block.vector
                def _(dve):
                    nc.vector.memset(half_pi[:], float(np.pi / 2)).then_inc(const_ready, 1)
                    for a in range(0, NA, 2):
                        dve.wait_ge(wt_turned, a + 1)
                        nc.vector.tensor_copy(WT[:, 2 * a:2 * a + 2, :], stage[:, a % 4, 0:2 * D].rearrange(
                            "p (u o) -> p u o", u=2)).then_inc(wt_kept_dve, 1)

                @block.scalar
                def _(act):
                    for a in range(1, NA, 2):
                        act.wait_ge(wt_turned, a + 1)
                        nc.scalar.activation(WT[:, 2 * a:2 * a + 2, :], stage[:, a % 4, 0:2 * D].rearrange(
                            "p (u o) -> p u o", u=2), ACT.Copy).then_inc(wt_kept_act, 1)

        with nc.Block() as block:
            @block.sync
            def _(sp):
                sp.dma_start(band[:], f_dram[0].partition_broadcast(P)).then_inc(small_loaded, 16)
                for b in range(B):
                    sp.dma_start(H[b:b + 1, CLS, :], A["cls_tok"][0]).then_inc(cls_loaded, 16)
                with sp.Fori(0, B) as b:
                    sp.wait_ge(x_turned, 5 * b)
                    sp.dma_start(XN[:, :, 0:JT], x_dram[b]).then_inc(x_loaded, 16)
                    sp.dma_start(XN[:, :, JT:JT + 64], x_dram[b, :, :, JT - 64:JT]).then_inc(x_loaded, 16)
                sp.wait_ge(cls_loaded, 16 * B)

            @block.tensor
            def _(pe):
                with pe.Fori(0, B) as b:
                    pe.wait_ge(x_loaded, 32 * b + 32)
                    pe.wait_ge(x_kept, 5 * b)
                    for c in range(5):
                        if c == 4:
                            pe.wait_ge(x_kept, 5 * b + 1)
                        for t in range(TPB):
                            last = nc.tensor.transpose(stage[:, c % 4, t * P:(t + 1) * P],
                                                       XN[:, t, c * P:(c + 1) * P], ident[:])
                        last.then_inc(x_turned, 1)
                    for u in range(NU):
                        if u == 0:
                            pe.wait_ge(acc_kept, TPB * b)
                        pe.wait_ge(feat_ready, NU * b + u + 1)
                        for t in range(TPB):
                            last = nc.tensor.matmul(acc[:, t, 0:D], feat[:, u % FR, t * P:(t + 1) * P], WT[:, u, :],
                                                    start=(u == 0), stop=(u == NU - 1))
                        last.then_inc(feat_used, 1)

            @block.gpsimd
            def _(pool):
                pool.wait_ge(small_loaded, 16)
                for k in range(2):
                    nc.gpsimd.tensor_copy(pair[64 * k:64 * k + 64, :], band[64 * k:64 * k + 64, k:BANDS:2]).then_inc(paired, 1)
                pool.wait_ge(paired, 2)
                with pool.Fori(0, B) as b:
                    for a, (c, k) in enumerate(ARGS):
                        if a % BANDS == 0:
                            pool.wait_ge(x_kept, 5 * b + c + 1)
                        if a >= XR:
                            pool.wait_ge(back_ready, NA * b + a - XR + 1)
                        f = band[:, k:k + 1] if c < 4 else pair[:, k:k + 1]
                        nc.gpsimd.tensor_tensor(turns[:, a % XR, :], XJ[:, c, :], f.broadcast_to((P, T)),
                                                ALU.mult).then_inc(turns_ready, 1)

            @block.vector
            def _(dve):
                with dve.Fori(0, B) as b:
                    for c in range(5):
                        if c == 0:
                            dve.wait_ge(turns_ready, NA * b)
                        dve.wait_ge(x_turned, 5 * b + c + 1)
                        nc.vector.tensor_copy(XJ[:, c, :], stage[:, c % 4, :]).then_inc(x_kept, 1)
                    for a in range(NA):
                        dve.wait_ge(turns_ready, NA * b + a + 1)
                        nc.vector.tensor_scalar(whole[:, a % 2, :], turns[:, a % XR, :], ROUND, None,
                                                ALU.add).then_inc(whole_ready, 1)
                        if a >= MR:
                            dve.wait_ge(feat_ready, NU * b + 2 * (a - MR) + 1)
                            dve.wait_ge(size_ready, NA * b + a - MR + 1)
                        else:
                            dve.wait_ge(feat_ready, NU * b)
                        dve.wait_ge(whole_ready, NA * b + a + 1)
                        nc.vector.scalar_tensor_tensor(out=back[:, a % MR, :], in0=whole[:, a % 2, :], scalar=-ROUND,
                                                       in1=turns[:, a % XR, :], op0=ALU.add,
                                                       op1=ALU.subtract).then_inc(back_ready, 1)

            @block.scalar
            def _(act):
                nc.scalar.preload_act_table_set("trig_and_small")
                with act.Fori(0, B) as b:
                    for a in range(NA):
                        act.wait_ge(back_ready, NA * b + a + 1)
                        for trig in range(2):
                            u = 2 * a + trig
                            if trig == 1:
                                act.wait_ge(size_ready, NA * b + a + 1)
                            if u >= FR:
                                act.wait_ge(feat_used, NU * b + u - FR + 1)
                            else:
                                act.wait_ge(feat_used, NU * b)
                            if trig == 0:
                                nc.scalar.activation(feat[:, u % FR, :], back[:, a % MR, :], ACT.Sin,
                                                     scale=-TWO_PI_BELOW).then_inc(feat_ready, 1)
                                nc.scalar.activation(size[:, a % 2, :], back[:, a % MR, :],
                                                     ACT.Abs).then_inc(size_ready, 1)
                            else:
                                nc.scalar.activation(feat[:, u % FR, :], size[:, a % 2, :], ACT.Sin,
                                                     bias=half_pi[:], scale=-TWO_PI_BELOW).then_inc(feat_ready, 1)
                    act.wait_ge(feat_used, NU * b + NU)
                    act.wait_ge(cls_loaded, 16 * B)
                    for t in range(TPB):
                        nc.scalar.activation(H[:, TPB * b + t, :], acc[:, t, 0:D], ACT.Copy).then_inc(acc_kept, 1)


def norm_stage(nc, sem, make_sb, make_ps, name, src, dst, dstT, ident, inner=None, gain=None, shift=None):
    with ExitStack() as ctx:
        sb, ps = make_sb(ctx), make_ps(ctx)
        stats = sb(name + "_stats", [P, NT, 6])
        moments = sb(name + "_moments", [P, NT, 2])
        power = sb(name + "_power", [P, NT])
        rstd = sb(name + "_rstd", [P, NT])
        turn = ps(name + "_turn", [P, 4, 512])
        stats_ready, moments_ready = sem(name + "_stats_ready"), sem(name + "_moments_ready")
        pool_done, rstd_ready = sem(name + "_pool_done"), sem(name + "_rstd_ready")
        normed, turned = sem(name + "_normed"), sem(name + "_turned")
        kept_dve, kept_act = sem(name + "_kept_dve"), sem(name + "_kept_act")
        rounds = [(src, inner), (inner, dst)] if inner is not None else [(src, dst)]

        with nc.Block() as block:
            @block.vector
            def _(dve):
                for r, (a, z) in enumerate(rounds):
                    if r:
                        dve.wait_ge(normed, NT)
                    for t in range(NT):
                        nc.vector.bn_stats(stats[:, t, :], a[:, t, :]).then_inc(stats_ready, 1)
                    for t in range(NT):
                        dve.wait_ge(stats_ready, NT * r + t + 1)
                        nc.vector.bn_aggr(moments[:, t, :], stats[:, t, :]).then_inc(moments_ready, 1)
                    dve.wait_ge(moments_ready, NT * (r + 1))
                    dve.wait_ge(rstd_ready, r + 1)
                    affine = r == len(rounds) - 1 and gain is not None
                    base = NT * r
                    for t in range(NT):
                        nc.vector.tensor_scalar(z[:, t, :], a[:, t, :], moments[:, t, 0:1], rstd[:, t:t + 1],
                                                ALU.subtract, ALU.mult).then_inc(normed, 1)
                    if affine:
                        for k, (op, v) in enumerate(((ALU.mult, gain), (ALU.add, shift))):
                            for t in range(NT):
                                dve.wait_ge(normed, base + NT * k + t + 1)
                                nc.vector.tensor_tensor(z[:, t, :], z[:, t, :], v[:], op).then_inc(normed, 1)
                for t in range(NT):
                    n = P if t < CLS else B
                    dve.wait_ge(turned, 2 * t + 1)
                    nc.vector.tensor_copy(dstT[:, 0, t * P:t * P + n], turn[0:HALF, (2 * t) % 4, 0:n]).then_inc(kept_dve, 1)

            @block.gpsimd
            def _(pool):
                nc.gpsimd.memset(power[:], -0.5).then_inc(pool_done, 1)
                for r in range(len(rounds)):
                    pool.wait_ge(moments_ready, NT * (r + 1))
                    pool.wait_ge(pool_done, r + 1)
                    nc.gpsimd.tensor_scalar(rstd[:], moments[:, :, 1], LN_EPS, None, ALU.add).then_inc(pool_done, 1)
                    pool.wait_ge(pool_done, r + 2)
                    nc.gpsimd.tensor_tensor(rstd[:], rstd[:], power[:], ALU.pow).then_inc(rstd_ready, 1)

            @block.tensor
            def _(pe):
                before = NT * (len(rounds) - 1) + (2 * NT if gain is not None else 0)
                for t in range(NT):
                    n = P if t < CLS else B
                    pe.wait_ge(normed, before + t + 1)
                    for h in range(2):
                        if t >= 2:
                            pe.wait_ge(kept_dve if h == 0 else kept_act, t - 1)
                        nc.tensor.transpose(turn[0:HALF, (2 * t + h) % 4, 0:n], dst[0:n, t, h * HALF:(h + 1) * HALF],
                                            ident[0:n, 0:n]).then_inc(turned, 1)

            @block.scalar
            def _(act):
                for t in range(NT):
                    n = P if t < CLS else B
                    act.wait_ge(turned, 2 * t + 2)
                    nc.scalar.activation(dstT[:, 1, t * P:t * P + n], turn[0:HALF, (2 * t + 1) % 4, 0:n],
                                         ACT.Copy).then_inc(kept_act, 1)


def sinkhorn_weights_stage(nc, sem, make_sb, make_ps, A, WqkvT, WprojT, bproj, ident):
    NB = 3 * D // HALF
    with ExitStack() as ctx:
        sb, ps = make_sb(ctx), make_ps(ctx)
        qkv = sb("skw_qkv", [HALF, NB, D])
        proj = sb("skw_proj", [HALF, 2, D])
        turn = ps("skw_turn", [P, 8, 512])
        loaded, turned, kept = sem("skw_loaded"), sem("skw_turned"), sem("skw_kept")
        with nc.Block() as block:
            @block.sync
            def _(sp):
                sp.dma_start(qkv[:], A["L0_attn_w_qkv"].rearrange("(k p) c -> p k c", p=HALF)).then_inc(loaded, 16)
                sp.dma_start(proj[:], A["L0_attn_w_proj"].rearrange("(k p) c -> p k c", p=HALF)).then_inc(loaded, 16)
                sp.dma_start(bproj[:], A["L0_attn_b_proj"].rearrange("(a c) -> a c", a=1)).then_inc(loaded, 16)
                sp.wait_ge(loaded, 48)

            @block.tensor
            def _(pe):
                pe.wait_ge(loaded, 48)
                for h in range(2):
                    for k in range(NB):
                        last = nc.tensor.transpose(turn[0:HALF, 3 * h + k // 2, (k % 2) * HALF:(k % 2 + 1) * HALF],
                                                   qkv[:, k, h * HALF:(h + 1) * HALF], ident[0:HALF, 0:HALF])
                last.then_inc(turned, 1)
                for g in range(GROUPS):
                    for k in range(2):
                        o = g * D + k * HALF
                        bank, o = (6, o) if g < 2 else (7, k * HALF)
                        last = nc.tensor.transpose(turn[0:64, bank, o:o + HALF], proj[:, k, 64 * g:64 * g + 64],
                                                   ident[0:HALF, 0:HALF])
                last.then_inc(turned, 1)

            @block.vector
            def _(dve):
                dve.wait_ge(turned, 2)
                for h in range(2):
                    nc.vector.tensor_copy(WqkvT[:, h, :].rearrange("p (a o) -> p a o", a=3),
                                          turn[0:HALF, 3 * h:3 * h + 3, 0:D])
                nc.vector.tensor_copy(WprojT[:, 0:2, :], turn[0:64, 6, 0:2 * D].rearrange("p (g o) -> p g o", g=2))
                nc.vector.tensor_copy(WprojT[:, 2, :], turn[0:64, 7, 0:D])


def sinkhorn_query_stage(nc, sem, make_sb, make_ps, XT, WqkvT, QT, V, VC, ident):
    with ExitStack() as ctx:
        sb, ps = make_sb(ctx), make_ps(ctx)
        Q = sb("skq_q", [P, NT, D])
        square = sb("skq_square", [P, 2, D])
        norm = sb("skq_norm", [P, NT * HEADS])
        half = sb("skq_half", [P, NT * HEADS])
        scale = sb("skq_scale", [P, NT * HEADS])
        qp = ps("skq_qp", [P, 2, 512])
        turn = ps("skq_turn", [P, 6, 512])
        q_ready, q_kept, sq_ready, n2_ready = sem("skq_q_ready"), sem("skq_q_kept"), sem("skq_sq_ready"), sem("skq_n2_ready")
        zeroed, pooled, scaled = sem("skq_zeroed"), sem("skq_pooled"), sem("skq_scaled")
        v_ready, v_kept = sem("skq_v_ready"), sem("skq_v_kept")
        q_normed, turned, kept = sem("skq_q_normed"), sem("skq_turned"), sem("skq_kept")
        with nc.Block() as block:
            @block.tensor
            def _(pe):
                for t in range(NT):
                    n = P if t < CLS else B
                    if t >= 2:
                        pe.wait_ge(q_kept, t - 1)
                    for h in range(2):
                        last = nc.tensor.matmul(qp[0:n, t % 2, 0:D], XT[:, h, t * P:t * P + n], WqkvT[:, h, 0:D],
                                                start=(h == 0), stop=(h == 1))
                    last.then_inc(q_ready, 1)
                pe.wait_ge(q_kept, NT)
                for t in range(CLS + B):
                    n, first = (P, t * P) if t < CLS else (1, t - CLS + B * T)
                    if t >= 2:
                        pe.wait_ge(v_kept, t - 1)
                    for h in range(2):
                        last = nc.tensor.matmul(qp[0:n, t % 2, 0:D], XT[:, h, first:first + n], WqkvT[:, h, 2 * D:3 * D],
                                                start=(h == 0), stop=(h == 1))
                    last.then_inc(v_ready, 1)
                for t in range(NT):
                    n = P if t < CLS else B
                    pe.wait_ge(q_normed, 1)
                    if t >= 2:
                        pe.wait_ge(kept, t - 1)
                    for g in range(GROUPS):
                        last = nc.tensor.transpose(turn[0:64, t % 2, g * P:g * P + n], Q[0:n, t, 64 * g:64 * g + 64],
                                                   ident[0:n, 0:n])
                    last.then_inc(turned, 1)

            @block.scalar
            def _(act):
                for t in range(NT):
                    n = P if t < CLS else B
                    act.wait_ge(q_ready, t + 1)
                    if t == CLS:
                        act.wait_ge(zeroed, 1)
                    nc.scalar.activation(Q[0:n, t, :], qp[0:n, t % 2, 0:D], ACT.Copy).then_inc(q_kept, 1)
                for t in range(CLS + B):
                    act.wait_ge(v_ready, t + 1)
                    n = P if t < CLS else 1
                    dst = V[:, t // TPB, t % TPB, :] if t < CLS else VC[:, t - CLS, :]
                    nc.scalar.activation(dst, qp[0:n, t % 2, 0:D], ACT.Copy).then_inc(v_kept, 1)

            @block.vector
            def _(dve):
                nc.vector.memset(Q[:, CLS, :], 0.0).then_inc(zeroed, 1)
                for t in range(NT):
                    dve.wait_ge(q_kept, t + 1)
                    nc.vector.tensor_tensor(square[:, t % 2, :], Q[:, t, :], Q[:, t, :], ALU.mult).then_inc(sq_ready, 1)
                    dve.wait_ge(sq_ready, t + 1)
                    nc.vector.reduce_sum(norm[:, t * HEADS:(t + 1) * HEADS],
                                         square[:, t % 2, :].rearrange("p (h d) -> p h d", d=HD), AX_X).then_inc(n2_ready, 1)
                dve.wait_ge(pooled, 3)
                nc.vector.reciprocal(scale[:], norm[:]).then_inc(scaled, 1)
                dve.wait_ge(scaled, 1)
                q_all = Q[:].rearrange("p t (h d) -> p (t h) d", d=HD)
                nc.vector.tensor_tensor(q_all, q_all, scale[:].unsqueeze(2).broadcast_to((P, NT * HEADS, HD)),
                                        ALU.mult).then_inc(q_normed, 1)
                for t in range(NT):
                    n = P if t < CLS else B
                    dve.wait_ge(turned, t + 1)
                    src = turn[0:64, t % 2, 0:GROUPS * P].rearrange("p (g n) -> p g n", g=GROUPS)[:, :, 0:n]
                    dst = QT[:, :, t // TPB, (t % TPB) * P:(t % TPB) * P + P] if t < CLS else QT[:, :, :, T]
                    nc.vector.tensor_copy(dst, src).then_inc(kept, 1)

            @block.gpsimd
            def _(pool):
                nc.gpsimd.memset(half[:], 0.5).then_inc(pooled, 1)
                pool.wait_ge(pooled, 1)
                pool.wait_ge(n2_ready, NT)
                nc.gpsimd.tensor_tensor(norm[:], norm[:], half[:], ALU.pow).then_inc(pooled, 1)
                pool.wait_ge(pooled, 2)
                nc.gpsimd.tensor_scalar(norm[:], norm[:], 1e-8, None, ALU.add).then_inc(pooled, 1)


def sinkhorn_stage(nc, sem, make_sb, make_ps, QT, V, VC, ones):
    L = 255
    S = 2
    HALVES = ((0, 512 - L), (512 - L, N))
    SCALE = float(HD) ** -0.5
    BPS = B // S
    JUNK = 3
    DVE_CONST = 8
    with ExitStack() as ctx:
        sb, ps = make_sb(ctx), make_ps(ctx)
        K = [sb(f"sk_K{s}", [P, CH, NP]) for s in range(S)]
        diag = [sb(f"sk_diag{s}", [P, CH, P]) for s in range(S)]
        row = sb("sk_row", [P, S, NP])
        logs = sb("sk_logs", [P, S, NP])
        junk = sb("sk_junk", [P, JUNK, NP])
        sums = sb("sk_sums", [P, S, CH])
        col = sb("sk_col", [P, S, CH])
        peak = sb("sk_peak", [P, S, CH])
        weight = sb("sk_weight", [P, S, CH])
        top = sb("sk_top", [P, 4])
        spread = sb("sk_spread", [P, 2, R])
        head_mask = sb("sk_head_mask", [P, HG])
        cls_head_mask = sb("sk_cls_head_mask", [P, HG])
        feat_mask = sb("sk_feat_mask", [64, HG])
        cls_mask = sb("sk_cls_mask", [P, 1])
        not_cls = sb("sk_not_cls", [P, 1])
        off_diag = sb("sk_off_diag", [P, R])
        on_diag = sb("sk_on_diag", [P, R])
        shift = sb("sk_shift", [P, 2])
        QB = sb("sk_QB", [64, S, NP])
        QS = sb("sk_QS", [64, CH, P])
        VS = sb("sk_VS", [P, CH, P])
        den = sb("sk_den", [64, 2, NP])
        w_ps = ps("sk_w", [P, 2 * S, 512])
        e_ps = ps("sk_e", [P, 4, 512])

        def pair(x, k):
            return x[:, 2 * k:2 * k + 2, :].rearrange("p a n -> p (a n)")[:, L:L + N]

        def sems(name):
            return [sem(f"sk_{name}{s}") for s in range(S)]

        const_pool, const_dve = sem("sk_const_pool"), sem("sk_const_dve")
        slot_ready, dots_ready, k_ready, k_masked = sems("slot_ready"), sems("dots_ready"), sems("k_ready"), sems("k_masked")
        qs_ready = sem("sk_qs_ready")
        diag_ready, w_ready, logs_ready, row_ready = sems("diag_ready"), sems("w_ready"), sems("logs_ready"), sems("row_ready")
        sums_ready, col_ready = sems("sums_ready"), sems("col_ready")
        top_step, weight_ready = sems("top_step"), sems("weight_ready")
        e_ready, e_cleared, e_set = sems("e_ready"), sems("e_cleared"), sems("e_set")
        vs_ready = sems("vs_ready")
        o_ready, den_log, den_ready, o_kept = sems("o_ready"), sems("den_log"), sems("den_ready"), sems("o_kept")

        def near_diagonal(s):
            flat = K[s][:].rearrange("p c n -> p (c n)")[:, 0:(CH - 1) * (NP + R)]
            return flat.rearrange("p (c n) -> p c n", n=NP + R)[:, :, 0:R]

        with nc.Block() as block:
            @block.gpsimd
            def _(pool):
                n = 0
                pool.wait_ge(const_dve, 1)
                nc.gpsimd.affine_select(out=feat_mask[:], in_=feat_mask[:], compare_op=ALU.is_ge, fill=0.0,
                                        base=0, pattern=[[-HD, HG]], channel_multiplier=1).then_inc(const_pool, 1)
                pool.wait_ge(const_pool, 1)
                nc.gpsimd.affine_select(out=feat_mask[:], in_=feat_mask[:], compare_op=ALU.is_ge, fill=0.0,
                                        base=HD - 1, pattern=[[HD, HG]], channel_multiplier=-1).then_inc(const_pool, 1)
                for k in range(HG):
                    pool.wait_ge(const_pool, k + 2)
                    nc.gpsimd.affine_select(out=on_diag[k * R:(k + 1) * R, :], in_=on_diag[k * R:(k + 1) * R, :],
                                            compare_op=ALU.not_equal, fill=1.0, base=0, pattern=[[-1, R]],
                                            channel_multiplier=1).then_inc(const_pool, 1)
                CONST = 2 + HG
                pool.wait_ge(const_pool, CONST)
                pool.wait_ge(const_dve, DVE_CONST)
                with pool.Fori(0, BPS) as half:
                    with pool.Fori(0, GROUPS) as g:
                        i = half * GROUPS + g
                        for s in range(S):
                            b = half + BPS * s
                            pool.wait_ge(dots_ready[s], CH * i)
                            pool.wait_ge(const_pool, CONST)
                            nc.gpsimd.tensor_copy(QB[:, s, 0:N], QT[:, g, b, 0:N]).then_inc(slot_ready[s], 1)
                            pool.wait_ge(dots_ready[1 - s], CH * (i + s))
                            pool.wait_ge(slot_ready[s], i + 1)
                            q = QB[:, s, 0:T].rearrange("p (c r) -> p c r", r=R)
                            for k in range(HG):
                                nc.gpsimd.tensor_tensor(
                                    QS[:, 0:CH - 1, k * R:(k + 1) * R], q,
                                    feat_mask[:, k:k + 1].unsqueeze(1).broadcast_to((64, CH - 1, R)),
                                    ALU.mult).then_inc(qs_ready, 1)
                            nc.gpsimd.tensor_tensor(
                                QS[:, CH - 1, :].rearrange("p (k r) -> p k r", r=R),
                                QB[:, s, T:N].unsqueeze(1).broadcast_to((64, HG, R)),
                                feat_mask[:].unsqueeze(2).broadcast_to((64, HG, R)), ALU.mult).then_inc(qs_ready, 1)
                        for s in range(S):
                            b = half + BPS * s
                            pool.wait_ge(o_ready[1 - s], i + s)
                            pool.wait_ge(const_pool, CONST)
                            for k in range(HG):
                                p, d = slice(k * R, (k + 1) * R), slice(k * HD, (k + 1) * HD)
                                for q in range(HG):
                                    pool.wait_ge(vs_ready[s], HG * (HG + 1) * i + k * (HG + 1) + q)
                                    pool.wait_ge(const_pool, CONST)
                                    nc.gpsimd.tensor_copy(
                                        VS[p, q:CH - 1:HG, d],
                                        V[q * R:(q + 1) * R, b, :, bass.ds(g * 64 + k * HD, HD)]).then_inc(vs_ready[s], 1)
                                pool.wait_ge(vs_ready[s], HG * (HG + 1) * i + k * (HG + 1) + HG)
                                pool.wait_ge(const_pool, CONST)
                                nc.gpsimd.tensor_copy(VS[k * R:k * R + 1, CH - 1, d],
                                                      VC[:, b, bass.ds(g * 64 + k * HD, HD)]).then_inc(vs_ready[s], 1)

            @block.tensor
            def _(pe):
                pe.wait_ge(const_dve, DVE_CONST)
                with pe.Fori(0, BPS) as half:
                    with pe.Fori(0, GROUPS) as g:
                        i = half * GROUPS + g
                        for s in range(S):
                            pe.wait_ge(qs_ready, (HG + 1) * (i * S + s + 1))
                            for c in range(CH):
                                if c >= 2:
                                    pe.wait_ge(k_ready[s], CH * i + c - 1)
                                elif s:
                                    pe.wait_ge(k_ready[0], CH * i + CH)
                                else:
                                    pe.wait_ge(k_ready[1], CH * i)
                                for a, z in HALVES:
                                    last = nc.tensor.matmul(pair(e_ps, c % 2)[:, a:z], QS[:, c, :], QB[:, s, a:z],
                                                            start=True, stop=True)
                                last.then_inc(dots_ready[s], 1)
                        with pe.Fori(0, ITERS) as it:
                            for s in range(S):
                                pe.wait_ge(o_kept[s], i)
                                pe.wait_ge(k_masked[s], 3 * i + 3)
                                pe.wait_ge(diag_ready[s], HG * (ITERS * i + it + 1))
                                for c in range(CH):
                                    for a, z in HALVES:
                                        last = nc.tensor.matmul(pair(w_ps, s)[:, a:z], diag[s][:, c, :], K[s][:, c, a:z],
                                                                start=(c == 0), stop=(c == CH - 1))
                                last.then_inc(w_ready[s], 1)
                        for s in range(S):
                            pe.wait_ge(vs_ready[s], HG * (HG + 1) * (i + 1))
                            pe.wait_ge(logs_ready[s], ITERS * (i + 1))
                            pe.wait_ge(e_set[s], 2 * i + 2)
                            for c in range(CH):
                                for a, z in HALVES:
                                    last = nc.tensor.matmul(pair(w_ps, s)[:, a:z], VS[:, c, :], K[s][:, c, a:z],
                                                            start=(c == 0), stop=(c == CH - 1))
                            last.then_inc(o_ready[s], 1)

            @block.scalar
            def _(act):
                act.wait_ge(const_dve, DVE_CONST)
                act.wait_ge(const_pool, 2 + HG)
                nc.scalar.preload_act_table_set("natural_log_exp_and_others")

                def u_row(s, i, it):
                    act.wait_ge(w_ready[s], i * ITERS + it + 1)
                    nc.scalar.activation(logs[:, s, 0:N], pair(w_ps, s), ACT.Ln, scale=float(N)).then_inc(logs_ready[s], 1)
                    act.wait_ge(logs_ready[s], i * ITERS + it + 1)
                    nc.scalar.activation(row[:, s, 0:N], logs[:, s, 0:N], ACT.Exp, scale=-1.0).then_inc(row_ready[s], 1)

                def v_blocks(s, source):
                    for k in range(HG):
                        p = slice(k * R, (k + 1) * R)
                        nc.scalar.activation(diag[s][p, :, p], source[p, :].unsqueeze(2).broadcast_to((R, CH, R)),
                                             ACT.Copy).then_inc(diag_ready[s], 1)

                with act.Fori(0, BPS) as half:
                    with act.Fori(0, GROUPS) as g:
                        i = half * GROUPS + g
                        for s in range(S):
                            act.wait_ge(w_ready[s], ITERS * i)
                            v_blocks(s, ones[:, 0:CH])
                            act.wait_ge(o_ready[s], i)
                            for c in range(CH):
                                act.wait_ge(dots_ready[s], CH * i + c + 1)
                                nc.scalar.activation(K[s][:, c, 0:N], pair(e_ps, c % 2), ACT.Exp, bias=shift[:, 0:1],
                                                     scale=INV_REG).then_inc(k_ready[s], 1)
                        with act.Fori(0, ITERS - 1) as it:
                            for s in range(S):
                                u_row(s, i, it)
                                act.wait_ge(col_ready[s], ITERS * i + it + 1)
                                v_blocks(s, col[:, s, :])
                        for s in range(S):
                            u_row(s, i, ITERS - 1)
                        for s in range(S):
                            act.wait_ge(weight_ready[s], i + 1)
                            for c in range(CH):
                                last = nc.scalar.activation(K[s][:, c, 0:N], K[s][:, c, 0:N], ACT.Exp,
                                                            bias=shift[:, 1:2], scale=weight[:, s, c:c + 1])
                            last.then_inc(e_ready[s], 1)
                        for s in range(S):
                            act.wait_ge(o_ready[s], i + 1)
                            if s == 0:
                                act.wait_ge(o_kept[1], i)
                            else:
                                act.wait_ge(o_kept[0], i + 1)
                            nc.scalar.activation(den[:, 0, 0:N], pair(w_ps, s)[64:P, :], ACT.Ln).then_inc(den_log[s], 1)
                            act.wait_ge(den_log[s], i + 1)
                            nc.scalar.activation(den[:, 1, 0:N], den[:, 0, 0:N], ACT.Exp, scale=-1.0).then_inc(den_ready[s], 1)

            @block.vector
            def _(dve):
                nc.vector.memset(feat_mask[:], 1.0)
                nc.vector.memset(on_diag[:], 0.0).then_inc(const_dve, 1)
                nc.vector.memset(shift[:, 0:1], -INV_REG)
                nc.vector.memset(shift[:, 1:2], -SCALE)
                for s in range(S):
                    nc.vector.memset(diag[s][:], 0.0)
                nc.vector.memset(head_mask[:], 0.0)
                nc.vector.memset(VS[:, :, 0:64], 0.0)
                nc.vector.memset(cls_mask[:], 0.0).then_inc(const_dve, 1)
                dve.wait_ge(const_dve, 2)
                for k in range(HG):
                    nc.vector.memset(head_mask[k * R:(k + 1) * R, k:k + 1], 1.0)
                    last = nc.vector.memset(cls_mask[k * R:k * R + 1, :], 1.0)
                last.then_inc(const_dve, 1)
                dve.wait_ge(const_dve, 3)
                dve.wait_ge(const_pool, 2 + HG)
                nc.vector.tensor_scalar(not_cls[:], cls_mask[:], -1.0, 1.0, ALU.mult, ALU.add).then_inc(const_dve, 1)
                nc.vector.tensor_scalar(off_diag[:], on_diag[:], -1.0, 1.0, ALU.mult, ALU.add).then_inc(const_dve, 1)
                nc.vector.tensor_scalar(cls_head_mask[:], head_mask[:], cls_mask[:], None, ALU.mult).then_inc(const_dve, 1)
                dve.wait_ge(const_dve, 6)
                for c0, c1, mask in ((0, CH - 1, head_mask), (CH - 1, CH, cls_head_mask)):
                    for k in range(HG):
                        last = nc.vector.tensor_copy(VS[:, c0:c1, 64 + k * HD:64 + (k + 1) * HD],
                                                     mask[:, k:k + 1].unsqueeze(1).broadcast_to((P, c1 - c0, HD)))
                    last.then_inc(const_dve, 1)

                def k_u(s, i, it):
                    dve.wait_ge(row_ready[s], i * ITERS + it + 1)
                    for c in range(CH):
                        if c >= JUNK:
                            dve.wait_ge(sums_ready[s], (i * ITERS + it) * CH + c - JUNK + 1)
                        nc.vector.tensor_tensor_reduce(
                            out=junk[:, c % JUNK, 0:N], in0=K[s][:, c, 0:N], in1=row[:, s, 0:N], scale=float(N),
                            scalar=not_cls[:] if c == CH - 1 else 0.0, op0=ALU.mult, op1=ALU.add,
                            accum_out=sums[:, s, c:c + 1]).then_inc(sums_ready[s], 1)
                    dve.wait_ge(sums_ready[s], (i * ITERS + it + 1) * CH)
                    nc.vector.reciprocal(col[:, s, :], sums[:, s, :]).then_inc(col_ready[s], 1)

                with dve.Fori(0, BPS) as half:
                    with dve.Fori(0, GROUPS) as g:
                        i = half * GROUPS + g
                        for s in range(S):
                            dve.wait_ge(k_ready[s], CH * (i + 1))
                            nc.vector.tensor_tensor(near_diagonal(s), near_diagonal(s),
                                                    off_diag[:].unsqueeze(1).broadcast_to((P, CH - 1, R)),
                                                    ALU.mult).then_inc(k_masked[s], 1)
                            nc.vector.tensor_scalar(K[s][:, CH - 1, 0:T], K[s][:, CH - 1, 0:T], cls_mask[:], None,
                                                    ALU.mult).then_inc(k_masked[s], 1)
                            nc.vector.memset(K[s][:, CH - 1, T:N], 0.0).then_inc(k_masked[s], 1)
                        with dve.Fori(0, ITERS) as it:
                            for s in range(S):
                                dve.wait_ge(k_masked[s], 3 * i + 3)
                                k_u(s, i, it)
                        for s in range(S):
                            for c in range(CH):
                                last = nc.vector.tensor_tensor_reduce(
                                    out=K[s][:, c, 0:N], in0=K[s][:, c, 0:N], in1=row[:, s, 0:N], scale=1.0, scalar=0.0,
                                    op0=ALU.mult, op1=ALU.max, accum_out=peak[:, s, c:c + 1])
                            last.then_inc(top_step[s], 1)
                            steps = 7
                            dve.wait_ge(top_step[s], steps * i + 1)
                            dve.wait_ge(col_ready[s], ITERS * (i + 1))
                            nc.vector.tensor_tensor(peak[:, s, :], peak[:, s, :], col[:, s, :], ALU.mult).then_inc(top_step[s], 1)
                            dve.wait_ge(top_step[s], steps * i + 2)
                            nc.vector.reduce_max(top[:, 0:1], peak[:, s, :], AX_X).then_inc(top_step[s], 1)
                            dve.wait_ge(top_step[s], steps * i + 3)
                            nc.vector.tensor_copy(spread[:, 0, :], top[:, 0:1].broadcast_to((P, R))).then_inc(top_step[s], 1)
                            dve.wait_ge(top_step[s], steps * i + 4)
                            nc.vector.transpose(spread[:, 1, :], spread[:, 0, :]).then_inc(top_step[s], 1)
                            dve.wait_ge(top_step[s], steps * i + 5)
                            nc.vector.reduce_max(top[:, 1:2], spread[:, 1, :], AX_X).then_inc(top_step[s], 1)
                            dve.wait_ge(top_step[s], steps * i + 6)
                            nc.vector.reciprocal(top[:, 2:3], top[:, 1:2]).then_inc(top_step[s], 1)
                            dve.wait_ge(top_step[s], steps * i + 7)
                            nc.vector.tensor_scalar(weight[:, s, :], col[:, s, :], top[:, 2:3], SCALE, ALU.mult,
                                                    ALU.mult).then_inc(weight_ready[s], 1)
                        for s in range(S):
                            dve.wait_ge(e_ready[s], i + 1)
                            nc.vector.memset(K[s][:, CH - 1, T:N], 1.0).then_inc(e_set[s], 1)
                            nc.vector.tensor_tensor(near_diagonal(s), near_diagonal(s),
                                                    off_diag[:].unsqueeze(1).broadcast_to((P, CH - 1, R)),
                                                    ALU.mult).then_inc(e_cleared[s], 1)
                            dve.wait_ge(e_cleared[s], i + 1)
                            nc.vector.tensor_tensor(near_diagonal(s), near_diagonal(s),
                                                    on_diag[:].unsqueeze(1).broadcast_to((P, CH - 1, R)),
                                                    ALU.add).then_inc(e_set[s], 1)
                        for s in range(S):
                            dve.wait_ge(den_ready[s], i + 1)
                            nc.vector.tensor_tensor(QT[:, g, half + BPS * s, 0:N], pair(w_ps, s)[0:64, :], den[:, 1, 0:N],
                                                    ALU.mult).then_inc(o_kept[s], 1)


def sinkhorn_out_stage(nc, sem, make_ps, AOT, WprojT, bproj, ones, H):
    with ExitStack() as ctx:
        o_ps = make_ps(ctx)("sko_o", [P, 4, 512])
        ready, kept = sem("sko_ready"), sem("sko_kept")
        with nc.Block() as block:
            @block.tensor
            def _(pe):
                for t in range(NT):
                    n = P if t < CLS else B
                    if t >= 4:
                        pe.wait_ge(kept, t - 3)
                    for g in range(GROUPS):
                        lhs = AOT[:, g, t // TPB, (t % TPB) * P:(t % TPB + 1) * P] if t < CLS else AOT[:, g, :, T]
                        nc.tensor.matmul(o_ps[0:n, t % 4, 0:D], lhs, WprojT[:, g, :], start=(g == 0), stop=False)
                    nc.tensor.matmul(o_ps[0:n, t % 4, 0:D], ones[0:1, 0:n], bproj[:], start=False,
                                     stop=True).then_inc(ready, 1)

            @block.vector
            def _(dve):
                for t in range(NT):
                    n = P if t < CLS else B
                    dve.wait_ge(ready, t + 1)
                    nc.vector.tensor_tensor(H[0:n, t, :], H[0:n, t, :], o_ps[0:n, t % 4, 0:D], ALU.add).then_inc(kept, 1)


def load(nc, sem, name, pairs):
    loaded = sem(name + "_loaded")
    with nc.Block() as block:
        @block.sync
        def _(sp):
            for dst, src in pairs:
                sp.dma_start(dst, src).then_inc(loaded, 16)
            sp.wait_ge(loaded, 16 * len(pairs))


def halves_of(w):
    return w.rearrange("(h p) n -> p h n", p=HALF)


def row_of(v):
    return v.rearrange("(a n) -> a n", a=1)


def tokens_of(t):
    return (P if t < CLS else B), t * P


TOPK = max(1, int(round(0.15 * N)))
HPH = HALF // HD
QROWS = HPH * TOPK
QB_ROWS = 116
QBLOCKS = [(r, min(QROWS, r + QB_ROWS)) for r in range(0, QROWS, QB_ROWS)]
F = 4 * D


def routed_stage(nc, sem, make_sb, make_ps, A, H, ident, ones):
    with ExitStack() as ctx:
        sb = make_sb(ctx)
        HH = sb("r_hh", [P, NT, D])
        bf2 = sb("r_bf2", [1, D])
        bf1 = sb("r_bf1", [P, F // P])
        W1 = sb("r_W1", [HALF, 2, F])
        W2 = sb("r_W2", [P, F // P, D])
        g2, b2 = sb("r_g2", [P, D]), sb("r_b2", [P, D])
        with ExitStack() as actx:
            asb = make_sb(actx)
            N1, N1T = asb("r_n1", [P, NT, D]), asb("r_n1T", [HALF, 2, NTOK])
            g1, b1 = asb("r_g1", [P, D]), asb("r_b1", [P, D])
            W = {k: asb("r_W" + k, [HALF, 2, D]) for k in "qkvom"}
            wr = asb("r_wr", [HALF, 2, 1])
            br = asb("r_br", [P, 1])
            bq, bk = asb("r_bq", [HALF, 2]), asb("r_bk", [HALF, 2])
            bv, bo, bm = asb("r_bv", [1, D]), asb("r_bo", [1, D]), asb("r_bm", [1, D])
            with nc.allow_non_contiguous_dma(reason="vectors of 192 and 768 numbers, one per partition"):
                load(nc, sem, "r", [
                    (g1[:], A["L0_ffn_g1"].partition_broadcast(P)), (b1[:], A["L0_ffn_b1"].partition_broadcast(P)),
                    (g2[:], A["L0_ffn_g2"].partition_broadcast(P)), (b2[:], A["L0_ffn_b2"].partition_broadcast(P)),
                    *[(W[k][:], halves_of(A["L0_ffn_W" + k])) for k in "qkvom"],
                    (W1[:], halves_of(A["L0_ffn_W1"])), (W2[:], A["L0_ffn_W2"].rearrange("(f p) n -> p f n", p=P)),
                    (wr[:], A["L0_ffn_Wr"].rearrange("(h p a) -> p h a", p=HALF, a=1)),
                    (br[:], A["L0_ffn_br"].partition_broadcast(P)),
                    (bq[:], A["L0_ffn_bq"].rearrange("(h p) -> p h", p=HALF)),
                    (bk[:], A["L0_ffn_bk"].rearrange("(h p) -> p h", p=HALF)),
                    (bv[:], row_of(A["L0_ffn_bv"])), (bo[:], row_of(A["L0_ffn_bo"])), (bm[:], row_of(A["L0_ffn_bm"])),
                    (bf2[:], row_of(A["L0_ffn_bf2"])), (bf1[:], A["L0_ffn_bf1"].rearrange("(f p) -> p f", p=P))])
            norm_stage(nc, sem, make_sb, make_ps, "rn1", H, N1, N1T, ident, inner=HH, gain=g1, shift=b1)
            KT = asb("r_KT", [HALF, 2, B, NP])
            V, VC = asb("r_V", [P, CLS, D]), asb("r_VC", [1, B, D])
            Z = asb("r_Z", [P, B, NP])
            routed_projections(nc, sem, make_ps, N1T, W, wr, br, bk, bv, ones, KT, V, VC, Z)
            sel = asb("r_sel", [P, B, TPB, TOPK])
            selc = asb("r_selc", [B, B, TOPK])
            score = asb("r_score", [P, B, TPB + 1])
            rest = asb("r_rest", [P, B, TPB + 1])
            score_cls, rest_cls = asb("r_score_cls", [B, 1]), asb("r_rest_cls", [B, 1])
            PM, PMC = asb("r_PM", [P, B, D]), asb("r_PMC", [B, D])
            routing(nc, sem, make_sb, make_ps, ident, ones, N1, W["m"], Z, sel, selc, score, rest, score_cls, rest_cls, PM, PMC)
            selT = asb("r_selT", [TOPK, B, T + B])
            AS = asb("r_AS", [TOPK, B, D])
            routed_attention(nc, sem, make_sb, make_ps, ident, ones, N1, W, bq, bo, KT, V, VC, sel, selc, selT, AS)
            merge(nc, sem, make_sb, make_ps, ones, N1T, W["m"], bm, selT, AS, score, rest, score_cls, rest_cls, PM, PMC, HH)
        with ExitStack() as mctx:
            msb = make_sb(mctx)
            N2, N2T = msb("r_n2", [P, NT, D]), msb("r_n2T", [HALF, 2, NTOK])
            norm_stage(nc, sem, make_sb, make_ps, "rn2", HH, N2, N2T, ident, gain=g2, shift=b2)
            gelu_mlp(nc, sem, make_sb, make_ps, ones, N2T, W1, bf1, W2, bf2, HH, H)


def routed_projections(nc, sem, make_ps, N1T, W, wr, br, bk, bv, ones, KT, V, VC, Z):
    with ExitStack() as ctx:
        ps = make_ps(ctx)
        k_ps, v_ps, z_ps = ps("rp_k", [P, 2, 512]), ps("rp_v", [P, 2, 512]), ps("rp_z", [P, 2, 1024])
        k_ready, k_kept, v_ready, v_kept = sem("rp_k_ready"), sem("rp_k_kept"), sem("rp_v_ready"), sem("rp_v_kept")
        z_ready, z_kept, z_done = sem("rp_z_ready"), sem("rp_z_kept"), sem("rp_z_done")
        KJOBS = [(o, b) for o in range(2) for b in range(B + 1)]
        with nc.Block() as block:
            @block.tensor
            def _(pe):
                for b in range(B):
                    if b >= 2:
                        pe.wait_ge(z_kept, b - 1)
                    for h in range(2):
                        nc.tensor.matmul(z_ps[:, b % 2, 0:T], wr[:, h, :].broadcast_to((HALF, P)),
                                         N1T[:, h, b * T:(b + 1) * T], start=(h == 0), stop=(h == 1))
                    for h in range(2):
                        last = nc.tensor.matmul(z_ps[:, b % 2, T:N], wr[:, h, :].broadcast_to((HALF, P)),
                                                N1T[:, h, B * T + b:B * T + b + 1], start=(h == 0), stop=(h == 1))
                    last.then_inc(z_ready, 1)
                for j, (o, b) in enumerate(KJOBS):
                    n = T if b < B else B
                    if j >= 2:
                        pe.wait_ge(k_kept, j - 1)
                    for h in range(2):
                        last = nc.tensor.matmul(k_ps[0:HALF, j % 2, 0:n], W["k"][:, h, o * HALF:(o + 1) * HALF],
                                                N1T[:, h, b * T:b * T + n], start=(h == 0), stop=(h == 1))
                    last.then_inc(k_ready, 1)
                for t in range(CLS + B):
                    n, first = (P, t * P) if t < CLS else (1, t - CLS + B * T)
                    if t >= 2:
                        pe.wait_ge(v_kept, t - 1)
                    for h in range(2):
                        nc.tensor.matmul(v_ps[0:n, t % 2, 0:D], N1T[:, h, first:first + n], W["v"][:, h, :],
                                         start=(h == 0), stop=False)
                    nc.tensor.matmul(v_ps[0:n, t % 2, 0:D], ones[0:1, 0:n], bv[:], start=False,
                                     stop=True).then_inc(v_ready, 1)

            @block.scalar
            def _(act):
                for j, (o, b) in enumerate(KJOBS):
                    act.wait_ge(k_ready, j + 1)
                    dst = KT[:, o, b, 0:T] if b < B else KT[:, o, :, T]
                    nc.scalar.activation(dst, k_ps[0:HALF, j % 2, 0:T if b < B else B], ACT.Identity,
                                         bias=bk[:, o:o + 1]).then_inc(k_kept, 1)

            @block.vector
            def _(dve):
                for b in range(B):
                    dve.wait_ge(z_ready, b + 1)
                    nc.vector.tensor_scalar(Z[:, b, 0:N], z_ps[:, b % 2, 0:N], br[:], 17.0, ALU.add,
                                            ALU.min).then_inc(z_kept, 1)
                    dve.wait_ge(z_kept, b + 1)
                    nc.vector.tensor_scalar(Z[:, b, 0:N], Z[:, b, 0:N], -88.0, None, ALU.max).then_inc(z_done, 1)
                for t in range(CLS + B):
                    dve.wait_ge(v_ready, t + 1)
                    dst = V[:, t, :] if t < CLS else VC[:, t - CLS, :]
                    nc.vector.tensor_copy(dst, v_ps[0:P if t < CLS else 1, t % 2, 0:D]).then_inc(v_kept, 1)


def routing(nc, sem, make_sb, make_ps, ident, ones, N1, Wm, Z, sel, selc, score, rest, score_cls, rest_cls, PM, PMC):
    C5 = TPB + 1
    with ExitStack() as ctx:
        sb, ps = make_sb(ctx), make_ps(ctx)
        before = sb("ro_before", [P, TPB, NP])
        slot = sb("ro_slot", [P, TOPK])
        picked = sb("ro_picked", [P, 2, P])
        zcol = sb("ro_zcol", [P, B, C5])
        less, same = sb("ro_less", [P, 2, NP]), sb("ro_same", [P, 2, NP])
        both = sb("ro_both", [P, 2, NP])
        rank = sb("ro_rank", [P, B, C5])
        counted = sb("ro_counted", [P, B, C5])
        expz = sb("ro_expz", [P, B, C5])
        cls_scores = sb("ro_cls_scores", [B, B])
        total = sb("ro_total", [P, B])
        pooled = sb("ro_pooled", [HALF, 2, B])
        small = sb("ro_small", [B, 2, B])
        t_ps, p_ps, m_ps = ps("ro_t", [P, 512]), ps("ro_p", [P, 512]), ps("ro_m", [P, 3, 512])
        const_ready, step = sem("ro_const_ready"), sem("ro_step")
        col_ready, pair_ready, rank_ready = sem("ro_col_ready"), sem("ro_pair_ready"), sem("ro_rank_ready")
        exp_ready, score_ready, total_ready, pooled_ready = (sem("ro_exp_ready"), sem("ro_score_ready"),
                                                             sem("ro_total_ready"), sem("ro_pooled_ready"))
        pooled_kept, mean_ready, mean_kept = sem("ro_pooled_kept"), sem("ro_mean_ready"), sem("ro_mean_kept")
        with nc.Block() as block:
            @block.gpsimd
            def _(pool):
                nc.gpsimd.memset(before[:], 1.0).then_inc(const_ready, 1)
                nc.gpsimd.iota(slot[:], pattern=[[1, TOPK]], base=0, channel_multiplier=0,
                               allow_small_or_imprecise_dtypes=True).then_inc(const_ready, 1)
                for t in range(TPB):
                    pool.wait_ge(const_ready, 2 + t)
                    nc.gpsimd.affine_select(out=before[:, t, 0:T], in_=before[:, t, 0:T], compare_op=ALU.is_gt,
                                            fill=0.0, base=t * P, pattern=[[-1, T]],
                                            channel_multiplier=1).then_inc(const_ready, 1)

            @block.vector
            def _(dve):
                steps = Tally(step)
                for b in range(B):
                    for t in range(TPB):
                        if b * TPB + t >= 2:
                            dve.wait_ge(col_ready, b * TPB + t - 1)
                        nc.vector.tensor_tensor_reduce(out=picked[:, t % 2, :], in0=Z[:, b, t * P:(t + 1) * P],
                                                       in1=ident[:], scale=1.0, scalar=0.0, op0=ALU.mult, op1=ALU.add,
                                                       accum_out=zcol[:, b, t:t + 1]).then_inc(col_ready, 1)
                nc.vector.tensor_copy(zcol[:, :, TPB], Z[:, :, T]).then_inc(col_ready, 1)
                dve.wait_ge(col_ready, CLS + 1)
                dve.wait_ge(const_ready, 2 + TPB)
                for b in range(B):
                    for t in range(C5):
                        n = b * C5 + t
                        if n >= 2:
                            dve.wait_ge(rank_ready, n - 1)
                        zc = zcol[:, b, t:t + 1]
                        nc.vector.tensor_scalar(less[:, n % 2, 0:N], Z[:, b, 0:N], zc, None,
                                                ALU.is_lt).then_inc(pair_ready, 1)
                        if t < TPB:
                            nc.vector.scalar_tensor_tensor(out=same[:, n % 2, 0:N], in0=Z[:, b, 0:N], scalar=zc,
                                                           in1=before[:, t, 0:N], op0=ALU.is_equal,
                                                           op1=ALU.mult).then_inc(pair_ready, 1)
                        else:
                            nc.vector.memset(same[:, n % 2, 0:N], 0.0).then_inc(pair_ready, 1)
                        dve.wait_ge(pair_ready, 2 * n + 2)
                        nc.vector.tensor_tensor_reduce(out=both[:, n % 2, 0:N], in0=less[:, n % 2, 0:N],
                                                       in1=same[:, n % 2, 0:N], scale=1.0, scalar=0.0, op0=ALU.add,
                                                       op1=ALU.add, accum_out=rank[:, b, t:t + 1]).then_inc(rank_ready, 1)
                dve.wait_ge(rank_ready, B * C5)
                for b in range(B):
                    for t in range(TPB):
                        nc.vector.tensor_scalar(sel[:, b, t, :], slot[:], rank[:, b, t:t + 1], None, ALU.is_equal)
                    nc.vector.tensor_scalar(selc[:, b, :], slot[0:B, :], rank[0:B, b, TPB:C5], ident[0:B, b:b + 1],
                                            ALU.is_equal, ALU.mult)
                steps.mark(nc.vector.tensor_scalar(rest[:], rank[:], TOPK - 0.5, None, ALU.is_gt))
                dve.wait_ge(exp_ready, 1)
                dve.wait_ge(step, steps.mark(nc.vector.tensor_scalar(expz[:], expz[:], 1.0, None, ALU.add)))
                dve.wait_ge(step, steps.mark(nc.vector.reciprocal(score[:], expz[:])))
                nc.vector.tensor_copy(counted[:, :, 0:TPB], score[:, :, 0:TPB])
                nc.vector.tensor_scalar(counted[:, :, TPB], score[:, :, TPB], ident[:, 0:1], None, ALU.mult)
                nc.vector.tensor_tensor(cls_scores[:], score[0:B, :, TPB], ident[0:B, 0:B], ALU.mult).then_inc(score_ready, 1)
                dve.wait_ge(step, steps.mark(nc.vector.tensor_tensor(small[:, 0, :], rest[0:B, :, TPB], ident[0:B, 0:B],
                                                                     ALU.mult)))
                nc.vector.reduce_sum(rest_cls[:], small[:, 0, :], AX_X)
                dve.wait_ge(score_ready, 1)
                nc.vector.reduce_sum(score_cls[:], cls_scores[:], AX_X)
                dve.wait_ge(total_ready, 1)
                dve.wait_ge(step, steps.mark(nc.vector.reduce_sum(
                    total[:], t_ps[:, 0:B * C5].rearrange("p (b c) -> p b c", b=B), AX_X)))
                dve.wait_ge(step, steps.mark(nc.vector.tensor_scalar(total[:], total[:], 1e-6, None, ALU.add)))
                dve.wait_ge(step, steps.mark(nc.vector.reciprocal(total[:], total[:])))
                dve.wait_ge(pooled_ready, 1)
                nc.vector.tensor_tensor(pooled[:], p_ps[0:HALF, 0:2 * B].rearrange("p (h b) -> p h b", h=2),
                                        total[0:HALF, :].unsqueeze(1).broadcast_to((HALF, 2, B)),
                                        ALU.mult).then_inc(pooled_kept, 1)
                dve.wait_ge(mean_ready, B + 1)
                for b in range(B):
                    nc.vector.tensor_copy(PM[:, b, :], m_ps[:, b // 2, (b % 2) * D:(b % 2 + 1) * D])
                nc.vector.tensor_copy(PMC[:], m_ps[0:B, 2, 0:D])

            @block.scalar
            def _(act):
                act.wait_ge(col_ready, CLS + 1)
                nc.scalar.activation(expz[:], zcol[:], ACT.Exp, scale=-1.0).then_inc(exp_ready, 1)

            @block.tensor
            def _(pe):
                pe.wait_ge(score_ready, 1)
                nc.tensor.matmul(t_ps[:, 0:B * C5], ones[:], counted[:].rearrange("p b c -> p (b c)"), start=True,
                                 stop=True).then_inc(total_ready, 1)
                for h in range(2):
                    for b in range(B):
                        for t in range(TPB):
                            nc.tensor.matmul(p_ps[0:HALF, h * B + b:h * B + b + 1],
                                             N1[:, b * TPB + t, h * HALF:(h + 1) * HALF], score[:, b, t:t + 1],
                                             start=(t == 0), stop=False)
                        last = nc.tensor.matmul(p_ps[0:HALF, h * B + b:h * B + b + 1],
                                                N1[0:B, CLS, h * HALF:(h + 1) * HALF], cls_scores[:, b:b + 1],
                                                start=False, stop=True)
                last.then_inc(pooled_ready, 1)
                pe.wait_ge(pooled_kept, 1)
                for b in range(B + 1):
                    n = P if b < B else B
                    for h in range(2):
                        lhs = pooled[:, h, b:b + 1].broadcast_to((HALF, P)) if b < B else pooled[:, h, :]
                        last = nc.tensor.matmul(m_ps[0:n, b // 2, (b % 2) * D:(b % 2 + 1) * D], lhs, Wm[:, h, :],
                                                start=(h == 0), stop=(h == 1))
                    last.then_inc(mean_ready, 1)


def routed_attention(nc, sem, make_sb, make_ps, ident, ones, N1, W, bq, bo, KT, V, VC, sel, selc, selT, AS):
    L = 255
    HALVES = ((0, 512 - L), (512 - L, N))
    NB = len(QBLOCKS)
    MT = TPB + 1
    with ExitStack() as ctx:
        sb, ps = make_sb(ctx), make_ps(ctx)
        picked = sb("ra_picked", [HALF, 2, TOPK])
        q = sb("ra_q", [HALF, 2, TOPK])
        heads = sb("ra_heads", [HALF, HPH])
        qd = sb("ra_qd", [HALF, 2, HPH, TOPK])
        prob = sb("ra_prob", [P, 2 * NB, NP])
        top, den, rden = sb("ra_top", [P, 2 * NB]), sb("ra_den", [P, 2 * NB]), sb("ra_rden", [P, 2 * NB])
        probT = sb("ra_probT", [P, 2, MT, QROWS])
        own = sb("ra_own", [HALF, 2, QROWS])
        ctxT = sb("ra_ctxT", [HALF, 2, TOPK])
        s_ps = ps("ra_s", [P, 2, 1024])
        t_ps = ps("ra_t", [P, 2, 512])
        x_ps = ps("ra_x", [P, 2, 512])
        names = ("picked_ready picked_kept q_ready q_kept qd_ready logit_ready top_ready prob_ready rden_ready "
                 "prob_normed turn_ready turn_kept ctx_ready own_ready ctx_kept as_ready as_kept st_ready st_kept const").split()
        M = {n: sem("ra_" + n) for n in names}
        with nc.Block() as block:
            @block.gpsimd
            def _(pool):
                nc.gpsimd.memset(heads[:], 1.0).then_inc(M["const"], 1)
                pool.wait_ge(M["const"], 1)
                nc.gpsimd.affine_select(out=heads[:], in_=heads[:], compare_op=ALU.is_ge, fill=0.0, base=0,
                                        pattern=[[-HD, HPH]], channel_multiplier=1).then_inc(M["const"], 1)
                pool.wait_ge(M["const"], 2)
                nc.gpsimd.affine_select(out=heads[:], in_=heads[:], compare_op=ALU.is_ge, fill=0.0, base=HD - 1,
                                        pattern=[[HD, HPH]], channel_multiplier=-1).then_inc(M["const"], 1)

            @block.tensor
            def _(pe):
                for b in range(B):
                    pe.wait_ge(M["as_kept"], b)
                    pe.wait_ge(M["ctx_kept"], 2 * b)
                    for h in range(2):
                        for t in range(TPB):
                            nc.tensor.matmul(x_ps[0:HALF, 0, h * TOPK:(h + 1) * TOPK],
                                             N1[:, b * TPB + t, h * HALF:(h + 1) * HALF], sel[:, b, t, :],
                                             start=(t == 0), stop=False)
                        last = nc.tensor.matmul(x_ps[0:HALF, 0, h * TOPK:(h + 1) * TOPK],
                                                N1[0:B, CLS, h * HALF:(h + 1) * HALF], selc[:, b, :],
                                                start=False, stop=True)
                    last.then_inc(M["picked_ready"], 1)
                    pe.wait_ge(M["picked_kept"], b + 1)
                    for o in range(2):
                        for h in range(2):
                            last = nc.tensor.matmul(x_ps[0:HALF, 1, o * TOPK:(o + 1) * TOPK],
                                                    W["q"][:, h, o * HALF:(o + 1) * HALF], picked[:, h, :],
                                                    start=(h == 0), stop=(h == 1))
                    last.then_inc(M["q_ready"], 1)
                    pe.wait_ge(M["turn_kept"], 2 * MT * b)
                    for t in range(TPB):
                        nc.tensor.transpose(t_ps[0:TOPK, 0, t * P:(t + 1) * P], sel[:, b, t, :], ident[:])
                    nc.tensor.transpose(t_ps[0:TOPK, 1, 0:B], selc[:, b, :], ident[0:B, 0:B]).then_inc(M["st_ready"], 1)
                    pe.wait_ge(M["qd_ready"], 2 * b + 2)
                    for j in range(2 * NB):
                        n = 2 * NB * b + j
                        o, (r0, r1) = j // NB, QBLOCKS[j % NB]
                        if n >= 2:
                            pe.wait_ge(M["prob_ready"], n - 1)
                        for a, z in HALVES:
                            last = nc.tensor.matmul(s_ps[0:r1 - r0, j % 2, L + a:L + z],
                                                    qd[:, o, :, :].rearrange("p h s -> p (h s)")[:, r0:r1],
                                                    KT[:, o, b, a:z], start=True, stop=True)
                        last.then_inc(M["logit_ready"], 1)
                    pe.wait_ge(M["st_kept"], b + 1)
                    for o in range(2):
                        pe.wait_ge(M["prob_normed"], 2 * NB * b + NB * (o + 1))
                        for m in range(MT):
                            j = o * MT + m
                            n = P if m < TPB else 1
                            if 2 * MT * b + j >= 2:
                                pe.wait_ge(M["turn_kept"], 2 * MT * b + j - 1)
                            for k, (r0, r1) in enumerate(QBLOCKS):
                                last = nc.tensor.transpose(t_ps[0:n, j % 2, r0:r1],
                                                           prob[0:r1 - r0, o * NB + k, m * P:m * P + n],
                                                           ident[0:r1 - r0, 0:r1 - r0])
                            last.then_inc(M["turn_ready"], 1)
                    for o in range(2):
                        pe.wait_ge(M["turn_kept"], 2 * MT * b + MT * (o + 1))
                        for m in range(MT):
                            v = V[:, b * TPB + m, o * HALF:(o + 1) * HALF] if m < TPB else VC[:, b, o * HALF:(o + 1) * HALF]
                            n = P if m < TPB else 1
                            last = nc.tensor.matmul(x_ps[0:HALF, o, 0:QROWS], v, probT[0:n, o, m, :], start=(m == 0),
                                                    stop=(m == MT - 1))
                        last.then_inc(M["ctx_ready"], 1)
                    pe.wait_ge(M["ctx_kept"], 2 * b + 2)
                    for h in range(2):
                        nc.tensor.matmul(x_ps[0:TOPK, 0, 0:D], ctxT[:, h, :], W["o"][:, h, :], start=(h == 0), stop=False)
                    nc.tensor.matmul(x_ps[0:TOPK, 0, 0:D], ones[0:1, 0:TOPK], bo[:], start=False,
                                     stop=True).then_inc(M["as_ready"], 1)

            @block.scalar
            def _(act):
                for b in range(B):
                    act.wait_ge(M["st_ready"], b + 1)
                    nc.scalar.activation(selT[:, b, 0:T], t_ps[0:TOPK, 0, :], ACT.Copy)
                    nc.scalar.activation(selT[:, b, T:T + B], t_ps[0:TOPK, 1, 0:B], ACT.Copy).then_inc(M["st_kept"], 1)
                    for j in range(2 * NB):
                        r = QBLOCKS[j % NB][1] - QBLOCKS[j % NB][0]
                        act.wait_ge(M["top_ready"], 2 * NB * b + j + 1)
                        if j % NB == 0:
                            act.wait_ge(M["turn_ready"], 2 * MT * b)
                        nc.scalar.activation(prob[0:r, j, 0:N], s_ps[0:r, j % 2, L:L + N], ACT.Exp,
                                             bias=top[0:r, j:j + 1],
                                             accum_out=den[0:r, j:j + 1]).then_inc(M["prob_ready"], 1)
                    for j in range(2 * MT):
                        act.wait_ge(M["turn_ready"], 2 * MT * b + j + 1)
                        act.wait_ge(M["ctx_ready"], 2 * b)
                        n = P if j % MT < TPB else 1
                        nc.scalar.activation(probT[0:n, j // MT, j % MT, :], t_ps[0:n, j % 2, 0:QROWS],
                                             ACT.Copy).then_inc(M["turn_kept"], 1)

            @block.vector
            def _(dve):
                dve.wait_ge(M["const"], 3)
                for b in range(B):
                    dve.wait_ge(M["picked_ready"], b + 1)
                    nc.vector.tensor_copy(picked[:], x_ps[0:HALF, 0, 0:2 * TOPK].rearrange(
                        "p (h s) -> p h s", h=2)).then_inc(M["picked_kept"], 1)
                    dve.wait_ge(M["q_ready"], b + 1)
                    for o in range(2):
                        nc.vector.tensor_scalar(q[:, o, :], x_ps[0:HALF, 1, o * TOPK:(o + 1) * TOPK], bq[:, o:o + 1],
                                                float(HD) ** -0.5, ALU.add, ALU.mult).then_inc(M["q_kept"], 1)
                    for o in range(2):
                        dve.wait_ge(M["q_kept"], 2 * b + o + 1)
                        dve.wait_ge(M["logit_ready"], 2 * NB * b)
                        nc.vector.tensor_tensor(qd[:, o, :, :], q[:, o, :].unsqueeze(1).broadcast_to((HALF, HPH, TOPK)),
                                                heads[:].unsqueeze(2).broadcast_to((HALF, HPH, TOPK)),
                                                ALU.mult).then_inc(M["qd_ready"], 1)

                    def normalise(j):
                        r = QBLOCKS[j % NB][1] - QBLOCKS[j % NB][0]
                        dve.wait_ge(M["prob_ready"], 2 * NB * b + j + 1)
                        nc.vector.reciprocal(rden[0:r, j:j + 1], den[0:r, j:j + 1]).then_inc(M["rden_ready"], 1)
                        dve.wait_ge(M["rden_ready"], 2 * NB * b + j + 1)
                        nc.vector.tensor_scalar(prob[0:r, j, 0:N], prob[0:r, j, 0:N], rden[0:r, j:j + 1], None,
                                                ALU.mult).then_inc(M["prob_normed"], 1)

                    for j in range(2 * NB):
                        r = QBLOCKS[j % NB][1] - QBLOCKS[j % NB][0]
                        dve.wait_ge(M["logit_ready"], 2 * NB * b + j + 1)
                        nc.vector.tensor_reduce(top[0:r, j:j + 1], s_ps[0:r, j % 2, L:L + N], AX_X, ALU.max,
                                                negate=True).then_inc(M["top_ready"], 1)
                        if j:
                            normalise(j - 1)
                    normalise(2 * NB - 1)
                    for o in range(2):
                        dve.wait_ge(M["ctx_ready"], 2 * b + o + 1)
                        nc.vector.tensor_tensor(own[:, o, :].rearrange("p (h s) -> p h s", h=HPH),
                                                x_ps[0:HALF, o, 0:QROWS].rearrange("p (h s) -> p h s", h=HPH),
                                                heads[:].unsqueeze(2).broadcast_to((HALF, HPH, TOPK)),
                                                ALU.mult).then_inc(M["own_ready"], 1)
                        dve.wait_ge(M["own_ready"], 2 * b + o + 1)
                        nc.vector.reduce_sum(ctxT[:, o, :], own[:, o, :].rearrange("p (h s) -> p s h", h=HPH),
                                             AX_X).then_inc(M["ctx_kept"], 1)
                    dve.wait_ge(M["as_ready"], b + 1)
                    nc.vector.tensor_copy(AS[:, b, :], x_ps[0:TOPK, 0, 0:D]).then_inc(M["as_kept"], 1)


def merge(nc, sem, make_sb, make_ps, ones, N1T, Wm, bm, selT, AS, score, rest, score_cls, rest_cls, PM, PMC, HH):
    with ExitStack() as ctx:
        mixed = make_sb(ctx)("rm_mixed", [P, 2, D])
        ps = make_ps(ctx)
        m_ps, a_ps = ps("rm_m", [P, 2, 512]), ps("rm_a", [P, 2, 512])
        ready, mixed_ready, added, kept = sem("rm_ready"), sem("rm_mixed_ready"), sem("rm_added"), sem("rm_kept")
        with nc.Block() as block:
            @block.tensor
            def _(pe):
                for t in range(NT):
                    n, first = tokens_of(t)
                    if t >= 2:
                        pe.wait_ge(kept, t - 1)
                    for h in range(2):
                        nc.tensor.matmul(m_ps[0:n, t % 2, 0:D], N1T[:, h, first:first + n], Wm[:, h, :], start=(h == 0),
                                         stop=False)
                    nc.tensor.matmul(m_ps[0:n, t % 2, 0:D], ones[0:1, 0:n], bm[:], start=False, stop=True)
                    if t < CLS:
                        last = nc.tensor.matmul(a_ps[:, t % 2, 0:D], selT[:, t // TPB, (t % TPB) * P:(t % TPB + 1) * P],
                                                AS[:, t // TPB, :], start=True, stop=True)
                    else:
                        for b in range(B):
                            last = nc.tensor.matmul(a_ps[0:B, t % 2, 0:D], selT[:, b, T:T + B], AS[:, b, :],
                                                    start=(b == 0), stop=(b == B - 1))
                    last.then_inc(ready, 1)

            @block.vector
            def _(dve):
                for t in range(NT):
                    n, _ = tokens_of(t)
                    b, k = t // TPB, t % TPB
                    s, r, pm = (score[:, b, k:k + 1], rest[:, b, k:k + 1], PM[:, b, :]) if t < CLS else \
                        (score_cls[:], rest_cls[:], PMC[:])
                    dve.wait_ge(ready, t + 1)
                    nc.vector.scalar_tensor_tensor(out=mixed[0:n, t % 2, :], in0=pm, scalar=s, in1=m_ps[0:n, t % 2, 0:D],
                                                   op0=ALU.mult, op1=ALU.add).then_inc(mixed_ready, 1)
                    dve.wait_ge(mixed_ready, t + 1)
                    nc.vector.scalar_tensor_tensor(out=HH[0:n, t, :], in0=mixed[0:n, t % 2, :], scalar=r, in1=HH[0:n, t, :],
                                                   op0=ALU.mult, op1=ALU.add).then_inc(added, 1)
                    dve.wait_ge(added, t + 1)
                    nc.vector.tensor_tensor(HH[0:n, t, :], HH[0:n, t, :], a_ps[0:n, t % 2, 0:D], ALU.add).then_inc(kept, 1)


def gelu_mlp(nc, sem, make_sb, make_ps, ones, N2T, W1, bf1, W2, bf2, HH, H):
    NF = F // P
    CHUNKS = [(b * T, T) for b in range(B)] + [(B * T, B)]
    with ExitStack() as ctx:
        sb, ps = make_sb(ctx), make_ps(ctx)
        hid = sb("gm_hid", [P, 2, NF, T])
        h_ps, o_ps = ps("gm_h", [P, 4, 512]), ps("gm_o", [P, 2, 512])
        h_ready, h_kept, o_ready, o_kept, added = (sem("gm_h_ready"), sem("gm_h_kept"), sem("gm_o_ready"),
                                                   sem("gm_o_kept"), sem("gm_added"))
        with nc.Block() as block:
            @block.tensor
            def _(pe):
                for k, (first, n) in enumerate(CHUNKS):
                    for f in range(NF):
                        j = k * NF + f
                        if j >= 4:
                            pe.wait_ge(h_kept, j - 3)
                        for h in range(2):
                            last = nc.tensor.matmul(h_ps[:, j % 4, 0:n], W1[:, h, f * P:(f + 1) * P],
                                                    N2T[:, h, first:first + n], start=(h == 0), stop=(h == 1))
                        last.then_inc(h_ready, 1)
                    pe.wait_ge(h_kept, (k + 1) * NF)
                    for t in range(k * TPB, min(NT, (k + 1) * TPB)):
                        n, c = tokens_of(t)
                        if t >= 2:
                            pe.wait_ge(o_kept, t - 1)
                        for f in range(NF):
                            nc.tensor.matmul(o_ps[0:n, t % 2, 0:D], hid[:, k % 2, f, c - first:c - first + n], W2[:, f, :],
                                             start=(f == 0), stop=False)
                        nc.tensor.matmul(o_ps[0:n, t % 2, 0:D], ones[0:1, 0:n], bf2[:], start=False,
                                         stop=True).then_inc(o_ready, 1)

            @block.scalar
            def _(act):
                for k, (first, n) in enumerate(CHUNKS):
                    for f in range(NF):
                        j = k * NF + f
                        act.wait_ge(h_ready, j + 1)
                        if f == 0 and k >= 2:
                            act.wait_ge(o_ready, (k - 1) * TPB)
                        nc.scalar.activation(hid[:, k % 2, f, 0:n], h_ps[:, j % 4, 0:n], ACT.Gelu,
                                             bias=bf1[:, f:f + 1]).then_inc(h_kept, 1)

            @block.vector
            def _(dve):
                for t in range(NT):
                    nc.vector.tensor_tensor(H[:, t, :], H[:, t, :], HH[:, t, :], ALU.add).then_inc(added, 1)
                for t in range(NT):
                    n, _ = tokens_of(t)
                    dve.wait_ge(added, t + 1)
                    dve.wait_ge(o_ready, t + 1)
                    nc.vector.tensor_tensor(H[0:n, t, :], H[0:n, t, :], o_ps[0:n, t % 2, 0:D], ALU.add).then_inc(o_kept, 1)


RH, DQK, DV = 6, 128, 64
RQ, RV = RH * DQK, RH * DV
SCALE_BASE = 512.0


def retention_tables():
    pos = np.concatenate([np.arange(1, N), [0]]).astype(np.float64)
    half = DQK // 2
    inv_freq = (1.0 / 10000.0 ** (np.arange(half, dtype=np.float32) / np.float32(half))).astype(np.float32)
    angles = (pos.astype(np.float32)[None, :] * inv_freq[:, None]).astype(np.float32).astype(np.float64)
    zeta = (np.arange(half) + half) / DQK
    rot = np.zeros((DQK, 2, 2, NP), np.float32)
    for x, sign in enumerate((1.0, -1.0)):
        decay = zeta[:, None] ** (sign * pos[None, :] / SCALE_BASE)
        c, s = np.cos(angles) * decay, np.sin(angles) * decay
        rot[:, x, 0, 0:N] = np.concatenate([c, c])
        rot[:, x, 1, 0:N] = np.concatenate([s, -s])
    gamma = 1.0 - 2.0 ** -(5.0 + np.arange(RH))
    rows = (1 - gamma[:, None] ** (pos + 1)) / (1 - gamma[:, None])
    q = gamma[:, None] ** pos / np.sqrt(rows)
    k = gamma[:, None] ** -pos * DQK ** -0.5

    def by_tile(v):
        out = np.zeros((P, RH, TPB + 1), np.float32)
        out[:, :, 0:TPB] = v[:, 0:T].reshape(RH, TPB, P).transpose(2, 0, 1)
        out[:, :, TPB] = v[None, :, T]
        return out
    return rot, by_tile(q), by_tile(k)


def retention_stage(nc, sem, make_sb, make_ps, A, H, ident, ones):
    L = 255
    HALVES = ((0, 512 - L), (512 - L, N))
    MT = TPB + 1
    CNT = float(DV * N)
    with ExitStack() as ctx:
        sb, ps = make_sb(ctx), make_ps(ctx)
        XT = sb("t_xT", [HALF, 2, NTOK])
        W = {k: sb("t_W" + k, [HALF, 2, n]) for k, n in (("q", RQ), ("k", RQ), ("v", RV), ("g", RV))}
        Wo = sb("t_Wo", [P, RV // P, D])
        gnw, gnb = sb("t_gnw", [P, RV]), sb("t_gnb", [P, RV])
        rot = sb("t_rot", [P, 2, 2, NP])
        qd, kd = sb("t_qd", [P, RH, MT]), sb("t_kd", [P, RH, MT])
        load(nc, sem, "t", [
            *[(W[k][:], halves_of(A["L1_attn_W" + k])) for k in "qkvg"],
            (Wo[:], A["L1_attn_Wo"].rearrange("(c p) n -> p c n", p=P)),
            (gnw[:], A["L1_attn_gn_weight"].partition_broadcast(P)),
            (gnb[:], A["L1_attn_gn_bias"].partition_broadcast(P)),
            (rot[:], A["rot"]), (qd[:], A["query_decay"]), (kd[:], A["key_decay"])])
        with ExitStack() as xctx:
            X = make_sb(xctx)("t_x", [P, NT, D])
            norm_stage(nc, sem, make_sb, make_ps, "tn", H, X, XT, ident)
        causal = sb("t_causal", [P, P])
        V, G, O = sb("t_V", [P, TPB, RV]), sb("t_G", [P, TPB, RV]), sb("t_O", [P, 2, TPB, RV])
        VC, GC, OC = sb("t_VC", [1, RV]), sb("t_GC", [1, RV]), sb("t_OC", [1, 2, RV])
        main = sb("t_main", [P, 2, NP])
        cross = sb("t_cross", [P, 2, NP])
        turned = sb("t_turned", [P, 2, 2, NP])
        S = sb("t_S", [P, 2, TPB, T])
        SC = sb("t_SC", [1, 2, NP])
        sums, csum = sb("t_sums", [P, RH]), sb("t_csum", [1, RH])
        mean, var = sb("t_mean", [P, RH]), sb("t_var", [P, RH])
        half_power = sb("t_half_power", [P, RH])
        gain = sb("t_gain", [P, RV])
        YT = sb("t_YT", [P, RV // P, T])
        YC = sb("t_YC", [P, RV // P, B])
        p_ps = ps("t_p", [P, 2, 1024])
        s_ps = ps("t_s", [P, 2, 512])
        o_ps = ps("t_o", [P, 2, 512])
        names = ("causal v_ready v_kept g_ready g_kept x_ready main_ready cross_ready turned s_ready s_act s_dve sc_ready "
                 "sc_kept o_ready o_kept sums_ready csum_ready sum_ready mean_ready total_ready centred sq_ready "
                 "ss_ready css_ready var_ready rstd_ready pool_ready gain_ready y_ready yt_ready yt_kept h_ready h_kept").split()
        M = {n: sem("t_" + n) for n in names}
        with nc.Block() as block:
            @block.tensor
            def _(pe):
                for b in range(B):
                    for w, wait, ready in (("v", "v_kept", "v_ready"), ("g", "g_kept", "g_ready")):
                        for t in range(MT):
                            n, first = (P, (b * TPB + t) * P) if t < TPB else (1, B * T + b)
                            if b or t >= 2:
                                pe.wait_ge(M[wait], b * MT + t - 1)
                            if w == "v" and t == 0:
                                pe.wait_ge(M["h_kept"], b * TPB)
                            for h in range(2):
                                last = nc.tensor.matmul(s_ps[0:n, t % 2, 0:RV] if w == "v" else o_ps[0:n, t % 2, 0:RV],
                                                        XT[:, h, first:first + n], W[w][:, h, :], start=(h == 0), stop=(h == 1))
                            last.then_inc(M[ready], 1)

                    for head in range(RH):
                        u = b * RH + head
                        if head == 0:
                            pe.wait_ge(M["v_kept"], MT * (b + 1))
                            pe.wait_ge(M["g_kept"], MT * (b + 1))
                        for x, w in enumerate("qk"):
                            if u:
                                pe.wait_ge(M["cross_ready"], 4 * (u - 1) + 2 * x + 2)
                                pe.wait_ge(M["main_ready"], 2 * (u - 1) + x + 1)
                                pe.wait_ge(M["sc_kept"], u)
                            for first, n, c in ((b * T, T, 0), (B * T + b, 1, T)):
                                for h in range(2):
                                    last = nc.tensor.matmul(p_ps[:, x, c:c + n], W[w][:, h, head * DQK:(head + 1) * DQK],
                                                            XT[:, h, first:first + n], start=(h == 0), stop=(h == 1))
                            last.then_inc(M["x_ready"], 1)
                        pe.wait_ge(M["turned"], 2 * u + 2)
                        q, k = turned[:, u % 2, 0, :], turned[:, u % 2, 1, :]
                        for m in range(TPB):
                            j = u * TPB + m
                            if j >= 2:
                                pe.wait_ge(M["s_act"], j - 1)
                            nc.tensor.matmul(s_ps[:, m % 2, m * P:T], k[:, m * P:(m + 1) * P], q[:, m * P:T], start=True,
                                             stop=True).then_inc(M["s_ready"], 1)
                        pe.wait_ge(M["main_ready"], 2 * u + 2)
                        pe.wait_ge(M["cross_ready"], 4 * u + 4)
                        for a, z in HALVES:
                            last = nc.tensor.matmul(p_ps[0:1, 0, L + a:L + z], k[:, T:N], q[:, a:z], start=True, stop=True)
                        last.then_inc(M["sc_ready"], 1)
                        pe.wait_ge(M["s_dve"], (u + 1) * TPB)
                        pe.wait_ge(M["s_act"], (u + 1) * TPB)
                        pe.wait_ge(M["sc_kept"], u + 1)
                        if u >= 2:
                            pe.wait_ge(M["o_kept"], 2 * (u - 1))
                        vh = slice(head * DV, (head + 1) * DV)
                        for t in range(TPB):
                            dst = o_ps[:, u % 2, t * DV:(t + 1) * DV]
                            for m in range(t + 1):
                                nc.tensor.matmul(dst, S[:, u % 2, m, t * P:(t + 1) * P], V[:, m, vh], start=(m == 0), stop=False)
                            nc.tensor.matmul(dst, SC[:, u % 2, t * P:(t + 1) * P], VC[:, vh], start=False, stop=True)
                        nc.tensor.matmul(o_ps[0:1, u % 2, TPB * DV:MT * DV], SC[:, u % 2, T:N], VC[:, vh], start=True,
                                         stop=True).then_inc(M["o_ready"], 1)
                    for k, m in enumerate(("sum_ready", "ss_ready")):
                        pe.wait_ge(M["sums_ready" if k == 0 else "css_ready"], b + 1)
                        if k == 0:
                            pe.wait_ge(M["o_kept"], 2 * RH * (b + 1))
                        nc.tensor.matmul(o_ps[:, k, 0:RH], ones[:], sums[:], start=True, stop=True).then_inc(M[m], 1)
                    pe.wait_ge(M["y_ready"], b + 1)
                    for c in range(RV // P):
                        if c >= 2:
                            pe.wait_ge(M["yt_kept"], b * (RV // P + 1) + c - 1)
                        for t in range(TPB):
                            last = nc.tensor.transpose(s_ps[:, c % 2, t * P:(t + 1) * P], O[:, b % 2, t, c * P:(c + 1) * P], ident[:])
                        last.then_inc(M["yt_ready"], 1)
                    for c in range(RV // P):
                        last = nc.tensor.transpose(p_ps[:, 0, c:c + 1], OC[:, b % 2, c * P:(c + 1) * P], ident[0:1, 0:1])
                    last.then_inc(M["yt_ready"], 1)
                    pe.wait_ge(M["yt_kept"], (b + 1) * (RV // P + 1) - 0)
                    for t in range(TPB):
                        n = b * TPB + t
                        if t >= 2:
                            pe.wait_ge(M["h_kept"], n - 1)
                        for c in range(RV // P):
                            last = nc.tensor.matmul(o_ps[:, t % 2, 0:D], YT[:, c, t * P:(t + 1) * P], Wo[:, c, :],
                                                    start=(c == 0), stop=(c == RV // P - 1))
                        last.then_inc(M["h_ready"], 1)
                pe.wait_ge(M["h_kept"], CLS)
                for c in range(RV // P):
                    last = nc.tensor.matmul(o_ps[0:B, 0, 0:D], YC[:, c, :], Wo[:, c, :], start=(c == 0),
                                            stop=(c == RV // P - 1))
                last.then_inc(M["h_ready"], 1)

            @block.scalar
            def _(act):
                for b in range(B):
                    for t in range(MT):
                        act.wait_ge(M["g_ready"], b * MT + t + 1)
                        if b and t == 0:
                            act.wait_ge(M["y_ready"], b)
                        dst, n = (G[:, t, :], P) if t < TPB else (GC[:], 1)
                        nc.scalar.activation(dst, o_ps[0:n, t % 2, 0:RV], ACT.Silu).then_inc(M["g_kept"], 1)
                    for head in range(RH):
                        u = b * RH + head
                        if u >= 2:
                            act.wait_ge(M["o_ready"], u - 1)
                        for m in range(TPB):
                            act.wait_ge(M["s_ready"], u * TPB + m + 1)
                            nc.scalar.activation(S[:, u % 2, m, m * P:T], s_ps[:, m % 2, m * P:T], ACT.Copy,
                                                 scale=kd[:, head, m:m + 1]).then_inc(M["s_act"], 1)
                        act.wait_ge(M["sc_ready"], u + 1)
                        nc.scalar.activation(SC[:, u % 2, 0:N], p_ps[0:1, 0, L:L + N], ACT.Copy,
                                             scale=kd[0:1, head, TPB:MT]).then_inc(M["sc_kept"], 1)
                    for c in range(RV // P):
                        act.wait_ge(M["yt_ready"], b * (RV // P + 1) + c + 1)
                        if c == 0:
                            act.wait_ge(M["h_ready"], b * TPB)
                        nc.scalar.activation(YT[:, c, :], s_ps[:, c % 2, :], ACT.Copy).then_inc(M["yt_kept"], 1)
                    act.wait_ge(M["yt_ready"], (b + 1) * (RV // P + 1))
                    nc.scalar.activation(YC[:, :, b], p_ps[:, 0, 0:RV // P], ACT.Copy).then_inc(M["yt_kept"], 1)

            @block.gpsimd
            def _(pool):
                nc.gpsimd.memset(causal[:], 1.0).then_inc(M["causal"], 1)
                pool.wait_ge(M["causal"], 1)
                nc.gpsimd.affine_select(out=causal[:], in_=causal[:], compare_op=ALU.is_ge, fill=0.0, base=0,
                                        pattern=[[1, P]], channel_multiplier=-1).then_inc(M["causal"], 1)
                nc.gpsimd.memset(half_power[:], -0.5).then_inc(M["causal"], 1)
                pool.wait_ge(M["causal"], 3)
                for b in range(B):
                    for u in range(b * RH, (b + 1) * RH):
                        for x in range(2):
                            pool.wait_ge(M["main_ready"], 2 * u + x + 1)
                            pool.wait_ge(M["cross_ready"], 4 * u + 2 * x + 2)
                            if u >= 2:
                                pool.wait_ge(M["sc_ready"], u - 1)
                            nc.gpsimd.tensor_tensor(turned[:, u % 2, x, 0:N], main[:, x, 0:N], cross[:, x, 0:N],
                                                    ALU.add).then_inc(M["turned"], 1)
                    pool.wait_ge(M["var_ready"], b + 1)
                    nc.gpsimd.tensor_scalar(var[:], var[:], LN_EPS, None, ALU.add).then_inc(M["pool_ready"], 1)
                    pool.wait_ge(M["pool_ready"], b + 1)
                    nc.gpsimd.tensor_tensor(var[:], var[:], half_power[:], ALU.pow).then_inc(M["rstd_ready"], 1)

            @block.vector
            def _(dve):
                dve.wait_ge(M["causal"], 3)
                by_head = "p t (h d) -> p h t d"
                for b in range(B):
                    Ob, OCb = O[:, b % 2, :, :], OC[:, b % 2, :]
                    for t in range(MT):
                        dve.wait_ge(M["v_ready"], b * MT + t + 1)
                        if b and t == 0:
                            dve.wait_ge(M["o_ready"], b * RH)
                        dst, n = (V[:, t, :], P) if t < TPB else (VC[:], 1)
                        nc.vector.tensor_copy(dst, s_ps[0:n, t % 2, 0:RV]).then_inc(M["v_kept"], 1)

                    def keep(head):
                        u = b * RH + head
                        dve.wait_ge(M["o_ready"], u + 1)
                        if b >= 2:
                            dve.wait_ge(M["yt_ready"], (b - 1) * (RV // P + 1))
                        vh = slice(head * DV, (head + 1) * DV)
                        nc.vector.tensor_tensor(Ob[:, :, vh], o_ps[:, u % 2, 0:TPB * DV].rearrange("p (t d) -> p t d", t=TPB),
                                                qd[:, head, 0:TPB].unsqueeze(2).broadcast_to((P, TPB, DV)),
                                                ALU.mult).then_inc(M["o_kept"], 1)
                        nc.vector.tensor_scalar(OCb[:, vh], o_ps[0:1, u % 2, TPB * DV:MT * DV], qd[0:1, head, TPB:MT], None,
                                                ALU.mult).then_inc(M["o_kept"], 1)

                    for head in range(RH):
                        u = b * RH + head
                        for x in range(2):
                            dve.wait_ge(M["x_ready"], 2 * u + x + 1)
                            dve.wait_ge(M["turned"], max(0, 2 * (u - 1) + x + 1))
                            nc.vector.tensor_tensor(main[:, x, 0:N], p_ps[:, x, 0:N], rot[:, x, 0, 0:N],
                                                    ALU.mult).then_inc(M["main_ready"], 1)
                            for src, dst in ((slice(64, P), slice(0, 64)), (slice(0, 64), slice(64, P))):
                                nc.vector.tensor_tensor(cross[dst, x, 0:N], p_ps[src, x, 0:N], rot[src, x, 1, 0:N],
                                                        ALU.mult).then_inc(M["cross_ready"], 1)
                        for m in range(TPB):
                            dve.wait_ge(M["s_act"], u * TPB + m + 1)
                            diagonal = S[:, u % 2, m, m * P:(m + 1) * P]
                            nc.vector.tensor_tensor(diagonal, diagonal, causal[:], ALU.mult).then_inc(M["s_dve"], 1)
                        if head:
                            keep(head - 1)
                    keep(RH - 1)

                    heads_of = Ob.rearrange(by_head, h=RH)
                    cls_heads = OCb.rearrange("p (h d) -> p h d", h=RH)

                    def total(values, cls_values, done):
                        nc.vector.tensor_reduce(sums[:], values, mybir.AxisListType.XY, ALU.add).then_inc(M["csum_ready"], 1)
                        nc.vector.reduce_sum(csum[:], cls_values, AX_X).then_inc(M["csum_ready"], 1)
                        dve.wait_ge(M["csum_ready"], 4 * b + (2 if done == "sums_ready" else 4))
                        nc.vector.tensor_tensor(sums[0:1, :], sums[0:1, :], csum[:], ALU.add).then_inc(M[done], 1)

                    dve.wait_ge(M["o_kept"], 2 * RH * (b + 1))
                    total(heads_of, cls_heads, "sums_ready")
                    dve.wait_ge(M["sum_ready"], b + 1)
                    nc.vector.tensor_scalar(mean[:], o_ps[:, 0, 0:RH], 1.0 / CNT, None, ALU.mult).then_inc(M["mean_ready"], 1)
                    dve.wait_ge(M["mean_ready"], b + 1)
                    tiles = "p t (h d) -> p t h d"
                    mean_b = mean[:].unsqueeze(2).broadcast_to((P, RH, DV))
                    for t in range(TPB):
                        v = Ob[:, t, :].rearrange("p (h d) -> p h d", h=RH)
                        nc.vector.tensor_tensor(v, v, mean_b, ALU.subtract).then_inc(M["centred"], 1)
                    nc.vector.tensor_tensor(cls_heads, cls_heads, mean[0:1, :].unsqueeze(2).broadcast_to((1, RH, DV)),
                                            ALU.subtract).then_inc(M["centred"], 1)
                    dve.wait_ge(M["centred"], MT * (b + 1))
                    sq = S[:, b % 2, 0:3, :].rearrange("p a n -> p (a n)")
                    sqc = SC[:, b % 2, 0:RV]
                    nc.vector.tensor_tensor(sq, Ob.rearrange("p t n -> p (t n)"), Ob.rearrange("p t n -> p (t n)"),
                                            ALU.mult).then_inc(M["sq_ready"], 1)
                    nc.vector.tensor_tensor(sqc, OCb, OCb, ALU.mult).then_inc(M["sq_ready"], 1)
                    dve.wait_ge(M["sq_ready"], 2 * b + 2)
                    total(sq.rearrange("p (t h d) -> p h t d", t=TPB, h=RH), sqc.rearrange("p (h d) -> p h d", h=RH),
                          "css_ready")
                    dve.wait_ge(M["ss_ready"], b + 1)
                    nc.vector.tensor_scalar(var[:], o_ps[:, 1, 0:RH], 1.0 / CNT, None, ALU.mult).then_inc(M["var_ready"], 1)
                    dve.wait_ge(M["rstd_ready"], b + 1)
                    nc.vector.tensor_tensor(gain[:].rearrange("p (h d) -> p h d", h=RH), gnw[:].rearrange("p (h d) -> p h d", h=RH),
                                            var[:].unsqueeze(2).broadcast_to((P, RH, DV)), ALU.mult).then_inc(M["gain_ready"], 1)
                    dve.wait_ge(M["gain_ready"], (2 * MT + 1) * b + 1)
                    dve.wait_ge(M["g_kept"], MT * (b + 1))
                    for k, (op, other) in enumerate(((ALU.mult, gain), (ALU.add, gnb), (ALU.mult, None))):
                        for t in range(MT):
                            v = Ob[:, t, :] if t < TPB else OCb
                            if other is None:
                                o = G[:, t, :] if t < TPB else GC[:]
                            else:
                                o = other[:] if t < TPB else other[0:1, :]
                            if k:
                                dve.wait_ge(M["gain_ready"], (2 * MT + 1) * b + 1 + MT * (k - 1) + t + 1)
                            last = nc.vector.tensor_tensor(v, v, o, op)
                            if k < 2:
                                last.then_inc(M["gain_ready"], 1)
                    last.then_inc(M["y_ready"], 1)
                    for t in range(TPB):
                        n = b * TPB + t
                        dve.wait_ge(M["h_ready"], n + 1)
                        nc.vector.tensor_tensor(H[:, n, :], H[:, n, :], o_ps[:, t % 2, 0:D], ALU.add).then_inc(M["h_kept"], 1)
                dve.wait_ge(M["h_ready"], CLS + 1)
                nc.vector.tensor_tensor(H[0:B, CLS, :], H[0:B, CLS, :], o_ps[0:B, 0, 0:D], ALU.add)


E = 8


def moe_stage(nc, sem, make_sb, make_ps, A, H, ident, ones):
    NF = F // P
    with ExitStack() as ctx:
        sb = make_sb(ctx)
        XT = sb("m_xT", [HALF, 2, NTOK])
        router = sb("m_router", [HALF, 2, E])
        combine = sb("m_combine", [P, NT, E])
        load(nc, sem, "m", [(router[:], halves_of(A["L1_ffn_router_w"]))])
        with ExitStack() as xctx:
            X = make_sb(xctx)("m_x", [P, NT, D])
            norm_stage(nc, sem, make_sb, make_ps, "mn", H, X, XT, ident)
        switch_routing(nc, sem, make_sb, make_ps, XT, router, combine)
        WI, WO = sb("m_wi", [HALF, 2, 2, F]), sb("m_wo", [P, 2, NF, D])
        hid = sb("m_hid", [P, 2, NF, T])
        ps = make_ps(ctx)
        h_ps, o_ps = ps("m_h", [P, 4, 512]), ps("m_o", [P, 4, 512])
        w_loaded = [sem("m_w_loaded0"), sem("m_w_loaded1")]
        h_ready, h_kept, o_ready, o_kept = sem("m_h_ready"), sem("m_h_kept"), sem("m_o_ready"), sem("m_o_kept")
        CHUNKS = [(b * T, T) for b in range(B)] + [(B * T, B)]
        NC = len(CHUNKS)
        HJ = NC * NF
        wi_d = A["L1_ffn_wi"].rearrange("e (h p) f -> e p h f", p=HALF)
        wo_d = A["L1_ffn_wo"].rearrange("e (f p) n -> e p f n", p=P)
        with nc.Block() as block:
            @block.sync
            def _(sp):
                with sp.Fori(0, E // 2) as i:
                    for s in range(2):
                        if s == 0:
                            sp.wait_ge(o_ready, NT * 2 * i)
                            sp.dma_start(WI[:, s, :, :], wi_d[2 * i + s]).then_inc(w_loaded[s], 16)
                            sp.dma_start(WO[:, s, :, :], wo_d[2 * i + s]).then_inc(w_loaded[s], 16)
                        else:
                            sp.wait_ge(o_ready, NT * 2 * i)
                            sp.dma_start(WI[:, s, :, :], wi_d[2 * i + s]).then_inc(w_loaded[s], 16)
                            sp.dma_start(WO[:, s, :, :], wo_d[2 * i + s]).then_inc(w_loaded[s], 16)

            @block.tensor
            def _(pe):
                with pe.Fori(0, E // 2) as i:
                    for s in range(2):
                        e = 2 * i + s
                        pe.wait_ge(w_loaded[s], 32 * i + 32)
                        for k, (first, n) in enumerate(CHUNKS):
                            for f in range(NF):
                                j = k * NF + f
                                pe.wait_ge(h_kept, e * HJ + j - 3 if j >= 4 else e * HJ)
                                for h in range(2):
                                    last = nc.tensor.matmul(h_ps[:, j % 4, 0:n], WI[:, s, h, f * P:(f + 1) * P],
                                                            XT[:, h, first:first + n], start=(h == 0), stop=(h == 1))
                                last.then_inc(h_ready, 1)
                            pe.wait_ge(h_kept, e * HJ + (k + 1) * NF)
                            for t in range(k * TPB, min(NT, (k + 1) * TPB)):
                                m, c = tokens_of(t)
                                pe.wait_ge(o_kept, e * NT + t - 3 if t >= 4 else e * NT)
                                for f in range(NF):
                                    last = nc.tensor.matmul(o_ps[0:m, t % 4, 0:D], hid[:, k % 2, f, c - first:c - first + m],
                                                            WO[:, s, f, :], start=(f == 0), stop=(f == NF - 1))
                                last.then_inc(o_ready, 1)

            @block.scalar
            def _(act):
                with act.Fori(0, E // 2) as i:
                    for s in range(2):
                        e = 2 * i + s
                        for k, (first, n) in enumerate(CHUNKS):
                            act.wait_ge(o_ready, e * NT + (k - 1) * TPB if k >= 2 else e * NT)
                            for f in range(NF):
                                j = k * NF + f
                                act.wait_ge(h_ready, e * HJ + j + 1)
                                nc.scalar.activation(hid[:, k % 2, f, 0:n], h_ps[:, j % 4, 0:n], ACT.Relu).then_inc(h_kept, 1)

            @block.vector
            def _(dve):
                with dve.Fori(0, E // 2) as i:
                    for s in range(2):
                        e = 2 * i + s
                        for t in range(NT):
                            m, _ = tokens_of(t)
                            dve.wait_ge(o_ready, e * NT + t + 1)
                            dve.wait_ge(o_kept, e * NT)
                            nc.vector.scalar_tensor_tensor(out=H[0:m, t, :], in0=o_ps[0:m, t % 4, 0:D],
                                                           scalar=combine[0:m, t, bass.ds(e, 1)], in1=H[0:m, t, :],
                                                           op0=ALU.mult, op1=ALU.add).then_inc(o_kept, 1)


def switch_routing(nc, sem, make_sb, make_ps, XT, router, combine):
    with ExitStack() as ctx:
        sb, ps = make_sb(ctx), make_ps(ctx)
        logit = sb("s_logit", [P, NT, E])
        top = sb("s_top", [P, NT])
        shifted = sb("s_shifted", [P, NT, E])
        index = sb("s_index", [P, E])
        key = sb("s_key", [P, NT, E])
        first = sb("s_first", [P, NT])
        chosen = sb("s_chosen", [P, NT, E])
        ex, exsum = sb("s_exp", [P, NT, E]), sb("s_expsum", [P, NT])
        l_ps = ps("s_l", [P, 512])
        const, l_ready, step = sem("s_const"), sem("s_l_ready"), sem("s_step")
        shifted_ready, exp_ready = sem("s_shifted_ready"), sem("s_exp_ready")
        with nc.Block() as block:
            @block.gpsimd
            def _(pool):
                nc.gpsimd.iota(index[:], pattern=[[1, E]], base=-E, channel_multiplier=0,
                               allow_small_or_imprecise_dtypes=True).then_inc(const, 1)

            @block.tensor
            def _(pe):
                for t in range(NT):
                    n, c = tokens_of(t)
                    for h in range(2):
                        last = nc.tensor.matmul(l_ps[0:n, t * E:(t + 1) * E], XT[:, h, c:c + n], router[:, h, :],
                                                start=(h == 0), stop=(h == 1))
                last.then_inc(l_ready, 1)

            @block.scalar
            def _(act):
                act.wait_ge(shifted_ready, 1)
                nc.scalar.activation(ex[:], shifted[:], ACT.Exp).then_inc(exp_ready, 1)

            @block.vector
            def _(dve):
                steps = Tally(step)

                def then(ins):
                    dve.wait_ge(step, steps.mark(ins))

                then(nc.vector.memset(logit[:, CLS, :], 0.0))
                dve.wait_ge(l_ready, 1)
                nc.vector.tensor_copy(logit[:, 0:CLS, :], l_ps[:, 0:CLS * E].rearrange("p (t e) -> p t e", e=E))
                then(nc.vector.tensor_copy(logit[0:B, CLS, :], l_ps[0:B, CLS * E:NT * E]))
                then(nc.vector.reduce_max(top[:], logit[:], AX_X))
                top_b = top[:].unsqueeze(2).broadcast_to((P, NT, E))
                nc.vector.tensor_tensor(shifted[:], logit[:], top_b, ALU.subtract).then_inc(shifted_ready, 1)
                dve.wait_ge(const, 1)
                dve.wait_ge(shifted_ready, 1)
                then(nc.vector.tensor_scalar(key[:], shifted[:], 0.0, None, ALU.is_equal))
                then(nc.vector.tensor_tensor(key[:], key[:], index[:].unsqueeze(1).broadcast_to((P, NT, E)), ALU.mult))
                then(nc.vector.tensor_reduce(first[:], key[:], AX_X, ALU.min))
                then(nc.vector.tensor_tensor(chosen[:], index[:].unsqueeze(1).broadcast_to((P, NT, E)),
                                             first[:].unsqueeze(2).broadcast_to((P, NT, E)), ALU.is_equal))
                dve.wait_ge(exp_ready, 1)
                then(nc.vector.reduce_sum(exsum[:], ex[:], AX_X))
                then(nc.vector.reciprocal(exsum[:], exsum[:]))
                nc.vector.tensor_tensor(combine[:], chosen[:], exsum[:].unsqueeze(2).broadcast_to((P, NT, E)), ALU.mult)

_INS = ['x', 'cls_tok', 'L0_tok_freq_bands', 'L0_tok_W', 'L0_attn_w_qkv', 'L0_attn_w_proj', 'L0_attn_b_proj',
        'L0_ffn_g1', 'L0_ffn_b1', 'L0_ffn_g2', 'L0_ffn_b2', 'L0_ffn_Wr', 'L0_ffn_br', 'L0_ffn_Wq', 'L0_ffn_bq',
        'L0_ffn_Wk', 'L0_ffn_bk', 'L0_ffn_Wv', 'L0_ffn_bv', 'L0_ffn_Wo', 'L0_ffn_bo', 'L0_ffn_Wm', 'L0_ffn_bm',
        'L0_ffn_W1', 'L0_ffn_bf1', 'L0_ffn_W2', 'L0_ffn_bf2', 'L1_attn_Wq', 'L1_attn_Wk', 'L1_attn_Wv', 'L1_attn_Wg',
        'L1_attn_Wo', 'L1_attn_gn_weight', 'L1_attn_gn_bias', 'L1_ffn_router_w', 'L1_ffn_wi', 'L1_ffn_wo']
DEBUG = ()


def kernel(**inputs):
    import concourse.bacc as _bacc
    from concourse.bass_utils import run_bass_kernel_spmd as _run

    nc = _bacc.Bacc("TRN2", target_bir_lowering=False, num_devices=1)
    arrays, A = {}, {}
    tables = dict(zip(("rot", "query_decay", "key_decay"), retention_tables()))
    for name in _INS + list(tables):
        a = np.ascontiguousarray(inputs[name] if name in _INS else tables[name])
        if a.ndim == 0:
            a = a.reshape(1)
        arrays[f"in_{name}"] = a
        A[name] = nc.dram_tensor(f"in_{name}", a.shape, mybir.dt.from_np(a.dtype), kind="ExternalInput").ap()
    out = nc.dram_tensor("out", (B, N, D), F32, kind="ExternalOutput").ap()
    dbg = {n: nc.dram_tensor("dbg_" + n, (P, NT, D), F32, kind="ExternalOutput").ap() for n in DEBUG}
    build_program(nc, A, out, dbg)
    r = _run(nc, [arrays], core_ids=[0])
    return r.results[0]["out"]
```

```python
from contextlib import ExitStack

import numpy as np

import concourse.bass as bass
from concourse import mybir

F32 = mybir.dt.float32
I32, U32 = mybir.dt.int32, mybir.dt.uint32
ALU = mybir.AluOpType
ACT = mybir.ActivationFunctionType
AX_X = mybir.AxisListType.X

B, C, T, D = 4, 3, 512, 192
N = T + 1
P = 128
TPB = T // P
NT = B * TPB + 1
CLS = B * TPB
NTOK = B * N
HALF = 96
NP = 514
BANDS = 6
JT = C * D
LN_EPS = 1e-5

HEADS, HD = 12, 16
HG = 4
GROUPS = HEADS // HG
R = P // HG
CH = T // R + 1
ITERS = 10
SLOTS = 2
BPS = B // SLOTS
INV_REG = 10.0

TWO_PI_BELOW = 6.283185
ROUND = 1.5 * 2.0 ** 23


class Tally:

    def __init__(self, sem):
        self.sem, self.n = sem, 0

    def mark(self, ins):
        ins.then_inc(self.sem, 1)
        self.n += 1
        return self.n


def later(i):
    return not isinstance(i, int) or i > 0


def build_program(nc, A, out, dbg):
    root = ExitStack()
    with root:
        taken = []

        def sem(name):
            s = nc.alloc_semaphore(name)
            taken.append(s)
            return s

        def recycle():
            with nc.Block() as block:
                @block.sync
                def _(sp):
                    for s in taken:
                        sp.sem_clear(s)
            for s in taken:
                nc.release_semaphore(s)
            taken.clear()

        def make_sb(ctx):
            return lambda name, shape, dt=F32: ctx.enter_context(nc.sbuf_tensor(name, shape, dt))

        def make_ps(ctx):
            return lambda name, shape: ctx.enter_context(nc.psum_tensor(name, shape, F32))

        rsb = make_sb(root)
        H = rsb("H", [P, NT, D])
        ident = rsb("ident", [P, P])
        ones = rsb("ones", [P, P])

        constants_stage(nc, sem, H, ident, ones)
        tokenizer_stage(nc, sem, make_sb, make_ps, A, H, ident)
        dump(nc, sem, dbg, "h1", H)
        with ExitStack() as attn:
            asb = make_sb(attn)
            WprojT = asb("WprojT", [64, GROUPS, D])
            bproj = asb("bproj", [1, D])
            QT = asb("QT", [64, B * GROUPS, NP])
            V = asb("V", [P, SLOTS, TPB, BPS * D])
            VC = asb("VC", [1, SLOTS, BPS * D])
            with ExitStack() as x_ctx:
                xsb = make_sb(x_ctx)
                WqkvT = xsb("WqkvT", [HALF, 2, 3 * D])
                XT = xsb("XT", [HALF, 2, NTOK])
                X = xsb("X", [P, NT, D])
                norm_stage(nc, sem, make_sb, make_ps, "ln1", H, X, XT, ident)
                sinkhorn_weights_stage(nc, sem, make_sb, make_ps, A, WqkvT, WprojT, bproj, ident)
                sinkhorn_query_stage(nc, sem, make_sb, make_ps, XT, WqkvT, QT, V, VC, ident)
            sinkhorn_stage(nc, sem, make_sb, make_ps, QT, V, VC, ones)
            sinkhorn_out_stage(nc, sem, make_ps, QT, WprojT, bproj, ones, H)
        dump(nc, sem, dbg, "h2", H)
        recycle()
        routed_stage(nc, sem, make_sb, make_ps, A, H, ident, ones)
        dump(nc, sem, dbg, "h3", H)
        recycle()
        retention_stage(nc, sem, make_sb, make_ps, A, H, ident, ones)
        dump(nc, sem, dbg, "h4", H)
        recycle()
        moe_stage(nc, sem, make_sb, make_ps, A, H, ident, ones)
        final_stage(nc, sem, H, out)


def dump(nc, sem, dbg, name, H):
    if name not in dbg:
        return
    s = sem("dump_" + name)
    with nc.Block() as block:
        @block.sync
        def _(sp):
            sp.dma_start(dbg[name], H[:]).then_inc(s, 16)
            sp.wait_ge(s, 16)


def final_stage(nc, sem, H, out):
    stored = sem("out_stored")
    with nc.Block() as block:
        @block.sync
        def _(sp):
            for b in range(B):
                sp.dma_start(out[b, 1:N, :].rearrange("(t p) d -> p t d", p=P),
                             H[:, TPB * b:TPB * b + TPB, :]).then_inc(stored, 16)
            sp.dma_start(out[:, 0, :], H[0:B, CLS, :]).then_inc(stored, 16)
            sp.wait_ge(stored, 16 * (B + 1))


def constants_stage(nc, sem, H, ident, ones):
    filled = sem("const_filled")
    done = sem("const_done")
    with nc.Block() as block:
        @block.gpsimd
        def _(pool):
            nc.gpsimd.memset(ident[:], 0.0).then_inc(filled, 1)
            pool.wait_ge(filled, 1)
            nc.gpsimd.affine_select(out=ident[:], in_=ident[:], compare_op=ALU.not_equal, fill=1.0, base=0,
                                    pattern=[[-1, P]], channel_multiplier=1).then_inc(done, 1)

        @block.vector
        def _(dve):
            nc.vector.memset(ones[:], 1.0)
            nc.vector.memset(H[:, CLS, :], 0.0)


def tokenizer_stage(nc, sem, make_sb, make_ps, A, H, ident):
    ARGS = [(c, k) for c in range(4) for k in range(BANDS)] + [(4, m) for m in range(BANDS // 2)]
    NA, NU = len(ARGS), 2 * len(ARGS)
    FR, MR, XR = 6, 3, 4
    with ExitStack() as ctx:
        sb, ps = make_sb(ctx), make_ps(ctx)
        WT = sb("tok_WT", [P, NU, D])
        XN = sb("tok_x", [P, TPB, JT + 64])
        XJ = sb("tok_xj", [P, 5, T])
        band = sb("tok_band", [P, BANDS])
        pair = sb("tok_pair", [P, BANDS // 2])
        half_pi = sb("tok_half_pi", [P, 1])
        turns = sb("tok_turns", [P, XR, T])
        whole = sb("tok_whole", [P, 2, T])
        back = sb("tok_back", [P, MR, T])
        size = sb("tok_size", [P, 2, T])
        feat = sb("tok_feat", [P, FR, T])
        acc = ps("tok_acc", [P, TPB, 512])
        stage = ps("tok_stage", [P, 4, 512])
        w_loaded = [sem(f"tok_w_loaded{c}") for c in range(5)]
        x_loaded, small_loaded = sem("tok_x_loaded"), sem("tok_small_loaded")
        cls_loaded = sem("tok_cls_loaded")
        wt_turned, wt_kept_dve, wt_kept_act = sem("tok_wt_turned"), sem("tok_wt_kept_dve"), sem("tok_wt_kept_act")
        x_turned, x_kept = sem("tok_x_turned"), sem("tok_x_kept")
        turns_ready, whole_ready, back_ready = sem("tok_turns_ready"), sem("tok_whole_ready"), sem("tok_back_ready")
        size_ready = sem("tok_size_ready")
        feat_ready, feat_used = sem("tok_feat_ready"), sem("tok_feat_used")
        acc_kept = sem("tok_acc_kept")
        const_ready, paired = sem("tok_const_ready"), sem("tok_paired")

        x_dram = A["x"].rearrange("b c n d -> (b c n d)").rearrange("(b t p j) -> b p t j", b=B, t=TPB, p=P)
        f_dram = A["L0_tok_freq_bands"].rearrange("(a s) -> a s", a=1)

        with ExitStack() as w_ctx:
            WN = make_sb(w_ctx)("tok_WN", [HALF, 2, JT * 2 * BANDS])
            WP = make_sb(w_ctx)("tok_WP", [HALF, 2, 2 * BANDS, 64])
            W_s = WN[:].rearrange("p h (j s) -> p h j s", s=2 * BANDS)
            w_paired = sem("tok_w_paired")
            w_dram = A["L0_tok_W"].rearrange("(h p) f -> p h f", p=HALF)
            with nc.Block() as block:
                @block.sync
                def _(sp):
                    for c in range(5):
                        a, z = c * P * 2 * BANDS, min(JT, (c + 1) * P) * 2 * BANDS
                        sp.dma_start(WN[:, :, a:z], w_dram[:, :, a:z]).then_inc(w_loaded[c], 16)

                @block.tensor
                def _(pe):
                    for a, (c, k) in enumerate(ARGS):
                        if c == 4:
                            pe.wait_ge(w_paired, 2)
                        elif a % BANDS == 0:
                            pe.wait_ge(w_loaded[c], 16)
                        if a >= 4:
                            pe.wait_ge(*((wt_kept_dve, (a - 4) // 2 + 1) if a % 2 == 0 else (wt_kept_act, (a - 5) // 2 + 1)))
                        for trig in range(2):
                            for h in range(2):
                                if c < 4:
                                    src = W_s[:, h, c * P:(c + 1) * P, trig * BANDS + k]
                                else:
                                    s = trig * BANDS + 2 * k
                                    src = WP[:, h, s:s + 2, :].rearrange("p s j -> p (s j)")
                                o = trig * D + h * HALF
                                last = nc.tensor.transpose(stage[:, a % 4, o:o + HALF], src, ident[0:HALF, 0:HALF])
                        last.then_inc(wt_turned, 1)

                @block.gpsimd
                def _(pool):
                    pool.wait_ge(w_loaded[4], 16)
                    for h in range(2):
                        nc.gpsimd.tensor_copy(WP[:, h, :, :],
                                              W_s[:, h, 4 * P:JT, :].rearrange("p j s -> p s j")).then_inc(w_paired, 1)

                @block.vector
                def _(dve):
                    nc.vector.memset(half_pi[:], float(np.pi / 2)).then_inc(const_ready, 1)
                    for a in range(0, NA, 2):
                        dve.wait_ge(wt_turned, a + 1)
                        nc.vector.tensor_copy(WT[:, 2 * a:2 * a + 2, :], stage[:, a % 4, 0:2 * D].rearrange(
                            "p (u o) -> p u o", u=2)).then_inc(wt_kept_dve, 1)

                @block.scalar
                def _(act):
                    for a in range(1, NA, 2):
                        act.wait_ge(wt_turned, a + 1)
                        nc.scalar.activation(WT[:, 2 * a:2 * a + 2, :], stage[:, a % 4, 0:2 * D].rearrange(
                            "p (u o) -> p u o", u=2), ACT.Copy).then_inc(wt_kept_act, 1)

        with nc.Block() as block:
            @block.sync
            def _(sp):
                sp.dma_start(band[:], f_dram[0].partition_broadcast(P)).then_inc(small_loaded, 16)
                for b in range(B):
                    sp.dma_start(H[b:b + 1, CLS, :], A["cls_tok"][0]).then_inc(cls_loaded, 16)
                with sp.Fori(0, B) as b:
                    sp.wait_ge(x_turned, 5 * b)
                    sp.dma_start(XN[:, :, 0:JT], x_dram[b]).then_inc(x_loaded, 16)
                    sp.dma_start(XN[:, :, JT:JT + 64], x_dram[b, :, :, JT - 64:JT]).then_inc(x_loaded, 16)
                sp.wait_ge(cls_loaded, 16 * B)

            @block.tensor
            def _(pe):
                with pe.Fori(0, B) as b:
                    pe.wait_ge(x_loaded, 32 * b + 32)
                    pe.wait_ge(x_kept, 5 * b)
                    for c in range(5):
                        if c == 4:
                            pe.wait_ge(x_kept, 5 * b + 1)
                        for t in range(TPB):
                            last = nc.tensor.transpose(stage[:, c % 4, t * P:(t + 1) * P],
                                                       XN[:, t, c * P:(c + 1) * P], ident[:])
                        last.then_inc(x_turned, 1)
                    for u in range(NU):
                        if u == 0:
                            pe.wait_ge(acc_kept, TPB * b)
                        pe.wait_ge(feat_ready, NU * b + u + 1)
                        for t in range(TPB):
                            last = nc.tensor.matmul(acc[:, t, 0:D], feat[:, u % FR, t * P:(t + 1) * P], WT[:, u, :],
                                                    start=(u == 0), stop=(u == NU - 1))
                        last.then_inc(feat_used, 1)

            @block.gpsimd
            def _(pool):
                pool.wait_ge(small_loaded, 16)
                for k in range(2):
                    nc.gpsimd.tensor_copy(pair[64 * k:64 * k + 64, :], band[64 * k:64 * k + 64, k:BANDS:2]).then_inc(paired, 1)
                pool.wait_ge(paired, 2)
                with pool.Fori(0, B) as b:
                    for a, (c, k) in enumerate(ARGS):
                        if a % BANDS == 0:
                            pool.wait_ge(x_kept, 5 * b + c + 1)
                        if a >= XR:
                            pool.wait_ge(back_ready, NA * b + a - XR + 1)
                        f = band[:, k:k + 1] if c < 4 else pair[:, k:k + 1]
                        nc.gpsimd.tensor_tensor(turns[:, a % XR, :], XJ[:, c, :], f.broadcast_to((P, T)),
                                                ALU.mult).then_inc(turns_ready, 1)

            @block.vector
            def _(dve):
                with dve.Fori(0, B) as b:
                    for c in range(5):
                        if c == 0:
                            dve.wait_ge(turns_ready, NA * b)
                        dve.wait_ge(x_turned, 5 * b + c + 1)
                        nc.vector.tensor_copy(XJ[:, c, :], stage[:, c % 4, :]).then_inc(x_kept, 1)
                    for a in range(NA):
                        dve.wait_ge(turns_ready, NA * b + a + 1)
                        nc.vector.tensor_scalar(whole[:, a % 2, :], turns[:, a % XR, :], ROUND, None,
                                                ALU.add).then_inc(whole_ready, 1)
                        if a >= MR:
                            dve.wait_ge(feat_ready, NU * b + 2 * (a - MR) + 1)
                            dve.wait_ge(size_ready, NA * b + a - MR + 1)
                        else:
                            dve.wait_ge(feat_ready, NU * b)
                        dve.wait_ge(whole_ready, NA * b + a + 1)
                        nc.vector.scalar_tensor_tensor(out=back[:, a % MR, :], in0=whole[:, a % 2, :], scalar=-ROUND,
                                                       in1=turns[:, a % XR, :], op0=ALU.add,
                                                       op1=ALU.subtract).then_inc(back_ready, 1)

            @block.scalar
            def _(act):
                nc.scalar.preload_act_table_set("trig_and_small")
                with act.Fori(0, B) as b:
                    for a in range(NA):
                        act.wait_ge(back_ready, NA * b + a + 1)
                        for trig in range(2):
                            u = 2 * a + trig
                            if trig == 1:
                                act.wait_ge(size_ready, NA * b + a + 1)
                            if u >= FR:
                                act.wait_ge(feat_used, NU * b + u - FR + 1)
                            else:
                                act.wait_ge(feat_used, NU * b)
                            if trig == 0:
                                nc.scalar.activation(feat[:, u % FR, :], back[:, a % MR, :], ACT.Sin,
                                                     scale=-TWO_PI_BELOW).then_inc(feat_ready, 1)
                                nc.scalar.activation(size[:, a % 2, :], back[:, a % MR, :],
                                                     ACT.Abs).then_inc(size_ready, 1)
                            else:
                                nc.scalar.activation(feat[:, u % FR, :], size[:, a % 2, :], ACT.Sin,
                                                     bias=half_pi[:], scale=-TWO_PI_BELOW).then_inc(feat_ready, 1)
                    act.wait_ge(feat_used, NU * b + NU)
                    act.wait_ge(cls_loaded, 16 * B)
                    for t in range(TPB):
                        nc.scalar.activation(H[:, TPB * b + t, :], acc[:, t, 0:D], ACT.Copy).then_inc(acc_kept, 1)


def norm_stage(nc, sem, make_sb, make_ps, name, src, dst, dstT, ident, inner=None, gain=None, shift=None):
    with ExitStack() as ctx:
        sb, ps = make_sb(ctx), make_ps(ctx)
        stats = sb(name + "_stats", [P, NT, 6])
        moments = sb(name + "_moments", [P, NT, 2])
        power = sb(name + "_power", [P, NT])
        rstd = sb(name + "_rstd", [P, NT])
        turn = ps(name + "_turn", [P, 4, 512])
        stats_ready, moments_ready = sem(name + "_stats_ready"), sem(name + "_moments_ready")
        pool_done, rstd_ready = sem(name + "_pool_done"), sem(name + "_rstd_ready")
        normed, turned = sem(name + "_normed"), sem(name + "_turned")
        kept_dve, kept_act = sem(name + "_kept_dve"), sem(name + "_kept_act")
        rounds = [(src, inner), (inner, dst)] if inner is not None else [(src, dst)]

        with nc.Block() as block:
            @block.vector
            def _(dve):
                for r, (a, z) in enumerate(rounds):
                    if r:
                        dve.wait_ge(normed, NT)
                    for t in range(NT):
                        nc.vector.bn_stats(stats[:, t, :], a[:, t, :]).then_inc(stats_ready, 1)
                    for t in range(NT):
                        dve.wait_ge(stats_ready, NT * r + t + 1)
                        nc.vector.bn_aggr(moments[:, t, :], stats[:, t, :]).then_inc(moments_ready, 1)
                    dve.wait_ge(moments_ready, NT * (r + 1))
                    dve.wait_ge(rstd_ready, r + 1)
                    affine = r == len(rounds) - 1 and gain is not None
                    base = NT * r
                    for t in range(NT):
                        nc.vector.tensor_scalar(z[:, t, :], a[:, t, :], moments[:, t, 0:1], rstd[:, t:t + 1],
                                                ALU.subtract, ALU.mult).then_inc(normed, 1)
                    if affine:
                        for k, (op, v) in enumerate(((ALU.mult, gain), (ALU.add, shift))):
                            for t in range(NT):
                                dve.wait_ge(normed, base + NT * k + t + 1)
                                nc.vector.tensor_tensor(z[:, t, :], z[:, t, :], v[:], op).then_inc(normed, 1)
                for t in range(NT):
                    n = P if t < CLS else B
                    dve.wait_ge(turned, 2 * t + 1)
                    nc.vector.tensor_copy(dstT[:, 0, t * P:t * P + n], turn[0:HALF, (2 * t) % 4, 0:n]).then_inc(kept_dve, 1)

            @block.gpsimd
            def _(pool):
                nc.gpsimd.memset(power[:], -0.5).then_inc(pool_done, 1)
                for r in range(len(rounds)):
                    pool.wait_ge(moments_ready, NT * (r + 1))
                    pool.wait_ge(pool_done, r + 1)
                    nc.gpsimd.tensor_scalar(rstd[:], moments[:, :, 1], LN_EPS, None, ALU.add).then_inc(pool_done, 1)
                    pool.wait_ge(pool_done, r + 2)
                    nc.gpsimd.tensor_tensor(rstd[:], rstd[:], power[:], ALU.pow).then_inc(rstd_ready, 1)

            @block.tensor
            def _(pe):
                before = NT * (len(rounds) - 1) + (2 * NT if gain is not None else 0)
                for t in range(NT):
                    n = P if t < CLS else B
                    pe.wait_ge(normed, before + t + 1)
                    for h in range(2):
                        if t >= 2:
                            pe.wait_ge(kept_dve if h == 0 else kept_act, t - 1)
                        nc.tensor.transpose(turn[0:HALF, (2 * t + h) % 4, 0:n], dst[0:n, t, h * HALF:(h + 1) * HALF],
                                            ident[0:n, 0:n]).then_inc(turned, 1)

            @block.scalar
            def _(act):
                for t in range(NT):
                    n = P if t < CLS else B
                    act.wait_ge(turned, 2 * t + 2)
                    nc.scalar.activation(dstT[:, 1, t * P:t * P + n], turn[0:HALF, (2 * t + 1) % 4, 0:n],
                                         ACT.Copy).then_inc(kept_act, 1)


def sinkhorn_weights_stage(nc, sem, make_sb, make_ps, A, WqkvT, WprojT, bproj, ident):
    NB = 3 * D // HALF
    with ExitStack() as ctx:
        sb, ps = make_sb(ctx), make_ps(ctx)
        qkv = sb("skw_qkv", [HALF, NB, D])
        proj = sb("skw_proj", [HALF, 2, D])
        turn = ps("skw_turn", [P, 8, 512])
        loaded, turned, kept = sem("skw_loaded"), sem("skw_turned"), sem("skw_kept")
        with nc.Block() as block:
            @block.sync
            def _(sp):
                sp.dma_start(qkv[:], A["L0_attn_w_qkv"].rearrange("(k p) c -> p k c", p=HALF)).then_inc(loaded, 16)
                sp.dma_start(proj[:], A["L0_attn_w_proj"].rearrange("(k p) c -> p k c", p=HALF)).then_inc(loaded, 16)
                sp.dma_start(bproj[:], A["L0_attn_b_proj"].rearrange("(a c) -> a c", a=1)).then_inc(loaded, 16)
                sp.wait_ge(loaded, 48)

            @block.tensor
            def _(pe):
                pe.wait_ge(loaded, 48)
                for h in range(2):
                    for k in range(NB):
                        last = nc.tensor.transpose(turn[0:HALF, 3 * h + k // 2, (k % 2) * HALF:(k % 2 + 1) * HALF],
                                                   qkv[:, k, h * HALF:(h + 1) * HALF], ident[0:HALF, 0:HALF])
                last.then_inc(turned, 1)
                for g in range(GROUPS):
                    for k in range(2):
                        o = g * D + k * HALF
                        bank, o = (6, o) if g < 2 else (7, k * HALF)
                        last = nc.tensor.transpose(turn[0:64, bank, o:o + HALF], proj[:, k, 64 * g:64 * g + 64],
                                                   ident[0:HALF, 0:HALF])
                last.then_inc(turned, 1)

            @block.vector
            def _(dve):
                dve.wait_ge(turned, 2)
                for h in range(2):
                    nc.vector.tensor_copy(WqkvT[:, h, :].rearrange("p (a o) -> p a o", a=3),
                                          turn[0:HALF, 3 * h:3 * h + 3, 0:D])
                nc.vector.tensor_copy(WprojT[:, 0:2, :], turn[0:64, 6, 0:2 * D].rearrange("p (g o) -> p g o", g=2))
                nc.vector.tensor_copy(WprojT[:, 2, :], turn[0:64, 7, 0:D])


def sinkhorn_query_stage(nc, sem, make_sb, make_ps, XT, WqkvT, QT, V, VC, ident):
    with ExitStack() as ctx:
        sb, ps = make_sb(ctx), make_ps(ctx)
        Q = sb("skq_q", [P, NT, D])
        square = sb("skq_square", [P, 2, D])
        norm = sb("skq_norm", [P, NT * HEADS])
        half = sb("skq_half", [P, NT * HEADS])
        scale = sb("skq_scale", [P, NT * HEADS])
        qp = ps("skq_qp", [P, 2, 512])
        turn = ps("skq_turn", [P, 6, 512])
        q_ready, q_kept, sq_ready, n2_ready = sem("skq_q_ready"), sem("skq_q_kept"), sem("skq_sq_ready"), sem("skq_n2_ready")
        zeroed, pooled, scaled = sem("skq_zeroed"), sem("skq_pooled"), sem("skq_scaled")
        v_ready, v_kept = sem("skq_v_ready"), sem("skq_v_kept")
        q_normed, turned, kept = sem("skq_q_normed"), sem("skq_turned"), sem("skq_kept")
        with nc.Block() as block:
            @block.tensor
            def _(pe):
                for t in range(NT):
                    n = P if t < CLS else B
                    if t >= 2:
                        pe.wait_ge(q_kept, t - 1)
                    for h in range(2):
                        last = nc.tensor.matmul(qp[0:n, t % 2, 0:D], XT[:, h, t * P:t * P + n], WqkvT[:, h, 0:D],
                                                start=(h == 0), stop=(h == 1))
                    last.then_inc(q_ready, 1)
                pe.wait_ge(q_kept, NT)
                for t in range(CLS + B):
                    n, first = (P, t * P) if t < CLS else (1, t - CLS + B * T)
                    if t >= 2:
                        pe.wait_ge(v_kept, t - 1)
                    for h in range(2):
                        last = nc.tensor.matmul(qp[0:n, t % 2, 0:D], XT[:, h, first:first + n], WqkvT[:, h, 2 * D:3 * D],
                                                start=(h == 0), stop=(h == 1))
                    last.then_inc(v_ready, 1)
                for t in range(NT):
                    n = P if t < CLS else B
                    pe.wait_ge(q_normed, 1)
                    if t >= 2:
                        pe.wait_ge(kept, t - 1)
                    for g in range(GROUPS):
                        last = nc.tensor.transpose(turn[0:64, t % 2, g * P:g * P + n], Q[0:n, t, 64 * g:64 * g + 64],
                                                   ident[0:n, 0:n])
                    last.then_inc(turned, 1)

            @block.scalar
            def _(act):
                for t in range(NT):
                    n = P if t < CLS else B
                    act.wait_ge(q_ready, t + 1)
                    if t == CLS:
                        act.wait_ge(zeroed, 1)
                    nc.scalar.activation(Q[0:n, t, :], qp[0:n, t % 2, 0:D], ACT.Copy).then_inc(q_kept, 1)
                for t in range(CLS + B):
                    act.wait_ge(v_ready, t + 1)
                    n = P if t < CLS else 1
                    b = t // TPB if t < CLS else t - CLS
                    cols = slice(b % BPS * D, (b % BPS + 1) * D)
                    dst = V[:, b // BPS, t % TPB, cols] if t < CLS else VC[:, b // BPS, cols]
                    nc.scalar.activation(dst, qp[0:n, t % 2, 0:D], ACT.Copy).then_inc(v_kept, 1)

            @block.vector
            def _(dve):
                nc.vector.memset(Q[:, CLS, :], 0.0).then_inc(zeroed, 1)
                for t in range(NT):
                    dve.wait_ge(q_kept, t + 1)
                    nc.vector.tensor_tensor(square[:, t % 2, :], Q[:, t, :], Q[:, t, :], ALU.mult).then_inc(sq_ready, 1)
                    dve.wait_ge(sq_ready, t + 1)
                    nc.vector.reduce_sum(norm[:, t * HEADS:(t + 1) * HEADS],
                                         square[:, t % 2, :].rearrange("p (h d) -> p h d", d=HD), AX_X).then_inc(n2_ready, 1)
                dve.wait_ge(pooled, 3)
                nc.vector.reciprocal(scale[:], norm[:]).then_inc(scaled, 1)
                dve.wait_ge(scaled, 1)
                q_all = Q[:].rearrange("p t (h d) -> p (t h) d", d=HD)
                nc.vector.tensor_tensor(q_all, q_all, scale[:].unsqueeze(2).broadcast_to((P, NT * HEADS, HD)),
                                        ALU.mult).then_inc(q_normed, 1)
                for t in range(NT):
                    n = P if t < CLS else B
                    dve.wait_ge(turned, t + 1)
                    src = turn[0:64, t % 2, 0:GROUPS * P].rearrange("p (g n) -> p g n", g=GROUPS)[:, :, 0:n]
                    b, c = t // TPB, (t % TPB) * P
                    dst = (QT[:, b * GROUPS:(b + 1) * GROUPS, c:c + P] if t < CLS else
                           QT[:, :, T].rearrange("p (b g) -> p g b", g=GROUPS))
                    nc.vector.tensor_copy(dst, src).then_inc(kept, 1)

            @block.gpsimd
            def _(pool):
                nc.gpsimd.memset(half[:], 0.5).then_inc(pooled, 1)
                pool.wait_ge(pooled, 1)
                pool.wait_ge(n2_ready, NT)
                nc.gpsimd.tensor_tensor(norm[:], norm[:], half[:], ALU.pow).then_inc(pooled, 1)
                pool.wait_ge(pooled, 2)
                nc.gpsimd.tensor_scalar(norm[:], norm[:], 1e-8, None, ALU.add).then_inc(pooled, 1)


def sinkhorn_stage(nc, sem, make_sb, make_ps, QT, V, VC, ones):
    L = 255
    S = SLOTS
    HALVES = ((0, 512 - L), (512 - L, N))
    SCALE = float(HD) ** -0.5
    ROUNDS = BPS * GROUPS
    LEAD = 3
    JUNK = 3
    DVE_CONST = 10
    with ExitStack() as ctx:
        sb, ps = make_sb(ctx), make_ps(ctx)
        K = [sb(f"sk_K{s}", [P, CH, NP]) for s in range(S)]
        diag = [sb(f"sk_diag{s}", [P, CH, P]) for s in range(S)]
        row = sb("sk_row", [P, S, NP])
        logs = sb("sk_logs", [P, S, NP])
        junk = sb("sk_junk", [P, JUNK, NP])
        sums = sb("sk_sums", [P, S, CH])
        col = sb("sk_col", [P, S, CH])
        peak = sb("sk_peak", [P, S, CH])
        weight = sb("sk_weight", [P, S, CH])
        top = sb("sk_top", [P, 4])
        spread = sb("sk_spread", [P, 2, R])
        head_mask = sb("sk_head_mask", [P, HG])
        cls_head_mask = sb("sk_cls_head_mask", [P, HG])
        feat_mask = sb("sk_feat_mask", [64, HG])
        cls_mask = sb("sk_cls_mask", [P, 1])
        not_cls = sb("sk_not_cls", [P, 1])
        off_diag = sb("sk_off_diag", [P, R])
        on_diag = sb("sk_on_diag", [P, R])
        diag_gain = sb("sk_diag_gain", [P, R])
        cls_gain = sb("sk_cls_gain", [P, 1])
        shift = sb("sk_shift", [P, 2])
        QB = sb("sk_QB", [P, S, NP])
        QS = sb("sk_QS", [P, CH, P])
        VS = sb("sk_VS", [P, CH, P])
        den = sb("sk_den", [64, 2, NP])
        w_ps = ps("sk_w", [P, 2 * S, 512])
        e_ps = ps("sk_e", [P, 4, 512])

        def pair(x, k):
            return x[:, 2 * k:2 * k + 2, :].rearrange("p a n -> p (a n)")[:, L:L + N]

        def sems(name):
            return [sem(f"sk_{name}{s}") for s in range(S)]

        const_pool, const_dve = sem("sk_const_pool"), sem("sk_const_dve")
        slot_ready, dots_ready, k_ready, k_masked = sems("slot_ready"), sems("dots_ready"), sems("k_ready"), sems("k_masked")
        qs_ready = sem("sk_qs_ready")
        diag_ready, w_ready, logs_ready, row_ready = sems("diag_ready"), sems("w_ready"), sems("logs_ready"), sems("row_ready")
        sums_ready, col_ready = sems("sums_ready"), sems("col_ready")
        top_step, weight_ready = sems("top_step"), sems("weight_ready")
        e_ready = sems("e_ready")
        vs_ready = sems("vs_ready")
        o_ready, den_log, den_ready, o_kept = sems("o_ready"), sems("den_log"), sems("den_ready"), sems("o_kept")

        def near_diagonal(s):
            flat = K[s][:].rearrange("p c n -> p (c n)")[:, 0:(CH - 1) * (NP + R)]
            return flat.rearrange("p (c n) -> p c n", n=NP + R)[:, :, 0:R]

        with nc.Block() as block:
            @block.gpsimd
            def _(pool):
                n = 0
                pool.wait_ge(const_dve, 1)
                nc.gpsimd.affine_select(out=feat_mask[:], in_=feat_mask[:], compare_op=ALU.is_ge, fill=0.0,
                                        base=0, pattern=[[-HD, HG]], channel_multiplier=1).then_inc(const_pool, 1)
                pool.wait_ge(const_pool, 1)
                nc.gpsimd.affine_select(out=feat_mask[:], in_=feat_mask[:], compare_op=ALU.is_ge, fill=0.0,
                                        base=HD - 1, pattern=[[HD, HG]], channel_multiplier=-1).then_inc(const_pool, 1)
                for k in range(HG):
                    pool.wait_ge(const_pool, k + 2)
                    nc.gpsimd.affine_select(out=on_diag[k * R:(k + 1) * R, :], in_=on_diag[k * R:(k + 1) * R, :],
                                            compare_op=ALU.not_equal, fill=1.0, base=0, pattern=[[-1, R]],
                                            channel_multiplier=1).then_inc(const_pool, 1)
                CONST = 2 + HG
                pool.wait_ge(const_pool, CONST)
                pool.wait_ge(const_dve, DVE_CONST)

                def queries(s, i):
                    if later(i):
                        pool.wait_ge(dots_ready[s], CH * i)
                        pool.wait_ge(const_pool, CONST)
                    nc.gpsimd.tensor_copy(QB[0:64, s, 0:N], QT[:, i + ROUNDS * s, 0:N]).then_inc(slot_ready[s], 1)
                    if later(i) or s:
                        pool.wait_ge(dots_ready[1 - s], CH * (i + s))
                    pool.wait_ge(slot_ready[s], i + 1)
                    q = QB[0:64, s, 0:T].rearrange("p (c r) -> p c r", r=R)
                    for k in range(HG):
                        nc.gpsimd.tensor_tensor(
                            QS[0:64, 0:CH - 1, k * R:(k + 1) * R], q,
                            feat_mask[:, k:k + 1].unsqueeze(1).broadcast_to((64, CH - 1, R)),
                            ALU.mult).then_inc(qs_ready, 1)
                    nc.gpsimd.tensor_tensor(
                        QS[0:64, CH - 1, :].rearrange("p (k r) -> p k r", r=R),
                        QB[0:64, s, T:N].unsqueeze(1).broadcast_to((64, HG, R)),
                        feat_mask[:].unsqueeze(2).broadcast_to((64, HG, R)), ALU.mult).then_inc(qs_ready, 1)

                def values(s, i):
                    if later(i) or s:
                        pool.wait_ge(o_ready[1 - s], i + s)
                        pool.wait_ge(const_pool, CONST)
                    for k in range(HG):
                        p, d = slice(k * R, (k + 1) * R), slice(k * HD, (k + 1) * HD)
                        for q in range(HG):
                            if later(i) or k or q:
                                pool.wait_ge(vs_ready[s], HG * (HG + 1) * i + k * (HG + 1) + q)
                                pool.wait_ge(const_pool, CONST)
                            nc.gpsimd.tensor_copy(VS[p, q:CH - 1:HG, d],
                                                  V[q * R:(q + 1) * R, s, :, bass.ds(i * 64 + k * HD, HD)]).then_inc(vs_ready[s], 1)
                        pool.wait_ge(vs_ready[s], HG * (HG + 1) * i + k * (HG + 1) + HG)
                        pool.wait_ge(const_pool, CONST)
                        nc.gpsimd.tensor_copy(VS[k * R:k * R + 1, CH - 1, d],
                                              VC[:, s, bass.ds(i * 64 + k * HD, HD)]).then_inc(vs_ready[s], 1)

                def round_of(i):
                    queries(0, i)
                    if later(i):
                        values(1, i - 1)
                    queries(1, i)
                    values(0, i)

                round_of(0)
                with pool.Fori(1, ROUNDS) as i:
                    round_of(i)
                values(1, ROUNDS - 1)

            @block.tensor
            def _(pe):
                pe.wait_ge(const_dve, DVE_CONST)

                def cosines(s, i):
                    pe.wait_ge(qs_ready, (HG + 1) * (i * S + s + 1))
                    for c in range(CH):
                        if c >= 2:
                            pe.wait_ge(k_ready[s], CH * i + c - 1)
                        elif s:
                            pe.wait_ge(k_ready[0], CH * i + CH)
                        elif later(i):
                            pe.wait_ge(k_ready[1], CH * i)
                        for a, z in HALVES:
                            last = nc.tensor.matmul(pair(e_ps, c % 2)[:, a:z], QS[:, c, :], QB[:, s, a:z],
                                                    start=True, stop=True)
                        last.then_inc(dots_ready[s], 1)

                def k_v(s, i, it):
                    if later(i):
                        pe.wait_ge(o_kept[s], i)
                    pe.wait_ge(k_masked[s], 3 * i + 3)
                    pe.wait_ge(diag_ready[s], HG * (ITERS * i + it + 1))
                    for c in range(CH):
                        for a, z in HALVES:
                            last = nc.tensor.matmul(pair(w_ps, s)[:, a:z], diag[s][:, c, :], K[s][:, c, a:z],
                                                    start=(c == 0), stop=(c == CH - 1))
                    last.then_inc(w_ready[s], 1)

                def diagonal(s):
                    for c in range(CH):
                        gain, first, end = (diag_gain, c * R, c * R + R) if c < CH - 1 else (cls_gain, T, N)
                        for a, z in HALVES:
                            a, z = max(a, first), min(z, end)
                            if a < z:
                                nc.tensor.matmul(pair(w_ps, s)[:, a:z], VS[:, c, :], gain[:, a - first:z - first],
                                                 start=False, stop=False)

                def attention(s, i):
                    pe.wait_ge(vs_ready[s], HG * (HG + 1) * (i + 1))
                    pe.wait_ge(logs_ready[s], ITERS * (i + 1))
                    for c in range(CH):
                        if c == CH - 1:
                            diagonal(s)
                        pe.wait_ge(e_ready[s], CH * i + c + 1)
                        for a, z in HALVES:
                            last = nc.tensor.matmul(pair(w_ps, s)[:, a:z], VS[:, c, :], K[s][:, c, a:z], start=(c == 0),
                                                    stop=(c == CH - 1))
                    last.then_inc(o_ready[s], 1)

                def round_of(i):
                    cosines(0, i)
                    if later(i):
                        k_v(1, i - 1, ITERS - 2)
                    k_v(0, i, 0)
                    if later(i):
                        k_v(1, i - 1, ITERS - 1)
                    k_v(0, i, 1)
                    if later(i):
                        attention(1, i - 1)
                    k_v(0, i, 2)
                    cosines(1, i)
                    with pe.Fori(0, ITERS - LEAD) as it:
                        k_v(0, i, it + LEAD)
                        k_v(1, i, it)
                    attention(0, i)
                    k_v(1, i, ITERS - LEAD)

                round_of(0)
                with pe.Fori(1, ROUNDS) as i:
                    round_of(i)
                k_v(1, ROUNDS - 1, ITERS - 2)
                k_v(1, ROUNDS - 1, ITERS - 1)
                attention(1, ROUNDS - 1)

            @block.scalar
            def _(act):
                act.wait_ge(const_dve, DVE_CONST)
                act.wait_ge(const_pool, 2 + HG)
                nc.scalar.preload_act_table_set("natural_log_exp_and_others")

                def u_row(s, i, it):
                    act.wait_ge(w_ready[s], i * ITERS + it + 1)
                    nc.scalar.activation(logs[:, s, 0:N], pair(w_ps, s), ACT.Ln, scale=float(N)).then_inc(logs_ready[s], 1)
                    act.wait_ge(logs_ready[s], i * ITERS + it + 1)
                    nc.scalar.activation(row[:, s, 0:N], logs[:, s, 0:N], ACT.Exp, scale=-1.0).then_inc(row_ready[s], 1)

                def v_blocks(s, source):
                    for k in range(HG):
                        p = slice(k * R, (k + 1) * R)
                        nc.scalar.activation(diag[s][p, :, p], source[p, :].unsqueeze(2).broadcast_to((R, CH, R)),
                                             ACT.Copy).then_inc(diag_ready[s], 1)

                def ones_as_v(s, i):
                    if later(i):
                        act.wait_ge(w_ready[s], ITERS * i)
                    v_blocks(s, ones[:, 0:CH])

                def kernel_matrix(s, i, first, end):
                    if later(i):
                        act.wait_ge(o_ready[s], i)
                    for c in range(first, end):
                        act.wait_ge(dots_ready[s], CH * i + c + 1)
                        nc.scalar.activation(K[s][:, c, 0:N], pair(e_ps, c % 2), ACT.Exp, bias=shift[:, 0:1],
                                             scale=INV_REG).then_inc(k_ready[s], 1)

                def new_v(s, i, it):
                    act.wait_ge(col_ready[s], ITERS * i + it + 1)
                    v_blocks(s, col[:, s, :])

                def attention_weights(s, i):
                    act.wait_ge(weight_ready[s], i + 1)
                    for c in range(CH):
                        nc.scalar.activation(K[s][:, c, 0:N], K[s][:, c, 0:N], ACT.Exp, bias=shift[:, 1:2],
                                             scale=weight[:, s, c:c + 1]).then_inc(e_ready[s], 1)

                def denominators(s, i):
                    act.wait_ge(o_ready[s], i + 1)
                    if s:
                        act.wait_ge(o_kept[0], i + 1)
                    elif later(i):
                        act.wait_ge(o_kept[1], i)
                    nc.scalar.activation(den[:, 0, 0:N], pair(w_ps, s)[64:P, :], ACT.Ln).then_inc(den_log[s], 1)
                    act.wait_ge(den_log[s], i + 1)
                    nc.scalar.activation(den[:, 1, 0:N], den[:, 0, 0:N], ACT.Exp, scale=-1.0).then_inc(den_ready[s], 1)

                def round_of(i):
                    if later(i):
                        denominators(0, i - 1)
                        u_row(1, i - 1, ITERS - LEAD)
                    kernel_matrix(0, i, 0, CH - 4)
                    if later(i):
                        new_v(1, i - 1, ITERS - LEAD)
                    kernel_matrix(0, i, CH - 4, CH)
                    ones_as_v(0, i)
                    if later(i):
                        u_row(1, i - 1, ITERS - 2)
                        new_v(1, i - 1, ITERS - 2)
                    u_row(0, i, 0)
                    new_v(0, i, 0)
                    if later(i):
                        u_row(1, i - 1, ITERS - 1)
                    u_row(0, i, 1)
                    if later(i):
                        attention_weights(1, i - 1)
                    new_v(0, i, 1)
                    if later(i):
                        denominators(1, i - 1)
                    u_row(0, i, 2)
                    kernel_matrix(1, i, 0, CH - 4)
                    new_v(0, i, 2)
                    kernel_matrix(1, i, CH - 4, CH)
                    ones_as_v(1, i)
                    with act.Fori(0, ITERS - LEAD - 1) as it:
                        u_row(0, i, it + LEAD)
                        new_v(0, i, it + LEAD)
                        u_row(1, i, it)
                        new_v(1, i, it)
                    u_row(0, i, ITERS - 1)
                    u_row(1, i, ITERS - LEAD - 1)
                    attention_weights(0, i)
                    new_v(1, i, ITERS - LEAD - 1)

                round_of(0)
                with act.Fori(1, ROUNDS) as i:
                    round_of(i)
                denominators(0, ROUNDS - 1)
                u_row(1, ROUNDS - 1, ITERS - LEAD)
                new_v(1, ROUNDS - 1, ITERS - LEAD)
                u_row(1, ROUNDS - 1, ITERS - 2)
                new_v(1, ROUNDS - 1, ITERS - 2)
                u_row(1, ROUNDS - 1, ITERS - 1)
                attention_weights(1, ROUNDS - 1)
                denominators(1, ROUNDS - 1)

            @block.vector
            def _(dve):
                nc.vector.memset(feat_mask[:], 1.0)
                nc.vector.memset(on_diag[:], 0.0).then_inc(const_dve, 1)
                nc.vector.memset(QB[64:P, :, :], 0.0)
                nc.vector.memset(QS[64:P, :, :], 0.0)
                nc.vector.memset(shift[:, 0:1], -INV_REG)
                nc.vector.memset(shift[:, 1:2], -SCALE)
                for s in range(S):
                    nc.vector.memset(diag[s][:], 0.0)
                nc.vector.memset(head_mask[:], 0.0)
                nc.vector.memset(VS[:, :, 0:64], 0.0)
                nc.vector.memset(cls_mask[:], 0.0).then_inc(const_dve, 1)
                dve.wait_ge(const_dve, 2)
                for k in range(HG):
                    nc.vector.memset(head_mask[k * R:(k + 1) * R, k:k + 1], 1.0)
                    last = nc.vector.memset(cls_mask[k * R:k * R + 1, :], 1.0)
                last.then_inc(const_dve, 1)
                dve.wait_ge(const_dve, 3)
                dve.wait_ge(const_pool, 2 + HG)
                nc.vector.tensor_scalar(not_cls[:], cls_mask[:], -1.0, 1.0, ALU.mult, ALU.add).then_inc(const_dve, 1)
                nc.vector.tensor_scalar(off_diag[:], on_diag[:], -1.0, 1.0, ALU.mult, ALU.add).then_inc(const_dve, 1)
                nc.vector.tensor_scalar(cls_head_mask[:], head_mask[:], cls_mask[:], None, ALU.mult).then_inc(const_dve, 1)
                nc.vector.tensor_scalar(diag_gain[:], on_diag[:], 1.0 - float(np.exp(-SCALE)), None,
                                        ALU.mult).then_inc(const_dve, 1)
                nc.vector.tensor_scalar(cls_gain[:], cls_mask[:], 1.0 - float(np.exp(-SCALE)), None,
                                        ALU.mult).then_inc(const_dve, 1)
                dve.wait_ge(const_dve, 8)
                for c0, c1, mask in ((0, CH - 1, head_mask), (CH - 1, CH, cls_head_mask)):
                    for k in range(HG):
                        last = nc.vector.tensor_copy(VS[:, c0:c1, 64 + k * HD:64 + (k + 1) * HD],
                                                     mask[:, k:k + 1].unsqueeze(1).broadcast_to((P, c1 - c0, HD)))
                    last.then_inc(const_dve, 1)

                def k_u(s, i, it):
                    dve.wait_ge(k_masked[s], 3 * i + 3)
                    dve.wait_ge(row_ready[s], i * ITERS + it + 1)
                    for c in range(CH):
                        if c >= JUNK:
                            dve.wait_ge(sums_ready[s], (i * ITERS + it) * CH + c - JUNK + 1)
                        nc.vector.tensor_tensor_reduce(
                            out=junk[:, c % JUNK, 0:N], in0=K[s][:, c, 0:N], in1=row[:, s, 0:N], scale=float(N),
                            scalar=not_cls[:] if c == CH - 1 else 0.0, op0=ALU.mult, op1=ALU.add,
                            accum_out=sums[:, s, c:c + 1]).then_inc(sums_ready[s], 1)
                    dve.wait_ge(sums_ready[s], (i * ITERS + it + 1) * CH)
                    nc.vector.reciprocal(col[:, s, :], sums[:, s, :]).then_inc(col_ready[s], 1)

                def mask(s, i):
                    dve.wait_ge(k_ready[s], CH * (i + 1))
                    nc.vector.tensor_tensor(near_diagonal(s), near_diagonal(s),
                                            off_diag[:].unsqueeze(1).broadcast_to((P, CH - 1, R)),
                                            ALU.mult).then_inc(k_masked[s], 1)
                    nc.vector.tensor_scalar(K[s][:, CH - 1, 0:T], K[s][:, CH - 1, 0:T], cls_mask[:], None,
                                            ALU.mult).then_inc(k_masked[s], 1)
                    nc.vector.memset(K[s][:, CH - 1, T:N], 0.0).then_inc(k_masked[s], 1)

                def maximum(s, i):
                    for c in range(CH):
                        last = nc.vector.tensor_tensor_reduce(
                            out=K[s][:, c, 0:N], in0=K[s][:, c, 0:N], in1=row[:, s, 0:N], scale=1.0, scalar=0.0,
                            op0=ALU.mult, op1=ALU.max, accum_out=peak[:, s, c:c + 1])
                    last.then_inc(top_step[s], 1)
                    steps = 7 * i
                    dve.wait_ge(top_step[s], steps + 1)
                    dve.wait_ge(col_ready[s], ITERS * (i + 1))
                    nc.vector.tensor_tensor(peak[:, s, :], peak[:, s, :], col[:, s, :], ALU.mult).then_inc(top_step[s], 1)
                    dve.wait_ge(top_step[s], steps + 2)
                    nc.vector.reduce_max(top[:, 0:1], peak[:, s, :], AX_X).then_inc(top_step[s], 1)
                    dve.wait_ge(top_step[s], steps + 3)
                    nc.vector.tensor_copy(spread[:, 0, :], top[:, 0:1].broadcast_to((P, R))).then_inc(top_step[s], 1)
                    dve.wait_ge(top_step[s], steps + 4)
                    nc.vector.transpose(spread[:, 1, :], spread[:, 0, :]).then_inc(top_step[s], 1)
                    dve.wait_ge(top_step[s], steps + 5)
                    nc.vector.reduce_max(top[:, 1:2], spread[:, 1, :], AX_X).then_inc(top_step[s], 1)
                    dve.wait_ge(top_step[s], steps + 6)
                    nc.vector.reciprocal(top[:, 2:3], top[:, 1:2]).then_inc(top_step[s], 1)
                    dve.wait_ge(top_step[s], steps + 7)
                    nc.vector.tensor_scalar(weight[:, s, :], col[:, s, :], top[:, 2:3], SCALE, ALU.mult,
                                            ALU.mult).then_inc(weight_ready[s], 1)

                def output(s, i):
                    dve.wait_ge(den_ready[s], i + 1)
                    nc.vector.tensor_tensor(QT[:, i + ROUNDS * s, 0:N], pair(w_ps, s)[0:64, :], den[:, 1, 0:N],
                                            ALU.mult).then_inc(o_kept[s], 1)

                def round_of(i):
                    if later(i):
                        k_u(1, i - 1, ITERS - LEAD)
                        output(0, i - 1)
                    mask(0, i)
                    if later(i):
                        k_u(1, i - 1, ITERS - 2)
                    k_u(0, i, 0)
                    if later(i):
                        k_u(1, i - 1, ITERS - 1)
                        maximum(1, i - 1)
                    k_u(0, i, 1)
                    k_u(0, i, 2)
                    if later(i):
                        output(1, i - 1)
                    mask(1, i)
                    with dve.Fori(0, ITERS - LEAD - 1) as it:
                        k_u(0, i, it + LEAD)
                        k_u(1, i, it)
                    k_u(0, i, ITERS - 1)
                    maximum(0, i)
                    k_u(1, i, ITERS - LEAD - 1)

                round_of(0)
                with dve.Fori(1, ROUNDS) as i:
                    round_of(i)
                k_u(1, ROUNDS - 1, ITERS - LEAD)
                output(0, ROUNDS - 1)
                k_u(1, ROUNDS - 1, ITERS - 2)
                k_u(1, ROUNDS - 1, ITERS - 1)
                maximum(1, ROUNDS - 1)
                output(1, ROUNDS - 1)


def sinkhorn_out_stage(nc, sem, make_ps, AOT, WprojT, bproj, ones, H):
    with ExitStack() as ctx:
        o_ps = make_ps(ctx)("sko_o", [P, 4, 512])
        ready, kept = sem("sko_ready"), sem("sko_kept")
        with nc.Block() as block:
            @block.tensor
            def _(pe):
                for t in range(NT):
                    n = P if t < CLS else B
                    if t >= 4:
                        pe.wait_ge(kept, t - 3)
                    for g in range(GROUPS):
                        lhs = (AOT[:, t // TPB * GROUPS + g, (t % TPB) * P:(t % TPB + 1) * P] if t < CLS else
                               AOT[:, g:B * GROUPS:GROUPS, T])
                        nc.tensor.matmul(o_ps[0:n, t % 4, 0:D], lhs, WprojT[:, g, :], start=(g == 0), stop=False)
                    nc.tensor.matmul(o_ps[0:n, t % 4, 0:D], ones[0:1, 0:n], bproj[:], start=False,
                                     stop=True).then_inc(ready, 1)

            @block.vector
            def _(dve):
                for t in range(NT):
                    n = P if t < CLS else B
                    dve.wait_ge(ready, t + 1)
                    nc.vector.tensor_tensor(H[0:n, t, :], H[0:n, t, :], o_ps[0:n, t % 4, 0:D], ALU.add).then_inc(kept, 1)


def load(nc, sem, name, pairs):
    loaded = sem(name + "_loaded")
    with nc.Block() as block:
        @block.sync
        def _(sp):
            for dst, src in pairs:
                sp.dma_start(dst, src).then_inc(loaded, 16)
            sp.wait_ge(loaded, 16 * len(pairs))


def halves_of(w):
    return w.rearrange("(h p) n -> p h n", p=HALF)


def row_of(v):
    return v.rearrange("(a n) -> a n", a=1)


def tokens_of(t):
    return (P if t < CLS else B), t * P


TOPK = max(1, int(round(0.15 * N)))
HPH = HALF // HD
QROWS = HPH * TOPK
QB_ROWS = 116
QBLOCKS = [(r, min(QROWS, r + QB_ROWS)) for r in range(0, QROWS, QB_ROWS)]
F = 4 * D


def routed_stage(nc, sem, make_sb, make_ps, A, H, ident, ones):
    with ExitStack() as ctx:
        sb = make_sb(ctx)
        HH = sb("r_hh", [P, NT, D])
        bf2 = sb("r_bf2", [1, D])
        bf1 = sb("r_bf1", [P, F // P])
        W1 = sb("r_W1", [HALF, 2, F])
        W2 = sb("r_W2", [P, F // P, D])
        g2, b2 = sb("r_g2", [P, D]), sb("r_b2", [P, D])
        with ExitStack() as actx:
            asb = make_sb(actx)
            N1, N1T = asb("r_n1", [P, NT, D]), asb("r_n1T", [HALF, 2, NTOK])
            g1, b1 = asb("r_g1", [P, D]), asb("r_b1", [P, D])
            W = {k: asb("r_W" + k, [HALF, 2, D]) for k in "qkvom"}
            wr = asb("r_wr", [HALF, 2, 1])
            br = asb("r_br", [P, 1])
            bq, bk = asb("r_bq", [HALF, 2]), asb("r_bk", [HALF, 2])
            bv, bo, bm = asb("r_bv", [1, D]), asb("r_bo", [1, D]), asb("r_bm", [1, D])
            with nc.allow_non_contiguous_dma(reason="vectors of 192 and 768 numbers, one per partition"):
                load(nc, sem, "r", [
                    (g1[:], A["L0_ffn_g1"].partition_broadcast(P)), (b1[:], A["L0_ffn_b1"].partition_broadcast(P)),
                    (g2[:], A["L0_ffn_g2"].partition_broadcast(P)), (b2[:], A["L0_ffn_b2"].partition_broadcast(P)),
                    *[(W[k][:], halves_of(A["L0_ffn_W" + k])) for k in "qkvom"],
                    (W1[:], halves_of(A["L0_ffn_W1"])), (W2[:], A["L0_ffn_W2"].rearrange("(f p) n -> p f n", p=P)),
                    (wr[:], A["L0_ffn_Wr"].rearrange("(h p a) -> p h a", p=HALF, a=1)),
                    (br[:], A["L0_ffn_br"].partition_broadcast(P)),
                    (bq[:], A["L0_ffn_bq"].rearrange("(h p) -> p h", p=HALF)),
                    (bk[:], A["L0_ffn_bk"].rearrange("(h p) -> p h", p=HALF)),
                    (bv[:], row_of(A["L0_ffn_bv"])), (bo[:], row_of(A["L0_ffn_bo"])), (bm[:], row_of(A["L0_ffn_bm"])),
                    (bf2[:], row_of(A["L0_ffn_bf2"])), (bf1[:], A["L0_ffn_bf1"].rearrange("(f p) -> p f", p=P))])
            norm_stage(nc, sem, make_sb, make_ps, "rn1", H, N1, N1T, ident, inner=HH, gain=g1, shift=b1)
            KT = asb("r_KT", [HALF, 2, B, NP])
            V, VC = asb("r_V", [P, CLS, D]), asb("r_VC", [1, B, D])
            Z = asb("r_Z", [P, B, NP])
            routed_projections(nc, sem, make_ps, N1T, W, wr, br, bk, bv, ones, KT, V, VC, Z)
            sel = asb("r_sel", [P, B, TPB, TOPK])
            selc = asb("r_selc", [B, B, TOPK])
            score = asb("r_score", [P, B, TPB + 1])
            rest = asb("r_rest", [P, B, TPB + 1])
            score_cls, rest_cls = asb("r_score_cls", [B, 1]), asb("r_rest_cls", [B, 1])
            PM, PMC = asb("r_PM", [P, B, D]), asb("r_PMC", [B, D])
            routing(nc, sem, make_sb, make_ps, ident, ones, N1, W["m"], Z, sel, selc, score, rest, score_cls, rest_cls, PM, PMC)
            selT = asb("r_selT", [TOPK, B, T + B])
            AS = asb("r_AS", [TOPK, B, D])
            routed_attention(nc, sem, make_sb, make_ps, ident, ones, N1, W, bq, bo, KT, V, VC, sel, selc, selT, AS)
            merge(nc, sem, make_sb, make_ps, ones, N1T, W["m"], bm, selT, AS, score, rest, score_cls, rest_cls, PM, PMC, HH)
        with ExitStack() as mctx:
            msb = make_sb(mctx)
            N2, N2T = msb("r_n2", [P, NT, D]), msb("r_n2T", [HALF, 2, NTOK])
            norm_stage(nc, sem, make_sb, make_ps, "rn2", HH, N2, N2T, ident, gain=g2, shift=b2)
            gelu_mlp(nc, sem, make_sb, make_ps, ones, N2T, W1, bf1, W2, bf2, HH, H)


def routed_projections(nc, sem, make_ps, N1T, W, wr, br, bk, bv, ones, KT, V, VC, Z):
    with ExitStack() as ctx:
        ps = make_ps(ctx)
        k_ps, v_ps, z_ps = ps("rp_k", [P, 2, 512]), ps("rp_v", [P, 2, 512]), ps("rp_z", [P, 2, 1024])
        k_ready, k_kept, v_ready, v_kept = sem("rp_k_ready"), sem("rp_k_kept"), sem("rp_v_ready"), sem("rp_v_kept")
        z_ready, z_kept, z_done = sem("rp_z_ready"), sem("rp_z_kept"), sem("rp_z_done")
        KJOBS = [(o, b) for o in range(2) for b in range(B + 1)]
        with nc.Block() as block:
            @block.tensor
            def _(pe):
                for b in range(B):
                    if b >= 2:
                        pe.wait_ge(z_kept, b - 1)
                    for h in range(2):
                        nc.tensor.matmul(z_ps[:, b % 2, 0:T], wr[:, h, :].broadcast_to((HALF, P)),
                                         N1T[:, h, b * T:(b + 1) * T], start=(h == 0), stop=(h == 1))
                    for h in range(2):
                        last = nc.tensor.matmul(z_ps[:, b % 2, T:N], wr[:, h, :].broadcast_to((HALF, P)),
                                                N1T[:, h, B * T + b:B * T + b + 1], start=(h == 0), stop=(h == 1))
                    last.then_inc(z_ready, 1)
                for j, (o, b) in enumerate(KJOBS):
                    n = T if b < B else B
                    if j >= 2:
                        pe.wait_ge(k_kept, j - 1)
                    for h in range(2):
                        last = nc.tensor.matmul(k_ps[0:HALF, j % 2, 0:n], W["k"][:, h, o * HALF:(o + 1) * HALF],
                                                N1T[:, h, b * T:b * T + n], start=(h == 0), stop=(h == 1))
                    last.then_inc(k_ready, 1)
                for t in range(CLS + B):
                    n, first = (P, t * P) if t < CLS else (1, t - CLS + B * T)
                    if t >= 2:
                        pe.wait_ge(v_kept, t - 1)
                    for h in range(2):
                        nc.tensor.matmul(v_ps[0:n, t % 2, 0:D], N1T[:, h, first:first + n], W["v"][:, h, :],
                                         start=(h == 0), stop=False)
                    nc.tensor.matmul(v_ps[0:n, t % 2, 0:D], ones[0:1, 0:n], bv[:], start=False,
                                     stop=True).then_inc(v_ready, 1)

            @block.scalar
            def _(act):
                for j, (o, b) in enumerate(KJOBS):
                    act.wait_ge(k_ready, j + 1)
                    dst = KT[:, o, b, 0:T] if b < B else KT[:, o, :, T]
                    nc.scalar.activation(dst, k_ps[0:HALF, j % 2, 0:T if b < B else B], ACT.Identity,
                                         bias=bk[:, o:o + 1]).then_inc(k_kept, 1)

            @block.vector
            def _(dve):
                for b in range(B):
                    dve.wait_ge(z_ready, b + 1)
                    nc.vector.tensor_scalar(Z[:, b, 0:N], z_ps[:, b % 2, 0:N], br[:], 17.0, ALU.add,
                                            ALU.min).then_inc(z_kept, 1)
                    dve.wait_ge(z_kept, b + 1)
                    nc.vector.tensor_scalar(Z[:, b, 0:N], Z[:, b, 0:N], -88.0, None, ALU.max).then_inc(z_done, 1)
                for t in range(CLS + B):
                    dve.wait_ge(v_ready, t + 1)
                    dst = V[:, t, :] if t < CLS else VC[:, t - CLS, :]
                    nc.vector.tensor_copy(dst, v_ps[0:P if t < CLS else 1, t % 2, 0:D]).then_inc(v_kept, 1)


def routing(nc, sem, make_sb, make_ps, ident, ones, N1, Wm, Z, sel, selc, score, rest, score_cls, rest_cls, PM, PMC):
    C5 = TPB + 1
    with ExitStack() as ctx:
        sb, ps = make_sb(ctx), make_ps(ctx)
        before = sb("ro_before", [P, TPB, NP])
        slot = sb("ro_slot", [P, TOPK])
        picked = sb("ro_picked", [P, 2, P])
        zcol = sb("ro_zcol", [P, B, C5])
        less, same = sb("ro_less", [P, 2, NP]), sb("ro_same", [P, 2, NP])
        both = sb("ro_both", [P, 2, NP])
        rank = sb("ro_rank", [P, B, C5])
        counted = sb("ro_counted", [P, B, C5])
        expz = sb("ro_expz", [P, B, C5])
        cls_scores = sb("ro_cls_scores", [B, B])
        total = sb("ro_total", [P, B])
        pooled = sb("ro_pooled", [HALF, 2, B])
        small = sb("ro_small", [B, 2, B])
        t_ps, p_ps, m_ps = ps("ro_t", [P, 512]), ps("ro_p", [P, 512]), ps("ro_m", [P, 3, 512])
        const_ready, step = sem("ro_const_ready"), sem("ro_step")
        col_ready, pair_ready, rank_ready = sem("ro_col_ready"), sem("ro_pair_ready"), sem("ro_rank_ready")
        exp_ready, score_ready, total_ready, pooled_ready = (sem("ro_exp_ready"), sem("ro_score_ready"),
                                                             sem("ro_total_ready"), sem("ro_pooled_ready"))
        pooled_kept, mean_ready, mean_kept = sem("ro_pooled_kept"), sem("ro_mean_ready"), sem("ro_mean_kept")
        with nc.Block() as block:
            @block.gpsimd
            def _(pool):
                nc.gpsimd.memset(before[:], 1.0).then_inc(const_ready, 1)
                nc.gpsimd.iota(slot[:], pattern=[[1, TOPK]], base=0, channel_multiplier=0,
                               allow_small_or_imprecise_dtypes=True).then_inc(const_ready, 1)
                for t in range(TPB):
                    pool.wait_ge(const_ready, 2 + t)
                    nc.gpsimd.affine_select(out=before[:, t, 0:T], in_=before[:, t, 0:T], compare_op=ALU.is_gt,
                                            fill=0.0, base=t * P, pattern=[[-1, T]],
                                            channel_multiplier=1).then_inc(const_ready, 1)

            @block.vector
            def _(dve):
                steps = Tally(step)
                for b in range(B):
                    for t in range(TPB):
                        if b * TPB + t >= 2:
                            dve.wait_ge(col_ready, b * TPB + t - 1)
                        nc.vector.tensor_tensor_reduce(out=picked[:, t % 2, :], in0=Z[:, b, t * P:(t + 1) * P],
                                                       in1=ident[:], scale=1.0, scalar=0.0, op0=ALU.mult, op1=ALU.add,
                                                       accum_out=zcol[:, b, t:t + 1]).then_inc(col_ready, 1)
                nc.vector.tensor_copy(zcol[:, :, TPB], Z[:, :, T]).then_inc(col_ready, 1)
                dve.wait_ge(col_ready, CLS + 1)
                dve.wait_ge(const_ready, 2 + TPB)
                for b in range(B):
                    for t in range(C5):
                        n = b * C5 + t
                        if n >= 2:
                            dve.wait_ge(rank_ready, n - 1)
                        zc = zcol[:, b, t:t + 1]
                        nc.vector.tensor_scalar(less[:, n % 2, 0:N], Z[:, b, 0:N], zc, None,
                                                ALU.is_lt).then_inc(pair_ready, 1)
                        if t < TPB:
                            nc.vector.scalar_tensor_tensor(out=same[:, n % 2, 0:N], in0=Z[:, b, 0:N], scalar=zc,
                                                           in1=before[:, t, 0:N], op0=ALU.is_equal,
                                                           op1=ALU.mult).then_inc(pair_ready, 1)
                        else:
                            nc.vector.memset(same[:, n % 2, 0:N], 0.0).then_inc(pair_ready, 1)
                        dve.wait_ge(pair_ready, 2 * n + 2)
                        nc.vector.tensor_tensor_reduce(out=both[:, n % 2, 0:N], in0=less[:, n % 2, 0:N],
                                                       in1=same[:, n % 2, 0:N], scale=1.0, scalar=0.0, op0=ALU.add,
                                                       op1=ALU.add, accum_out=rank[:, b, t:t + 1]).then_inc(rank_ready, 1)
                dve.wait_ge(rank_ready, B * C5)
                for b in range(B):
                    for t in range(TPB):
                        nc.vector.tensor_scalar(sel[:, b, t, :], slot[:], rank[:, b, t:t + 1], None, ALU.is_equal)
                    nc.vector.tensor_scalar(selc[:, b, :], slot[0:B, :], rank[0:B, b, TPB:C5], ident[0:B, b:b + 1],
                                            ALU.is_equal, ALU.mult)
                steps.mark(nc.vector.tensor_scalar(rest[:], rank[:], TOPK - 0.5, None, ALU.is_gt))
                dve.wait_ge(exp_ready, 1)
                dve.wait_ge(step, steps.mark(nc.vector.tensor_scalar(expz[:], expz[:], 1.0, None, ALU.add)))
                dve.wait_ge(step, steps.mark(nc.vector.reciprocal(score[:], expz[:])))
                nc.vector.tensor_copy(counted[:, :, 0:TPB], score[:, :, 0:TPB])
                nc.vector.tensor_scalar(counted[:, :, TPB], score[:, :, TPB], ident[:, 0:1], None, ALU.mult)
                nc.vector.tensor_tensor(cls_scores[:], score[0:B, :, TPB], ident[0:B, 0:B], ALU.mult).then_inc(score_ready, 1)
                dve.wait_ge(step, steps.mark(nc.vector.tensor_tensor(small[:, 0, :], rest[0:B, :, TPB], ident[0:B, 0:B],
                                                                     ALU.mult)))
                nc.vector.reduce_sum(rest_cls[:], small[:, 0, :], AX_X)
                dve.wait_ge(score_ready, 1)
                nc.vector.reduce_sum(score_cls[:], cls_scores[:], AX_X)
                dve.wait_ge(total_ready, 1)
                dve.wait_ge(step, steps.mark(nc.vector.reduce_sum(
                    total[:], t_ps[:, 0:B * C5].rearrange("p (b c) -> p b c", b=B), AX_X)))
                dve.wait_ge(step, steps.mark(nc.vector.tensor_scalar(total[:], total[:], 1e-6, None, ALU.add)))
                dve.wait_ge(step, steps.mark(nc.vector.reciprocal(total[:], total[:])))
                dve.wait_ge(pooled_ready, 1)
                nc.vector.tensor_tensor(pooled[:], p_ps[0:HALF, 0:2 * B].rearrange("p (h b) -> p h b", h=2),
                                        total[0:HALF, :].unsqueeze(1).broadcast_to((HALF, 2, B)),
                                        ALU.mult).then_inc(pooled_kept, 1)
                dve.wait_ge(mean_ready, B + 1)
                for b in range(B):
                    nc.vector.tensor_copy(PM[:, b, :], m_ps[:, b // 2, (b % 2) * D:(b % 2 + 1) * D])
                nc.vector.tensor_copy(PMC[:], m_ps[0:B, 2, 0:D])

            @block.scalar
            def _(act):
                act.wait_ge(col_ready, CLS + 1)
                nc.scalar.activation(expz[:], zcol[:], ACT.Exp, scale=-1.0).then_inc(exp_ready, 1)

            @block.tensor
            def _(pe):
                pe.wait_ge(score_ready, 1)
                nc.tensor.matmul(t_ps[:, 0:B * C5], ones[:], counted[:].rearrange("p b c -> p (b c)"), start=True,
                                 stop=True).then_inc(total_ready, 1)
                for h in range(2):
                    for b in range(B):
                        for t in range(TPB):
                            nc.tensor.matmul(p_ps[0:HALF, h * B + b:h * B + b + 1],
                                             N1[:, b * TPB + t, h * HALF:(h + 1) * HALF], score[:, b, t:t + 1],
                                             start=(t == 0), stop=False)
                        last = nc.tensor.matmul(p_ps[0:HALF, h * B + b:h * B + b + 1],
                                                N1[0:B, CLS, h * HALF:(h + 1) * HALF], cls_scores[:, b:b + 1],
                                                start=False, stop=True)
                last.then_inc(pooled_ready, 1)
                pe.wait_ge(pooled_kept, 1)
                for b in range(B + 1):
                    n = P if b < B else B
                    for h in range(2):
                        lhs = pooled[:, h, b:b + 1].broadcast_to((HALF, P)) if b < B else pooled[:, h, :]
                        last = nc.tensor.matmul(m_ps[0:n, b // 2, (b % 2) * D:(b % 2 + 1) * D], lhs, Wm[:, h, :],
                                                start=(h == 0), stop=(h == 1))
                    last.then_inc(mean_ready, 1)


def routed_attention(nc, sem, make_sb, make_ps, ident, ones, N1, W, bq, bo, KT, V, VC, sel, selc, selT, AS):
    L = 255
    HALVES = ((0, 512 - L), (512 - L, N))
    NB = len(QBLOCKS)
    MT = TPB + 1
    with ExitStack() as ctx:
        sb, ps = make_sb(ctx), make_ps(ctx)
        picked = sb("ra_picked", [HALF, 2, TOPK])
        q = sb("ra_q", [HALF, 2, TOPK])
        heads = sb("ra_heads", [HALF, HPH])
        qd = sb("ra_qd", [HALF, 2, HPH, TOPK])
        prob = sb("ra_prob", [P, 2 * NB, NP])
        top, den, rden = sb("ra_top", [P, 2 * NB]), sb("ra_den", [P, 2 * NB]), sb("ra_rden", [P, 2 * NB])
        probT = sb("ra_probT", [P, 2, MT, QROWS])
        own = sb("ra_own", [HALF, 2, QROWS])
        ctxT = sb("ra_ctxT", [HALF, 2, TOPK])
        s_ps = ps("ra_s", [P, 2, 1024])
        t_ps = ps("ra_t", [P, 2, 512])
        x_ps = ps("ra_x", [P, 2, 512])
        names = ("picked_ready picked_kept q_ready q_kept qd_ready logit_ready top_ready prob_ready rden_ready "
                 "prob_normed turn_ready turn_kept ctx_ready own_ready ctx_kept as_ready as_kept st_ready st_kept const").split()
        M = {n: sem("ra_" + n) for n in names}
        with nc.Block() as block:
            @block.gpsimd
            def _(pool):
                nc.gpsimd.memset(heads[:], 1.0).then_inc(M["const"], 1)
                pool.wait_ge(M["const"], 1)
                nc.gpsimd.affine_select(out=heads[:], in_=heads[:], compare_op=ALU.is_ge, fill=0.0, base=0,
                                        pattern=[[-HD, HPH]], channel_multiplier=1).then_inc(M["const"], 1)
                pool.wait_ge(M["const"], 2)
                nc.gpsimd.affine_select(out=heads[:], in_=heads[:], compare_op=ALU.is_ge, fill=0.0, base=HD - 1,
                                        pattern=[[HD, HPH]], channel_multiplier=-1).then_inc(M["const"], 1)

            @block.tensor
            def _(pe):
                for b in range(B):
                    pe.wait_ge(M["as_kept"], b)
                    pe.wait_ge(M["ctx_kept"], 2 * b)
                    for h in range(2):
                        for t in range(TPB):
                            nc.tensor.matmul(x_ps[0:HALF, 0, h * TOPK:(h + 1) * TOPK],
                                             N1[:, b * TPB + t, h * HALF:(h + 1) * HALF], sel[:, b, t, :],
                                             start=(t == 0), stop=False)
                        last = nc.tensor.matmul(x_ps[0:HALF, 0, h * TOPK:(h + 1) * TOPK],
                                                N1[0:B, CLS, h * HALF:(h + 1) * HALF], selc[:, b, :],
                                                start=False, stop=True)
                    last.then_inc(M["picked_ready"], 1)
                    pe.wait_ge(M["picked_kept"], b + 1)
                    for o in range(2):
                        for h in range(2):
                            last = nc.tensor.matmul(x_ps[0:HALF, 1, o * TOPK:(o + 1) * TOPK],
                                                    W["q"][:, h, o * HALF:(o + 1) * HALF], picked[:, h, :],
                                                    start=(h == 0), stop=(h == 1))
                    last.then_inc(M["q_ready"], 1)
                    pe.wait_ge(M["turn_kept"], 2 * MT * b)
                    for t in range(TPB):
                        nc.tensor.transpose(t_ps[0:TOPK, 0, t * P:(t + 1) * P], sel[:, b, t, :], ident[:])
                    nc.tensor.transpose(t_ps[0:TOPK, 1, 0:B], selc[:, b, :], ident[0:B, 0:B]).then_inc(M["st_ready"], 1)
                    pe.wait_ge(M["qd_ready"], 2 * b + 2)
                    for j in range(2 * NB):
                        n = 2 * NB * b + j
                        o, (r0, r1) = j // NB, QBLOCKS[j % NB]
                        if n >= 2:
                            pe.wait_ge(M["prob_ready"], n - 1)
                        for a, z in HALVES:
                            last = nc.tensor.matmul(s_ps[0:r1 - r0, j % 2, L + a:L + z],
                                                    qd[:, o, :, :].rearrange("p h s -> p (h s)")[:, r0:r1],
                                                    KT[:, o, b, a:z], start=True, stop=True)
                        last.then_inc(M["logit_ready"], 1)
                    pe.wait_ge(M["st_kept"], b + 1)
                    for o in range(2):
                        pe.wait_ge(M["prob_normed"], 2 * NB * b + NB * (o + 1))
                        for m in range(MT):
                            j = o * MT + m
                            n = P if m < TPB else 1
                            if 2 * MT * b + j >= 2:
                                pe.wait_ge(M["turn_kept"], 2 * MT * b + j - 1)
                            for k, (r0, r1) in enumerate(QBLOCKS):
                                last = nc.tensor.transpose(t_ps[0:n, j % 2, r0:r1],
                                                           prob[0:r1 - r0, o * NB + k, m * P:m * P + n],
                                                           ident[0:r1 - r0, 0:r1 - r0])
                            last.then_inc(M["turn_ready"], 1)
                    for o in range(2):
                        pe.wait_ge(M["turn_kept"], 2 * MT * b + MT * (o + 1))
                        for m in range(MT):
                            v = V[:, b * TPB + m, o * HALF:(o + 1) * HALF] if m < TPB else VC[:, b, o * HALF:(o + 1) * HALF]
                            n = P if m < TPB else 1
                            last = nc.tensor.matmul(x_ps[0:HALF, o, 0:QROWS], v, probT[0:n, o, m, :], start=(m == 0),
                                                    stop=(m == MT - 1))
                        last.then_inc(M["ctx_ready"], 1)
                    pe.wait_ge(M["ctx_kept"], 2 * b + 2)
                    for h in range(2):
                        nc.tensor.matmul(x_ps[0:TOPK, 0, 0:D], ctxT[:, h, :], W["o"][:, h, :], start=(h == 0), stop=False)
                    nc.tensor.matmul(x_ps[0:TOPK, 0, 0:D], ones[0:1, 0:TOPK], bo[:], start=False,
                                     stop=True).then_inc(M["as_ready"], 1)

            @block.scalar
            def _(act):
                for b in range(B):
                    act.wait_ge(M["st_ready"], b + 1)
                    nc.scalar.activation(selT[:, b, 0:T], t_ps[0:TOPK, 0, :], ACT.Copy)
                    nc.scalar.activation(selT[:, b, T:T + B], t_ps[0:TOPK, 1, 0:B], ACT.Copy).then_inc(M["st_kept"], 1)
                    for j in range(2 * NB):
                        r = QBLOCKS[j % NB][1] - QBLOCKS[j % NB][0]
                        act.wait_ge(M["top_ready"], 2 * NB * b + j + 1)
                        if j % NB == 0:
                            act.wait_ge(M["turn_ready"], 2 * MT * b)
                        nc.scalar.activation(prob[0:r, j, 0:N], s_ps[0:r, j % 2, L:L + N], ACT.Exp,
                                             bias=top[0:r, j:j + 1],
                                             accum_out=den[0:r, j:j + 1]).then_inc(M["prob_ready"], 1)
                    for j in range(2 * MT):
                        act.wait_ge(M["turn_ready"], 2 * MT * b + j + 1)
                        act.wait_ge(M["ctx_ready"], 2 * b)
                        n = P if j % MT < TPB else 1
                        nc.scalar.activation(probT[0:n, j // MT, j % MT, :], t_ps[0:n, j % 2, 0:QROWS],
                                             ACT.Copy).then_inc(M["turn_kept"], 1)

            @block.vector
            def _(dve):
                dve.wait_ge(M["const"], 3)
                for b in range(B):
                    dve.wait_ge(M["picked_ready"], b + 1)
                    nc.vector.tensor_copy(picked[:], x_ps[0:HALF, 0, 0:2 * TOPK].rearrange(
                        "p (h s) -> p h s", h=2)).then_inc(M["picked_kept"], 1)
                    dve.wait_ge(M["q_ready"], b + 1)
                    for o in range(2):
                        nc.vector.tensor_scalar(q[:, o, :], x_ps[0:HALF, 1, o * TOPK:(o + 1) * TOPK], bq[:, o:o + 1],
                                                float(HD) ** -0.5, ALU.add, ALU.mult).then_inc(M["q_kept"], 1)
                    for o in range(2):
                        dve.wait_ge(M["q_kept"], 2 * b + o + 1)
                        dve.wait_ge(M["logit_ready"], 2 * NB * b)
                        nc.vector.tensor_tensor(qd[:, o, :, :], q[:, o, :].unsqueeze(1).broadcast_to((HALF, HPH, TOPK)),
                                                heads[:].unsqueeze(2).broadcast_to((HALF, HPH, TOPK)),
                                                ALU.mult).then_inc(M["qd_ready"], 1)

                    def normalise(j):
                        r = QBLOCKS[j % NB][1] - QBLOCKS[j % NB][0]
                        dve.wait_ge(M["prob_ready"], 2 * NB * b + j + 1)
                        nc.vector.reciprocal(rden[0:r, j:j + 1], den[0:r, j:j + 1]).then_inc(M["rden_ready"], 1)
                        dve.wait_ge(M["rden_ready"], 2 * NB * b + j + 1)
                        nc.vector.tensor_scalar(prob[0:r, j, 0:N], prob[0:r, j, 0:N], rden[0:r, j:j + 1], None,
                                                ALU.mult).then_inc(M["prob_normed"], 1)

                    for j in range(2 * NB):
                        r = QBLOCKS[j % NB][1] - QBLOCKS[j % NB][0]
                        dve.wait_ge(M["logit_ready"], 2 * NB * b + j + 1)
                        nc.vector.tensor_reduce(top[0:r, j:j + 1], s_ps[0:r, j % 2, L:L + N], AX_X, ALU.max,
                                                negate=True).then_inc(M["top_ready"], 1)
                        if j:
                            normalise(j - 1)
                    normalise(2 * NB - 1)
                    for o in range(2):
                        dve.wait_ge(M["ctx_ready"], 2 * b + o + 1)
                        nc.vector.tensor_tensor(own[:, o, :].rearrange("p (h s) -> p h s", h=HPH),
                                                x_ps[0:HALF, o, 0:QROWS].rearrange("p (h s) -> p h s", h=HPH),
                                                heads[:].unsqueeze(2).broadcast_to((HALF, HPH, TOPK)),
                                                ALU.mult).then_inc(M["own_ready"], 1)
                        dve.wait_ge(M["own_ready"], 2 * b + o + 1)
                        nc.vector.reduce_sum(ctxT[:, o, :], own[:, o, :].rearrange("p (h s) -> p s h", h=HPH),
                                             AX_X).then_inc(M["ctx_kept"], 1)
                    dve.wait_ge(M["as_ready"], b + 1)
                    nc.vector.tensor_copy(AS[:, b, :], x_ps[0:TOPK, 0, 0:D]).then_inc(M["as_kept"], 1)


def merge(nc, sem, make_sb, make_ps, ones, N1T, Wm, bm, selT, AS, score, rest, score_cls, rest_cls, PM, PMC, HH):
    with ExitStack() as ctx:
        mixed = make_sb(ctx)("rm_mixed", [P, 2, D])
        ps = make_ps(ctx)
        m_ps, a_ps = ps("rm_m", [P, 2, 512]), ps("rm_a", [P, 2, 512])
        ready, mixed_ready, added, kept = sem("rm_ready"), sem("rm_mixed_ready"), sem("rm_added"), sem("rm_kept")
        with nc.Block() as block:
            @block.tensor
            def _(pe):
                for t in range(NT):
                    n, first = tokens_of(t)
                    if t >= 2:
                        pe.wait_ge(kept, t - 1)
                    for h in range(2):
                        nc.tensor.matmul(m_ps[0:n, t % 2, 0:D], N1T[:, h, first:first + n], Wm[:, h, :], start=(h == 0),
                                         stop=False)
                    nc.tensor.matmul(m_ps[0:n, t % 2, 0:D], ones[0:1, 0:n], bm[:], start=False, stop=True)
                    if t < CLS:
                        last = nc.tensor.matmul(a_ps[:, t % 2, 0:D], selT[:, t // TPB, (t % TPB) * P:(t % TPB + 1) * P],
                                                AS[:, t // TPB, :], start=True, stop=True)
                    else:
                        for b in range(B):
                            last = nc.tensor.matmul(a_ps[0:B, t % 2, 0:D], selT[:, b, T:T + B], AS[:, b, :],
                                                    start=(b == 0), stop=(b == B - 1))
                    last.then_inc(ready, 1)

            @block.vector
            def _(dve):
                for t in range(NT):
                    n, _ = tokens_of(t)
                    b, k = t // TPB, t % TPB
                    s, r, pm = (score[:, b, k:k + 1], rest[:, b, k:k + 1], PM[:, b, :]) if t < CLS else \
                        (score_cls[:], rest_cls[:], PMC[:])
                    dve.wait_ge(ready, t + 1)
                    nc.vector.scalar_tensor_tensor(out=mixed[0:n, t % 2, :], in0=pm, scalar=s, in1=m_ps[0:n, t % 2, 0:D],
                                                   op0=ALU.mult, op1=ALU.add).then_inc(mixed_ready, 1)
                    dve.wait_ge(mixed_ready, t + 1)
                    nc.vector.scalar_tensor_tensor(out=HH[0:n, t, :], in0=mixed[0:n, t % 2, :], scalar=r, in1=HH[0:n, t, :],
                                                   op0=ALU.mult, op1=ALU.add).then_inc(added, 1)
                    dve.wait_ge(added, t + 1)
                    nc.vector.tensor_tensor(HH[0:n, t, :], HH[0:n, t, :], a_ps[0:n, t % 2, 0:D], ALU.add).then_inc(kept, 1)


def gelu_mlp(nc, sem, make_sb, make_ps, ones, N2T, W1, bf1, W2, bf2, HH, H):
    NF = F // P
    CHUNKS = [(b * T, T) for b in range(B)] + [(B * T, B)]
    with ExitStack() as ctx:
        sb, ps = make_sb(ctx), make_ps(ctx)
        hid = sb("gm_hid", [P, 2, NF, T])
        h_ps, o_ps = ps("gm_h", [P, 4, 512]), ps("gm_o", [P, 2, 512])
        h_ready, h_kept, o_ready, o_kept, added = (sem("gm_h_ready"), sem("gm_h_kept"), sem("gm_o_ready"),
                                                   sem("gm_o_kept"), sem("gm_added"))
        with nc.Block() as block:
            @block.tensor
            def _(pe):
                for k, (first, n) in enumerate(CHUNKS):
                    for f in range(NF):
                        j = k * NF + f
                        if j >= 4:
                            pe.wait_ge(h_kept, j - 3)
                        for h in range(2):
                            last = nc.tensor.matmul(h_ps[:, j % 4, 0:n], W1[:, h, f * P:(f + 1) * P],
                                                    N2T[:, h, first:first + n], start=(h == 0), stop=(h == 1))
                        last.then_inc(h_ready, 1)
                    pe.wait_ge(h_kept, (k + 1) * NF)
                    for t in range(k * TPB, min(NT, (k + 1) * TPB)):
                        n, c = tokens_of(t)
                        if t >= 2:
                            pe.wait_ge(o_kept, t - 1)
                        for f in range(NF):
                            nc.tensor.matmul(o_ps[0:n, t % 2, 0:D], hid[:, k % 2, f, c - first:c - first + n], W2[:, f, :],
                                             start=(f == 0), stop=False)
                        nc.tensor.matmul(o_ps[0:n, t % 2, 0:D], ones[0:1, 0:n], bf2[:], start=False,
                                         stop=True).then_inc(o_ready, 1)

            @block.scalar
            def _(act):
                for k, (first, n) in enumerate(CHUNKS):
                    for f in range(NF):
                        j = k * NF + f
                        act.wait_ge(h_ready, j + 1)
                        if f == 0 and k >= 2:
                            act.wait_ge(o_ready, (k - 1) * TPB)
                        nc.scalar.activation(hid[:, k % 2, f, 0:n], h_ps[:, j % 4, 0:n], ACT.Gelu,
                                             bias=bf1[:, f:f + 1]).then_inc(h_kept, 1)

            @block.vector
            def _(dve):
                for t in range(NT):
                    nc.vector.tensor_tensor(H[:, t, :], H[:, t, :], HH[:, t, :], ALU.add).then_inc(added, 1)
                for t in range(NT):
                    n, _ = tokens_of(t)
                    dve.wait_ge(added, t + 1)
                    dve.wait_ge(o_ready, t + 1)
                    nc.vector.tensor_tensor(H[0:n, t, :], H[0:n, t, :], o_ps[0:n, t % 2, 0:D], ALU.add).then_inc(o_kept, 1)


RH, DQK, DV = 6, 128, 64
RQ, RV = RH * DQK, RH * DV
RC = RV // P
SCALE_BASE = 512.0


def retention_tables():
    pos = np.arange(1, N).astype(np.float64)
    half = DQK // 2
    inv_freq = (1.0 / 10000.0 ** (np.arange(half, dtype=np.float32) / np.float32(half))).astype(np.float32)
    angles = (pos.astype(np.float32)[None, :] * inv_freq[:, None]).astype(np.float32).astype(np.float64)
    zeta = (np.arange(half) + half) / DQK
    rot = np.zeros((DQK, 2, 2, T), np.float32)
    for x, sign in enumerate((1.0, -1.0)):
        decay = zeta[:, None] ** (sign * pos[None, :] / SCALE_BASE)
        c, s = np.cos(angles) * decay, np.sin(angles) * decay
        rot[:, x, 0] = np.concatenate([c, c])
        rot[:, x, 1] = np.concatenate([s, -s])
    gamma = 1.0 - 2.0 ** -(5.0 + np.arange(RH))
    rows = (1 - gamma[:, None] ** (pos + 1)) / (1 - gamma[:, None])
    q = gamma[:, None] ** pos / np.sqrt(rows)
    k = gamma[:, None] ** -pos * DQK ** -0.5

    def by_tile(v):
        return np.ascontiguousarray(v.reshape(RH, TPB, P).transpose(2, 0, 1)).astype(np.float32)
    return rot, by_tile(q), by_tile(k)


def retention_stage(nc, sem, make_sb, make_ps, A, H, ident, ones):
    with ExitStack() as ctx:
        sb = make_sb(ctx)
        R_ = {}
        R_["XT"] = sb("t_xT", [HALF, 2, NTOK])
        for k, n in (("q", RQ), ("k", RQ), ("v", RV), ("g", RV)):
            R_["W" + k] = sb("t_W" + k, [HALF, 2, n])
        R_["Wo"] = sb("t_Wo", [P, RC, D])
        R_["gnw"], R_["gnb"] = sb("t_gnw", [P, RV]), sb("t_gnb", [P, RV])
        R_["rot"] = sb("t_rot", [P, 2, 2, T])
        R_["qd"], R_["kd"] = sb("t_qd", [P, RH, TPB]), sb("t_kd", [P, RH, TPB])
        for name, n in (("OC", RV), ("GC", RV), ("centredC", RV), ("rstdC", RH), ("csum", RH)):
            R_[name] = sb("t_" + name, [B, n])
        R_["QC"] = sb("t_QC", [P, 2, RH, B])
        load(nc, sem, "t", [
            *[(R_["W" + k][:], halves_of(A["L1_attn_W" + k])) for k in "qkvg"],
            (R_["Wo"][:], A["L1_attn_Wo"].rearrange("(c p) n -> p c n", p=P)),
            (R_["gnw"][:], A["L1_attn_gn_weight"].partition_broadcast(P)),
            (R_["gnb"][:], A["L1_attn_gn_bias"].partition_broadcast(P)),
            (R_["rot"][:], A["rot"]), (R_["qd"][:], A["query_decay"]), (R_["kd"][:], A["key_decay"])])
        with ExitStack() as xctx:
            X = make_sb(xctx)("t_x", [P, NT, D])
            norm_stage(nc, sem, make_sb, make_ps, "tn", H, X, R_["XT"], ident)
        retention_cls_outputs(nc, sem, make_sb, make_ps, R_, ones)
        retention_heads(nc, sem, make_sb, make_ps, R_, H, ident, ones)
        retention_cls_rows(nc, sem, make_sb, make_ps, R_, H, ident)


def retention_cls_outputs(nc, sem, make_sb, make_ps, R_, ones):
    with ExitStack() as ctx:
        sb, ps = make_sb(ctx), make_ps(ctx)
        prod = sb("tc_prod", [P, RH, B])
        dots = sb("tc_dots", [B, RH])
        q_ps, v_ps, g_ps, d_ps = (ps("tc_" + k, [P, 512]) for k in "qvgd")
        qk_ready, kept, prod_ready, v_ready = sem("tc_qk_ready"), sem("tc_kept"), sem("tc_prod_ready"), sem("tc_v_ready")
        g_ready, dots_ready, dots_kept, out_ready = (sem("tc_g_ready"), sem("tc_dots_ready"), sem("tc_dots_kept"),
                                                     sem("tc_out_ready"))
        XT, QC, OC, csum = R_["XT"], R_["QC"], R_["OC"], R_["csum"]
        with nc.Block() as block:
            @block.tensor
            def _(pe):
                for x, w in enumerate("qk"):
                    for head in range(RH):
                        c = (x * RH + head) * B
                        for h in range(2):
                            last = nc.tensor.matmul(q_ps[:, c:c + B], R_["W" + w][:, h, head * DQK:(head + 1) * DQK],
                                                    XT[:, h, B * T:NTOK], start=(h == 0), stop=(h == 1))
                last.then_inc(qk_ready, 1)
                for w, dst, ready in (("v", v_ps, v_ready), ("g", g_ps, g_ready)):
                    for h in range(2):
                        last = nc.tensor.matmul(dst[0:B, 0:RV], XT[:, h, B * T:NTOK], R_["W" + w][:, h, :], start=(h == 0),
                                                stop=(h == 1))
                    last.then_inc(ready, 1)
                pe.wait_ge(prod_ready, 1)
                for head in range(RH):
                    last = nc.tensor.matmul(d_ps[0:B, head:head + 1], prod[:, head, :], ones[:, 0:1], start=True, stop=True)
                last.then_inc(dots_ready, 1)

            @block.scalar
            def _(act):
                act.wait_ge(g_ready, 1)
                nc.scalar.activation(R_["GC"][:], g_ps[0:B, 0:RV], ACT.Silu)

            @block.vector
            def _(dve):
                nc.vector.memset(R_["centredC"][:], 0.0)
                nc.vector.memset(R_["rstdC"][:], 0.0)
                dve.wait_ge(qk_ready, 1)
                nc.vector.tensor_copy(QC[:].rearrange("p x h b -> p (x h b)"), q_ps[:, 0:2 * RH * B]).then_inc(kept, 1)
                dve.wait_ge(kept, 1)
                nc.vector.tensor_tensor(prod[:], QC[:, 0], QC[:, 1], ALU.mult).then_inc(prod_ready, 1)
                dve.wait_ge(dots_ready, 1)
                nc.vector.tensor_scalar(dots[:], d_ps[0:B, 0:RH], float(DQK) ** -0.5, None, ALU.mult).then_inc(dots_kept, 1)
                dve.wait_ge(dots_kept, 1)
                dve.wait_ge(v_ready, 1)
                by_head = OC[:].rearrange("b (h d) -> b h d", h=RH)
                nc.vector.tensor_tensor(by_head, v_ps[0:B, 0:RV].rearrange("b (h d) -> b h d", h=RH),
                                        dots[:].unsqueeze(2).broadcast_to((B, RH, DV)), ALU.mult).then_inc(out_ready, 1)
                dve.wait_ge(out_ready, 1)
                nc.vector.reduce_sum(csum[:], by_head, AX_X)


def retention_heads(nc, sem, make_sb, make_ps, R_, H, ident, ones):
    STEPS = RH * (B + 1)
    ITEMS = {-1: [("v", 0, t) for t in range(TPB)] + [("vc", 0, 0)] + [("g", 0, t) for t in range(TPB)]}
    for u in range(STEPS):
        b, head = divmod(u, RH)
        done, coming = b - 1, b + 1
        ITEMS[u] = []
        if done >= 0:
            ITEMS[u] += {1: [("sum", done, 0)], 2: [("square", done, 0)], 4: [("yt", done, c) for c in range(RC)],
                         5: [("h", done, t) for t in range(TPB)]}.get(head, [])
        if coming < B:
            ITEMS[u] += {3: [("v", coming, t) for t in range(TPB)] + [("vc", coming, 0)],
                         4: [("g", coming, t) for t in range(TPB)]}.get(head, [])
    ORDER = [item for u in range(-1, STEPS) for item in ITEMS[u]]
    USE = {item: n for n, item in enumerate(ORDER)}
    BY_ACT = ("g", "yt")

    def kept(item):
        return 1 + sum((a[0] in BY_ACT) == (item[0] in BY_ACT) for a in ORDER[:USE[item]])

    with ExitStack() as ctx:
        sb, ps = make_sb(ctx), make_ps(ctx)
        causal = sb("t_causal", [P, P])
        V, G, O = sb("t_V", [P, 2, TPB, RV]), sb("t_G", [P, 2, TPB, RV]), sb("t_O", [P, 2, TPB, RV])
        VC = sb("t_VC", [1, 2, RV])
        main = sb("t_main", [P, 2, T])
        cross = sb("t_cross", [P, 2, T])
        turned = sb("t_turned", [P, 2, 2, T])
        S = sb("t_S", [P, 2, TPB, T])
        SC = sb("t_SC", [1, 2, T])
        squares, squaresC = sb("t_squares", [P, TPB, RV]), sb("t_squaresC", [B, RV])
        centred = sb("t_cls_centred", [B, RV])
        sums, cls_sums = sb("t_sums", [P, RH]), sb("t_cls_sums", [B, RH])
        mean, var = sb("t_mean", [P, RH]), sb("t_var", [P, RH])
        half_power = sb("t_half_power", [P, RH])
        gain = sb("t_gain", [P, RV])
        YT = sb("t_YT", [P, RC, T])
        p_ps = ps("t_p", [P, 2, 512])
        s_ps = ps("t_s", [P, 2, 512])
        o_ps = ps("t_o", [P, 2, 512])
        x_ps = ps("t_x2", [P, 2, 512])
        names = ("causal x_ready x_kept_dve x_kept_act qk_ready main_ready cross_ready turned s_ready s_kept diag_ready "
                 "o_ready o_kept sums_ready squares_ready rstd_ready pool_step step y_ready ").split()
        M = {n: sem("t_" + n) for n in names}
        XT, rot, qd, kd, QC, OC = (R_[k] for k in ("XT", "rot", "qd", "kd", "QC", "OC"))
        SPH = TPB + 1
        CNT = float(DV * N)

        def x_wait(engine, item):
            engine.wait_ge(M["x_ready"], USE[item] + 1)

        with nc.Block() as block:
            @block.tensor
            def _(pe):
                def project(u):
                    b, head = divmod(u, RH)
                    for x, w in enumerate("qk"):
                        if u:
                            pe.wait_ge(M["main_ready"], 2 * (u - 1) + x + 1)
                            pe.wait_ge(M["cross_ready"], 4 * (u - 1) + 2 * x + 2)
                        for h in range(2):
                            last = nc.tensor.matmul(p_ps[:, x, :], R_["W" + w][:, h, head * DQK:(head + 1) * DQK],
                                                    XT[:, h, b * T:(b + 1) * T], start=(h == 0), stop=(h == 1))
                        last.then_inc(M["qk_ready"], 1)

                def scores(u):
                    b, head = divmod(u, RH)
                    pe.wait_ge(M["turned"], 2 * u + 2)
                    q, k = turned[:, u % 2, 0, :], turned[:, u % 2, 1, :]
                    for m in range(SPH):
                        j = u * SPH + m
                        if j >= 2:
                            pe.wait_ge(M["s_kept"], j - 1)
                        if m < TPB:
                            nc.tensor.matmul(s_ps[:, j % 2, m * P:T], k[:, m * P:(m + 1) * P], q[:, m * P:T], start=True,
                                             stop=True).then_inc(M["s_ready"], 1)
                        else:
                            nc.tensor.matmul(s_ps[0:1, j % 2, :], QC[:, 1, head, b:b + 1], q, start=True,
                                             stop=True).then_inc(M["s_ready"], 1)

                def outputs(u):
                    b, head = divmod(u, RH)
                    pe.wait_ge(M["diag_ready"], TPB * (u + 1))
                    pe.wait_ge(M["s_kept"], SPH * (u + 1))
                    if head == 0:
                        pe.wait_ge(M["x_kept_dve"], kept(("vc", b, 0)))
                    if u >= 2:
                        pe.wait_ge(M["o_kept"], u - 1)
                    vh = slice(head * DV, (head + 1) * DV)
                    for t in range(TPB):
                        dst = o_ps[:, u % 2, t * DV:(t + 1) * DV]
                        for m in range(t + 1):
                            nc.tensor.matmul(dst, S[:, u % 2, m, t * P:(t + 1) * P], V[:, b % 2, m, vh], start=(m == 0),
                                             stop=False)
                        last = nc.tensor.matmul(dst, SC[:, u % 2, t * P:(t + 1) * P], VC[:, b % 2, vh], start=False, stop=True)
                    last.then_inc(M["o_ready"], 1)

                def item_product(item):
                    what, b, i = item
                    n = USE[item]
                    if n >= 2:
                        before = ORDER[n - 2]
                        pe.wait_ge(M["x_kept_act" if before[0] in BY_ACT else "x_kept_dve"], kept(before))
                    dst = x_ps[:, n % 2, :]
                    if what in ("v", "g"):
                        first = (b * TPB + i) * P
                        for h in range(2):
                            last = nc.tensor.matmul(dst[:, 0:RV], XT[:, h, first:first + P], R_["W" + what][:, h, :],
                                                    start=(h == 0), stop=(h == 1))
                    elif what == "vc":
                        for h in range(2):
                            last = nc.tensor.matmul(dst[0:1, 0:RV], XT[:, h, B * T + b:B * T + b + 1], R_["Wv"][:, h, :],
                                                    start=(h == 0), stop=(h == 1))
                    elif what in ("sum", "square"):
                        pe.wait_ge(M["sums_ready" if what == "sum" else "squares_ready"], b + 1)
                        nc.tensor.matmul(dst[:, 0:RH], ones[:], sums[:], start=True, stop=False)
                        last = nc.tensor.matmul(dst[:, 0:RH], ident[0:B, b:b + 1].broadcast_to((B, P)),
                                                R_["csum"][:] if what == "sum" else cls_sums[:], start=False, stop=True)
                    elif what == "yt":
                        pe.wait_ge(M["y_ready"], b + 1)
                        for t in range(TPB):
                            last = nc.tensor.transpose(dst[:, t * P:(t + 1) * P], O[:, b % 2, t, i * P:(i + 1) * P], ident[:])
                    else:
                        pe.wait_ge(M["x_kept_act"], kept(("yt", b, RC - 1)))
                        for c in range(RC):
                            last = nc.tensor.matmul(dst[:, 0:D], YT[:, c, i * P:(i + 1) * P], R_["Wo"][:, c, :],
                                                    start=(c == 0), stop=(c == RC - 1))
                    last.then_inc(M["x_ready"], 1)

                for u in range(-1, STEPS):
                    if u + 1 < B * RH:
                        project(u + 1)
                    if 0 <= u < B * RH:
                        scores(u)
                    if 0 <= u - 1 < B * RH:
                        outputs(u - 1)
                    for item in ITEMS[u]:
                        item_product(item)

            @block.scalar
            def _(act):
                for u in range(-1, STEPS):
                    if 0 <= u < B * RH:
                        head = u % RH
                        if u >= 2:
                            act.wait_ge(M["o_ready"], u - 1)
                        for m in range(SPH):
                            j = u * SPH + m
                            act.wait_ge(M["s_ready"], j + 1)
                            if m < TPB:
                                nc.scalar.activation(S[:, u % 2, m, m * P:T], s_ps[:, j % 2, m * P:T], ACT.Copy,
                                                     scale=kd[:, head, m:m + 1]).then_inc(M["s_kept"], 1)
                            else:
                                nc.scalar.activation(SC[:, u % 2, :], s_ps[0:1, j % 2, :], ACT.Copy,
                                                     scale=float(DQK) ** -0.5).then_inc(M["s_kept"], 1)
                    for item in ITEMS[u]:
                        what, b, i = item
                        if what == "g":
                            x_wait(act, item)
                            if b >= 2 and i == 0:
                                act.wait_ge(M["y_ready"], b - 1)
                            nc.scalar.activation(G[:, b % 2, i, :], x_ps[:, USE[item] % 2, 0:RV],
                                                 ACT.Silu).then_inc(M["x_kept_act"], 1)
                        elif what == "yt":
                            x_wait(act, item)
                            if b and i == 0:
                                act.wait_ge(M["x_ready"], USE["h", b - 1, TPB - 1] + 1)
                            nc.scalar.activation(YT[:, i, :], x_ps[:, USE[item] % 2, :], ACT.Copy).then_inc(M["x_kept_act"], 1)

            @block.gpsimd
            def _(pool):
                nc.gpsimd.memset(causal[:], 1.0).then_inc(M["causal"], 1)
                pool.wait_ge(M["causal"], 1)
                nc.gpsimd.affine_select(out=causal[:], in_=causal[:], compare_op=ALU.is_ge, fill=0.0, base=0,
                                        pattern=[[1, P]], channel_multiplier=-1).then_inc(M["causal"], 1)
                nc.gpsimd.memset(half_power[:], -0.5).then_inc(M["causal"], 1)
                pool.wait_ge(M["causal"], 3)
                for u in range(STEPS):
                    if u < B * RH:
                        for x in range(2):
                            pool.wait_ge(M["main_ready"], 2 * u + x + 1)
                            pool.wait_ge(M["cross_ready"], 4 * u + 2 * x + 2)
                            if u >= 2:
                                pool.wait_ge(M["s_ready"], SPH * (u - 1))
                            nc.gpsimd.tensor_tensor(turned[:, u % 2, x, :], main[:, x, :], cross[:, x, :],
                                                    ALU.add).then_inc(M["turned"], 1)
                    for what, b, _ in ITEMS[u]:
                        if what == "square":
                            pool.wait_ge(M["x_kept_dve"], kept((what, b, 0)))
                            nc.gpsimd.tensor_scalar(var[:], var[:], LN_EPS, None, ALU.add).then_inc(M["pool_step"], 1)
                            pool.wait_ge(M["pool_step"], b + 1)
                            nc.gpsimd.tensor_tensor(var[:], var[:], half_power[:], ALU.pow).then_inc(M["rstd_ready"], 1)

            @block.vector
            def _(dve):
                steps = Tally(M["step"])

                def then(ins):
                    dve.wait_ge(M["step"], steps.mark(ins))

                def rotate(u):
                    for x in range(2):
                        dve.wait_ge(M["qk_ready"], 2 * u + x + 1)
                        if u:
                            dve.wait_ge(M["turned"], 2 * (u - 1) + x + 1)
                        nc.vector.tensor_tensor(main[:, x, :], p_ps[:, x, :], rot[:, x, 0, :],
                                                ALU.mult).then_inc(M["main_ready"], 1)
                        for src, dst in ((slice(64, P), slice(0, 64)), (slice(0, 64), slice(64, P))):
                            nc.vector.tensor_tensor(cross[dst, x, :], p_ps[src, x, :], rot[src, x, 1, :],
                                                    ALU.mult).then_inc(M["cross_ready"], 1)

                def diagonal_blocks(u):
                    for m in range(TPB):
                        dve.wait_ge(M["s_kept"], u * SPH + m + 1)
                        diagonal = S[:, u % 2, m, m * P:(m + 1) * P]
                        nc.vector.tensor_tensor(diagonal, diagonal, causal[:], ALU.mult).then_inc(M["diag_ready"], 1)

                def keep(u):
                    b, head = divmod(u, RH)
                    dve.wait_ge(M["o_ready"], u + 1)
                    if head == 0 and b >= 2:
                        dve.wait_ge(M["x_ready"], USE["yt", b - 2, RC - 1] + 1)
                    nc.vector.tensor_tensor(O[:, b % 2, :, head * DV:(head + 1) * DV],
                                            o_ps[:, u % 2, 0:TPB * DV].rearrange("p (t d) -> p t d", t=TPB),
                                            qd[:, head, :].unsqueeze(2).broadcast_to((P, TPB, DV)),
                                            ALU.mult).then_inc(M["o_kept"], 1)

                def heads_first(x):
                    return x.rearrange("p t (h d) -> p h t d", h=RH)

                def per_head(x, n):
                    return x.unsqueeze(2).broadcast_to((n, RH, DV))

                def group_sums(b):
                    dve.wait_ge(M["o_kept"], RH * (b + 1))
                    if b:
                        dve.wait_ge(M["x_ready"], USE["square", b - 1, 0] + 1)
                    nc.vector.tensor_reduce(sums[:], heads_first(O[:, b % 2]), mybir.AxisListType.XY,
                                            ALU.add).then_inc(M["sums_ready"], 1)

                def centre(b, x):
                    nc.vector.tensor_scalar(mean[:], x[:, 0:RH], 1.0 / CNT, None, ALU.mult).then_inc(M["x_kept_dve"], 1)
                    dve.wait_ge(M["x_kept_dve"], kept(("sum", b, 0)))
                    for t in range(TPB):
                        v = O[:, b % 2, t, :].rearrange("p (h d) -> p h d", h=RH)
                        nc.vector.tensor_tensor(v, v, per_head(mean[:], P), ALU.subtract)
                    then(nc.vector.tensor_tensor(centred[:].rearrange("p (h d) -> p h d", h=RH),
                                                 OC[:].rearrange("p (h d) -> p h d", h=RH), per_head(mean[0:B, :], B),
                                                 ALU.subtract))
                    nc.vector.scalar_tensor_tensor(out=R_["centredC"][:], in0=centred[:], scalar=ident[0:B, b:b + 1],
                                                   in1=R_["centredC"][:], op0=ALU.mult, op1=ALU.add)
                    nc.vector.tensor_tensor(squaresC[:], centred[:], centred[:], ALU.mult)
                    Ob = O[:, b % 2].rearrange("p t n -> p (t n)")
                    then(nc.vector.tensor_tensor(squares[:].rearrange("p t n -> p (t n)"), Ob, Ob, ALU.mult))
                    nc.vector.reduce_sum(cls_sums[:], squaresC[:].rearrange("p (h d) -> p h d", h=RH), AX_X)
                    last = nc.vector.tensor_reduce(sums[:], heads_first(squares[:]), mybir.AxisListType.XY, ALU.add)
                    last.then_inc(M["squares_ready"], 1)

                def normalise(b):
                    dve.wait_ge(M["rstd_ready"], b + 1)
                    then(nc.vector.tensor_tensor(gain[:].rearrange("p (h d) -> p h d", h=RH),
                                                 R_["gnw"][:].rearrange("p (h d) -> p h d", h=RH), per_head(var[:], P), ALU.mult))
                    then(nc.vector.scalar_tensor_tensor(out=R_["rstdC"][:], in0=var[0:B, :], scalar=ident[0:B, b:b + 1],
                                                        in1=R_["rstdC"][:], op0=ALU.mult, op1=ALU.add))
                    y = O[:, b % 2]
                    then(nc.vector.tensor_tensor(y, y, gain[:].unsqueeze(1).broadcast_to((P, TPB, RV)), ALU.mult))
                    then(nc.vector.tensor_tensor(y, y, R_["gnb"][:].unsqueeze(1).broadcast_to((P, TPB, RV)), ALU.add))
                    dve.wait_ge(M["x_kept_act"], kept(("g", b, TPB - 1)))
                    nc.vector.tensor_tensor(y, y, G[:, b % 2], ALU.mult).then_inc(M["y_ready"], 1)

                dve.wait_ge(M["causal"], 3)
                for u in range(-1, STEPS):
                    if u + 1 < B * RH:
                        rotate(u + 1)
                    if 0 <= u < B * RH:
                        diagonal_blocks(u)
                    if 0 <= u - 1 < B * RH:
                        keep(u - 1)
                    b, head = divmod(u, RH)
                    if u >= RH and head == 0:
                        group_sums(b - 1)
                    if u >= RH and head == 3:
                        normalise(b - 1)
                    for item in ITEMS[u]:
                        what, b, i = item
                        if what in BY_ACT:
                            continue
                        x_wait(dve, item)
                        x = x_ps[:, USE[item] % 2, :]
                        if what == "v":
                            if b >= 2 and i == 0:
                                dve.wait_ge(M["o_ready"], RH * (b - 1))
                            nc.vector.tensor_copy(V[:, b % 2, i, :], x[:, 0:RV]).then_inc(M["x_kept_dve"], 1)
                        elif what == "vc":
                            nc.vector.tensor_copy(VC[:, b % 2, :], x[0:1, 0:RV]).then_inc(M["x_kept_dve"], 1)
                        elif what == "sum":
                            centre(b, x)
                        elif what == "square":
                            nc.vector.tensor_scalar(var[:], x[:, 0:RH], 1.0 / CNT, None, ALU.mult).then_inc(M["x_kept_dve"], 1)
                        else:
                            tile = b * TPB + i
                            nc.vector.tensor_tensor(H[:, tile, :], H[:, tile, :], x[:, 0:D],
                                                    ALU.add).then_inc(M["x_kept_dve"], 1)


def retention_cls_rows(nc, sem, make_sb, make_ps, R_, H, ident):
    with ExitStack() as ctx:
        sb, ps = make_sb(ctx), make_ps(ctx)
        YC = sb("tr_YC", [P, RC, B])
        t_ps, h_ps = ps("tr_t", [P, 512]), ps("tr_h", [P, 512])
        step, y_ready, t_ready, t_kept, h_ready = (sem("tr_step"), sem("tr_y_ready"), sem("tr_t_ready"), sem("tr_t_kept"),
                                                   sem("tr_h_ready"))
        with nc.Block() as block:
            @block.tensor
            def _(pe):
                pe.wait_ge(y_ready, 1)
                for c in range(RC):
                    last = nc.tensor.transpose(t_ps[:, c * B:(c + 1) * B], R_["centredC"][:, c * P:(c + 1) * P],
                                               ident[0:B, 0:B])
                last.then_inc(t_ready, 1)
                pe.wait_ge(t_kept, 1)
                for c in range(RC):
                    last = nc.tensor.matmul(h_ps[0:B, 0:D], YC[:, c, :], R_["Wo"][:, c, :], start=(c == 0), stop=(c == RC - 1))
                last.then_inc(h_ready, 1)

            @block.vector
            def _(dve):
                steps = Tally(step)

                def then(ins):
                    dve.wait_ge(step, steps.mark(ins))

                y = R_["centredC"]
                by_head = y[:].rearrange("b (h d) -> b h d", h=RH)
                then(nc.vector.tensor_tensor(by_head, by_head, R_["rstdC"][:].unsqueeze(2).broadcast_to((B, RH, DV)), ALU.mult))
                then(nc.vector.tensor_tensor(y[:], y[:], R_["gnw"][0:B, :], ALU.mult))
                then(nc.vector.tensor_tensor(y[:], y[:], R_["gnb"][0:B, :], ALU.add))
                nc.vector.tensor_tensor(y[:], y[:], R_["GC"][:], ALU.mult).then_inc(y_ready, 1)
                dve.wait_ge(t_ready, 1)
                nc.vector.tensor_copy(YC[:].rearrange("p c b -> p (c b)"), t_ps[:, 0:RC * B]).then_inc(t_kept, 1)
                dve.wait_ge(h_ready, 1)
                nc.vector.tensor_tensor(H[0:B, CLS, :], H[0:B, CLS, :], h_ps[0:B, 0:D], ALU.add)


E = 8
SPARE = (NTOK + E * (P - 1)) // P


def moe_stage(nc, sem, make_sb, make_ps, A, H, ident, ones):
    FF = 2 * F
    with ExitStack() as ctx:
        sb = make_sb(ctx)
        XT = sb("m_xT", [HALF, 2, NTOK])
        X = sb("m_x", [P, NT, D])
        router = sb("m_router", [HALF, 2, E])
        WI, WO = sb("m_wi", [HALF, E, FF]), sb("m_wo", [P, E, (F // P) * D])
        share = sb("m_share", [P, NT])
        place = sb("m_place", [P, NT], U32)
        expert = sb("m_expert", [1, SPARE], I32)
        zeros = sb("m_zeros", [P, SPARE * D // 8])
        sorted_x = nc.dram_tensor("sorted_x", (SPARE * P, D), F32, kind="Internal").ap()
        sorted_y = nc.dram_tensor("sorted_y", (SPARE * P, D), F32, kind="Internal").ap()
        router_loaded, w_loaded, cleared = sem("m_router_loaded"), sem("m_w_loaded"), sem("m_cleared")
        zeroed, scattered = sem("m_zeroed"), sem("m_scattered")
        with nc.Block() as block:
            @block.vector
            def _(dve):
                nc.vector.memset(zeros[:], 0.0).then_inc(zeroed, 1)

            @block.sync
            def _(sp):
                sp.dma_start(router[:], halves_of(A["L1_ffn_router_w"])).then_inc(router_loaded, 16)
                sp.wait_ge(zeroed, 1)
                rows = sorted_x.rearrange("(p r) d -> p (r d)", p=P)
                for k in range(8):
                    n = SPARE * D // 8
                    sp.dma_start(rows[:, k * n:(k + 1) * n], zeros[:]).then_inc(cleared, 16)
                for e in range(E):
                    sp.dma_start(WI[:, e, :].rearrange("p (h f) -> p h f", h=2), halves_of(A["L1_ffn_wi"][e])).then_inc(w_loaded, 16)
                    sp.dma_start(WO[:, e, :].rearrange("p (f n) -> p f n", n=D),
                                 A["L1_ffn_wo"][e].rearrange("(f p) n -> p f n", p=P)).then_inc(w_loaded, 16)
        norm_stage(nc, sem, make_sb, make_ps, "mn", H, X, XT, ident)
        switch_routing(nc, sem, make_sb, make_ps, XT, router, router_loaded, ones, share, place, expert)
        with nc.Block() as block:
            @block.gpsimd
            def _(pool):
                pool.wait_ge(cleared, 16 * 8)
                for t in range(NT):
                    n, _ = tokens_of(t)
                    pool.indirect_dma_start(sorted_x, bass.IndirectOffsetOnAxis(ap=place[0:n, t:t + 1], axis=0),
                                            X[0:n, t, :], None).then_inc(scattered, 16)
                pool.wait_ge(scattered, 16 * NT)
        experts_stage(nc, sem, make_sb, make_ps, WI, WO, w_loaded, expert, sorted_x, sorted_y, ident)
        with ExitStack() as yctx:
            Y = make_sb(yctx)("m_y", [P, NT, D])
            gathered = [sem(f"m_gathered{t}") for t in range(NT)]
            with nc.Block() as block:
                @block.gpsimd
                def _(pool):
                    for t in range(NT):
                        n, _ = tokens_of(t)
                        pool.indirect_dma_start(Y[0:n, t, :], None, sorted_y,
                                                bass.IndirectOffsetOnAxis(ap=place[0:n, t:t + 1], axis=0)
                                                ).then_inc(gathered[t], 16)

                @block.vector
                def _(dve):
                    for t in range(NT):
                        n, _ = tokens_of(t)
                        dve.wait_ge(gathered[t], 16)
                        nc.vector.scalar_tensor_tensor(out=H[0:n, t, :], in0=Y[0:n, t, :], scalar=share[0:n, t:t + 1],
                                                       in1=H[0:n, t, :], op0=ALU.mult, op1=ALU.add)


def experts_stage(nc, sem, make_sb, make_ps, WI, WO, w_loaded, expert, sorted_x, sorted_y, ident):
    NF = F // P
    HF = F // 2
    with ExitStack() as ctx:
        sb, ps = make_sb(ctx), make_ps(ctx)
        X = sb("e_x", [P, SPARE, D])
        xT = sb("e_xT", [HALF, 2, 2, P])
        hid = sb("e_hid", [P, 2, F])
        hidT = sb("e_hidT", [P, 2, NF, P])
        Y = sb("e_y", [P, 4, D])
        x_ps, h_ps, t_ps, y_ps = ps("e_xp", [P, 512]), ps("e_hp", [P, 4, 512]), ps("e_tp", [P, 2, 512]), ps("e_yp", [P, 512])
        names = "x_turned x_kept h_ready h_kept turned turned_kept y_ready y_kept".split()
        M = {n: sem("e_" + n) for n in names}
        x_loaded = [sem(f"e_x_loaded{k}") for k in range(4)]
        stored = [sem(f"e_stored{k}") for k in range(4)]
        PART = (SPARE + 3) // 4
        with nc.Block() as block:
            @block.sync
            def _(sp):
                tiles = sorted_x.rearrange("(j p) d -> p j d", p=P)
                for k in range(4):
                    a, z = k * PART, min(SPARE, (k + 1) * PART)
                    sp.dma_start(X[:, a:z, :], tiles[:, a:z, :]).then_inc(x_loaded[k], 16)
                for j in range(SPARE):
                    sp.wait_ge(M["y_kept"], j + 1)
                    sp.dma_start(sorted_y[j * P:(j + 1) * P, :], Y[:, j % 4, :]).then_inc(stored[j % 4], 16)
                for k in range(4):
                    sp.wait_ge(stored[k], 16 * len(range(k, SPARE, 4)))

            @block.tensor
            def _(pe):
                def turn_inputs(j):
                    if j % PART == 0:
                        pe.wait_ge(x_loaded[j // PART], 16)
                    if j >= 1:
                        pe.wait_ge(M["x_kept"], j)
                    for h in range(2):
                        last = nc.tensor.transpose(x_ps[0:HALF, h * P:(h + 1) * P], X[:, j, h * HALF:(h + 1) * HALF], ident[:])
                    last.then_inc(M["x_turned"], 1)

                def times_wi(j, e):
                    pe.wait_ge(M["x_kept"], j + 1)
                    if j >= 2:
                        pe.wait_ge(M["h_kept"], j - 1)
                    for n in range(2):
                        for h in range(2):
                            last = nc.tensor.matmul(h_ps[:, j % 2 * 2 + n, 0:HF], xT[:, j % 2, h, :],
                                                    WI[:, bass.ds(e, 1), h * F + n * HF:h * F + (n + 1) * HF].rearrange(
                                                        "p a n -> p (a n)"), start=(h == 0), stop=(h == 1))
                    last.then_inc(M["h_ready"], 1)

                def turn_hidden(j):
                    pe.wait_ge(M["h_kept"], j + 1)
                    if j >= 1:
                        pe.wait_ge(M["turned_kept"], j)
                    for f in range(NF):
                        last = nc.tensor.transpose(t_ps[:, f // 3, f % 3 * P:(f % 3 + 1) * P], hid[:, j % 2, f * P:(f + 1) * P],
                                                   ident[:])
                    last.then_inc(M["turned"], 1)

                def times_wo(j, e):
                    pe.wait_ge(M["turned_kept"], j + 1)
                    if j >= 1:
                        pe.wait_ge(M["y_kept"], j)
                    for f in range(NF):
                        last = nc.tensor.matmul(y_ps[:, 0:D], hidT[:, j % 2, f, :],
                                                WO[:, bass.ds(e, 1), f * D:(f + 1) * D].rearrange("p a n -> p (a n)"),
                                                start=(f == 0), stop=(f == NF - 1))
                    last.then_inc(M["y_ready"], 1)

                def number(j):
                    return nc.values_load(expert[0:1, j:j + 1], engines=[mybir.EngineType.PE], min_val=0, max_val=E - 1,
                                          skip_runtime_bounds_check_because="switch_routing limits it to E - 1")

                pe.wait_ge(w_loaded, 16 * 2 * E)
                turn_inputs(0)
                turn_inputs(1)
                numbers = {0: number(0)}
                times_wi(0, numbers[0])
                for j in range(SPARE + 1):
                    if j + 2 < SPARE:
                        turn_inputs(j + 2)
                    if j + 1 < SPARE:
                        numbers[j + 1] = number(j + 1)
                        times_wi(j + 1, numbers[j + 1])
                    if j < SPARE:
                        turn_hidden(j)
                    if j:
                        times_wo(j - 1, numbers.pop(j - 1))

            @block.scalar
            def _(act):
                for j in range(SPARE + 1):
                    if j < SPARE:
                        act.wait_ge(M["h_ready"], j + 1)
                        if j >= 2:
                            act.wait_ge(M["turned"], j - 1)
                        nc.scalar.activation(hid[:, j % 2, :].rearrange("p (n f) -> p n f", n=2),
                                             h_ps[:, j % 2 * 2:j % 2 * 2 + 2, 0:HF], ACT.Relu).then_inc(M["h_kept"], 1)
                    if j:
                        act.wait_ge(M["y_ready"], j)
                        if j > 4:
                            act.wait_ge(stored[(j - 1) % 4], 16 * ((j - 1) // 4))
                        nc.scalar.activation(Y[:, (j - 1) % 4, :], y_ps[:, 0:D], ACT.Copy).then_inc(M["y_kept"], 1)

            @block.vector
            def _(dve):
                def keep_inputs(j):
                    dve.wait_ge(M["x_turned"], j + 1)
                    if j >= 2:
                        dve.wait_ge(M["h_ready"], j - 1)
                    nc.vector.tensor_copy(xT[:, j % 2].rearrange("p h n -> p (h n)"),
                                          x_ps[0:HALF, 0:2 * P]).then_inc(M["x_kept"], 1)

                keep_inputs(0)
                keep_inputs(1)
                for j in range(SPARE):
                    if j + 2 < SPARE:
                        keep_inputs(j + 2)
                    dve.wait_ge(M["turned"], j + 1)
                    if j >= 2:
                        dve.wait_ge(M["y_ready"], j - 1)
                    nc.vector.tensor_copy(hidT[:, j % 2].rearrange("p (n f) c -> p n (f c)", n=2),
                                          t_ps[:, :, 0:3 * P]).then_inc(M["turned_kept"], 1)


def switch_routing(nc, sem, make_sb, make_ps, XT, router, router_loaded, ones, share, place, expert):
    with ExitStack() as ctx:
        sb, ps = make_sb(ctx), make_ps(ctx)
        logit = sb("s_logit", [P, NT, E])
        top = sb("s_top", [P, NT])
        shifted = sb("s_shifted", [P, NT, E])
        index = sb("s_index", [P, E])
        key = sb("s_key", [P, NT, E])
        first = sb("s_first", [P, NT])
        chosen = sb("s_chosen", [P, NT, E])
        ex, exsum = sb("s_exp", [P, NT, E]), sb("s_expsum", [P, NT])
        upto = sb("s_upto", [P, P])
        prior = sb("s_prior", [P, 2, NT, E])
        per_tile = sb("s_per_tile", [P, NT, E])
        count = sb("s_count", [P, E])
        edges = sb("s_edges", [P, E, NT])
        over = sb("s_over", [P, E, NT])
        ends = sb("s_ends", [P, 2, E])
        tiles = sb("s_tiles", [P, E])
        start = sb("s_start", [P, E])
        where = sb("s_where", [P, NT, E])
        where_sum = sb("s_where_sum", [P, NT])
        number = sb("s_number", [1, SPARE, E])
        passed = sb("s_passed", [1, SPARE, E])
        number_sum = sb("s_number_sum", [1, SPARE])
        l_ps, c_ps, t_ps = ps("s_l", [P, 512]), ps("s_c", [P, 512]), ps("s_t", [P, 512])
        const, l_ready, step, chosen_ready = sem("s_const"), sem("s_l_ready"), sem("s_step"), sem("s_chosen_ready")
        shifted_ready, exp_ready, t_ready, c_ready = sem("s_shifted_ready"), sem("s_exp_ready"), sem("s_t_ready"), sem("s_c_ready")
        with nc.Block() as block:
            @block.gpsimd
            def _(pool):
                def table(x, pattern, base):
                    nc.gpsimd.iota(x[:], pattern=pattern, base=base, channel_multiplier=0,
                                   allow_small_or_imprecise_dtypes=True).then_inc(const, 1)

                table(index, [[1, E]], -E)
                table(edges, [[0, E], [P, NT]], 0)
                table(number, [[1, SPARE], [0, E]], 0)
                nc.gpsimd.memset(upto[:], 1.0).then_inc(const, 1)
                pool.wait_ge(const, 4)
                nc.gpsimd.affine_select(out=upto[:], in_=upto[:], compare_op=ALU.is_ge, fill=0.0, base=0,
                                        pattern=[[1, P]], channel_multiplier=-1).then_inc(const, 1)

            @block.tensor
            def _(pe):
                pe.wait_ge(router_loaded, 16)
                for t in range(NT):
                    n, c = tokens_of(t)
                    for h in range(2):
                        last = nc.tensor.matmul(l_ps[0:n, t * E:(t + 1) * E], XT[:, h, c:c + n], router[:, h, :],
                                                start=(h == 0), stop=(h == 1))
                last.then_inc(l_ready, 1)
                pe.wait_ge(chosen_ready, 1)
                pe.wait_ge(const, 5)
                flat = chosen[:].rearrange("p t e -> p (t e)")
                nc.tensor.matmul(t_ps[:, 0:NT * E], ones[:], flat, start=True, stop=True).then_inc(t_ready, 1)
                nc.tensor.matmul(c_ps[:, 0:NT * E], upto[:], flat, start=True, stop=True).then_inc(c_ready, 1)

            @block.scalar
            def _(act):
                act.wait_ge(shifted_ready, 1)
                nc.scalar.activation(ex[:], shifted[:], ACT.Exp).then_inc(exp_ready, 1)

            @block.vector
            def _(dve):
                steps = Tally(step)

                def then(ins):
                    dve.wait_ge(step, steps.mark(ins))

                then(nc.vector.memset(logit[:, CLS, :], 0.0))
                dve.wait_ge(l_ready, 1)
                nc.vector.tensor_copy(logit[:, 0:CLS, :], l_ps[:, 0:CLS * E].rearrange("p (t e) -> p t e", e=E))
                then(nc.vector.tensor_copy(logit[0:B, CLS, :], l_ps[0:B, CLS * E:NT * E]))
                then(nc.vector.reduce_max(top[:], logit[:], AX_X))
                top_b = top[:].unsqueeze(2).broadcast_to((P, NT, E))
                nc.vector.tensor_tensor(shifted[:], logit[:], top_b, ALU.subtract).then_inc(shifted_ready, 1)
                dve.wait_ge(const, 5)
                dve.wait_ge(shifted_ready, 1)
                index_b = index[:].unsqueeze(1).broadcast_to((P, NT, E))
                then(nc.vector.tensor_scalar(key[:], shifted[:], 0.0, None, ALU.is_equal))
                then(nc.vector.tensor_tensor(key[:], key[:], index_b, ALU.mult))
                then(nc.vector.tensor_reduce(first[:], key[:], AX_X, ALU.min))
                then(nc.vector.memset(chosen[:, CLS, :], 0.0))
                nc.vector.tensor_tensor(chosen[:, 0:CLS, :], index[:].unsqueeze(1).broadcast_to((P, CLS, E)),
                                        first[:, 0:CLS].unsqueeze(2).broadcast_to((P, CLS, E)), ALU.is_equal)
                nc.vector.tensor_scalar(chosen[0:B, CLS, :], index[0:B, :], first[0:B, CLS:NT], None,
                                        ALU.is_equal).then_inc(chosen_ready, 1)
                dve.wait_ge(exp_ready, 1)
                then(nc.vector.reduce_sum(exsum[:], ex[:], AX_X))
                nc.vector.reciprocal(share[:], exsum[:])
                dve.wait_ge(t_ready, 1)
                nc.vector.memset(prior[:, 0, 0, :], 0.0)
                nc.vector.tensor_copy(per_tile[:].rearrange("p t e -> p (t e)"), t_ps[:, 0:NT * E])
                then(nc.vector.tensor_copy(prior[:, 0, 1:NT, :].rearrange("p t e -> p (t e)"), t_ps[:, 0:(NT - 1) * E]))
                side = 0
                for gap in (1, 2, 4, 8, 16):
                    nc.vector.tensor_copy(prior[:, 1 - side, 0:gap, :], prior[:, side, 0:gap, :])
                    then(nc.vector.tensor_tensor(prior[:, 1 - side, gap:NT, :], prior[:, side, gap:NT, :],
                                                 prior[:, side, 0:NT - gap, :], ALU.add))
                    side = 1 - side
                then(nc.vector.tensor_tensor(count[:], prior[:, side, CLS, :], per_tile[:, CLS, :], ALU.add))
                then(nc.vector.tensor_tensor(over[:], count[:].unsqueeze(2).broadcast_to((P, E, NT)), edges[:], ALU.is_gt))
                then(nc.vector.reduce_sum(tiles[:], over[:], AX_X))
                then(nc.vector.tensor_copy(ends[:, 0, :], tiles[:]))
                end = 0
                for gap in (1, 2, 4):
                    nc.vector.tensor_copy(ends[:, 1 - end, 0:gap], ends[:, end, 0:gap])
                    then(nc.vector.tensor_tensor(ends[:, 1 - end, gap:E], ends[:, end, gap:E], ends[:, end, 0:E - gap], ALU.add))
                    end = 1 - end
                then(nc.vector.tensor_tensor(start[:], ends[:, end, :], tiles[:], ALU.subtract))
                then(nc.vector.tensor_scalar(start[:], start[:], float(P), -1.0, ALU.mult, ALU.add))
                then(nc.vector.tensor_tensor(passed[:], number[:], ends[0:1, end, :].unsqueeze(1).broadcast_to((1, SPARE, E)),
                                             ALU.is_ge))
                then(nc.vector.reduce_sum(number_sum[:], passed[:], AX_X))
                nc.vector.tensor_scalar(expert[:], number_sum[:], float(E - 1), None, ALU.min)
                dve.wait_ge(c_ready, 1)
                then(nc.vector.tensor_tensor(where[:].rearrange("p t e -> p (t e)"), c_ps[:, 0:NT * E],
                                             prior[:, side].rearrange("p t e -> p (t e)"), ALU.add))
                then(nc.vector.tensor_tensor(where[:], where[:], start[:].unsqueeze(1).broadcast_to((P, NT, E)), ALU.add))
                then(nc.vector.tensor_tensor(where[:], where[:], chosen[:], ALU.mult))
                then(nc.vector.reduce_sum(where_sum[:], where[:], AX_X))
                nc.vector.tensor_copy(place[:], where_sum[:])



_INS = ['x', 'cls_tok', 'L0_tok_freq_bands', 'L0_tok_W', 'L0_attn_w_qkv', 'L0_attn_w_proj', 'L0_attn_b_proj',
        'L0_ffn_g1', 'L0_ffn_b1', 'L0_ffn_g2', 'L0_ffn_b2', 'L0_ffn_Wr', 'L0_ffn_br', 'L0_ffn_Wq', 'L0_ffn_bq',
        'L0_ffn_Wk', 'L0_ffn_bk', 'L0_ffn_Wv', 'L0_ffn_bv', 'L0_ffn_Wo', 'L0_ffn_bo', 'L0_ffn_Wm', 'L0_ffn_bm',
        'L0_ffn_W1', 'L0_ffn_bf1', 'L0_ffn_W2', 'L0_ffn_bf2', 'L1_attn_Wq', 'L1_attn_Wk', 'L1_attn_Wv', 'L1_attn_Wg',
        'L1_attn_Wo', 'L1_attn_gn_weight', 'L1_attn_gn_bias', 'L1_ffn_router_w', 'L1_ffn_wi', 'L1_ffn_wo']
DEBUG = ()


def kernel(**inputs):
    import concourse.bacc as _bacc
    from concourse.bass_utils import run_bass_kernel_spmd as _run

    nc = _bacc.Bacc("TRN2", target_bir_lowering=False, num_devices=1)
    arrays, A = {}, {}
    tables = dict(zip(("rot", "query_decay", "key_decay"), retention_tables()))
    for name in _INS + list(tables):
        a = np.ascontiguousarray(inputs[name] if name in _INS else tables[name])
        if a.ndim == 0:
            a = a.reshape(1)
        arrays[f"in_{name}"] = a
        A[name] = nc.dram_tensor(f"in_{name}", a.shape, mybir.dt.from_np(a.dtype), kind="ExternalInput").ap()
    out = nc.dram_tensor("out", (B, N, D), F32, kind="ExternalOutput").ap()
    dbg = {n: nc.dram_tensor("dbg_" + n, (P, NT, D), F32, kind="ExternalOutput").ap() for n in DEBUG}
    build_program(nc, A, out, dbg)
    r = _run(nc, [arrays], core_ids=[0])
    return r.results[0]["out"]
```

```python
from contextlib import ExitStack

import numpy as np

import concourse.bass as bass
from concourse import mybir

F32 = mybir.dt.float32
I32, U32 = mybir.dt.int32, mybir.dt.uint32
ALU = mybir.AluOpType
ACT = mybir.ActivationFunctionType
AX_X = mybir.AxisListType.X

B, C, T, D = 4, 3, 512, 192
N = T + 1
P = 128
TPB = T // P
NT = B * TPB + 1
CLS = B * TPB
NTOK = B * N
HALF = 96
NP = 514
BANDS = 6
JT = C * D
LN_EPS = 1e-5
ZERO_ROWS = 3

HEADS, HD = 12, 16
HG = 4
GROUPS = HEADS // HG
R = P // HG
CH = T // R + 1
ITERS = 10
SLOTS = 2
BPS = B // SLOTS
INV_REG = 10.0

TWO_PI_BELOW = 6.283185
ROUND = 1.5 * 2.0 ** 23


class Tally:

    def __init__(self, sem):
        self.sem, self.n = sem, 0

    def mark(self, ins):
        ins.then_inc(self.sem, 1)
        self.n += 1
        return self.n


def later(i):
    return not isinstance(i, int) or i > 0


def build_program(nc, A, out):
    root = ExitStack()
    with root:
        taken = []

        def sem(name):
            s = nc.alloc_semaphore(name)
            taken.append(s)
            return s

        def recycle():
            with nc.Block() as block:
                @block.sync
                def _(sp):
                    for s in taken:
                        sp.sem_clear(s)
            for s in taken:
                nc.release_semaphore(s)
            taken.clear()

        def make_sb(ctx):
            return lambda name, shape, dt=F32: ctx.enter_context(nc.sbuf_tensor(name, shape, dt))

        def make_ps(ctx):
            return lambda name, shape: ctx.enter_context(nc.psum_tensor(name, shape, F32))

        rsb = make_sb(root)
        H = rsb("H", [P, NT, D])
        ident = rsb("ident", [P, P])
        ones = rsb("ones", [P, P])
        zeros = rsb("zeros", [P, ZERO_ROWS, D])

        constants_stage(nc, sem, H, ident, ones, zeros)
        tokenizer_stage(nc, sem, make_sb, make_ps, A, H, ident)
        with ExitStack() as attn:
            asb = make_sb(attn)
            WprojT = asb("WprojT", [P, GROUPS, D])
            QT = asb("QT", [P, B * GROUPS, NP])
            V = asb("V", [P, SLOTS, TPB, BPS * D])
            VC = asb("VC", [1, SLOTS, BPS * D])
            with ExitStack() as x_ctx:
                xsb = make_sb(x_ctx)
                WqkvT = xsb("WqkvT", [HALF, 2, 3 * D])
                XT = xsb("XT", [HALF, 2, NTOK])
                X = xsb("X", [P, NT, D])
                Wqkv = xsb("Wqkv", [HALF, 3 * D // HALF, D])
                Wproj = xsb("Wproj", [HALF, 2, D])
                norm_stage(nc, sem, make_sb, make_ps, "ln1", H, X, XT, ident, loads=[
                    (Wqkv[:], A["L0_attn_w_qkv"].rearrange("(k p) c -> p k c", p=HALF)),
                    (Wproj[:], A["L0_attn_w_proj"].rearrange("(k p) c -> p k c", p=HALF))])
                sinkhorn_weights_stage(nc, sem, make_ps, A, Wqkv, Wproj, WqkvT, WprojT, ident)
                sinkhorn_query_stage(nc, sem, make_sb, make_ps, XT, WqkvT, QT, V, VC, ident)
            sinkhorn_stage(nc, sem, make_sb, make_ps, QT, V, VC, ones)
            sinkhorn_out_stage(nc, sem, make_ps, QT, WprojT, H)
        recycle()
        routed_stage(nc, sem, make_sb, make_ps, A, H, ident, ones)
        recycle()
        retention_stage(nc, sem, make_sb, make_ps, A, H, ident, ones)
        recycle()
        moe_stage(nc, sem, make_sb, make_ps, A, H, ident, ones, zeros)
        final_stage(nc, sem, H, out)


def final_stage(nc, sem, H, out):
    stored = sem("out_stored")
    with nc.Block() as block:
        @block.sync
        def _(sp):
            for b in range(B):
                sp.dma_start(out[b, 1:N, :].rearrange("(t p) d -> p t d", p=P),
                             H[:, TPB * b:TPB * b + TPB, :]).then_inc(stored, 16)
            sp.dma_start(out[:, 0, :], H[0:B, CLS, :]).then_inc(stored, 16)
            sp.wait_ge(stored, 16 * (B + 1))


def constants_stage(nc, sem, H, ident, ones, zeros):
    filled = sem("const_filled")
    done = sem("const_done")
    with nc.Block() as block:
        @block.gpsimd
        def _(pool):
            nc.gpsimd.memset(ident[:], 0.0).then_inc(filled, 1)
            pool.wait_ge(filled, 1)
            nc.gpsimd.affine_select(out=ident[:], in_=ident[:], compare_op=ALU.not_equal, fill=1.0, base=0,
                                    pattern=[[-1, P]], channel_multiplier=1).then_inc(done, 1)

        @block.vector
        def _(dve):
            nc.vector.memset(ones[:], 1.0)
            nc.vector.memset(zeros[:], 0.0)
            nc.vector.memset(H[:, CLS, :], 0.0)


def tokenizer_stage(nc, sem, make_sb, make_ps, A, H, ident):
    ARGS = [(c, k) for c in range(4) for k in range(BANDS)] + [(4, m) for m in range(BANDS // 2)]
    NA, NU = len(ARGS), 2 * len(ARGS)
    FR, MR, XR = 6, 3, 4
    with ExitStack() as ctx:
        sb, ps = make_sb(ctx), make_ps(ctx)
        WT = sb("tok_WT", [P, NU, D])
        XN = sb("tok_x", [P, TPB, JT + 64])
        XJ = sb("tok_xj", [P, 5, T])
        band = sb("tok_band", [P, BANDS])
        pair = sb("tok_pair", [P, BANDS // 2])
        half_pi = sb("tok_half_pi", [P, 1])
        turns = sb("tok_turns", [P, XR, T])
        whole = sb("tok_whole", [P, 2, T])
        back = sb("tok_back", [P, MR, T])
        size = sb("tok_size", [P, 2, T])
        feat = sb("tok_feat", [P, FR, T])
        acc = ps("tok_acc", [P, TPB, 512])
        stage = ps("tok_stage", [P, 4, 512])
        w_loaded = [sem(f"tok_w_loaded{c}") for c in range(5)]
        x_loaded, small_loaded = sem("tok_x_loaded"), sem("tok_small_loaded")
        cls_loaded = sem("tok_cls_loaded")
        wt_turned, wt_kept_dve, wt_kept_act = sem("tok_wt_turned"), sem("tok_wt_kept_dve"), sem("tok_wt_kept_act")
        x_turned, x_kept = sem("tok_x_turned"), sem("tok_x_kept")
        turns_ready, whole_ready, back_ready = sem("tok_turns_ready"), sem("tok_whole_ready"), sem("tok_back_ready")
        size_ready = sem("tok_size_ready")
        feat_ready, feat_used = sem("tok_feat_ready"), sem("tok_feat_used")
        acc_kept = sem("tok_acc_kept")
        const_ready, paired = sem("tok_const_ready"), sem("tok_paired")

        x_dram = A["x"].rearrange("b c n d -> (b c n d)").rearrange("(b t p j) -> b p t j", b=B, t=TPB, p=P)
        f_dram = A["L0_tok_freq_bands"].rearrange("(a s) -> a s", a=1)

        with ExitStack() as w_ctx:
            WN = make_sb(w_ctx)("tok_WN", [HALF, 2, JT * 2 * BANDS])
            WP = make_sb(w_ctx)("tok_WP", [HALF, 2, 2 * BANDS, 64])
            W_s = WN[:].rearrange("p h (j s) -> p h j s", s=2 * BANDS)
            w_paired = sem("tok_w_paired")
            w_dram = A["L0_tok_W"].rearrange("(h p) f -> p h f", p=HALF)
            with nc.Block() as block:
                @block.sync
                def _(sp):
                    for c in range(5):
                        a, z = c * P * 2 * BANDS, min(JT, (c + 1) * P) * 2 * BANDS
                        sp.dma_start(WN[:, :, a:z], w_dram[:, :, a:z]).then_inc(w_loaded[c], 16)

                @block.tensor
                def _(pe):
                    for a, (c, k) in enumerate(ARGS):
                        if c == 4:
                            pe.wait_ge(w_paired, 2)
                        elif a % BANDS == 0:
                            pe.wait_ge(w_loaded[c], 16)
                        if a >= 4:
                            pe.wait_ge(*((wt_kept_dve, (a - 4) // 2 + 1) if a % 2 == 0 else (wt_kept_act, (a - 5) // 2 + 1)))
                        for trig in range(2):
                            for h in range(2):
                                if c < 4:
                                    src = W_s[:, h, c * P:(c + 1) * P, trig * BANDS + k]
                                else:
                                    s = trig * BANDS + 2 * k
                                    src = WP[:, h, s:s + 2, :].rearrange("p s j -> p (s j)")
                                o = trig * D + h * HALF
                                last = nc.tensor.transpose(stage[:, a % 4, o:o + HALF], src, ident[0:HALF, 0:HALF])
                        last.then_inc(wt_turned, 1)

                @block.gpsimd
                def _(pool):
                    pool.wait_ge(w_loaded[4], 16)
                    for h in range(2):
                        nc.gpsimd.tensor_copy(WP[:, h, :, :],
                                              W_s[:, h, 4 * P:JT, :].rearrange("p j s -> p s j")).then_inc(w_paired, 1)

                @block.vector
                def _(dve):
                    nc.vector.memset(half_pi[:], float(np.pi / 2)).then_inc(const_ready, 1)
                    for a in range(0, NA, 2):
                        dve.wait_ge(wt_turned, a + 1)
                        nc.vector.tensor_copy(WT[:, 2 * a:2 * a + 2, :], stage[:, a % 4, 0:2 * D].rearrange(
                            "p (u o) -> p u o", u=2)).then_inc(wt_kept_dve, 1)

                @block.scalar
                def _(act):
                    for a in range(1, NA, 2):
                        act.wait_ge(wt_turned, a + 1)
                        nc.scalar.activation(WT[:, 2 * a:2 * a + 2, :], stage[:, a % 4, 0:2 * D].rearrange(
                            "p (u o) -> p u o", u=2), ACT.Copy).then_inc(wt_kept_act, 1)

        with nc.Block() as block:
            @block.sync
            def _(sp):
                sp.dma_start(band[:], f_dram[0].partition_broadcast(P)).then_inc(small_loaded, 16)
                for b in range(B):
                    sp.dma_start(H[b:b + 1, CLS, :], A["cls_tok"][0]).then_inc(cls_loaded, 16)

                def load_x(b):
                    if later(b):
                        sp.wait_ge(x_turned, 5 * b)
                    sp.dma_start(XN[:, :, 0:JT], x_dram[b]).then_inc(x_loaded, 16)
                    sp.dma_start(XN[:, :, JT:JT + 64], x_dram[b, :, :, JT - 64:JT]).then_inc(x_loaded, 16)

                load_x(0)
                with sp.Fori(1, B) as b:
                    load_x(b)
                sp.wait_ge(cls_loaded, 16 * B)

            @block.tensor
            def _(pe):
                def turn(b, first, end):
                    for c in range(first, end):
                        if c == 0:
                            pe.wait_ge(x_loaded, 32 * b + 32)
                            if later(b):
                                pe.wait_ge(x_kept, 5 * b)
                        if c == 4:
                            pe.wait_ge(x_kept, 5 * b + 1)
                        for t in range(TPB):
                            last = nc.tensor.transpose(stage[:, c % 4, t * P:(t + 1) * P],
                                                       XN[:, t, c * P:(c + 1) * P], ident[:])
                        last.then_inc(x_turned, 1)

                def batch(b, more):
                    turn(b, 4, 5)
                    for u in range(NU):
                        if u == NU - 6 and more:
                            turn(b + 1, 0, 4)
                        if u == 0 and later(b):
                            pe.wait_ge(acc_kept, TPB * b)
                        pe.wait_ge(feat_ready, NU * b + u + 1)
                        for t in range(TPB):
                            last = nc.tensor.matmul(acc[:, t, 0:D], feat[:, u % FR, t * P:(t + 1) * P], WT[:, u, :],
                                                    start=(u == 0), stop=(u == NU - 1))
                        last.then_inc(feat_used, 1)

                turn(0, 0, 4)
                batch(0, True)
                with pe.Fori(1, B - 1) as b:
                    batch(b, True)
                batch(B - 1, False)

            @block.gpsimd
            def _(pool):
                pool.wait_ge(small_loaded, 16)
                for k in range(2):
                    nc.gpsimd.tensor_copy(pair[64 * k:64 * k + 64, :], band[64 * k:64 * k + 64, k:BANDS:2]).then_inc(paired, 1)
                pool.wait_ge(paired, 2)
                with pool.Fori(0, B) as b:
                    for a, (c, k) in enumerate(ARGS):
                        if a % BANDS == 0:
                            pool.wait_ge(x_kept, 5 * b + c + 1)
                        if a >= XR:
                            pool.wait_ge(back_ready, NA * b + a - XR + 1)
                        f = band[:, k:k + 1] if c < 4 else pair[:, k:k + 1]
                        nc.gpsimd.tensor_tensor(turns[:, a % XR, :], XJ[:, c, :], f.broadcast_to((P, T)),
                                                ALU.mult).then_inc(turns_ready, 1)

            @block.vector
            def _(dve):
                def batch(b):
                    for c in range(4):
                        keep_x(b, c)
                    for a in range(NA):
                        if a == 4 * BANDS:
                            keep_x(b, 4)
                        dve.wait_ge(turns_ready, NA * b + a + 1)
                        nc.vector.tensor_scalar(whole[:, a % 2, :], turns[:, a % XR, :], ROUND, None,
                                                ALU.add).then_inc(whole_ready, 1)
                        if a >= MR:
                            dve.wait_ge(feat_ready, NU * b + 2 * (a - MR) + 1)
                            dve.wait_ge(size_ready, NA * b + a - MR + 1)
                        elif later(b):
                            dve.wait_ge(feat_ready, NU * b)
                        dve.wait_ge(whole_ready, NA * b + a + 1)
                        nc.vector.scalar_tensor_tensor(out=back[:, a % MR, :], in0=whole[:, a % 2, :], scalar=-ROUND,
                                                       in1=turns[:, a % XR, :], op0=ALU.add,
                                                       op1=ALU.subtract).then_inc(back_ready, 1)

                def keep_x(b, c):
                    if c == 0 and later(b):
                        dve.wait_ge(turns_ready, NA * b)
                    dve.wait_ge(x_turned, 5 * b + c + 1)
                    nc.vector.tensor_copy(XJ[:, c, :], stage[:, c % 4, :]).then_inc(x_kept, 1)

                batch(0)
                with dve.Fori(1, B) as b:
                    batch(b)

            @block.scalar
            def _(act):
                nc.scalar.preload_act_table_set("trig_and_small")
                def batch(b):
                    for a in range(NA):
                        act.wait_ge(back_ready, NA * b + a + 1)
                        for trig in range(2):
                            u = 2 * a + trig
                            if trig == 1:
                                act.wait_ge(size_ready, NA * b + a + 1)
                            if u >= FR:
                                act.wait_ge(feat_used, NU * b + u - FR + 1)
                            elif later(b):
                                act.wait_ge(feat_used, NU * b)
                            if trig == 0:
                                nc.scalar.activation(feat[:, u % FR, :], back[:, a % MR, :], ACT.Sin,
                                                     scale=-TWO_PI_BELOW).then_inc(feat_ready, 1)
                                nc.scalar.activation(size[:, a % 2, :], back[:, a % MR, :],
                                                     ACT.Abs).then_inc(size_ready, 1)
                            else:
                                nc.scalar.activation(feat[:, u % FR, :], size[:, a % 2, :], ACT.Sin,
                                                     bias=half_pi[:], scale=-TWO_PI_BELOW).then_inc(feat_ready, 1)
                    act.wait_ge(feat_used, NU * b + NU)
                    act.wait_ge(cls_loaded, 16 * B)
                    for t in range(TPB):
                        nc.scalar.activation(H[:, TPB * b + t, :], acc[:, t, 0:D], ACT.Copy).then_inc(acc_kept, 1)

                batch(0)
                with act.Fori(1, B) as b:
                    batch(b)


def norm_stage(nc, sem, make_sb, make_ps, name, src, dst, dstT, ident, inner=None, gain=None, shift=None, loads=(),
               start=None):
    with ExitStack() as ctx:
        sb, ps = make_sb(ctx), make_ps(ctx)
        stats = sb(name + "_stats", [P, NT, 6])
        moments = sb(name + "_moments", [P, NT, 2])
        power = sb(name + "_power", [P, NT])
        rstd = sb(name + "_rstd", [P, NT])
        turn = ps(name + "_turn", [P, 4, 512])
        stats_ready, moments_ready = sem(name + "_stats_ready"), sem(name + "_moments_ready")
        pool_done, rstd_ready = sem(name + "_pool_done"), sem(name + "_rstd_ready")
        normed, affine_done = [sem(name + "_normed0"), sem(name + "_normed1")], [sem(name + "_affine0"), sem(name + "_affine1")]
        turned, bias_ready = sem(name + "_turned"), sem(name + "_bias_ready")
        nmr = sb(name + "_nmr", [P, NT])
        EVEN, ODD = (NT + 1) // 2, NT // 2
        kept_dve, kept_act = sem(name + "_kept_dve"), sem(name + "_kept_act")
        loaded = sem(name + "_loaded")
        rounds = [(src, inner), (inner, dst)] if inner is not None else [(src, dst)]

        with nc.Block() as block:
            @block.sync
            def _(sp):
                if start is not None:
                    start(sp)
                for to, source in loads:
                    sp.dma_start(to, source).then_inc(loaded, 16)
                if loads:
                    sp.wait_ge(loaded, 16 * len(loads))

            @block.vector
            def _(dve):
                for r, (a, z) in enumerate(rounds):
                    for t in range(NT):
                        if r:
                            dve.wait_ge(normed[t % 2], t // 2 + 1)
                        nc.vector.bn_stats(stats[:, t, :], a[:, t, :]).then_inc(stats_ready, 1)
                    for t in range(NT):
                        dve.wait_ge(stats_ready, NT * r + t + 1)
                        nc.vector.bn_aggr(moments[:, t, :], stats[:, t, :]).then_inc(moments_ready, 1)
                    dve.wait_ge(moments_ready, NT * (r + 1))
                    dve.wait_ge(rstd_ready, r + 1)
                    nc.vector.scalar_tensor_tensor(out=nmr[:], in0=moments[:, :, 0], scalar=-1.0, in1=rstd[:], op0=ALU.mult,
                                                   op1=ALU.mult).then_inc(bias_ready, 1)
                    for t in range(0, NT, 2):
                        nc.vector.tensor_scalar(z[:, t, :], a[:, t, :], moments[:, t, 0:1], rstd[:, t:t + 1],
                                                ALU.subtract, ALU.mult).then_inc(normed[0], 1)
                if gain is not None:
                    if loads:
                        dve.wait_ge(loaded, 16 * len(loads))
                    for t in range(0, NT, 2):
                        dve.wait_ge(normed[0], EVEN * (len(rounds) - 1) + t // 2 + 1)
                        nc.vector.tensor_tensor(dst[:, t, :], dst[:, t, :], gain[:], ALU.mult).then_inc(affine_done[0], 1)
                        if t:
                            dve.wait_ge(affine_done[0], t - 1)
                            nc.vector.tensor_tensor(dst[:, t - 2, :], dst[:, t - 2, :], shift[:],
                                                    ALU.add).then_inc(affine_done[0], 1)
                    dve.wait_ge(affine_done[0], 2 * EVEN - 1)
                    nc.vector.tensor_tensor(dst[:, NT - 1, :], dst[:, NT - 1, :], shift[:], ALU.add).then_inc(affine_done[0], 1)
                for t in range(NT):
                    n = P if t < CLS else B
                    dve.wait_ge(turned, 2 * t + 1)
                    nc.vector.tensor_copy(dstT[:, 0, t * P:t * P + n], turn[0:HALF, (2 * t) % 4, 0:n]).then_inc(kept_dve, 1)

            @block.gpsimd
            def _(pool):
                nc.gpsimd.memset(power[:], -0.5).then_inc(pool_done, 1)
                for r in range(len(rounds)):
                    pool.wait_ge(moments_ready, NT * (r + 1))
                    pool.wait_ge(pool_done, r + 1)
                    nc.gpsimd.tensor_scalar(rstd[:], moments[:, :, 1], LN_EPS, None, ALU.add).then_inc(pool_done, 1)
                    pool.wait_ge(pool_done, r + 2)
                    nc.gpsimd.tensor_tensor(rstd[:], rstd[:], power[:], ALU.pow).then_inc(rstd_ready, 1)
                if gain is not None:
                    if loads:
                        pool.wait_ge(loaded, 16 * len(loads))
                    for t in range(1, NT, 2):
                        pool.wait_ge(normed[1], ODD * (len(rounds) - 1) + t // 2 + 1)
                        nc.gpsimd.tensor_tensor(dst[:, t, :], dst[:, t, :], gain[:], ALU.mult).then_inc(affine_done[1], 1)
                        pool.wait_ge(affine_done[1], t)
                        nc.gpsimd.tensor_tensor(dst[:, t, :], dst[:, t, :], shift[:], ALU.add).then_inc(affine_done[1], 1)

            @block.tensor
            def _(pe):
                for t in range(NT):
                    n = P if t < CLS else B
                    if gain is None:
                        pe.wait_ge(normed[t % 2], (ODD if t % 2 else EVEN) * (len(rounds) - 1) + t // 2 + 1)
                    elif t % 2:
                        pe.wait_ge(affine_done[1], t + 1)
                    else:
                        pe.wait_ge(affine_done[0], min(t + 3, 2 * EVEN))
                    for h in range(2):
                        if t >= 2:
                            pe.wait_ge(kept_dve if h == 0 else kept_act, t - 1)
                        nc.tensor.transpose(turn[0:HALF, (2 * t + h) % 4, 0:n], dst[0:n, t, h * HALF:(h + 1) * HALF],
                                            ident[0:n, 0:n]).then_inc(turned, 1)

            @block.scalar
            def _(act):
                for r, (a, z) in enumerate(rounds):
                    act.wait_ge(bias_ready, r + 1)
                    for t in range(1, NT, 2):
                        nc.scalar.activation(z[:, t, :], a[:, t, :], ACT.Identity, bias=nmr[:, t:t + 1],
                                             scale=rstd[:, t:t + 1]).then_inc(normed[1], 1)
                for t in range(NT):
                    n = P if t < CLS else B
                    act.wait_ge(turned, 2 * t + 2)
                    nc.scalar.activation(dstT[:, 1, t * P:t * P + n], turn[0:HALF, (2 * t + 1) % 4, 0:n],
                                         ACT.Copy).then_inc(kept_act, 1)


def sinkhorn_weights_stage(nc, sem, make_ps, A, qkv, proj, WqkvT, WprojT, ident):
    NB = 3 * D // HALF
    with ExitStack() as ctx:
        turn = make_ps(ctx)("skw_turn", [P, 8, 512])
        turned = sem("skw_turned")
        zeroed, bias_loaded = sem("skw_zeroed"), sem("skw_bias_loaded")
        with nc.Block() as block:
            @block.sync
            def _(sp):
                sp.wait_ge(zeroed, 1)
                sp.dma_start(WprojT[64:65, 0, :], A["L0_attn_b_proj"].rearrange("(a c) -> a c", a=1)).then_inc(bias_loaded, 16)
                sp.wait_ge(bias_loaded, 16)

            @block.tensor
            def _(pe):
                for h in range(2):
                    for k in range(NB):
                        last = nc.tensor.transpose(turn[0:HALF, 3 * h + k // 2, (k % 2) * HALF:(k % 2 + 1) * HALF],
                                                   qkv[:, k, h * HALF:(h + 1) * HALF], ident[0:HALF, 0:HALF])
                last.then_inc(turned, 1)
                for g in range(GROUPS):
                    for k in range(2):
                        o = g * D + k * HALF
                        bank, o = (6, o) if g < 2 else (7, k * HALF)
                        last = nc.tensor.transpose(turn[0:64, bank, o:o + HALF], proj[:, k, 64 * g:64 * g + 64],
                                                   ident[0:HALF, 0:HALF])
                last.then_inc(turned, 1)

            @block.vector
            def _(dve):
                nc.vector.memset(WprojT[64:P, :, :], 0.0).then_inc(zeroed, 1)
                dve.wait_ge(turned, 2)
                for h in range(2):
                    nc.vector.tensor_copy(WqkvT[:, h, :].rearrange("p (a o) -> p a o", a=3),
                                          turn[0:HALF, 3 * h:3 * h + 3, 0:D])
                nc.vector.tensor_copy(WprojT[0:64, 0:2, :], turn[0:64, 6, 0:2 * D].rearrange("p (g o) -> p g o", g=2))
                nc.vector.tensor_copy(WprojT[0:64, 2, :], turn[0:64, 7, 0:D])


def sinkhorn_query_stage(nc, sem, make_sb, make_ps, XT, WqkvT, QT, V, VC, ident):
    with ExitStack() as ctx:
        sb, ps = make_sb(ctx), make_ps(ctx)
        Q = sb("skq_q", [P, NT, D])
        square = sb("skq_square", [P, 2, D])
        norm = sb("skq_norm", [P, NT * HEADS])
        logs = sb("skq_logs", [P, NT * HEADS])
        root = sb("skq_root", [P, NT * HEADS])
        scale = sb("skq_scale", [P, NT * HEADS])
        qp = ps("skq_qp", [P, 2, 512])
        turn = ps("skq_turn", [P, 6, 512])
        q_ready, q_kept, sq_ready, n2_ready = sem("skq_q_ready"), sem("skq_q_kept"), sem("skq_sq_ready"), sem("skq_n2_ready")
        zeroed, bias_row, step, root_ready = sem("skq_zeroed"), sem("skq_bias_row"), sem("skq_step"), sem("skq_root_ready")
        v_ready, v_kept = sem("skq_v_ready"), sem("skq_v_kept")
        q_normed, turned, kept = sem("skq_q_normed"), sem("skq_turned"), sem("skq_kept")
        with nc.Block() as block:
            @block.tensor
            def _(pe):
                for t in range(NT):
                    n = P if t < CLS else B
                    if t >= 2:
                        pe.wait_ge(q_kept, t - 1)
                    for h in range(2):
                        last = nc.tensor.matmul(qp[0:n, t % 2, 0:D], XT[:, h, t * P:t * P + n], WqkvT[:, h, 0:D],
                                                start=(h == 0), stop=(h == 1))
                    last.then_inc(q_ready, 1)
                pe.wait_ge(q_kept, NT)
                for t in range(CLS + B):
                    n, first = (P, t * P) if t < CLS else (1, t - CLS + B * T)
                    if t >= 2:
                        pe.wait_ge(v_kept, t - 1)
                    for h in range(2):
                        last = nc.tensor.matmul(qp[0:n, t % 2, 0:D], XT[:, h, first:first + n], WqkvT[:, h, 2 * D:3 * D],
                                                start=(h == 0), stop=(h == 1))
                    last.then_inc(v_ready, 1)
                for t in range(NT):
                    n = P if t < CLS else B
                    pe.wait_ge(q_normed, 1)
                    if t >= 2:
                        pe.wait_ge(kept, t - 1)
                    for g in range(GROUPS):
                        last = nc.tensor.transpose(turn[0:64, t % 2, g * P:g * P + n], Q[0:n, t, 64 * g:64 * g + 64],
                                                   ident[0:n, 0:n])
                    last.then_inc(turned, 1)

            @block.scalar
            def _(act):
                nc.scalar.preload_act_table_set("natural_log_exp_and_others")
                for t in range(NT):
                    n = P if t < CLS else B
                    act.wait_ge(q_ready, t + 1)
                    if t == CLS:
                        act.wait_ge(zeroed, 1)
                    nc.scalar.activation(Q[0:n, t, :], qp[0:n, t % 2, 0:D], ACT.Copy).then_inc(q_kept, 1)

                def roots():
                    act.wait_ge(step, 1)
                    nc.scalar.activation(logs[:], norm[:], ACT.Ln).then_inc(root_ready, 1)
                    act.wait_ge(root_ready, 1)
                    nc.scalar.activation(root[:], logs[:], ACT.Exp, scale=0.5).then_inc(root_ready, 1)

                for t in range(CLS + B):
                    act.wait_ge(v_ready, t + 1)
                    n = P if t < CLS else 1
                    b = t // TPB if t < CLS else t - CLS
                    cols = slice(b % BPS * D, (b % BPS + 1) * D)
                    dst = V[:, b // BPS, t % TPB, cols] if t < CLS else VC[:, b // BPS, cols]
                    nc.scalar.activation(dst, qp[0:n, t % 2, 0:D], ACT.Copy).then_inc(v_kept, 1)
                    if t == 4:
                        roots()

            @block.vector
            def _(dve):
                nc.vector.memset(Q[:, CLS, :], 0.0).then_inc(zeroed, 1)
                for t in range(NT):
                    dve.wait_ge(q_kept, t + 1)
                    nc.vector.tensor_tensor(square[:, t % 2, :], Q[:, t, :], Q[:, t, :], ALU.mult).then_inc(sq_ready, 1)
                    dve.wait_ge(sq_ready, t + 1)
                    nc.vector.reduce_sum(norm[:, t * HEADS:(t + 1) * HEADS],
                                         square[:, t % 2, :].rearrange("p (h d) -> p h d", d=HD), AX_X).then_inc(n2_ready, 1)
                steps = Tally(step)

                def then(ins):
                    dve.wait_ge(step, steps.mark(ins))

                dve.wait_ge(n2_ready, NT)
                then(nc.vector.tensor_scalar(norm[:], norm[:], 1e-30, None, ALU.max))
                dve.wait_ge(root_ready, 2)
                then(nc.vector.reciprocal(scale[:], root[:]))
                then(nc.vector.tensor_tensor(scale[:], scale[:], norm[:], ALU.mult))
                then(nc.vector.tensor_tensor(root[:], root[:], scale[:], ALU.add))
                then(nc.vector.tensor_scalar(root[:], root[:], 0.5, 1e-8, ALU.mult, ALU.add))
                then(nc.vector.reciprocal(scale[:], root[:]))
                q_all = Q[:].rearrange("p t (h d) -> p (t h) d", d=HD)
                nc.vector.tensor_tensor(q_all, q_all, scale[:].unsqueeze(2).broadcast_to((P, NT * HEADS, HD)),
                                        ALU.mult).then_inc(q_normed, 1)
                for t in range(NT):
                    n = P if t < CLS else B
                    dve.wait_ge(turned, t + 1)
                    src = turn[0:64, t % 2, 0:GROUPS * P].rearrange("p (g n) -> p g n", g=GROUPS)[:, :, 0:n]
                    b, c = t // TPB, (t % TPB) * P
                    dst = (QT[0:64, b * GROUPS:(b + 1) * GROUPS, c:c + P] if t < CLS else
                           QT[0:64, :, T].rearrange("p (b g) -> p g b", g=GROUPS))
                    nc.vector.tensor_copy(dst, src).then_inc(kept, 1)

            @block.gpsimd
            def _(pool):
                nc.gpsimd.memset(QT[64:P, :, :], 0.0).then_inc(bias_row, 1)
                pool.wait_ge(bias_row, 1)
                nc.gpsimd.memset(QT[64:65, 0:B * GROUPS:GROUPS, :], 1.0).then_inc(bias_row, 1)


def sinkhorn_stage(nc, sem, make_sb, make_ps, QT, V, VC, ones):
    L = 255
    S = SLOTS
    HALVES = ((0, 512 - L), (512 - L, N))
    SCALE = float(HD) ** -0.5
    ROUNDS = BPS * GROUPS
    LEAD = 4
    PARTS = ((0, 2), (2, 5), (5, 9), (9, 13), (13, CH))
    NPART = len(PARTS)
    AFTER = (7, 9, 11, 13, 15)
    EARLY = 6
    JUNK = 3
    DVE_CONST = 10
    with ExitStack() as ctx:
        sb, ps = make_sb(ctx), make_ps(ctx)
        K = [sb(f"sk_K{s}", [P, CH, NP]) for s in range(S)]
        diag = [sb(f"sk_diag{s}", [P, CH, P]) for s in range(S)]
        row = sb("sk_row", [P, S, NP])
        logs = sb("sk_logs", [P, S, NP])
        junk = sb("sk_junk", [P, JUNK, NP])
        sums = sb("sk_sums", [P, S, CH])
        col = sb("sk_col", [P, S, CH])
        peak = sb("sk_peak", [P, S, CH])
        weight = sb("sk_weight", [P, S, CH])
        top = sb("sk_top", [P, 4])
        spread = sb("sk_spread", [P, 2, R])
        head_mask = sb("sk_head_mask", [P, HG])
        cls_head_mask = sb("sk_cls_head_mask", [P, HG])
        feat_mask = sb("sk_feat_mask", [64, HG])
        cls_mask = sb("sk_cls_mask", [P, 1])
        not_cls = sb("sk_not_cls", [P, 1])
        off_diag = sb("sk_off_diag", [P, R])
        on_diag = sb("sk_on_diag", [P, R])
        block_ones = sb("sk_block_ones", [P, P])
        first_sums = sb("sk_first_sums", [P, 2, CH])
        first_u = sb("sk_first_u", [P, S, CH * R])
        diag_gain = sb("sk_diag_gain", [P, R])
        cls_gain = sb("sk_cls_gain", [P, 1])
        shift = sb("sk_shift", [P, 2])
        QB = sb("sk_QB", [P, S, NP])
        QS = sb("sk_QS", [P, CH, P])
        VS = sb("sk_VS", [P, CH, P])
        den = sb("sk_den", [64, 2, NP])
        w_ps = ps("sk_w", [P, 2 * S, 512])
        e_ps = ps("sk_e", [P, 4, 512])

        def pair(x, k):
            return x[:, 2 * k:2 * k + 2, :].rearrange("p a n -> p (a n)")[:, L:L + N]

        def sems(name):
            return [sem(f"sk_{name}{s}") for s in range(S)]

        const_pool, const_dve = sem("sk_const_pool"), sem("sk_const_dve")
        slot_ready, dots_ready, k_ready, k_masked = sems("slot_ready"), sems("dots_ready"), sems("k_ready"), sems("k_masked")
        qs_ready = sem("sk_qs_ready")
        diag_ready, w_ready, logs_ready, row_ready = sems("diag_ready"), sems("w_ready"), sems("logs_ready"), sems("row_ready")
        sums_ready, col_ready = sems("sums_ready"), sems("col_ready")
        first_step, first_ready = sems("first_step"), sems("first_ready")
        top_step, weight_ready = sems("top_step"), sems("weight_ready")
        e_ready = sems("e_ready")
        vs_ready = sems("vs_ready")
        o_ready, den_log, den_ready, o_kept = sems("o_ready"), sems("den_log"), sems("den_ready"), sems("o_kept")

        def near_diagonal(s):
            flat = K[s][:].rearrange("p c n -> p (c n)")[:, 0:(CH - 1) * (NP + R)]
            return flat.rearrange("p (c n) -> p c n", n=NP + R)[:, :, 0:R]

        with nc.Block() as block:
            @block.gpsimd
            def _(pool):
                CONST = 2 + HG

                def queries(s, i):
                    if later(i):
                        pool.wait_ge(dots_ready[s], CH * i)
                        pool.wait_ge(const_pool, CONST)
                    nc.gpsimd.tensor_copy(QB[0:64, s, 0:N], QT[0:64, i + ROUNDS * s, 0:N]).then_inc(slot_ready[s], 1)
                    if later(i) or s:
                        pool.wait_ge(dots_ready[1 - s], CH * (i + s))
                    pool.wait_ge(slot_ready[s], i + 1)
                    q = QB[0:64, s, 0:T].rearrange("p (c r) -> p c r", r=R)
                    for k in range(HG):
                        nc.gpsimd.tensor_tensor(
                            QS[0:64, 0:CH - 1, k * R:(k + 1) * R], q,
                            feat_mask[:, k:k + 1].unsqueeze(1).broadcast_to((64, CH - 1, R)),
                            ALU.mult).then_inc(qs_ready, 1)
                    nc.gpsimd.tensor_tensor(
                        QS[0:64, CH - 1, :].rearrange("p (k r) -> p k r", r=R),
                        QB[0:64, s, T:N].unsqueeze(1).broadcast_to((64, HG, R)),
                        feat_mask[:].unsqueeze(2).broadcast_to((64, HG, R)), ALU.mult).then_inc(qs_ready, 1)

                pool.wait_ge(const_dve, 1)
                nc.gpsimd.affine_select(out=feat_mask[:], in_=feat_mask[:], compare_op=ALU.is_ge, fill=0.0,
                                        base=0, pattern=[[-HD, HG]], channel_multiplier=1).then_inc(const_pool, 1)
                pool.wait_ge(const_pool, 1)
                nc.gpsimd.affine_select(out=feat_mask[:], in_=feat_mask[:], compare_op=ALU.is_ge, fill=0.0,
                                        base=HD - 1, pattern=[[HD, HG]], channel_multiplier=-1).then_inc(const_pool, 1)
                pool.wait_ge(const_pool, 2)
                queries(0, 0)
                pool.wait_ge(qs_ready, HG + 1)
                for k in range(HG):
                    pool.wait_ge(const_pool, k + 2)
                    nc.gpsimd.affine_select(out=on_diag[k * R:(k + 1) * R, :], in_=on_diag[k * R:(k + 1) * R, :],
                                            compare_op=ALU.not_equal, fill=1.0, base=0, pattern=[[-1, R]],
                                            channel_multiplier=1).then_inc(const_pool, 1)
                pool.wait_ge(const_pool, CONST)
                pool.wait_ge(const_dve, DVE_CONST)

                def values(s, i):
                    if later(i) or s:
                        pool.wait_ge(o_ready[1 - s], i + s)
                        pool.wait_ge(const_pool, CONST)
                    for k in range(HG):
                        p, d = slice(k * R, (k + 1) * R), slice(k * HD, (k + 1) * HD)
                        for q in range(HG):
                            if later(i) or k or q:
                                pool.wait_ge(vs_ready[s], HG * (HG + 1) * i + k * (HG + 1) + q)
                                pool.wait_ge(const_pool, CONST)
                            nc.gpsimd.tensor_copy(VS[p, q:CH - 1:HG, d],
                                                  V[q * R:(q + 1) * R, s, :, bass.ds(i * 64 + k * HD, HD)]).then_inc(vs_ready[s], 1)
                        pool.wait_ge(vs_ready[s], HG * (HG + 1) * i + k * (HG + 1) + HG)
                        pool.wait_ge(const_pool, CONST)
                        nc.gpsimd.tensor_copy(VS[k * R:k * R + 1, CH - 1, d],
                                              VC[:, s, bass.ds(i * 64 + k * HD, HD)]).then_inc(vs_ready[s], 1)

                def round_of(i):
                    if later(i):
                        queries(0, i)
                        values(1, i - 1)
                    queries(1, i)
                    values(0, i)

                round_of(0)
                with pool.Fori(1, ROUNDS) as i:
                    round_of(i)
                values(1, ROUNDS - 1)

            @block.tensor
            def _(pe):
                pe.wait_ge(const_dve, 2)

                def cosines(s, i):
                    pe.wait_ge(qs_ready, (HG + 1) * (i * S + s + 1))
                    for c in range(CH):
                        if c >= 2:
                            pe.wait_ge(k_ready[s], CH * i + c - 1)
                        elif s:
                            pe.wait_ge(k_ready[0], CH * i + CH)
                        elif later(i):
                            pe.wait_ge(k_ready[1], CH * i)
                        for a, z in HALVES:
                            last = nc.tensor.matmul(pair(e_ps, c % 2)[:, a:z], QS[:, c, :], QB[:, s, a:z],
                                                    start=True, stop=True)
                        last.then_inc(dots_ready[s], 1)

                def first_row(s, i):
                    if later(i):
                        pe.wait_ge(o_kept[s], i)
                    pe.wait_ge(const_dve, DVE_CONST)
                    pe.wait_ge(first_ready[s], i + 1)
                    for a, z in HALVES:
                        last = nc.tensor.matmul(pair(w_ps, s)[:, a:z], block_ones[:], first_u[:, s, a:z], start=True, stop=True)
                    last.then_inc(w_ready[s], 1)

                def k_v(s, i, it):
                    if later(i):
                        pe.wait_ge(o_kept[s], i)
                    pe.wait_ge(k_masked[s], 3 * i + 3)
                    for c in range(CH):
                        for k, (first, _) in enumerate(PARTS):
                            if c == first:
                                pe.wait_ge(diag_ready[s], HG * (NPART * ((ITERS - 1) * i + it - 1) + k + 1))
                        for a, z in HALVES:
                            last = nc.tensor.matmul(pair(w_ps, s)[:, a:z], diag[s][:, c, :], K[s][:, c, a:z],
                                                    start=(c == 0), stop=(c == CH - 1))
                    last.then_inc(w_ready[s], 1)

                def diagonal(s):
                    for c in range(CH):
                        gain, first, end = (diag_gain, c * R, c * R + R) if c < CH - 1 else (cls_gain, T, N)
                        for a, z in HALVES:
                            a, z = max(a, first), min(z, end)
                            if a < z:
                                nc.tensor.matmul(pair(w_ps, s)[:, a:z], VS[:, c, :], gain[:, a - first:z - first],
                                                 start=False, stop=False)

                def attention(s, i):
                    pe.wait_ge(vs_ready[s], HG * (HG + 1) * (i + 1))
                    pe.wait_ge(logs_ready[s], (ITERS - 1) * (i + 1))
                    for c in range(CH):
                        if c == CH - 1:
                            diagonal(s)
                        pe.wait_ge(e_ready[s], CH * i + c + 1)
                        for a, z in HALVES:
                            last = nc.tensor.matmul(pair(w_ps, s)[:, a:z], VS[:, c, :], K[s][:, c, a:z], start=(c == 0),
                                                    stop=(c == CH - 1))
                    last.then_inc(o_ready[s], 1)

                def round_of(i):
                    if later(i):
                        k_v(1, i - 1, ITERS - 2)
                    cosines(0, i)
                    if later(i):
                        k_v(1, i - 1, ITERS - 1)
                    first_row(0, i)
                    k_v(0, i, 1)
                    k_v(0, i, 2)
                    if later(i):
                        attention(1, i - 1)
                    k_v(0, i, 3)
                    cosines(1, i)
                    k_v(0, i, LEAD)
                    first_row(1, i)
                    with pe.Fori(1, ITERS - LEAD) as it:
                        k_v(1, i, it)
                        k_v(0, i, it + LEAD)
                    k_v(1, i, ITERS - LEAD)
                    k_v(1, i, ITERS - LEAD + 1)
                    attention(0, i)

                round_of(0)
                with pe.Fori(1, ROUNDS) as i:
                    round_of(i)
                k_v(1, ROUNDS - 1, ITERS - 2)
                k_v(1, ROUNDS - 1, ITERS - 1)
                attention(1, ROUNDS - 1)

            @block.scalar
            def _(act):
                act.wait_ge(const_dve, 2)
                nc.scalar.preload_act_table_set("natural_log_exp_and_others")

                def u_row(s, i, it):
                    act.wait_ge(w_ready[s], i * ITERS + it + 1)
                    nc.scalar.activation(logs[:, s, 0:N], pair(w_ps, s), ACT.Ln, scale=float(N)).then_inc(logs_ready[s], 1)
                    act.wait_ge(logs_ready[s], i * (ITERS - 1) + it)
                    nc.scalar.activation(row[:, s, 0:N], logs[:, s, 0:N], ACT.Exp, scale=-1.0).then_inc(row_ready[s], 1)

                def v_blocks(s, source, a, z):
                    for k in range(HG):
                        p = slice(k * R, (k + 1) * R)
                        nc.scalar.activation(diag[s][p, a:z, p], source[p, a:z].unsqueeze(2).broadcast_to((R, z - a, R)),
                                             ACT.Copy).then_inc(diag_ready[s], 1)

                def first_u_row(s, i):
                    act.wait_ge(w_ready[s], i * ITERS + 1)
                    nc.scalar.activation(row[:, s, 0:N], pair(w_ps, s), ACT.Copy).then_inc(row_ready[s], 1)

                def kernel_matrix(s, i, beside=None):
                    if later(i):
                        act.wait_ge(o_ready[s], i)
                    for c in range(CH):
                        act.wait_ge(dots_ready[s], CH * i + c + 1)
                        nc.scalar.activation(K[s][:, c, 0:N], pair(e_ps, c % 2), ACT.Exp, bias=shift[:, 0:1],
                                             scale=INV_REG).then_inc(k_ready[s], 1)
                        if beside is not None and c in AFTER:
                            new_v_part(1 - s, *beside, AFTER.index(c))

                def new_v_part(s, i, it, k):
                    act.wait_ge(col_ready[s], NPART * (ITERS * i + it) + k + 1)
                    v_blocks(s, col[:, s, :], *PARTS[k])

                def new_v(s, i, it):
                    for k in range(NPART):
                        new_v_part(s, i, it, k)

                def attention_weights(s, i):
                    act.wait_ge(weight_ready[s], i + 1)
                    for c in range(CH):
                        nc.scalar.activation(K[s][:, c, 0:N], K[s][:, c, 0:N], ACT.Exp, bias=shift[:, 1:2],
                                             scale=weight[:, s, c:c + 1]).then_inc(e_ready[s], 1)

                def denominators(s, i):
                    act.wait_ge(o_ready[s], i + 1)
                    if s:
                        act.wait_ge(o_kept[0], i + 1)
                    elif later(i):
                        act.wait_ge(o_kept[1], i)
                    nc.scalar.activation(den[:, 0, 0:N], pair(w_ps, s)[64:P, :], ACT.Ln).then_inc(den_log[s], 1)
                    act.wait_ge(den_log[s], i + 1)
                    nc.scalar.activation(den[:, 1, 0:N], den[:, 0, 0:N], ACT.Exp, scale=-1.0).then_inc(den_ready[s], 1)

                def round_of(i):
                    if later(i):
                        u_row(1, i - 1, ITERS - 2)
                    kernel_matrix(0, i, (i - 1, ITERS - 2) if later(i) else None)
                    if later(i):
                        u_row(1, i - 1, ITERS - 1)
                    first_u_row(0, i)
                    new_v(0, i, 0)
                    u_row(0, i, 1)
                    new_v(0, i, 1)
                    if later(i):
                        attention_weights(1, i - 1)
                    u_row(0, i, 2)
                    new_v(0, i, 2)
                    if later(i):
                        denominators(1, i - 1)
                    u_row(0, i, 3)
                    kernel_matrix(1, i, (i, 3))
                    u_row(0, i, LEAD)
                    first_u_row(1, i)
                    new_v(1, i, 0)
                    new_v(0, i, LEAD)
                    with act.Fori(1, ITERS - LEAD - 1) as it:
                        u_row(1, i, it)
                        new_v(1, i, it)
                        u_row(0, i, it + LEAD)
                        new_v(0, i, it + LEAD)
                    u_row(1, i, ITERS - LEAD - 1)
                    new_v(1, i, ITERS - LEAD - 1)
                    u_row(0, i, ITERS - 1)
                    u_row(1, i, ITERS - LEAD)
                    new_v(1, i, ITERS - LEAD)
                    attention_weights(0, i)
                    u_row(1, i, ITERS - LEAD + 1)
                    new_v(1, i, ITERS - LEAD + 1)
                    denominators(0, i)

                round_of(0)
                with act.Fori(1, ROUNDS) as i:
                    round_of(i)
                u_row(1, ROUNDS - 1, ITERS - 2)
                new_v(1, ROUNDS - 1, ITERS - 2)
                u_row(1, ROUNDS - 1, ITERS - 1)
                attention_weights(1, ROUNDS - 1)
                denominators(1, ROUNDS - 1)

            @block.vector
            def _(dve):
                nc.vector.memset(feat_mask[:], 1.0)
                nc.vector.memset(on_diag[:], 0.0).then_inc(const_dve, 1)
                nc.vector.memset(QB[64:P, :, :], 0.0)
                nc.vector.memset(QS[64:P, :, :], 0.0)
                nc.vector.memset(shift[:, 0:1], -INV_REG)
                nc.vector.memset(shift[:, 1:2], -SCALE)
                for s in range(S):
                    nc.vector.memset(diag[s][:], 0.0)
                nc.vector.memset(head_mask[:], 0.0)
                nc.vector.memset(block_ones[:], 0.0)
                nc.vector.memset(VS[:, :, 0:64], 0.0)
                nc.vector.memset(cls_mask[:], 0.0).then_inc(const_dve, 1)
                dve.wait_ge(const_dve, 2)
                for k in range(HG):
                    nc.vector.memset(head_mask[k * R:(k + 1) * R, k:k + 1], 1.0)
                    nc.vector.memset(block_ones[k * R:(k + 1) * R, k * R:(k + 1) * R], 1.0)
                    last = nc.vector.memset(cls_mask[k * R:k * R + 1, :], 1.0)
                last.then_inc(const_dve, 1)
                dve.wait_ge(const_dve, 3)
                dve.wait_ge(const_pool, 2 + HG)
                nc.vector.tensor_scalar(not_cls[:], cls_mask[:], -1.0, 1.0, ALU.mult, ALU.add).then_inc(const_dve, 1)
                nc.vector.tensor_scalar(off_diag[:], on_diag[:], -1.0, 1.0, ALU.mult, ALU.add).then_inc(const_dve, 1)
                nc.vector.tensor_scalar(cls_head_mask[:], head_mask[:], cls_mask[:], None, ALU.mult).then_inc(const_dve, 1)
                nc.vector.tensor_scalar(diag_gain[:], on_diag[:], 1.0 - float(np.exp(-SCALE)), None,
                                        ALU.mult).then_inc(const_dve, 1)
                nc.vector.tensor_scalar(cls_gain[:], cls_mask[:], 1.0 - float(np.exp(-SCALE)), None,
                                        ALU.mult).then_inc(const_dve, 1)
                dve.wait_ge(const_dve, 8)
                for c0, c1, mask in ((0, CH - 1, head_mask), (CH - 1, CH, cls_head_mask)):
                    for k in range(HG):
                        last = nc.vector.tensor_copy(VS[:, c0:c1, 64 + k * HD:64 + (k + 1) * HD],
                                                     mask[:, k:k + 1].unsqueeze(1).broadcast_to((P, c1 - c0, HD)))
                    last.then_inc(const_dve, 1)

                def k_u(s, i, it):
                    last = isinstance(it, int) and it == ITERS - 1
                    dve.wait_ge(k_masked[s], 3 * i + 3)
                    dve.wait_ge(row_ready[s], i * ITERS + it + 1)
                    for c in range(CH):
                        if c >= JUNK:
                            dve.wait_ge(sums_ready[s], (i * ITERS + it) * CH + c - JUNK + 1)
                        nc.vector.tensor_tensor_reduce(
                            out=K[s][:, c, 0:N] if last else junk[:, c % JUNK, 0:N], in0=K[s][:, c, 0:N], in1=row[:, s, 0:N], scale=float(N),
                            scalar=not_cls[:] if c == CH - 1 else 0.0, op0=ALU.mult, op1=ALU.add,
                            accum_out=sums[:, s, c:c + 1]).then_inc(sums_ready[s], 1)
                        for a, z in PARTS:
                            if c == min(z, CH - 1):
                                dve.wait_ge(sums_ready[s], (i * ITERS + it) * CH + z)
                                nc.vector.reciprocal(col[:, s, a:z], sums[:, s, a:z]).then_inc(col_ready[s], 1)

                def mask(s, i):
                    dve.wait_ge(k_ready[s], CH * (i + 1))
                    nc.vector.tensor_tensor(near_diagonal(s), near_diagonal(s),
                                            off_diag[:].unsqueeze(1).broadcast_to((P, CH - 1, R)),
                                            ALU.mult).then_inc(k_masked[s], 1)
                    nc.vector.tensor_scalar(K[s][:, CH - 1, 0:T], K[s][:, CH - 1, 0:T], cls_mask[:], None,
                                            ALU.mult).then_inc(k_masked[s], 1)
                    nc.vector.memset(K[s][:, CH - 1, T:N], 0.0).then_inc(k_masked[s], 1)

                def first_sums_of(s, i):
                    total, scaled = first_sums[:, 0, :], first_sums[:, 1, :]
                    dve.wait_ge(k_masked[s], 3 * i + 3)
                    nc.vector.reduce_sum(total, K[s][:, :, 0:N], AX_X).then_inc(first_step[s], 1)
                    dve.wait_ge(first_step[s], 4 * i + 1)
                    nc.vector.tensor_scalar(scaled, total, float(N), None, ALU.mult).then_inc(first_step[s], 1)
                    dve.wait_ge(first_step[s], 4 * i + 2)
                    nc.vector.tensor_tensor(scaled[:, CH - 1:CH], scaled[:, CH - 1:CH], not_cls[:], ALU.add).then_inc(first_step[s], 1)
                    dve.wait_ge(first_step[s], 4 * i + 3)
                    nc.vector.reciprocal(total, scaled).then_inc(first_step[s], 1)
                    dve.wait_ge(first_step[s], 4 * i + 4)
                    nc.vector.tensor_tensor(first_u[:, s, :].rearrange("p (c r) -> p c r", r=R),
                                            total.unsqueeze(2).broadcast_to((P, CH, R)),
                                            on_diag[:].unsqueeze(1).broadcast_to((P, CH, R)), ALU.mult).then_inc(first_ready[s], 1)

                def maxima(s, i, a, z):
                    dve.wait_ge(sums_ready[s], CH * ITERS * (i + 1))
                    last = nc.vector.tensor_reduce(peak[:, s, a:z], K[s][:, a:z, 0:N], AX_X, ALU.max)
                    if z == CH:
                        last.then_inc(top_step[s], 1)

                def largest(s, i):
                    steps = 7 * i
                    dve.wait_ge(top_step[s], steps + 1)
                    dve.wait_ge(col_ready[s], NPART * ITERS * (i + 1))
                    nc.vector.tensor_tensor(peak[:, s, :], peak[:, s, :], col[:, s, :], ALU.mult).then_inc(top_step[s], 1)
                    dve.wait_ge(top_step[s], steps + 2)
                    nc.vector.reduce_max(top[:, 0:1], peak[:, s, :], AX_X).then_inc(top_step[s], 1)
                    dve.wait_ge(top_step[s], steps + 3)
                    nc.vector.tensor_copy(spread[:, 0, :], top[:, 0:1].broadcast_to((P, R))).then_inc(top_step[s], 1)
                    dve.wait_ge(top_step[s], steps + 4)
                    nc.vector.transpose(spread[:, 1, :], spread[:, 0, :]).then_inc(top_step[s], 1)
                    dve.wait_ge(top_step[s], steps + 5)
                    nc.vector.reduce_max(top[:, 1:2], spread[:, 1, :], AX_X).then_inc(top_step[s], 1)
                    dve.wait_ge(top_step[s], steps + 6)
                    nc.vector.reciprocal(top[:, 2:3], top[:, 1:2]).then_inc(top_step[s], 1)
                    dve.wait_ge(top_step[s], steps + 7)
                    nc.vector.tensor_scalar(weight[:, s, :], col[:, s, :], top[:, 2:3], SCALE, ALU.mult,
                                            ALU.mult).then_inc(weight_ready[s], 1)

                def output(s, i):
                    dve.wait_ge(den_ready[s], i + 1)
                    nc.vector.tensor_tensor(QT[0:64, i + ROUNDS * s, 0:N], pair(w_ps, s)[0:64, :], den[:, 1, 0:N],
                                            ALU.mult).then_inc(o_kept[s], 1)

                def round_of(i):
                    if later(i):
                        k_u(1, i - 1, ITERS - 2)
                    mask(0, i)
                    first_sums_of(0, i)
                    k_u(0, i, 0)
                    if later(i):
                        k_u(1, i - 1, ITERS - 1)
                    k_u(0, i, 1)
                    if later(i):
                        maxima(1, i - 1, 0, CH)
                        largest(1, i - 1)
                    k_u(0, i, 2)
                    if later(i):
                        output(1, i - 1)
                    k_u(0, i, 3)
                    mask(1, i)
                    first_sums_of(1, i)
                    k_u(1, i, 0)
                    k_u(0, i, LEAD)
                    with dve.Fori(1, ITERS - LEAD - 1) as it:
                        k_u(1, i, it)
                        k_u(0, i, it + LEAD)
                    k_u(1, i, ITERS - LEAD - 1)
                    k_u(0, i, ITERS - 1)
                    maxima(0, i, 0, EARLY)
                    k_u(1, i, ITERS - LEAD)
                    maxima(0, i, EARLY, CH)
                    largest(0, i)
                    k_u(1, i, ITERS - LEAD + 1)
                    output(0, i)

                round_of(0)
                with dve.Fori(1, ROUNDS) as i:
                    round_of(i)
                k_u(1, ROUNDS - 1, ITERS - 2)
                k_u(1, ROUNDS - 1, ITERS - 1)
                maxima(1, ROUNDS - 1, 0, CH)
                largest(1, ROUNDS - 1)
                output(1, ROUNDS - 1)


def sinkhorn_out_stage(nc, sem, make_ps, AOT, WprojT, H):
    with ExitStack() as ctx:
        o_ps = make_ps(ctx)("sko_o", [P, 4, 512])
        ready, kept = sem("sko_ready"), sem("sko_kept")
        with nc.Block() as block:
            @block.tensor
            def _(pe):
                for t in range(NT):
                    n = P if t < CLS else B
                    if t >= 4:
                        pe.wait_ge(kept, t - 3)
                    for g in range(GROUPS):
                        lhs = (AOT[:, t // TPB * GROUPS + g, (t % TPB) * P:(t % TPB + 1) * P] if t < CLS else
                               AOT[:, g:B * GROUPS:GROUPS, T])
                        last = nc.tensor.matmul(o_ps[0:n, t % 4, 0:D], lhs, WprojT[:, g, :], start=(g == 0),
                                                stop=(g == GROUPS - 1))
                    last.then_inc(ready, 1)

            @block.vector
            def _(dve):
                for t in range(NT):
                    n = P if t < CLS else B
                    dve.wait_ge(ready, t + 1)
                    nc.vector.tensor_tensor(H[0:n, t, :], H[0:n, t, :], o_ps[0:n, t % 4, 0:D], ALU.add).then_inc(kept, 1)


def halves_of(w):
    return w.rearrange("(h p) n -> p h n", p=HALF)


def row_of(v):
    return v.rearrange("(a n) -> a n", a=1)


def tokens_of(t):
    return (P if t < CLS else B), t * P


TOPK = max(1, int(round(0.15 * N)))
HPH = HALF // HD
QROWS = HPH * TOPK
QB_ROWS = 116
QBLOCKS = [(r, min(QROWS, r + QB_ROWS)) for r in range(0, QROWS, QB_ROWS)]
F = 4 * D


def routed_stage(nc, sem, make_sb, make_ps, A, H, ident, ones):
    with ExitStack() as ctx:
        sb = make_sb(ctx)
        HH = sb("r_hh", [P, NT, D])
        bf2 = sb("r_bf2", [1, D])
        bf1 = sb("r_bf1", [P, F // P])
        W1 = sb("r_W1", [HALF, 2, F])
        W2 = sb("r_W2", [P, F // P, D])
        g2, b2 = sb("r_g2", [P, D]), sb("r_b2", [P, D])
        with ExitStack() as actx:
            asb = make_sb(actx)
            N1, N1T = asb("r_n1", [P, NT, D]), asb("r_n1T", [HALF, 2, NTOK])
            g1, b1 = asb("r_g1", [P, D]), asb("r_b1", [P, D])
            W = {k: asb("r_W" + k, [HALF, 2, D]) for k in "qkvom"}
            wr = asb("r_wr", [HALF, 2, 1])
            br = asb("r_br", [P, 1])
            bq, bk = asb("r_bq", [HALF, 2]), asb("r_bk", [HALF, 2])
            bv, bo, bm = asb("r_bv", [1, D]), asb("r_bo", [1, D]), asb("r_bm", [P, D])
            with nc.allow_non_contiguous_dma(reason="vectors of 192 and 768 numbers, one per partition"):
                loads = [
                    (g1[:], A["L0_ffn_g1"].partition_broadcast(P)), (b1[:], A["L0_ffn_b1"].partition_broadcast(P)),
                    (g2[:], A["L0_ffn_g2"].partition_broadcast(P)), (b2[:], A["L0_ffn_b2"].partition_broadcast(P)),
                    *[(W[k][:], halves_of(A["L0_ffn_W" + k])) for k in "qkvom"],
                    (W1[:], halves_of(A["L0_ffn_W1"])), (W2[:], A["L0_ffn_W2"].rearrange("(f p) n -> p f n", p=P)),
                    (wr[:], A["L0_ffn_Wr"].rearrange("(h p a) -> p h a", p=HALF, a=1)),
                    (br[:], A["L0_ffn_br"].partition_broadcast(P)),
                    (bq[:], A["L0_ffn_bq"].rearrange("(h p) -> p h", p=HALF)),
                    (bk[:], A["L0_ffn_bk"].rearrange("(h p) -> p h", p=HALF)),
                    (bv[:], row_of(A["L0_ffn_bv"])), (bo[:], row_of(A["L0_ffn_bo"])), (bm[:], A["L0_ffn_bm"].partition_broadcast(P)),
                    (bf2[:], row_of(A["L0_ffn_bf2"])), (bf1[:], A["L0_ffn_bf1"].rearrange("(f p) -> p f", p=P))]
                norm_stage(nc, sem, make_sb, make_ps, "rn1", H, N1, N1T, ident, inner=HH, gain=g1, shift=b1, loads=loads)
            KT = asb("r_KT", [HALF, 2, B, NP])
            V, VC = asb("r_V", [P, CLS, D]), asb("r_VC", [1, B, D])
            Z = asb("r_Z", [P, B, NP])
            router_logits(nc, sem, make_ps, N1T, wr, br, Z)
            sel = asb("r_sel", [P, B, TPB, TOPK])
            selc = asb("r_selc", [B, B, TOPK])
            score = asb("r_score", [P, B, TPB + 1])
            rest = asb("r_rest", [P, B, TPB + 1])
            score_cls, rest_cls = asb("r_score_cls", [B, 1]), asb("r_rest_cls", [B, 1])
            PM, PMC = asb("r_PM", [P, B, D]), asb("r_PMC", [B, D])
            routing(nc, sem, make_sb, make_ps, ident, ones, N1, N1T, W, bk, bv, KT, V, VC, Z, sel, selc, score, rest, score_cls, rest_cls, PM, PMC)
            selT = asb("r_selT", [P, B, T + B])
            AS = asb("r_AS", [P, B, D])
            routed_attention(nc, sem, make_sb, make_ps, ident, ones, N1, W, bq, bo, KT, V, VC, sel, selc, selT, AS)
            merge(nc, sem, make_sb, make_ps, ident, N1T, W["m"], bm, selT, AS, score, rest, score_cls, rest_cls, PM, PMC, HH)
        with ExitStack() as mctx:
            msb = make_sb(mctx)
            N2, N2T = msb("r_n2", [P, NT, D]), msb("r_n2T", [HALF, 2, NTOK])
            norm_stage(nc, sem, make_sb, make_ps, "rn2", HH, N2, N2T, ident, gain=g2, shift=b2)
            gelu_mlp(nc, sem, make_sb, make_ps, ones, N2T, W1, bf1, W2, bf2, HH, H)


def router_logits(nc, sem, make_ps, N1T, wr, br, Z):
    with ExitStack() as ctx:
        z_ps = make_ps(ctx)("rp_z", [P, 2, 1024])
        z_ready, z_kept, z_done = sem("rp_z_ready"), sem("rp_z_kept"), sem("rp_z_done")
        with nc.Block() as block:
            @block.tensor
            def _(pe):
                for b in range(B):
                    if b >= 2:
                        pe.wait_ge(z_kept, b - 1)
                    for h in range(2):
                        nc.tensor.matmul(z_ps[:, b % 2, 0:T], wr[:, h, :].broadcast_to((HALF, P)),
                                         N1T[:, h, b * T:(b + 1) * T], start=(h == 0), stop=(h == 1))
                    for h in range(2):
                        last = nc.tensor.matmul(z_ps[:, b % 2, T:N], wr[:, h, :].broadcast_to((HALF, P)),
                                                N1T[:, h, B * T + b:B * T + b + 1], start=(h == 0), stop=(h == 1))
                    last.then_inc(z_ready, 1)

            @block.vector
            def _(dve):
                for b in range(B):
                    dve.wait_ge(z_ready, b + 1)
                    nc.vector.tensor_scalar(Z[:, b, 0:N], z_ps[:, b % 2, 0:N], br[:], 17.0, ALU.add,
                                            ALU.min).then_inc(z_kept, 1)
                    dve.wait_ge(z_kept, b + 1)
                    nc.vector.tensor_scalar(Z[:, b, 0:N], Z[:, b, 0:N], -88.0, None, ALU.max).then_inc(z_done, 1)


def routing(nc, sem, make_sb, make_ps, ident, ones, N1, N1T, W, bk, bv, KT, V, VC, Z, sel, selc, score, rest, score_cls,
            rest_cls, PM, PMC):
    C5 = TPB + 1
    with ExitStack() as ctx:
        sb, ps = make_sb(ctx), make_ps(ctx)
        before = sb("ro_before", [P, TPB, NP])
        slot = sb("ro_slot", [P, TOPK])
        picked = sb("ro_picked", [P, 2, P])
        zcol = sb("ro_zcol", [P, B, C5])
        same = sb("ro_same", [P, 2, NP])
        both = sb("ro_both", [P, 2, NP])
        rank = sb("ro_rank", [P, B, C5])
        counted = sb("ro_counted", [P, B, C5])
        expz = sb("ro_expz", [P, B, C5])
        cls_scores = sb("ro_cls_scores", [B, B])
        total = sb("ro_total", [P, B])
        pooled = sb("ro_pooled", [HALF, 2, B])
        small = sb("ro_small", [B, 2, B])
        t_ps, p_ps, m_ps = ps("ro_t", [P, 512]), ps("ro_p", [P, 512]), ps("ro_m", [P, 3, 512])
        k_ps = ps("ro_k", [P, 2, 512])
        v_ps = m_ps
        k_ready, k_kept, v_ready, v_kept = sem("ro_k_ready"), sem("ro_k_kept"), sem("ro_v_ready"), sem("ro_v_kept")
        KJOBS = [(o, b) for o in range(2) for b in range(B + 1)]
        const_ready, step = sem("ro_const_ready"), sem("ro_step")
        col_ready, pair_ready, rank_ready = sem("ro_col_ready"), sem("ro_pair_ready"), sem("ro_rank_ready")
        exp_ready, score_ready, total_ready, pooled_ready = (sem("ro_exp_ready"), sem("ro_score_ready"),
                                                             sem("ro_total_ready"), sem("ro_pooled_ready"))
        pooled_kept, mean_ready = sem("ro_pooled_kept"), sem("ro_mean_ready")
        with nc.Block() as block:
            @block.gpsimd
            def _(pool):
                nc.gpsimd.memset(before[:], 1.0).then_inc(const_ready, 1)
                nc.gpsimd.iota(slot[:], pattern=[[1, TOPK]], base=0, channel_multiplier=0,
                               allow_small_or_imprecise_dtypes=True).then_inc(const_ready, 1)
                for t in range(TPB):
                    pool.wait_ge(const_ready, 2 + t)
                    nc.gpsimd.affine_select(out=before[:, t, 0:T], in_=before[:, t, 0:T], compare_op=ALU.is_gt,
                                            fill=0.0, base=t * P, pattern=[[-1, T]],
                                            channel_multiplier=1).then_inc(const_ready, 1)

            @block.vector
            def _(dve):
                steps = Tally(step)
                for b in range(B):
                    for t in range(TPB):
                        if b * TPB + t >= 2:
                            dve.wait_ge(col_ready, b * TPB + t - 1)
                        nc.vector.tensor_tensor_reduce(out=picked[:, t % 2, :], in0=Z[:, b, t * P:(t + 1) * P],
                                                       in1=ident[:], scale=1.0, scalar=0.0, op0=ALU.mult, op1=ALU.add,
                                                       accum_out=zcol[:, b, t:t + 1]).then_inc(col_ready, 1)
                nc.vector.tensor_copy(zcol[:, :, TPB], Z[:, :, T]).then_inc(col_ready, 1)
                dve.wait_ge(col_ready, CLS + 1)
                dve.wait_ge(const_ready, 2 + TPB)
                for n in range(B * C5 + 1):
                    if n < B * C5:
                        b, t = n // C5, n % C5
                        if n >= 2:
                            dve.wait_ge(rank_ready, n - 1)
                        if t < TPB:
                            nc.vector.scalar_tensor_tensor(out=same[:, n % 2, 0:N], in0=Z[:, b, 0:N], scalar=zcol[:, b, t:t + 1],
                                                           in1=before[:, t, 0:N], op0=ALU.is_equal,
                                                           op1=ALU.mult).then_inc(pair_ready, 1)
                        else:
                            nc.vector.memset(same[:, n % 2, 0:N], 0.0).then_inc(pair_ready, 1)
                    if n:
                        b, t = (n - 1) // C5, (n - 1) % C5
                        dve.wait_ge(pair_ready, n)
                        nc.vector.scalar_tensor_tensor(out=both[:, (n - 1) % 2, 0:N], in0=Z[:, b, 0:N], scalar=zcol[:, b, t:t + 1],
                                                       in1=same[:, (n - 1) % 2, 0:N], op0=ALU.is_lt, op1=ALU.add,
                                                       accum_out=rank[:, b, t:t + 1]).then_inc(rank_ready, 1)
                dve.wait_ge(rank_ready, B * C5)
                for b in range(B):
                    for t in range(TPB):
                        nc.vector.tensor_scalar(sel[:, b, t, :], slot[:], rank[:, b, t:t + 1], None, ALU.is_equal)
                    nc.vector.tensor_scalar(selc[:, b, :], slot[0:B, :], rank[0:B, b, TPB:C5], ident[0:B, b:b + 1],
                                            ALU.is_equal, ALU.mult)
                steps.mark(nc.vector.tensor_scalar(rest[:], rank[:], TOPK - 0.5, None, ALU.is_gt))
                dve.wait_ge(exp_ready, 1)
                dve.wait_ge(step, steps.mark(nc.vector.tensor_scalar(expz[:], expz[:], 1.0, None, ALU.add)))
                dve.wait_ge(step, steps.mark(nc.vector.reciprocal(score[:], expz[:])))
                nc.vector.tensor_copy(counted[:, :, 0:TPB], score[:, :, 0:TPB])
                nc.vector.tensor_scalar(counted[:, :, TPB], score[:, :, TPB], ident[:, 0:1], None, ALU.mult)
                nc.vector.tensor_tensor(cls_scores[:], score[0:B, :, TPB], ident[0:B, 0:B], ALU.mult).then_inc(score_ready, 1)
                dve.wait_ge(step, steps.mark(nc.vector.tensor_tensor(small[:, 0, :], rest[0:B, :, TPB], ident[0:B, 0:B],
                                                                     ALU.mult)))
                nc.vector.reduce_sum(rest_cls[:], small[:, 0, :], AX_X)
                dve.wait_ge(score_ready, 1)
                nc.vector.reduce_sum(score_cls[:], cls_scores[:], AX_X)
                dve.wait_ge(total_ready, 1)
                dve.wait_ge(step, steps.mark(nc.vector.reduce_sum(
                    total[:], t_ps[:, 0:B * C5].rearrange("p (b c) -> p b c", b=B), AX_X)))
                dve.wait_ge(step, steps.mark(nc.vector.tensor_scalar(total[:], total[:], 1e-6, None, ALU.add)))
                dve.wait_ge(step, steps.mark(nc.vector.reciprocal(total[:], total[:])))
                dve.wait_ge(pooled_ready, 1)
                nc.vector.tensor_tensor(pooled[:], p_ps[0:HALF, 0:2 * B].rearrange("p (h b) -> p h b", h=2),
                                        total[0:HALF, :].unsqueeze(1).broadcast_to((HALF, 2, B)),
                                        ALU.mult).then_inc(pooled_kept, 1)
                dve.wait_ge(mean_ready, B + 1)
                for b in range(B):
                    nc.vector.tensor_copy(PM[:, b, :], m_ps[:, b // 2, (b % 2) * D:(b % 2 + 1) * D])
                nc.vector.tensor_copy(PMC[:], m_ps[0:B, 2, 0:D])

            @block.scalar
            def _(act):
                def exponentials():
                    act.wait_ge(col_ready, CLS + 1)
                    nc.scalar.activation(expz[:], zcol[:], ACT.Exp, scale=-1.0).then_inc(exp_ready, 1)

                for j, (o, b) in enumerate(KJOBS):
                    act.wait_ge(k_ready, j + 1)
                    dst = KT[:, o, b, 0:T] if b < B else KT[:, o, :, T]
                    nc.scalar.activation(dst, k_ps[0:HALF, j % 2, 0:T if b < B else B], ACT.Identity,
                                         bias=bk[:, o:o + 1]).then_inc(k_kept, 1)
                for t in range(CLS + B):
                    act.wait_ge(v_ready, t + 1)
                    dst = V[:, t, :] if t < CLS else VC[:, t - CLS, :]
                    nc.scalar.activation(dst, v_ps[0:P if t < CLS else 1, t % 2, 0:D], ACT.Copy).then_inc(v_kept, 1)
                    if t == CLS:
                        exponentials()

            @block.tensor
            def _(pe):
                for j, (o, b) in enumerate(KJOBS):
                    n = T if b < B else B
                    if j >= 2:
                        pe.wait_ge(k_kept, j - 1)
                    for h in range(2):
                        last = nc.tensor.matmul(k_ps[0:HALF, j % 2, 0:n], W["k"][:, h, o * HALF:(o + 1) * HALF],
                                                N1T[:, h, b * T:b * T + n], start=(h == 0), stop=(h == 1))
                    last.then_inc(k_ready, 1)
                for t in range(CLS + B):
                    n, first = (P, t * P) if t < CLS else (1, t - CLS + B * T)
                    if t >= 2:
                        pe.wait_ge(v_kept, t - 1)
                    for h in range(2):
                        nc.tensor.matmul(v_ps[0:n, t % 2, 0:D], N1T[:, h, first:first + n], W["v"][:, h, :],
                                         start=(h == 0), stop=False)
                    nc.tensor.matmul(v_ps[0:n, t % 2, 0:D], ones[0:1, 0:n], bv[:], start=False,
                                     stop=True).then_inc(v_ready, 1)
                pe.wait_ge(v_kept, CLS + B)
                pe.wait_ge(score_ready, 1)
                nc.tensor.matmul(t_ps[:, 0:B * C5], ones[:], counted[:].rearrange("p b c -> p (b c)"), start=True,
                                 stop=True).then_inc(total_ready, 1)
                for h in range(2):
                    for b in range(B):
                        for t in range(TPB):
                            nc.tensor.matmul(p_ps[0:HALF, h * B + b:h * B + b + 1],
                                             N1[:, b * TPB + t, h * HALF:(h + 1) * HALF], score[:, b, t:t + 1],
                                             start=(t == 0), stop=False)
                        last = nc.tensor.matmul(p_ps[0:HALF, h * B + b:h * B + b + 1],
                                                N1[0:B, CLS, h * HALF:(h + 1) * HALF], cls_scores[:, b:b + 1],
                                                start=False, stop=True)
                last.then_inc(pooled_ready, 1)
                pe.wait_ge(pooled_kept, 1)
                for b in range(B + 1):
                    n = P if b < B else B
                    for h in range(2):
                        lhs = pooled[:, h, b:b + 1].broadcast_to((HALF, P)) if b < B else pooled[:, h, :]
                        last = nc.tensor.matmul(m_ps[0:n, b // 2, (b % 2) * D:(b % 2 + 1) * D], lhs, W["m"][:, h, :],
                                                start=(h == 0), stop=(h == 1))
                    last.then_inc(mean_ready, 1)


def routed_attention(nc, sem, make_sb, make_ps, ident, ones, N1, W, bq, bo, KT, V, VC, sel, selc, selT, AS):
    L = 255
    HALVES = ((0, 512 - L), (512 - L, N))
    NB = len(QBLOCKS)
    MT = TPB + 1
    with ExitStack() as ctx:
        sb, ps = make_sb(ctx), make_ps(ctx)
        picked = sb("ra_picked", [HALF, 2, TOPK])
        q = sb("ra_q", [HALF, 2, TOPK])
        heads = sb("ra_heads", [HALF, HPH])
        qd = sb("ra_qd", [HALF, 2, HPH, TOPK])
        prob = sb("ra_prob", [P, 2 * NB, NP])
        top, den, rden = sb("ra_top", [P, 2 * NB]), sb("ra_den", [P, 2 * NB]), sb("ra_rden", [P, 2 * NB])
        probT = sb("ra_probT", [P, 2, MT, QROWS])
        own = sb("ra_own", [HALF, 2, QROWS])
        ctxT = sb("ra_ctxT", [HALF, 2, TOPK])
        s_ps = ps("ra_s", [P, 2, 1024])
        t_ps = ps("ra_t", [P, 2, 512])
        x_ps = ps("ra_x", [P, 2, 512])
        names = ("picked_ready picked_kept q_ready q_kept qd_ready logit_ready top_ready prob_ready rden_ready "
                 "prob_normed turn_ready turn_kept ctx_ready own_ready ctx_kept as_ready as_kept st_ready st_kept const").split()
        M = {n: sem("ra_" + n) for n in names}
        with nc.Block() as block:
            @block.gpsimd
            def _(pool):
                nc.gpsimd.memset(heads[:], 1.0).then_inc(M["const"], 1)
                pool.wait_ge(M["const"], 1)
                nc.gpsimd.affine_select(out=heads[:], in_=heads[:], compare_op=ALU.is_ge, fill=0.0, base=0,
                                        pattern=[[-HD, HPH]], channel_multiplier=1).then_inc(M["const"], 1)
                pool.wait_ge(M["const"], 2)
                nc.gpsimd.affine_select(out=heads[:], in_=heads[:], compare_op=ALU.is_ge, fill=0.0, base=HD - 1,
                                        pattern=[[HD, HPH]], channel_multiplier=-1).then_inc(M["const"], 1)
                pool.wait_ge(M["const"], 3)
                nc.gpsimd.memset(selT[64:P, :, :], 0.0).then_inc(M["const"], 1)
                pool.wait_ge(M["const"], 4)
                nc.gpsimd.memset(AS[64:P, :, :], 0.0).then_inc(M["const"], 1)

            @block.tensor
            def _(pe):
                for b in range(B):
                    pe.wait_ge(M["as_kept"], b)
                    pe.wait_ge(M["ctx_kept"], 2 * b)
                    for h in range(2):
                        for t in range(TPB):
                            nc.tensor.matmul(x_ps[0:HALF, 0, h * TOPK:(h + 1) * TOPK],
                                             N1[:, b * TPB + t, h * HALF:(h + 1) * HALF], sel[:, b, t, :],
                                             start=(t == 0), stop=False)
                        last = nc.tensor.matmul(x_ps[0:HALF, 0, h * TOPK:(h + 1) * TOPK],
                                                N1[0:B, CLS, h * HALF:(h + 1) * HALF], selc[:, b, :],
                                                start=False, stop=True)
                    last.then_inc(M["picked_ready"], 1)
                    pe.wait_ge(M["picked_kept"], b + 1)
                    for o in range(2):
                        for h in range(2):
                            last = nc.tensor.matmul(x_ps[0:HALF, 1, o * TOPK:(o + 1) * TOPK],
                                                    W["q"][:, h, o * HALF:(o + 1) * HALF], picked[:, h, :],
                                                    start=(h == 0), stop=(h == 1))
                    last.then_inc(M["q_ready"], 1)
                    pe.wait_ge(M["turn_kept"], 2 * MT * b)
                    for t in range(TPB):
                        nc.tensor.transpose(t_ps[0:TOPK, 0, t * P:(t + 1) * P], sel[:, b, t, :], ident[:])
                    nc.tensor.transpose(t_ps[0:TOPK, 1, 0:B], selc[:, b, :], ident[0:B, 0:B]).then_inc(M["st_ready"], 1)
                    pe.wait_ge(M["qd_ready"], 2 * b + 2)
                    for j in range(2 * NB):
                        n = 2 * NB * b + j
                        o, (r0, r1) = j // NB, QBLOCKS[j % NB]
                        if n >= 2:
                            pe.wait_ge(M["prob_ready"], n - 1)
                        for a, z in HALVES:
                            last = nc.tensor.matmul(s_ps[0:r1 - r0, j % 2, L + a:L + z],
                                                    qd[:, o, :, :].rearrange("p h s -> p (h s)")[:, r0:r1],
                                                    KT[:, o, b, a:z], start=True, stop=True)
                        last.then_inc(M["logit_ready"], 1)
                    pe.wait_ge(M["st_kept"], b + 1)
                    for o in range(2):
                        pe.wait_ge(M["prob_normed"], 2 * NB * b + NB * (o + 1))
                        for m in range(MT):
                            j = o * MT + m
                            n = P if m < TPB else 1
                            if 2 * MT * b + j >= 2:
                                pe.wait_ge(M["turn_kept"], 2 * MT * b + j - 1)
                            for k, (r0, r1) in enumerate(QBLOCKS):
                                last = nc.tensor.transpose(t_ps[0:n, j % 2, r0:r1],
                                                           prob[0:r1 - r0, o * NB + k, m * P:m * P + n],
                                                           ident[0:r1 - r0, 0:r1 - r0])
                            last.then_inc(M["turn_ready"], 1)
                    for o in range(2):
                        pe.wait_ge(M["turn_kept"], 2 * MT * b + MT * (o + 1))
                        for m in range(MT):
                            v = V[:, b * TPB + m, o * HALF:(o + 1) * HALF] if m < TPB else VC[:, b, o * HALF:(o + 1) * HALF]
                            n = P if m < TPB else 1
                            last = nc.tensor.matmul(x_ps[0:HALF, o, 0:QROWS], v, probT[0:n, o, m, :], start=(m == 0),
                                                    stop=(m == MT - 1))
                        last.then_inc(M["ctx_ready"], 1)
                    pe.wait_ge(M["ctx_kept"], 2 * b + 2)
                    for h in range(2):
                        nc.tensor.matmul(x_ps[0:TOPK, 0, 0:D], ctxT[:, h, :], W["o"][:, h, :], start=(h == 0), stop=False)
                    nc.tensor.matmul(x_ps[0:TOPK, 0, 0:D], ones[0:1, 0:TOPK], bo[:], start=False,
                                     stop=True).then_inc(M["as_ready"], 1)

            @block.scalar
            def _(act):
                act.wait_ge(M["const"], 5)
                for b in range(B):
                    act.wait_ge(M["st_ready"], b + 1)
                    nc.scalar.activation(selT[0:TOPK, b, 0:T], t_ps[0:TOPK, 0, :], ACT.Copy)
                    nc.scalar.activation(selT[0:TOPK, b, T:T + B], t_ps[0:TOPK, 1, 0:B], ACT.Copy).then_inc(M["st_kept"], 1)
                    for j in range(2 * NB):
                        r = QBLOCKS[j % NB][1] - QBLOCKS[j % NB][0]
                        act.wait_ge(M["top_ready"], 2 * NB * b + j + 1)
                        if j % NB == 0:
                            act.wait_ge(M["turn_ready"], 2 * MT * b)
                        nc.scalar.activation(prob[0:r, j, 0:N], s_ps[0:r, j % 2, L:L + N], ACT.Exp,
                                             bias=top[0:r, j:j + 1],
                                             accum_out=den[0:r, j:j + 1]).then_inc(M["prob_ready"], 1)
                    for j in range(2 * MT):
                        act.wait_ge(M["turn_ready"], 2 * MT * b + j + 1)
                        act.wait_ge(M["ctx_ready"], 2 * b)
                        n = P if j % MT < TPB else 1
                        nc.scalar.activation(probT[0:n, j // MT, j % MT, :], t_ps[0:n, j % 2, 0:QROWS],
                                             ACT.Copy).then_inc(M["turn_kept"], 1)

            @block.vector
            def _(dve):
                dve.wait_ge(M["const"], 5)
                for b in range(B):
                    dve.wait_ge(M["picked_ready"], b + 1)
                    nc.vector.tensor_copy(picked[:], x_ps[0:HALF, 0, 0:2 * TOPK].rearrange(
                        "p (h s) -> p h s", h=2)).then_inc(M["picked_kept"], 1)
                    dve.wait_ge(M["q_ready"], b + 1)
                    for o in range(2):
                        nc.vector.tensor_scalar(q[:, o, :], x_ps[0:HALF, 1, o * TOPK:(o + 1) * TOPK], bq[:, o:o + 1],
                                                float(HD) ** -0.5, ALU.add, ALU.mult).then_inc(M["q_kept"], 1)
                    for o in range(2):
                        dve.wait_ge(M["q_kept"], 2 * b + o + 1)
                        dve.wait_ge(M["logit_ready"], 2 * NB * b)
                        nc.vector.tensor_tensor(qd[:, o, :, :], q[:, o, :].unsqueeze(1).broadcast_to((HALF, HPH, TOPK)),
                                                heads[:].unsqueeze(2).broadcast_to((HALF, HPH, TOPK)),
                                                ALU.mult).then_inc(M["qd_ready"], 1)

                    def normalise(j):
                        r = QBLOCKS[j % NB][1] - QBLOCKS[j % NB][0]
                        dve.wait_ge(M["prob_ready"], 2 * NB * b + j + 1)
                        nc.vector.reciprocal(rden[0:r, j:j + 1], den[0:r, j:j + 1]).then_inc(M["rden_ready"], 1)
                        dve.wait_ge(M["rden_ready"], 2 * NB * b + j + 1)
                        nc.vector.tensor_scalar(prob[0:r, j, 0:N], prob[0:r, j, 0:N], rden[0:r, j:j + 1], None,
                                                ALU.mult).then_inc(M["prob_normed"], 1)

                    for j in range(2 * NB):
                        r = QBLOCKS[j % NB][1] - QBLOCKS[j % NB][0]
                        dve.wait_ge(M["logit_ready"], 2 * NB * b + j + 1)
                        nc.vector.tensor_reduce(top[0:r, j:j + 1], s_ps[0:r, j % 2, L:L + N], AX_X, ALU.max,
                                                negate=True).then_inc(M["top_ready"], 1)
                        if j:
                            normalise(j - 1)
                    normalise(2 * NB - 1)
                    for o in range(2):
                        dve.wait_ge(M["ctx_ready"], 2 * b + o + 1)
                        nc.vector.tensor_tensor(own[:, o, :].rearrange("p (h s) -> p h s", h=HPH),
                                                x_ps[0:HALF, o, 0:QROWS].rearrange("p (h s) -> p h s", h=HPH),
                                                heads[:].unsqueeze(2).broadcast_to((HALF, HPH, TOPK)),
                                                ALU.mult).then_inc(M["own_ready"], 1)
                        dve.wait_ge(M["own_ready"], 2 * b + o + 1)
                        nc.vector.reduce_sum(ctxT[:, o, :], own[:, o, :].rearrange("p (h s) -> p s h", h=HPH),
                                             AX_X).then_inc(M["ctx_kept"], 1)
                    dve.wait_ge(M["as_ready"], b + 1)
                    nc.vector.tensor_copy(AS[0:TOPK, b, :], x_ps[0:TOPK, 0, 0:D]).then_inc(M["as_kept"], 1)


def merge(nc, sem, make_sb, make_ps, ident, N1T, Wm, bm, selT, AS, score, rest, score_cls, rest_cls, PM, PMC, HH):
    with ExitStack() as ctx:
        mixed = make_sb(ctx)("rm_mixed", [P, 2, D])
        ps = make_ps(ctx)
        m_ps, a_ps = ps("rm_m", [P, 2, 512]), ps("rm_a", [P, 2, 512])
        ready, mixed_ready, added, kept = sem("rm_ready"), sem("rm_mixed_ready"), sem("rm_added"), sem("rm_kept")
        with nc.Block() as block:
            @block.tensor
            def _(pe):
                for t in range(NT):
                    n, first = tokens_of(t)
                    if t >= 2:
                        pe.wait_ge(kept, t - 1)
                    for h in range(2):
                        nc.tensor.matmul(m_ps[0:n, t % 2, 0:D], N1T[:, h, first:first + n], Wm[:, h, :], start=(h == 0),
                                         stop=False)
                    nc.tensor.matmul(m_ps[0:n, t % 2, 0:D], ident[:, 0:1].broadcast_to((P, n)), bm[:], start=False, stop=True)
                    if t < CLS:
                        last = nc.tensor.matmul(a_ps[:, t % 2, 0:D], selT[:, t // TPB, (t % TPB) * P:(t % TPB + 1) * P],
                                                AS[:, t // TPB, :], start=True, stop=True)
                    else:
                        for b in range(B):
                            last = nc.tensor.matmul(a_ps[0:B, t % 2, 0:D], selT[:, b, T:T + B], AS[:, b, :],
                                                    start=(b == 0), stop=(b == B - 1))
                    last.then_inc(ready, 1)

            @block.vector
            def _(dve):
                for t in range(NT):
                    n, _ = tokens_of(t)
                    b, k = t // TPB, t % TPB
                    s, r, pm = (score[:, b, k:k + 1], rest[:, b, k:k + 1], PM[:, b, :]) if t < CLS else \
                        (score_cls[:], rest_cls[:], PMC[:])
                    dve.wait_ge(ready, t + 1)
                    nc.vector.scalar_tensor_tensor(out=mixed[0:n, t % 2, :], in0=pm, scalar=s, in1=m_ps[0:n, t % 2, 0:D],
                                                   op0=ALU.mult, op1=ALU.add).then_inc(mixed_ready, 1)
                    dve.wait_ge(mixed_ready, t + 1)
                    nc.vector.scalar_tensor_tensor(out=HH[0:n, t, :], in0=mixed[0:n, t % 2, :], scalar=r, in1=HH[0:n, t, :],
                                                   op0=ALU.mult, op1=ALU.add).then_inc(added, 1)
                    dve.wait_ge(added, t + 1)
                    nc.vector.tensor_tensor(HH[0:n, t, :], HH[0:n, t, :], a_ps[0:n, t % 2, 0:D], ALU.add).then_inc(kept, 1)


def gelu_mlp(nc, sem, make_sb, make_ps, ones, N2T, W1, bf1, W2, bf2, HH, H):
    NF = F // P
    CHUNKS = [(b * T, T) for b in range(B)] + [(B * T, B)]
    with ExitStack() as ctx:
        sb, ps = make_sb(ctx), make_ps(ctx)
        hid = sb("gm_hid", [P, 2, NF, T])
        h_ps, o_ps = ps("gm_h", [P, 4, 512]), ps("gm_o", [P, 2, 512])
        h_ready, h_kept, o_ready, o_kept, added = (sem("gm_h_ready"), sem("gm_h_kept"), sem("gm_o_ready"),
                                                   sem("gm_o_kept"), sem("gm_added"))
        with nc.Block() as block:
            @block.tensor
            def _(pe):
                for k, (first, n) in enumerate(CHUNKS):
                    for f in range(NF):
                        j = k * NF + f
                        if j >= 4:
                            pe.wait_ge(h_kept, j - 3)
                        for h in range(2):
                            last = nc.tensor.matmul(h_ps[:, j % 4, 0:n], W1[:, h, f * P:(f + 1) * P],
                                                    N2T[:, h, first:first + n], start=(h == 0), stop=(h == 1))
                        last.then_inc(h_ready, 1)
                    pe.wait_ge(h_kept, (k + 1) * NF)
                    for t in range(k * TPB, min(NT, (k + 1) * TPB)):
                        n, c = tokens_of(t)
                        if t >= 2:
                            pe.wait_ge(o_kept, t - 1)
                        for f in range(NF):
                            nc.tensor.matmul(o_ps[0:n, t % 2, 0:D], hid[:, k % 2, f, c - first:c - first + n], W2[:, f, :],
                                             start=(f == 0), stop=False)
                        nc.tensor.matmul(o_ps[0:n, t % 2, 0:D], ones[0:1, 0:n], bf2[:], start=False,
                                         stop=True).then_inc(o_ready, 1)

            @block.scalar
            def _(act):
                for k, (first, n) in enumerate(CHUNKS):
                    for f in range(NF):
                        j = k * NF + f
                        act.wait_ge(h_ready, j + 1)
                        if f == 0 and k >= 2:
                            act.wait_ge(o_ready, (k - 1) * TPB)
                        nc.scalar.activation(hid[:, k % 2, f, 0:n], h_ps[:, j % 4, 0:n], ACT.Gelu,
                                             bias=bf1[:, f:f + 1]).then_inc(h_kept, 1)

            @block.vector
            def _(dve):
                for t in range(NT):
                    nc.vector.tensor_tensor(H[:, t, :], H[:, t, :], HH[:, t, :], ALU.add).then_inc(added, 1)
                for t in range(NT):
                    n, _ = tokens_of(t)
                    dve.wait_ge(added, t + 1)
                    dve.wait_ge(o_ready, t + 1)
                    nc.vector.tensor_tensor(H[0:n, t, :], H[0:n, t, :], o_ps[0:n, t % 2, 0:D], ALU.add).then_inc(o_kept, 1)


RH, DQK, DV = 6, 128, 64
RQ, RV = RH * DQK, RH * DV
RC = RV // P
SCALE_BASE = 512.0


def retention_tables():
    pos = np.arange(1, N).astype(np.float64)
    half = DQK // 2
    inv_freq = (1.0 / 10000.0 ** (np.arange(half, dtype=np.float32) / np.float32(half))).astype(np.float32)
    angles = (pos.astype(np.float32)[None, :] * inv_freq[:, None]).astype(np.float32).astype(np.float64)
    zeta = (np.arange(half) + half) / DQK
    rot = np.zeros((DQK, 2, 2, T), np.float32)
    for x, sign in enumerate((1.0, -1.0)):
        decay = zeta[:, None] ** (sign * pos[None, :] / SCALE_BASE)
        c, s = np.cos(angles) * decay, np.sin(angles) * decay
        rot[:, x, 0] = np.concatenate([c, c])
        rot[:, x, 1] = np.concatenate([s, -s])
    gamma = 1.0 - 2.0 ** -(5.0 + np.arange(RH))
    rows = (1 - gamma[:, None] ** (pos + 1)) / (1 - gamma[:, None])
    q = gamma[:, None] ** pos / np.sqrt(rows)
    k = gamma[:, None] ** -pos * DQK ** -0.5

    def by_tile(v):
        return np.ascontiguousarray(v.reshape(RH, TPB, P).transpose(2, 0, 1)).astype(np.float32)
    return rot, by_tile(q), by_tile(k)


def retention_stage(nc, sem, make_sb, make_ps, A, H, ident, ones):
    with ExitStack() as ctx:
        sb = make_sb(ctx)
        R_ = {}
        R_["XT"] = sb("t_xT", [HALF, 2, NTOK])
        for k, n in (("q", RQ), ("k", RQ), ("v", RV), ("g", RV)):
            R_["W" + k] = sb("t_W" + k, [HALF, 2, n])
        R_["Wo"] = sb("t_Wo", [P, RC, D])
        R_["gnw"], R_["gnb"] = sb("t_gnw", [P, RV]), sb("t_gnb", [P, RV])
        R_["rot"] = sb("t_rot", [P, 2, 2, T])
        R_["qd"], R_["kd"] = sb("t_qd", [P, RH, TPB]), sb("t_kd", [P, RH, TPB])
        for name, n in (("OC", RV), ("GC", RV), ("centredC", RV), ("rstdC", RH), ("csum", RH)):
            R_[name] = sb("t_" + name, [B, n])
        R_["QC"] = sb("t_QC", [P, 2, RH, B])
        loads = [
            *[(R_["W" + k][:], halves_of(A["L1_attn_W" + k])) for k in "qkvg"],
            (R_["Wo"][:], A["L1_attn_Wo"].rearrange("(c p) n -> p c n", p=P)),
            (R_["gnw"][:], A["L1_attn_gn_weight"].partition_broadcast(P)),
            (R_["gnb"][:], A["L1_attn_gn_bias"].partition_broadcast(P)),
            (R_["rot"][:], A["rot"]), (R_["qd"][:], A["query_decay"]), (R_["kd"][:], A["key_decay"])]
        with ExitStack() as xctx:
            X = make_sb(xctx)("t_x", [P, NT, D])
            norm_stage(nc, sem, make_sb, make_ps, "tn", H, X, R_["XT"], ident, loads=loads)
        retention_cls_outputs(nc, sem, make_sb, make_ps, R_, ones)
        retention_heads(nc, sem, make_sb, make_ps, R_, H, ident, ones)
        retention_cls_rows(nc, sem, make_sb, make_ps, R_, H, ident)


def retention_cls_outputs(nc, sem, make_sb, make_ps, R_, ones):
    with ExitStack() as ctx:
        sb, ps = make_sb(ctx), make_ps(ctx)
        prod = sb("tc_prod", [P, RH, B])
        dots = sb("tc_dots", [B, RH])
        q_ps, v_ps, g_ps, d_ps = (ps("tc_" + k, [P, 512]) for k in "qvgd")
        qk_ready, kept, prod_ready, v_ready = sem("tc_qk_ready"), sem("tc_kept"), sem("tc_prod_ready"), sem("tc_v_ready")
        g_ready, dots_ready, dots_kept, out_ready = (sem("tc_g_ready"), sem("tc_dots_ready"), sem("tc_dots_kept"),
                                                     sem("tc_out_ready"))
        XT, QC, OC, csum = R_["XT"], R_["QC"], R_["OC"], R_["csum"]
        with nc.Block() as block:
            @block.tensor
            def _(pe):
                for x, w in enumerate("qk"):
                    for head in range(RH):
                        c = (x * RH + head) * B
                        for h in range(2):
                            last = nc.tensor.matmul(q_ps[:, c:c + B], R_["W" + w][:, h, head * DQK:(head + 1) * DQK],
                                                    XT[:, h, B * T:NTOK], start=(h == 0), stop=(h == 1))
                last.then_inc(qk_ready, 1)
                for w, dst, ready in (("v", v_ps, v_ready), ("g", g_ps, g_ready)):
                    for h in range(2):
                        last = nc.tensor.matmul(dst[0:B, 0:RV], XT[:, h, B * T:NTOK], R_["W" + w][:, h, :], start=(h == 0),
                                                stop=(h == 1))
                    last.then_inc(ready, 1)
                pe.wait_ge(prod_ready, 1)
                for head in range(RH):
                    last = nc.tensor.matmul(d_ps[0:B, head:head + 1], prod[:, head, :], ones[:, 0:1], start=True, stop=True)
                last.then_inc(dots_ready, 1)

            @block.scalar
            def _(act):
                act.wait_ge(g_ready, 1)
                nc.scalar.activation(R_["GC"][:], g_ps[0:B, 0:RV], ACT.Silu)

            @block.vector
            def _(dve):
                nc.vector.memset(R_["centredC"][:], 0.0)
                nc.vector.memset(R_["rstdC"][:], 0.0)
                dve.wait_ge(qk_ready, 1)
                nc.vector.tensor_copy(QC[:].rearrange("p x h b -> p (x h b)"), q_ps[:, 0:2 * RH * B]).then_inc(kept, 1)
                dve.wait_ge(kept, 1)
                nc.vector.tensor_tensor(prod[:], QC[:, 0], QC[:, 1], ALU.mult).then_inc(prod_ready, 1)
                dve.wait_ge(dots_ready, 1)
                nc.vector.tensor_scalar(dots[:], d_ps[0:B, 0:RH], float(DQK) ** -0.5, None, ALU.mult).then_inc(dots_kept, 1)
                dve.wait_ge(dots_kept, 1)
                dve.wait_ge(v_ready, 1)
                by_head = OC[:].rearrange("b (h d) -> b h d", h=RH)
                nc.vector.tensor_tensor(by_head, v_ps[0:B, 0:RV].rearrange("b (h d) -> b h d", h=RH),
                                        dots[:].unsqueeze(2).broadcast_to((B, RH, DV)), ALU.mult).then_inc(out_ready, 1)
                dve.wait_ge(out_ready, 1)
                nc.vector.reduce_sum(csum[:], by_head, AX_X)


def retention_heads(nc, sem, make_sb, make_ps, R_, H, ident, ones):
    STEPS = RH * (B + 1)
    ITEMS = {-1: [("v", 0, t) for t in range(TPB)] + [("vc", 0, 0)] + [("g", 0, t) for t in range(TPB)]}
    for u in range(STEPS):
        b, head = divmod(u, RH)
        done, coming = b - 1, b + 1
        ITEMS[u] = []
        if done >= 0:
            ITEMS[u] += {1: [("sum", done, 0)], 2: [("square", done, 0)], 4: [("yt", done, c) for c in range(RC)],
                         5: [("h", done, t) for t in range(TPB)]}.get(head, [])
        if coming < B:
            ITEMS[u] += {3: [("v", coming, t) for t in range(TPB)] + [("vc", coming, 0)],
                         4: [("g", coming, t) for t in range(TPB)]}.get(head, [])
    ORDER = [item for u in range(-1, STEPS) for item in ITEMS[u]]
    USE = {item: n for n, item in enumerate(ORDER)}
    BY_ACT = ("g", "yt")

    def kept(item):
        return 1 + sum((a[0] in BY_ACT) == (item[0] in BY_ACT) for a in ORDER[:USE[item]])

    with ExitStack() as ctx:
        sb, ps = make_sb(ctx), make_ps(ctx)
        causal = sb("t_causal", [P, P])
        V, G, O = sb("t_V", [P, 2, TPB, RV]), sb("t_G", [P, 2, TPB, RV]), sb("t_O", [P, 2, TPB, RV])
        VC = sb("t_VC", [1, 2, RV])
        main = sb("t_main", [P, 2, T])
        cross = sb("t_cross", [P, 2, T])
        turned = sb("t_turned", [P, 2, 2, T])
        S = sb("t_S", [P, 2, TPB, T])
        SC = sb("t_SC", [1, 2, T])
        squares, squaresC = sb("t_squares", [P, TPB, RV]), sb("t_squaresC", [B, RV])
        centred = sb("t_cls_centred", [B, RV])
        sums, cls_sums = sb("t_sums", [P, RH]), sb("t_cls_sums", [B, RH])
        mean, var = sb("t_mean", [P, RH]), sb("t_var", [P, RH])
        half_power = sb("t_half_power", [P, RH])
        gain = sb("t_gain", [P, RV])
        YT = sb("t_YT", [P, RC, T])
        p_ps = ps("t_p", [P, 2, 512])
        s_ps = ps("t_s", [P, 2, 512])
        o_ps = ps("t_o", [P, 2, 512])
        x_ps = ps("t_projected", [P, 2, 512])
        names = ("causal x_ready x_kept_dve x_kept_act qk_ready main_ready cross_ready turned s_ready s_kept diag_ready "
                 "o_ready o_kept sums_ready squares_ready rstd_ready pool_step step y_ready ").split()
        M = {n: sem("t_" + n) for n in names}
        XT, rot, qd, kd, QC, OC = (R_[k] for k in ("XT", "rot", "qd", "kd", "QC", "OC"))
        SPH = TPB + 1
        CNT = float(DV * N)

        def x_wait(engine, item):
            engine.wait_ge(M["x_ready"], USE[item] + 1)

        with nc.Block() as block:
            @block.tensor
            def _(pe):
                def project(u):
                    b, head = divmod(u, RH)
                    for x, w in enumerate("qk"):
                        if u:
                            pe.wait_ge(M["main_ready"], 2 * (u - 1) + x + 1)
                            pe.wait_ge(M["cross_ready"], 4 * (u - 1) + 2 * x + 2)
                        for h in range(2):
                            last = nc.tensor.matmul(p_ps[:, x, :], R_["W" + w][:, h, head * DQK:(head + 1) * DQK],
                                                    XT[:, h, b * T:(b + 1) * T], start=(h == 0), stop=(h == 1))
                        last.then_inc(M["qk_ready"], 1)

                def scores(u):
                    b, head = divmod(u, RH)
                    pe.wait_ge(M["turned"], 2 * u + 2)
                    q, k = turned[:, u % 2, 0, :], turned[:, u % 2, 1, :]
                    for m in range(SPH):
                        j = u * SPH + m
                        if j >= 2:
                            pe.wait_ge(M["s_kept"], j - 1)
                        if m < TPB:
                            nc.tensor.matmul(s_ps[:, j % 2, m * P:T], k[:, m * P:(m + 1) * P], q[:, m * P:T], start=True,
                                             stop=True).then_inc(M["s_ready"], 1)
                        else:
                            nc.tensor.matmul(s_ps[0:1, j % 2, :], QC[:, 1, head, b:b + 1], q, start=True,
                                             stop=True).then_inc(M["s_ready"], 1)

                def outputs(u):
                    b, head = divmod(u, RH)
                    pe.wait_ge(M["diag_ready"], TPB * (u + 1))
                    pe.wait_ge(M["s_kept"], SPH * (u + 1))
                    if head == 0:
                        pe.wait_ge(M["x_kept_dve"], kept(("vc", b, 0)))
                    if u >= 2:
                        pe.wait_ge(M["o_kept"], u - 1)
                    vh = slice(head * DV, (head + 1) * DV)
                    for t in range(TPB):
                        dst = o_ps[:, u % 2, t * DV:(t + 1) * DV]
                        for m in range(t + 1):
                            nc.tensor.matmul(dst, S[:, u % 2, m, t * P:(t + 1) * P], V[:, b % 2, m, vh], start=(m == 0),
                                             stop=False)
                        last = nc.tensor.matmul(dst, SC[:, u % 2, t * P:(t + 1) * P], VC[:, b % 2, vh], start=False, stop=True)
                    last.then_inc(M["o_ready"], 1)

                def item_product(item):
                    what, b, i = item
                    n = USE[item]
                    if n >= 2:
                        before = ORDER[n - 2]
                        pe.wait_ge(M["x_kept_act" if before[0] in BY_ACT else "x_kept_dve"], kept(before))
                    dst = x_ps[:, n % 2, :]
                    if what in ("v", "g"):
                        first = (b * TPB + i) * P
                        for h in range(2):
                            last = nc.tensor.matmul(dst[:, 0:RV], XT[:, h, first:first + P], R_["W" + what][:, h, :],
                                                    start=(h == 0), stop=(h == 1))
                    elif what == "vc":
                        for h in range(2):
                            last = nc.tensor.matmul(dst[0:1, 0:RV], XT[:, h, B * T + b:B * T + b + 1], R_["Wv"][:, h, :],
                                                    start=(h == 0), stop=(h == 1))
                    elif what in ("sum", "square"):
                        pe.wait_ge(M["sums_ready" if what == "sum" else "squares_ready"], b + 1)
                        nc.tensor.matmul(dst[:, 0:RH], ones[:], sums[:], start=True, stop=False)
                        last = nc.tensor.matmul(dst[:, 0:RH], ident[0:B, b:b + 1].broadcast_to((B, P)),
                                                R_["csum"][:] if what == "sum" else cls_sums[:], start=False, stop=True)
                    elif what == "yt":
                        pe.wait_ge(M["y_ready"], b + 1)
                        for t in range(TPB):
                            last = nc.tensor.transpose(dst[:, t * P:(t + 1) * P], O[:, b % 2, t, i * P:(i + 1) * P], ident[:])
                    else:
                        pe.wait_ge(M["x_kept_act"], kept(("yt", b, RC - 1)))
                        for c in range(RC):
                            last = nc.tensor.matmul(dst[:, 0:D], YT[:, c, i * P:(i + 1) * P], R_["Wo"][:, c, :],
                                                    start=(c == 0), stop=(c == RC - 1))
                    last.then_inc(M["x_ready"], 1)

                for u in range(-1, STEPS):
                    if u + 1 < B * RH:
                        project(u + 1)
                    if 0 <= u < B * RH:
                        scores(u)
                    if 0 <= u - 1 < B * RH:
                        outputs(u - 1)
                    for item in ITEMS[u]:
                        item_product(item)

            @block.scalar
            def _(act):
                for u in range(-1, STEPS):
                    if 0 <= u < B * RH:
                        head = u % RH
                        if u >= 2:
                            act.wait_ge(M["o_ready"], u - 1)
                        for m in range(SPH):
                            j = u * SPH + m
                            act.wait_ge(M["s_ready"], j + 1)
                            if m < TPB:
                                nc.scalar.activation(S[:, u % 2, m, m * P:T], s_ps[:, j % 2, m * P:T], ACT.Copy,
                                                     scale=kd[:, head, m:m + 1]).then_inc(M["s_kept"], 1)
                            else:
                                nc.scalar.activation(SC[:, u % 2, :], s_ps[0:1, j % 2, :], ACT.Copy,
                                                     scale=float(DQK) ** -0.5).then_inc(M["s_kept"], 1)
                    for item in ITEMS[u]:
                        what, b, i = item
                        if what == "g":
                            x_wait(act, item)
                            if b >= 2 and i == 0:
                                act.wait_ge(M["y_ready"], b - 1)
                            nc.scalar.activation(G[:, b % 2, i, :], x_ps[:, USE[item] % 2, 0:RV],
                                                 ACT.Silu).then_inc(M["x_kept_act"], 1)
                        elif what == "yt":
                            x_wait(act, item)
                            if b and i == 0:
                                act.wait_ge(M["x_ready"], USE["h", b - 1, TPB - 1] + 1)
                            nc.scalar.activation(YT[:, i, :], x_ps[:, USE[item] % 2, :], ACT.Copy).then_inc(M["x_kept_act"], 1)

            @block.gpsimd
            def _(pool):
                nc.gpsimd.memset(causal[:], 1.0).then_inc(M["causal"], 1)
                pool.wait_ge(M["causal"], 1)
                nc.gpsimd.affine_select(out=causal[:], in_=causal[:], compare_op=ALU.is_ge, fill=0.0, base=0,
                                        pattern=[[1, P]], channel_multiplier=-1).then_inc(M["causal"], 1)
                nc.gpsimd.memset(half_power[:], -0.5).then_inc(M["causal"], 1)
                pool.wait_ge(M["causal"], 3)
                for u in range(STEPS):
                    if u < B * RH:
                        for x in range(2):
                            pool.wait_ge(M["main_ready"], 2 * u + x + 1)
                            pool.wait_ge(M["cross_ready"], 4 * u + 2 * x + 2)
                            if u >= 2:
                                pool.wait_ge(M["s_ready"], SPH * (u - 1))
                            nc.gpsimd.tensor_tensor(turned[:, u % 2, x, :], main[:, x, :], cross[:, x, :],
                                                    ALU.add).then_inc(M["turned"], 1)
                    for what, b, _ in ITEMS[u]:
                        if what == "square":
                            pool.wait_ge(M["x_kept_dve"], kept((what, b, 0)))
                            nc.gpsimd.tensor_scalar(var[:], var[:], LN_EPS, None, ALU.add).then_inc(M["pool_step"], 1)
                            pool.wait_ge(M["pool_step"], b + 1)
                            nc.gpsimd.tensor_tensor(var[:], var[:], half_power[:], ALU.pow).then_inc(M["rstd_ready"], 1)

            @block.vector
            def _(dve):
                steps = Tally(M["step"])

                def then(ins):
                    dve.wait_ge(M["step"], steps.mark(ins))

                def rotate(u):
                    for x in range(2):
                        dve.wait_ge(M["qk_ready"], 2 * u + x + 1)
                        if u:
                            dve.wait_ge(M["turned"], 2 * (u - 1) + x + 1)
                        nc.vector.tensor_tensor(main[:, x, :], p_ps[:, x, :], rot[:, x, 0, :],
                                                ALU.mult).then_inc(M["main_ready"], 1)
                        for src, dst in ((slice(64, P), slice(0, 64)), (slice(0, 64), slice(64, P))):
                            nc.vector.tensor_tensor(cross[dst, x, :], p_ps[src, x, :], rot[src, x, 1, :],
                                                    ALU.mult).then_inc(M["cross_ready"], 1)

                def diagonal_blocks(u):
                    for m in range(TPB):
                        dve.wait_ge(M["s_kept"], u * SPH + m + 1)
                        diagonal = S[:, u % 2, m, m * P:(m + 1) * P]
                        nc.vector.tensor_tensor(diagonal, diagonal, causal[:], ALU.mult).then_inc(M["diag_ready"], 1)

                def keep(u):
                    b, head = divmod(u, RH)
                    dve.wait_ge(M["o_ready"], u + 1)
                    if head == 0 and b >= 2:
                        dve.wait_ge(M["x_ready"], USE["yt", b - 2, RC - 1] + 1)
                    nc.vector.tensor_tensor(O[:, b % 2, :, head * DV:(head + 1) * DV],
                                            o_ps[:, u % 2, 0:TPB * DV].rearrange("p (t d) -> p t d", t=TPB),
                                            qd[:, head, :].unsqueeze(2).broadcast_to((P, TPB, DV)),
                                            ALU.mult).then_inc(M["o_kept"], 1)

                def heads_first(x):
                    return x.rearrange("p t (h d) -> p h t d", h=RH)

                def per_head(x, n):
                    return x.unsqueeze(2).broadcast_to((n, RH, DV))

                def group_sums(b):
                    dve.wait_ge(M["o_kept"], RH * (b + 1))
                    if b:
                        dve.wait_ge(M["x_ready"], USE["square", b - 1, 0] + 1)
                    nc.vector.tensor_reduce(sums[:], heads_first(O[:, b % 2]), mybir.AxisListType.XY,
                                            ALU.add).then_inc(M["sums_ready"], 1)

                def centre(b, x):
                    nc.vector.tensor_scalar(mean[:], x[:, 0:RH], 1.0 / CNT, None, ALU.mult).then_inc(M["x_kept_dve"], 1)
                    dve.wait_ge(M["x_kept_dve"], kept(("sum", b, 0)))
                    for t in range(TPB):
                        v = O[:, b % 2, t, :].rearrange("p (h d) -> p h d", h=RH)
                        nc.vector.tensor_tensor(v, v, per_head(mean[:], P), ALU.subtract)
                    then(nc.vector.tensor_tensor(centred[:].rearrange("p (h d) -> p h d", h=RH),
                                                 OC[:].rearrange("p (h d) -> p h d", h=RH), per_head(mean[0:B, :], B),
                                                 ALU.subtract))
                    nc.vector.scalar_tensor_tensor(out=R_["centredC"][:], in0=centred[:], scalar=ident[0:B, b:b + 1],
                                                   in1=R_["centredC"][:], op0=ALU.mult, op1=ALU.add)
                    nc.vector.tensor_tensor(squaresC[:], centred[:], centred[:], ALU.mult)
                    Ob = O[:, b % 2].rearrange("p t n -> p (t n)")
                    then(nc.vector.tensor_tensor(squares[:].rearrange("p t n -> p (t n)"), Ob, Ob, ALU.mult))
                    nc.vector.reduce_sum(cls_sums[:], squaresC[:].rearrange("p (h d) -> p h d", h=RH), AX_X)
                    last = nc.vector.tensor_reduce(sums[:], heads_first(squares[:]), mybir.AxisListType.XY, ALU.add)
                    last.then_inc(M["squares_ready"], 1)

                def normalise(b):
                    dve.wait_ge(M["rstd_ready"], b + 1)
                    then(nc.vector.tensor_tensor(gain[:].rearrange("p (h d) -> p h d", h=RH),
                                                 R_["gnw"][:].rearrange("p (h d) -> p h d", h=RH), per_head(var[:], P), ALU.mult))
                    then(nc.vector.scalar_tensor_tensor(out=R_["rstdC"][:], in0=var[0:B, :], scalar=ident[0:B, b:b + 1],
                                                        in1=R_["rstdC"][:], op0=ALU.mult, op1=ALU.add))
                    y = O[:, b % 2]
                    then(nc.vector.tensor_tensor(y, y, gain[:].unsqueeze(1).broadcast_to((P, TPB, RV)), ALU.mult))
                    then(nc.vector.tensor_tensor(y, y, R_["gnb"][:].unsqueeze(1).broadcast_to((P, TPB, RV)), ALU.add))
                    dve.wait_ge(M["x_kept_act"], kept(("g", b, TPB - 1)))
                    nc.vector.tensor_tensor(y, y, G[:, b % 2], ALU.mult).then_inc(M["y_ready"], 1)

                dve.wait_ge(M["causal"], 3)
                for u in range(-1, STEPS):
                    if u + 1 < B * RH:
                        rotate(u + 1)
                    if 0 <= u < B * RH:
                        diagonal_blocks(u)
                    if 0 <= u - 1 < B * RH:
                        keep(u - 1)
                    b, head = divmod(u, RH)
                    if u >= RH and head == 0:
                        group_sums(b - 1)
                    if u >= RH and head == 3:
                        normalise(b - 1)
                    for item in ITEMS[u]:
                        what, b, i = item
                        if what in BY_ACT:
                            continue
                        x_wait(dve, item)
                        x = x_ps[:, USE[item] % 2, :]
                        if what == "v":
                            if b >= 2 and i == 0:
                                dve.wait_ge(M["o_ready"], RH * (b - 1))
                            nc.vector.tensor_copy(V[:, b % 2, i, :], x[:, 0:RV]).then_inc(M["x_kept_dve"], 1)
                        elif what == "vc":
                            nc.vector.tensor_copy(VC[:, b % 2, :], x[0:1, 0:RV]).then_inc(M["x_kept_dve"], 1)
                        elif what == "sum":
                            centre(b, x)
                        elif what == "square":
                            nc.vector.tensor_scalar(var[:], x[:, 0:RH], 1.0 / CNT, None, ALU.mult).then_inc(M["x_kept_dve"], 1)
                        else:
                            tile = b * TPB + i
                            nc.vector.tensor_tensor(H[:, tile, :], H[:, tile, :], x[:, 0:D],
                                                    ALU.add).then_inc(M["x_kept_dve"], 1)


def retention_cls_rows(nc, sem, make_sb, make_ps, R_, H, ident):
    with ExitStack() as ctx:
        sb, ps = make_sb(ctx), make_ps(ctx)
        YC = sb("tr_YC", [P, RC, B])
        t_ps, h_ps = ps("tr_t", [P, 512]), ps("tr_h", [P, 512])
        step, y_ready, t_ready, t_kept, h_ready = (sem("tr_step"), sem("tr_y_ready"), sem("tr_t_ready"), sem("tr_t_kept"),
                                                   sem("tr_h_ready"))
        with nc.Block() as block:
            @block.tensor
            def _(pe):
                pe.wait_ge(y_ready, 1)
                for c in range(RC):
                    last = nc.tensor.transpose(t_ps[:, c * B:(c + 1) * B], R_["centredC"][:, c * P:(c + 1) * P],
                                               ident[0:B, 0:B])
                last.then_inc(t_ready, 1)
                pe.wait_ge(t_kept, 1)
                for c in range(RC):
                    last = nc.tensor.matmul(h_ps[0:B, 0:D], YC[:, c, :], R_["Wo"][:, c, :], start=(c == 0), stop=(c == RC - 1))
                last.then_inc(h_ready, 1)

            @block.vector
            def _(dve):
                steps = Tally(step)

                def then(ins):
                    dve.wait_ge(step, steps.mark(ins))

                y = R_["centredC"]
                by_head = y[:].rearrange("b (h d) -> b h d", h=RH)
                then(nc.vector.tensor_tensor(by_head, by_head, R_["rstdC"][:].unsqueeze(2).broadcast_to((B, RH, DV)), ALU.mult))
                then(nc.vector.tensor_tensor(y[:], y[:], R_["gnw"][0:B, :], ALU.mult))
                then(nc.vector.tensor_tensor(y[:], y[:], R_["gnb"][0:B, :], ALU.add))
                nc.vector.tensor_tensor(y[:], y[:], R_["GC"][:], ALU.mult).then_inc(y_ready, 1)
                dve.wait_ge(t_ready, 1)
                nc.vector.tensor_copy(YC[:].rearrange("p c b -> p (c b)"), t_ps[:, 0:RC * B]).then_inc(t_kept, 1)
                dve.wait_ge(h_ready, 1)
                nc.vector.tensor_tensor(H[0:B, CLS, :], H[0:B, CLS, :], h_ps[0:B, 0:D], ALU.add)


E = 8
SPARE = (NTOK + E * (P - 1)) // P


def moe_stage(nc, sem, make_sb, make_ps, A, H, ident, ones, zeros):
    FF = 2 * F
    with ExitStack() as ctx:
        sb = make_sb(ctx)
        XT = sb("m_xT", [HALF, 2, NTOK])
        X = sb("m_x", [P, NT, D])
        router = sb("m_router", [HALF, 2, E])
        WI, WO = sb("m_wi", [HALF, E, FF]), sb("m_wo", [P, E, (F // P) * D])
        share = sb("m_share", [P, NT])
        place = sb("m_place", [P, NT], U32)
        expert = sb("m_expert", [1, SPARE], I32)
        sorted_x = nc.dram_tensor("sorted_x", (SPARE * P, D), F32, kind="Internal").ap()
        sorted_y = nc.dram_tensor("sorted_y", (SPARE * P, D), F32, kind="Internal").ap()
        router_loaded, w_loaded, cleared = sem("m_router_loaded"), sem("m_w_loaded"), sem("m_cleared")
        scattered = sem("m_scattered")

        def start_loads(sp):
            sp.dma_start(router[:], halves_of(A["L1_ffn_router_w"])).then_inc(router_loaded, 16)
            rows = sorted_x.rearrange("(p r) d -> p r d", p=P)
            for r in range(0, SPARE, ZERO_ROWS):
                n = min(SPARE - r, ZERO_ROWS)
                sp.dma_start(rows[:, r:r + n, :], zeros[:, 0:n, :]).then_inc(cleared, 16)
            for e in range(E):
                sp.dma_start(WI[:, e, :].rearrange("p (h f) -> p h f", h=2), halves_of(A["L1_ffn_wi"][e])).then_inc(w_loaded, 16)
                sp.dma_start(WO[:, e, :].rearrange("p (f n) -> p f n", n=D),
                             A["L1_ffn_wo"][e].rearrange("(f p) n -> p f n", p=P)).then_inc(w_loaded, 16)

        norm_stage(nc, sem, make_sb, make_ps, "mn", H, X, XT, ident, start=start_loads)
        switch_routing(nc, sem, make_sb, make_ps, XT, router, router_loaded, ones, share, place, expert)
        with nc.Block() as block:
            @block.gpsimd
            def _(pool):
                pool.wait_ge(cleared, 16 * -(-SPARE // ZERO_ROWS))
                for t in range(NT):
                    n, _ = tokens_of(t)
                    pool.indirect_dma_start(sorted_x, bass.IndirectOffsetOnAxis(ap=place[0:n, t:t + 1], axis=0),
                                            X[0:n, t, :], None).then_inc(scattered, 16)
                pool.wait_ge(scattered, 16 * NT)
        experts_stage(nc, sem, make_sb, make_ps, WI, WO, w_loaded, expert, sorted_x, sorted_y, ident)
        with ExitStack() as yctx:
            Y = make_sb(yctx)("m_y", [P, NT, D])
            gathered = [sem(f"m_gathered{t}") for t in range(NT)]
            with nc.Block() as block:
                @block.gpsimd
                def _(pool):
                    for t in range(NT):
                        n, _ = tokens_of(t)
                        pool.indirect_dma_start(Y[0:n, t, :], None, sorted_y,
                                                bass.IndirectOffsetOnAxis(ap=place[0:n, t:t + 1], axis=0)
                                                ).then_inc(gathered[t], 16)

                @block.vector
                def _(dve):
                    for t in range(NT):
                        n, _ = tokens_of(t)
                        dve.wait_ge(gathered[t], 16)
                        nc.vector.scalar_tensor_tensor(out=H[0:n, t, :], in0=Y[0:n, t, :], scalar=share[0:n, t:t + 1],
                                                       in1=H[0:n, t, :], op0=ALU.mult, op1=ALU.add)


def experts_stage(nc, sem, make_sb, make_ps, WI, WO, w_loaded, expert, sorted_x, sorted_y, ident):
    NF = F // P
    HF = F // 2
    with ExitStack() as ctx:
        sb, ps = make_sb(ctx), make_ps(ctx)
        X = sb("e_x", [P, SPARE, D])
        xT = sb("e_xT", [HALF, 2, 2, P])
        hid = sb("e_hid", [P, 2, F])
        hidT = sb("e_hidT", [P, 2, NF, P])
        Y = sb("e_y", [P, 4, D])
        x_ps, h_ps, t_ps, y_ps = ps("e_xp", [P, 512]), ps("e_hp", [P, 4, 512]), ps("e_tp", [P, 2, 512]), ps("e_yp", [P, 512])
        names = "x_turned x_kept h_ready h_kept turned turned_kept y_ready y_kept".split()
        M = {n: sem("e_" + n) for n in names}
        x_loaded = [sem(f"e_x_loaded{k}") for k in range(4)]
        stored = [sem(f"e_stored{k}") for k in range(4)]
        PART = (SPARE + 3) // 4
        with nc.Block() as block:
            @block.sync
            def _(sp):
                tiles = sorted_x.rearrange("(j p) d -> p j d", p=P)
                for k in range(4):
                    a, z = k * PART, min(SPARE, (k + 1) * PART)
                    sp.dma_start(X[:, a:z, :], tiles[:, a:z, :]).then_inc(x_loaded[k], 16)
                for j in range(SPARE):
                    sp.wait_ge(M["y_kept"], j + 1)
                    sp.dma_start(sorted_y[j * P:(j + 1) * P, :], Y[:, j % 4, :]).then_inc(stored[j % 4], 16)
                for k in range(4):
                    sp.wait_ge(stored[k], 16 * len(range(k, SPARE, 4)))

            @block.tensor
            def _(pe):
                def turn_inputs(j):
                    if j % PART == 0:
                        pe.wait_ge(x_loaded[j // PART], 16)
                    if j >= 1:
                        pe.wait_ge(M["x_kept"], j)
                    for h in range(2):
                        last = nc.tensor.transpose(x_ps[0:HALF, h * P:(h + 1) * P], X[:, j, h * HALF:(h + 1) * HALF], ident[:])
                    last.then_inc(M["x_turned"], 1)

                def times_wi(j, e):
                    pe.wait_ge(M["x_kept"], j + 1)
                    if j >= 2:
                        pe.wait_ge(M["h_kept"], j - 1)
                    for n in range(2):
                        for h in range(2):
                            last = nc.tensor.matmul(h_ps[:, j % 2 * 2 + n, 0:HF], xT[:, j % 2, h, :],
                                                    WI[:, bass.ds(e, 1), h * F + n * HF:h * F + (n + 1) * HF].rearrange(
                                                        "p a n -> p (a n)"), start=(h == 0), stop=(h == 1))
                    last.then_inc(M["h_ready"], 1)

                def turn_hidden(j):
                    pe.wait_ge(M["h_kept"], j + 1)
                    if j >= 1:
                        pe.wait_ge(M["turned_kept"], j)
                    for f in range(NF):
                        last = nc.tensor.transpose(t_ps[:, f // 3, f % 3 * P:(f % 3 + 1) * P], hid[:, j % 2, f * P:(f + 1) * P],
                                                   ident[:])
                    last.then_inc(M["turned"], 1)

                def times_wo(j, e):
                    pe.wait_ge(M["turned_kept"], j + 1)
                    if j >= 1:
                        pe.wait_ge(M["y_kept"], j)
                    for f in range(NF):
                        last = nc.tensor.matmul(y_ps[:, 0:D], hidT[:, j % 2, f, :],
                                                WO[:, bass.ds(e, 1), f * D:(f + 1) * D].rearrange("p a n -> p (a n)"),
                                                start=(f == 0), stop=(f == NF - 1))
                    last.then_inc(M["y_ready"], 1)

                def number(j):
                    return nc.values_load(expert[0:1, j:j + 1], engines=[mybir.EngineType.PE], min_val=0, max_val=E - 1,
                                          skip_runtime_bounds_check_because="switch_routing limits it to E - 1")

                pe.wait_ge(w_loaded, 16 * 2 * E)
                turn_inputs(0)
                turn_inputs(1)
                numbers = {0: number(0)}
                times_wi(0, numbers[0])
                for j in range(SPARE + 1):
                    if j + 2 < SPARE:
                        turn_inputs(j + 2)
                    if j + 1 < SPARE:
                        numbers[j + 1] = number(j + 1)
                        times_wi(j + 1, numbers[j + 1])
                    if j < SPARE:
                        turn_hidden(j)
                    if j:
                        times_wo(j - 1, numbers.pop(j - 1))

            @block.scalar
            def _(act):
                for j in range(SPARE + 1):
                    if j < SPARE:
                        act.wait_ge(M["h_ready"], j + 1)
                        if j >= 2:
                            act.wait_ge(M["turned"], j - 1)
                        nc.scalar.activation(hid[:, j % 2, :].rearrange("p (n f) -> p n f", n=2),
                                             h_ps[:, j % 2 * 2:j % 2 * 2 + 2, 0:HF], ACT.Relu).then_inc(M["h_kept"], 1)
                    if j:
                        act.wait_ge(M["y_ready"], j)
                        if j > 4:
                            act.wait_ge(stored[(j - 1) % 4], 16 * ((j - 1) // 4))
                        nc.scalar.activation(Y[:, (j - 1) % 4, :], y_ps[:, 0:D], ACT.Copy).then_inc(M["y_kept"], 1)

            @block.vector
            def _(dve):
                def keep_inputs(j):
                    dve.wait_ge(M["x_turned"], j + 1)
                    if j >= 2:
                        dve.wait_ge(M["h_ready"], j - 1)
                    nc.vector.tensor_copy(xT[:, j % 2].rearrange("p h n -> p (h n)"),
                                          x_ps[0:HALF, 0:2 * P]).then_inc(M["x_kept"], 1)

                keep_inputs(0)
                keep_inputs(1)
                for j in range(SPARE):
                    if j + 2 < SPARE:
                        keep_inputs(j + 2)
                    dve.wait_ge(M["turned"], j + 1)
                    if j >= 2:
                        dve.wait_ge(M["y_ready"], j - 1)
                    nc.vector.tensor_copy(hidT[:, j % 2].rearrange("p (n f) c -> p n (f c)", n=2),
                                          t_ps[:, :, 0:3 * P]).then_inc(M["turned_kept"], 1)


def switch_routing(nc, sem, make_sb, make_ps, XT, router, router_loaded, ones, share, place, expert):
    with ExitStack() as ctx:
        sb, ps = make_sb(ctx), make_ps(ctx)
        logit = sb("s_logit", [P, NT, E])
        top = sb("s_top", [P, NT])
        shifted = sb("s_shifted", [P, NT, E])
        index = sb("s_index", [P, E])
        key = sb("s_key", [P, NT, E])
        first = sb("s_first", [P, NT])
        chosen = sb("s_chosen", [P, NT, E])
        ex, exsum = sb("s_exp", [P, NT, E]), sb("s_expsum", [P, NT])
        upto = sb("s_upto", [P, P])
        prior = sb("s_prior", [P, 2, NT, E])
        per_tile = sb("s_per_tile", [P, NT, E])
        count = sb("s_count", [P, E])
        edges = sb("s_edges", [P, E, NT])
        over = sb("s_over", [P, E, NT])
        ends = sb("s_ends", [P, 2, E])
        tiles = sb("s_tiles", [P, E])
        start = sb("s_start", [P, E])
        where = sb("s_where", [P, NT, E])
        where_sum = sb("s_where_sum", [P, NT])
        number = sb("s_number", [1, SPARE, E])
        passed = sb("s_passed", [1, SPARE, E])
        number_sum = sb("s_number_sum", [1, SPARE])
        l_ps, c_ps, t_ps = ps("s_l", [P, 512]), ps("s_c", [P, 512]), ps("s_t", [P, 512])
        const, l_ready, step, chosen_ready = sem("s_const"), sem("s_l_ready"), sem("s_step"), sem("s_chosen_ready")
        shifted_ready, exp_ready, t_ready, c_ready = sem("s_shifted_ready"), sem("s_exp_ready"), sem("s_t_ready"), sem("s_c_ready")
        with nc.Block() as block:
            @block.gpsimd
            def _(pool):
                def table(x, pattern, base):
                    nc.gpsimd.iota(x[:], pattern=pattern, base=base, channel_multiplier=0,
                                   allow_small_or_imprecise_dtypes=True).then_inc(const, 1)

                table(index, [[1, E]], -E)
                table(edges, [[0, E], [P, NT]], 0)
                table(number, [[1, SPARE], [0, E]], 0)
                nc.gpsimd.memset(upto[:], 1.0).then_inc(const, 1)
                pool.wait_ge(const, 4)
                nc.gpsimd.affine_select(out=upto[:], in_=upto[:], compare_op=ALU.is_ge, fill=0.0, base=0,
                                        pattern=[[1, P]], channel_multiplier=-1).then_inc(const, 1)

            @block.tensor
            def _(pe):
                pe.wait_ge(router_loaded, 16)
                for t in range(NT):
                    n, c = tokens_of(t)
                    for h in range(2):
                        last = nc.tensor.matmul(l_ps[0:n, t * E:(t + 1) * E], XT[:, h, c:c + n], router[:, h, :],
                                                start=(h == 0), stop=(h == 1))
                last.then_inc(l_ready, 1)
                pe.wait_ge(chosen_ready, 1)
                pe.wait_ge(const, 5)
                flat = chosen[:].rearrange("p t e -> p (t e)")
                nc.tensor.matmul(t_ps[:, 0:NT * E], ones[:], flat, start=True, stop=True).then_inc(t_ready, 1)
                nc.tensor.matmul(c_ps[:, 0:NT * E], upto[:], flat, start=True, stop=True).then_inc(c_ready, 1)

            @block.scalar
            def _(act):
                act.wait_ge(shifted_ready, 1)
                nc.scalar.activation(ex[:], shifted[:], ACT.Exp).then_inc(exp_ready, 1)

            @block.vector
            def _(dve):
                steps = Tally(step)

                def then(ins):
                    dve.wait_ge(step, steps.mark(ins))

                then(nc.vector.memset(logit[:, CLS, :], 0.0))
                dve.wait_ge(l_ready, 1)
                nc.vector.tensor_copy(logit[:, 0:CLS, :], l_ps[:, 0:CLS * E].rearrange("p (t e) -> p t e", e=E))
                then(nc.vector.tensor_copy(logit[0:B, CLS, :], l_ps[0:B, CLS * E:NT * E]))
                then(nc.vector.reduce_max(top[:], logit[:], AX_X))
                top_b = top[:].unsqueeze(2).broadcast_to((P, NT, E))
                nc.vector.tensor_tensor(shifted[:], logit[:], top_b, ALU.subtract).then_inc(shifted_ready, 1)
                dve.wait_ge(const, 5)
                dve.wait_ge(shifted_ready, 1)
                index_b = index[:].unsqueeze(1).broadcast_to((P, NT, E))
                then(nc.vector.tensor_scalar(key[:], shifted[:], 0.0, None, ALU.is_equal))
                then(nc.vector.tensor_tensor(key[:], key[:], index_b, ALU.mult))
                then(nc.vector.tensor_reduce(first[:], key[:], AX_X, ALU.min))
                then(nc.vector.memset(chosen[:, CLS, :], 0.0))
                nc.vector.tensor_tensor(chosen[:, 0:CLS, :], index[:].unsqueeze(1).broadcast_to((P, CLS, E)),
                                        first[:, 0:CLS].unsqueeze(2).broadcast_to((P, CLS, E)), ALU.is_equal)
                nc.vector.tensor_scalar(chosen[0:B, CLS, :], index[0:B, :], first[0:B, CLS:NT], None,
                                        ALU.is_equal).then_inc(chosen_ready, 1)
                dve.wait_ge(exp_ready, 1)
                then(nc.vector.reduce_sum(exsum[:], ex[:], AX_X))
                nc.vector.reciprocal(share[:], exsum[:])
                dve.wait_ge(t_ready, 1)
                nc.vector.memset(prior[:, 0, 0, :], 0.0)
                nc.vector.tensor_copy(per_tile[:].rearrange("p t e -> p (t e)"), t_ps[:, 0:NT * E])
                then(nc.vector.tensor_copy(prior[:, 0, 1:NT, :].rearrange("p t e -> p (t e)"), t_ps[:, 0:(NT - 1) * E]))
                side = 0
                for gap in (1, 2, 4, 8, 16):
                    nc.vector.tensor_copy(prior[:, 1 - side, 0:gap, :], prior[:, side, 0:gap, :])
                    then(nc.vector.tensor_tensor(prior[:, 1 - side, gap:NT, :], prior[:, side, gap:NT, :],
                                                 prior[:, side, 0:NT - gap, :], ALU.add))
                    side = 1 - side
                then(nc.vector.tensor_tensor(count[:], prior[:, side, CLS, :], per_tile[:, CLS, :], ALU.add))
                then(nc.vector.tensor_tensor(over[:], count[:].unsqueeze(2).broadcast_to((P, E, NT)), edges[:], ALU.is_gt))
                then(nc.vector.reduce_sum(tiles[:], over[:], AX_X))
                then(nc.vector.tensor_copy(ends[:, 0, :], tiles[:]))
                end = 0
                for gap in (1, 2, 4):
                    nc.vector.tensor_copy(ends[:, 1 - end, 0:gap], ends[:, end, 0:gap])
                    then(nc.vector.tensor_tensor(ends[:, 1 - end, gap:E], ends[:, end, gap:E], ends[:, end, 0:E - gap], ALU.add))
                    end = 1 - end
                then(nc.vector.tensor_tensor(start[:], ends[:, end, :], tiles[:], ALU.subtract))
                then(nc.vector.tensor_scalar(start[:], start[:], float(P), -1.0, ALU.mult, ALU.add))
                then(nc.vector.tensor_tensor(passed[:], number[:], ends[0:1, end, :].unsqueeze(1).broadcast_to((1, SPARE, E)),
                                             ALU.is_ge))
                then(nc.vector.reduce_sum(number_sum[:], passed[:], AX_X))
                nc.vector.tensor_scalar(expert[:], number_sum[:], float(E - 1), None, ALU.min)
                dve.wait_ge(c_ready, 1)
                then(nc.vector.tensor_tensor(where[:].rearrange("p t e -> p (t e)"), c_ps[:, 0:NT * E],
                                             prior[:, side].rearrange("p t e -> p (t e)"), ALU.add))
                then(nc.vector.tensor_tensor(where[:], where[:], start[:].unsqueeze(1).broadcast_to((P, NT, E)), ALU.add))
                then(nc.vector.tensor_tensor(where[:], where[:], chosen[:], ALU.mult))
                then(nc.vector.reduce_sum(where_sum[:], where[:], AX_X))
                nc.vector.tensor_copy(place[:], where_sum[:])



_INS = ['x', 'cls_tok', 'L0_tok_freq_bands', 'L0_tok_W', 'L0_attn_w_qkv', 'L0_attn_w_proj', 'L0_attn_b_proj',
        'L0_ffn_g1', 'L0_ffn_b1', 'L0_ffn_g2', 'L0_ffn_b2', 'L0_ffn_Wr', 'L0_ffn_br', 'L0_ffn_Wq', 'L0_ffn_bq',
        'L0_ffn_Wk', 'L0_ffn_bk', 'L0_ffn_Wv', 'L0_ffn_bv', 'L0_ffn_Wo', 'L0_ffn_bo', 'L0_ffn_Wm', 'L0_ffn_bm',
        'L0_ffn_W1', 'L0_ffn_bf1', 'L0_ffn_W2', 'L0_ffn_bf2', 'L1_attn_Wq', 'L1_attn_Wk', 'L1_attn_Wv', 'L1_attn_Wg',
        'L1_attn_Wo', 'L1_attn_gn_weight', 'L1_attn_gn_bias', 'L1_ffn_router_w', 'L1_ffn_wi', 'L1_ffn_wo']


def kernel(**inputs):
    import concourse.bacc as _bacc
    from concourse.bass_utils import run_bass_kernel_spmd as _run

    nc = _bacc.Bacc("TRN2", target_bir_lowering=False, num_devices=1)
    arrays, A = {}, {}
    tables = dict(zip(("rot", "query_decay", "key_decay"), retention_tables()))
    for name in _INS + list(tables):
        a = np.ascontiguousarray(inputs[name] if name in _INS else tables[name])
        if a.ndim == 0:
            a = a.reshape(1)
        arrays[f"in_{name}"] = a
        A[name] = nc.dram_tensor(f"in_{name}", a.shape, mybir.dt.from_np(a.dtype), kind="ExternalInput").ap()
    out = nc.dram_tensor("out", (B, N, D), F32, kind="ExternalOutput").ap()
    build_program(nc, A, out)
    r = _run(nc, [arrays], core_ids=[0])
    return r.results[0]["out"]
```
